# Optimizing a Trainium2 kernel written in Bass

```python
import numpy as np
import jax
import jax.numpy as jnp

def _softmax(x, axis=-1):
    return jax.nn.softmax(x, axis=axis)

def _gelu(x):
    return jax.nn.gelu(x, approximate=True)

def _silu(x):
    return jax.nn.silu(x)

def _sigmoid(x):
    return jax.nn.sigmoid(x)

def _layernorm(x, axis=-1, eps=1e-05):
    m = jnp.mean(x, axis=axis, keepdims=True)
    v = jnp.var(x, axis=axis, keepdims=True)
    return (x - m) / jnp.sqrt(v + eps)

def _scatter_add(tgt, idx, src, axis=0):
    return tgt.at[idx].add(src)

def _segment_sum(src, seg, n):
    return jax.ops.segment_sum(src, seg, n)
kernel_name = 'mk_adaln_d4_jaxref_r8_f0eff5'

def setup_inputs(seed: int=0):
    np.random.seed(seed)
    _w = jnp.asarray

    def _L0_attn_setup():
        import jax, jax.numpy as jnp
        import numpy as np
        EPS = 1e-06

        def _feature_map(x):
            return jax.nn.elu(x) + 1.0
        key = jax.random.key(seed)
        ks = jax.random.split(key, 4)
        B, L, C = (4, 1024, 128)
        s = 1.0 / np.sqrt(C)
        x = jax.random.normal(ks[0], (B, L, C), dtype=jnp.float32)
        Wq = jax.random.normal(ks[1], (C, C), dtype=jnp.float32) * s
        Wk = jax.random.normal(ks[2], (C, C), dtype=jnp.float32) * s
        Wv = jax.random.normal(ks[3], (C, C), dtype=jnp.float32) * s
        bq = jnp.zeros((C,), jnp.float32)
        bk = jnp.zeros((C,), jnp.float32)
        bv = jnp.zeros((C,), jnp.float32)
        return {'x': x, 'Wq': Wq, 'bq': bq, 'Wk': Wk, 'bk': bk, 'Wv': Wv, 'bv': bv}
    _L0_attn_in = _L0_attn_setup()

    def _L0_ffn_setup():
        import jax, jax.numpy as jnp
        import numpy as np
        DM, NE, ES, ESZ = (128, 16, 4, 64)
        BATCH, SEQ = (8, 256)
        key = jax.random.key(seed)
        k = jax.random.split(key, 5)
        scale = 0.02
        return {'x': jax.random.normal(k[0], (BATCH, SEQ, DM), dtype=jnp.float32), 'controller': jax.random.normal(k[1], (DM, NE, ES), dtype=jnp.float32) * scale, 'f1': jax.random.normal(k[2], (DM, NE, ES, ESZ), dtype=jnp.float32) * scale, 'f2': jax.random.normal(k[3], (NE, ES, ESZ, DM), dtype=jnp.float32) * scale, 'bias': jax.random.normal(k[4], (NE, ES, ESZ), dtype=jnp.float32) * scale}
    _L0_ffn_in = _L0_ffn_setup()
    _L0_c = _w((lambda *s: np.random.randn(*s).astype(np.float32) * 0.05)(8, 128))
    _L0_wmod = _w((lambda *s: np.random.randn(*s).astype(np.float32) * 0.05)(128, 6 * 128) * 128 ** (-0.5))

    def _L1_attn_setup():
        import jax, jax.numpy as jnp
        import numpy as np
        B, T, C = (4, 128, 128)
        HEAD_SIZE = 64
        H = C // HEAD_SIZE
        N_LAYER, LAYER_ID = (24, 12)
        D_MIX_LORA, D_DECAY_LORA = (32, 64)
        HEAD_SIZE_DIVISOR = 8
        LN_EPS = 1e-05 * HEAD_SIZE_DIVISOR ** 2

        def _wkv6(r, k, v, w, u):

            def step(S, inp):
                r_t, k_t, v_t, w_t = inp
                y = jnp.einsum('bhj,bhji->bhi', r_t, S) + jnp.sum(r_t * u * k_t, axis=-1, keepdims=True) * v_t
                decay = jnp.exp(-jnp.exp(w_t))
                S = decay[..., None] * S + k_t[..., None] * v_t[..., None, :]
                return (S, y)
            to_t = lambda a: jnp.transpose(a, (1, 0, 2, 3))
            S0 = jnp.zeros(r.shape[:1] + (r.shape[2], r.shape[3], r.shape[3]), r.dtype)
            _, ys = jax.lax.scan(step, S0, (to_t(r), to_t(k), to_t(v), to_t(w)))
            return jnp.transpose(ys, (1, 0, 2, 3))
        key = jax.random.key(seed)
        ks = jax.random.split(key, 16)
        x = jax.random.normal(ks[0], (B, T, C), jnp.float32)
        r01 = LAYER_ID / (N_LAYER - 1)
        r10 = 1.0 - LAYER_ID / N_LAYER
        ddd = np.arange(C, dtype=np.float64) / C
        time_maa_x = jnp.asarray((1.0 - ddd ** r10).astype(np.float32))
        time_maa_w = jnp.asarray((1.0 - ddd ** r10).astype(np.float32))
        time_maa_k = jnp.asarray((1.0 - ddd ** r10).astype(np.float32))
        time_maa_v = jnp.asarray((1.0 - (ddd ** r10 + 0.3 * r01)).astype(np.float32))
        time_maa_r = jnp.asarray((1.0 - ddd ** (0.5 * r10)).astype(np.float32))
        time_maa_g = jnp.asarray((1.0 - ddd ** (0.5 * r10)).astype(np.float32))
        n = np.arange(C, dtype=np.float64)
        time_decay = jnp.asarray((-6.0 + 5.0 * (n / (C - 1)) ** (0.7 + 1.3 * r01)).astype(np.float32))
        zigzag = ((n + 1) % 3 - 1) * 0.1
        time_faaaa = jnp.asarray((r01 * (1.0 - n / (C - 1)) + zigzag).astype(np.float32)).reshape(H, HEAD_SIZE)
        u = lambda k, shp: jax.random.uniform(k, shp, jnp.float32, -0.01, 0.01)
        time_maa_w1 = u(ks[1], (C, D_MIX_LORA * 5))
        time_maa_w2 = u(ks[2], (5, D_MIX_LORA, C))
        time_decay_w1 = u(ks[3], (C, D_DECAY_LORA))
        time_decay_w2 = u(ks[4], (D_DECAY_LORA, C))
        s = 1.0 / np.sqrt(C)
        Wr = jax.random.normal(ks[5], (C, C), jnp.float32) * s
        Wk = jax.random.normal(ks[6], (C, C), jnp.float32) * s
        Wv = jax.random.normal(ks[7], (C, C), jnp.float32) * s
        Wg = jax.random.normal(ks[8], (C, C), jnp.float32) * s
        Wo = jax.random.normal(ks[9], (C, C), jnp.float32) * s
        ln_w = jnp.ones((C,), jnp.float32)
        ln_b = jnp.zeros((C,), jnp.float32)
        return dict(x=x, time_maa_x=time_maa_x, time_maa_w=time_maa_w, time_maa_k=time_maa_k, time_maa_v=time_maa_v, time_maa_r=time_maa_r, time_maa_g=time_maa_g, time_maa_w1=time_maa_w1, time_maa_w2=time_maa_w2, time_decay=time_decay, time_decay_w1=time_decay_w1, time_decay_w2=time_decay_w2, time_faaaa=time_faaaa, Wr=Wr, Wk=Wk, Wv=Wv, Wg=Wg, Wo=Wo, ln_w=ln_w, ln_b=ln_b)
    _L1_attn_in = _L1_attn_setup()

    def _L1_ffn_setup():
        import jax, jax.numpy as jnp
        import numpy as np
        TOP_K = 2
        key = jax.random.key(seed)
        k_x, k_g, k_w1, k_w2, k_w3 = jax.random.split(key, 5)
        B, S, D, H, E = (2, 64, 128, 64, 8)
        x = jax.random.normal(k_x, (B, S, D), dtype=jnp.float32)
        gate_w = jax.random.normal(k_g, (D, E), dtype=jnp.float32) * D ** (-0.5)
        w1 = jax.random.normal(k_w1, (E, D, H), dtype=jnp.float32) * 0.02
        w2 = jax.random.normal(k_w2, (E, H, D), dtype=jnp.float32) * 0.02
        w3 = jax.random.normal(k_w3, (E, D, H), dtype=jnp.float32) * 0.02
        return {'x': x, 'gate_w': gate_w, 'w1': w1, 'w2': w2, 'w3': w3}
    _L1_ffn_in = _L1_ffn_setup()
    _L1_c = _w((lambda *s: np.random.randn(*s).astype(np.float32) * 0.05)(8, 128))
    _L1_wmod = _w((lambda *s: np.random.randn(*s).astype(np.float32) * 0.05)(128, 6 * 128) * 128 ** (-0.5))

    def _L2_attn_setup():
        import jax, jax.numpy as jnp
        import numpy as np
        N_HEAD = 16
        key = jax.random.key(seed)
        k1, k2, k3 = jax.random.split(key, 3)
        B, T, C = (4, 256, 128)
        x = jax.random.normal(k1, (B, T, C), dtype=jnp.float32)
        w_qkv = jax.random.normal(k2, (C, 3 * C), dtype=jnp.float32) * (1.0 / np.sqrt(C))
        b_qkv = jnp.zeros((3 * C,), dtype=jnp.float32)
        w_out = jax.random.normal(k3, (C, C), dtype=jnp.float32) * (1.0 / np.sqrt(C))
        b_out = jnp.zeros((C,), dtype=jnp.float32)
        return {'x': x, 'w_qkv': w_qkv, 'b_qkv': b_qkv, 'w_out': w_out, 'b_out': b_out}
    _L2_attn_in = _L2_attn_setup()

    def _L2_ffn_setup():
        import jax, jax.numpy as jnp
        import numpy as np
        E = 8
        TOPK = 2
        SCALE = 2.0
        key = jax.random.key(seed)
        ks = jax.random.split(key, 12)
        B, S, D, F, R = (2, 64, 128, 512, 16)
        w = lambda k, shp: jax.random.normal(k, shp, dtype=jnp.float32) * 0.02
        return {'hidden_states': jax.random.normal(ks[0], (B, S, D), dtype=jnp.float32), 'gate_w': w(ks[1], (E, D)), 'w_gate': w(ks[2], (F, D)), 'w_up': w(ks[3], (F, D)), 'w_down': w(ks[4], (D, F)), 'A1': w(ks[5], (E, R, D)), 'B1': w(ks[6], (E, F, R)), 'A3': w(ks[7], (E, R, D)), 'B3': w(ks[8], (E, F, R)), 'A2': w(ks[9], (E, R, F)), 'B2': w(ks[10], (E, D, R))}
    _L2_ffn_in = _L2_ffn_setup()
    _L2_c = _w((lambda *s: np.random.randn(*s).astype(np.float32) * 0.05)(8, 128))
    _L2_wmod = _w((lambda *s: np.random.randn(*s).astype(np.float32) * 0.05)(128, 6 * 128) * 128 ** (-0.5))

    def _L3_attn_setup():
        import jax, jax.numpy as jnp
        import numpy as np
        H = 8
        LN_EPS = 1e-05
        key = jax.random.key(seed)
        ks = jax.random.split(key, 4)
        B, S, D = (4, 256, 128)
        x = jax.random.normal(ks[0], (B, S, D), dtype=jnp.float32)
        sc = 1.0 / np.sqrt(D)
        Wq = jax.random.normal(ks[1], (D, D), dtype=jnp.float32) * sc
        Wk = jax.random.normal(ks[2], (D, D), dtype=jnp.float32) * sc
        Wv = jax.random.normal(ks[3], (D, D * H), dtype=jnp.float32) * sc
        return {'x': x, 'Wq': Wq, 'bq': jnp.zeros((D,), jnp.float32), 'Wk': Wk, 'bk': jnp.zeros((D,), jnp.float32), 'Wv': Wv, 'bv': jnp.zeros((D * H,), jnp.float32), 'gamma': jnp.ones((D,), jnp.float32), 'beta': jnp.zeros((D,), jnp.float32)}
    _L3_attn_in = _L3_attn_setup()

    def _L3_ffn_setup():
        import jax, jax.numpy as jnp
        import numpy as np
        B, S, D, H, F = (4, 512, 128, 16, 512)
        CAP = 0.125
        ROPE_BASE = 10000.0

        def rmsnorm(x, g):
            return x * jax.lax.rsqrt(jnp.mean(x * x, -1, keepdims=True) + 1e-06) * g

        def rope(t, pos):
            hd = t.shape[-1]
            inv = 1.0 / ROPE_BASE ** (jnp.arange(0, hd, 2, dtype=jnp.float32) / hd)
            f = pos[:, None, :, None].astype(jnp.float32) * inv
            emb = jnp.concatenate([f, f], axis=-1)
            cos, sin = (jnp.cos(emb), jnp.sin(emb))
            rot = jnp.concatenate([-t[..., hd // 2:], t[..., :hd // 2]], axis=-1)
            return t * cos + rot * sin
        key = jax.random.key(seed)
        ks = jax.random.split(key, 9)
        scale = 0.02
        x = jax.random.normal(ks[0], (B, S, D), jnp.float32)
        causal = jnp.where(jnp.tril(jnp.ones((S, S), bool)), 0.0, -1000000000.0).astype(jnp.float32)
        attention_mask = jnp.broadcast_to(causal[None, None], (B, 1, S, S))
        position_ids = jnp.broadcast_to(jnp.arange(S, dtype=jnp.int32), (B, S))
        return {'x': x, 'attention_mask': attention_mask, 'position_ids': position_ids, 'router_w': jax.random.normal(ks[1], (D, 1), jnp.float32) * scale, 'router_b': jnp.zeros((1,), jnp.float32), 'wq': jax.random.normal(ks[2], (D, D), jnp.float32) * scale, 'wk': jax.random.normal(ks[3], (D, D), jnp.float32) * scale, 'wv': jax.random.normal(ks[4], (D, D), jnp.float32) * scale, 'wo': jax.random.normal(ks[5], (D, D), jnp.float32) * scale, 'w1': jax.random.normal(ks[6], (D, F), jnp.float32) * scale, 'w2': jax.random.normal(ks[7], (F, D), jnp.float32) * scale, 'ln1': jnp.ones((D,), jnp.float32), 'ln2': jnp.ones((D,), jnp.float32)}
    _L3_ffn_in = _L3_ffn_setup()
    _L3_c = _w((lambda *s: np.random.randn(*s).astype(np.float32) * 0.05)(8, 128))
    _L3_wmod = _w((lambda *s: np.random.randn(*s).astype(np.float32) * 0.05)(128, 6 * 128) * 128 ** (-0.5))
    _d = {'L0_attn_x': _L0_attn_in['x'], 'L0_attn_Wq': _L0_attn_in['Wq'], 'L0_attn_bq': _L0_attn_in['bq'], 'L0_attn_Wk': _L0_attn_in['Wk'], 'L0_attn_bk': _L0_attn_in['bk'], 'L0_attn_Wv': _L0_attn_in['Wv'], 'L0_attn_bv': _L0_attn_in['bv'], 'L0_ffn_controller': _L0_ffn_in['controller'], 'L0_ffn_f1': _L0_ffn_in['f1'], 'L0_ffn_f2': _L0_ffn_in['f2'], 'L0_ffn_bias': _L0_ffn_in['bias'], 'L0_c': _L0_c, 'L0_wmod': _L0_wmod, 'L1_attn_time_maa_x': _L1_attn_in['time_maa_x'], 'L1_attn_time_maa_w': _L1_attn_in['time_maa_w'], 'L1_attn_time_maa_k': _L1_attn_in['time_maa_k'], 'L1_attn_time_maa_v': _L1_attn_in['time_maa_v'], 'L1_attn_time_maa_r': _L1_attn_in['time_maa_r'], 'L1_attn_time_maa_g': _L1_attn_in['time_maa_g'], 'L1_attn_time_maa_w1': _L1_attn_in['time_maa_w1'], 'L1_attn_time_maa_w2': _L1_attn_in['time_maa_w2'], 'L1_attn_time_decay': _L1_attn_in['time_decay'], 'L1_attn_time_decay_w1': _L1_attn_in['time_decay_w1'], 'L1_attn_time_decay_w2': _L1_attn_in['time_decay_w2'], 'L1_attn_time_faaaa': _L1_attn_in['time_faaaa'], 'L1_attn_Wr': _L1_attn_in['Wr'], 'L1_attn_Wk': _L1_attn_in['Wk'], 'L1_attn_Wv': _L1_attn_in['Wv'], 'L1_attn_Wg': _L1_attn_in['Wg'], 'L1_attn_Wo': _L1_attn_in['Wo'], 'L1_attn_ln_w': _L1_attn_in['ln_w'], 'L1_attn_ln_b': _L1_attn_in['ln_b'], 'L1_ffn_gate_w': _L1_ffn_in['gate_w'], 'L1_ffn_w1': _L1_ffn_in['w1'], 'L1_ffn_w2': _L1_ffn_in['w2'], 'L1_ffn_w3': _L1_ffn_in['w3'], 'L1_c': _L1_c, 'L1_wmod': _L1_wmod, 'L2_attn_w_qkv': _L2_attn_in['w_qkv'], 'L2_attn_b_qkv': _L2_attn_in['b_qkv'], 'L2_attn_w_out': _L2_attn_in['w_out'], 'L2_attn_b_out': _L2_attn_in['b_out'], 'L2_ffn_gate_w': _L2_ffn_in['gate_w'], 'L2_ffn_w_gate': _L2_ffn_in['w_gate'], 'L2_ffn_w_up': _L2_ffn_in['w_up'], 'L2_ffn_w_down': _L2_ffn_in['w_down'], 'L2_ffn_A1': _L2_ffn_in['A1'], 'L2_ffn_B1': _L2_ffn_in['B1'], 'L2_ffn_A3': _L2_ffn_in['A3'], 'L2_ffn_B3': _L2_ffn_in['B3'], 'L2_ffn_A2': _L2_ffn_in['A2'], 'L2_ffn_B2': _L2_ffn_in['B2'], 'L2_c': _L2_c, 'L2_wmod': _L2_wmod, 'L3_attn_Wq': _L3_attn_in['Wq'], 'L3_attn_bq': _L3_attn_in['bq'], 'L3_attn_Wk': _L3_attn_in['Wk'], 'L3_attn_bk': _L3_attn_in['bk'], 'L3_attn_Wv': _L3_attn_in['Wv'], 'L3_attn_bv': _L3_attn_in['bv'], 'L3_attn_gamma': _L3_attn_in['gamma'], 'L3_attn_beta': _L3_attn_in['beta'], 'L3_ffn_attention_mask': _L3_ffn_in['attention_mask'], 'L3_ffn_position_ids': _L3_ffn_in['position_ids'], 'L3_ffn_router_w': _L3_ffn_in['router_w'], 'L3_ffn_router_b': _L3_ffn_in['router_b'], 'L3_ffn_wq': _L3_ffn_in['wq'], 'L3_ffn_wk': _L3_ffn_in['wk'], 'L3_ffn_wv': _L3_ffn_in['wv'], 'L3_ffn_wo': _L3_ffn_in['wo'], 'L3_ffn_w1': _L3_ffn_in['w1'], 'L3_ffn_w2': _L3_ffn_in['w2'], 'L3_ffn_ln1': _L3_ffn_in['ln1'], 'L3_ffn_ln2': _L3_ffn_in['ln2'], 'L3_c': _L3_c, 'L3_wmod': _L3_wmod}
    _x0 = _d['L0_attn_x']
    _d['L0_attn_x'] = jax.random.normal(jax.random.fold_in(jax.random.key(seed), 1), (8, 512, 128), dtype=_x0.dtype)
    del _x0
    return _d

def reference(L0_attn_x, L0_attn_Wq, L0_attn_bq, L0_attn_Wk, L0_attn_bk, L0_attn_Wv, L0_attn_bv, L0_ffn_controller, L0_ffn_f1, L0_ffn_f2, L0_ffn_bias, L0_c, L0_wmod, L1_attn_time_maa_x, L1_attn_time_maa_w, L1_attn_time_maa_k, L1_attn_time_maa_v, L1_attn_time_maa_r, L1_attn_time_maa_g, L1_attn_time_maa_w1, L1_attn_time_maa_w2, L1_attn_time_decay, L1_attn_time_decay_w1, L1_attn_time_decay_w2, L1_attn_time_faaaa, L1_attn_Wr, L1_attn_Wk, L1_attn_Wv, L1_attn_Wg, L1_attn_Wo, L1_attn_ln_w, L1_attn_ln_b, L1_ffn_gate_w, L1_ffn_w1, L1_ffn_w2, L1_ffn_w3, L1_c, L1_wmod, L2_attn_w_qkv, L2_attn_b_qkv, L2_attn_w_out, L2_attn_b_out, L2_ffn_gate_w, L2_ffn_w_gate, L2_ffn_w_up, L2_ffn_w_down, L2_ffn_A1, L2_ffn_B1, L2_ffn_A3, L2_ffn_B3, L2_ffn_A2, L2_ffn_B2, L2_c, L2_wmod, L3_attn_Wq, L3_attn_bq, L3_attn_Wk, L3_attn_bk, L3_attn_Wv, L3_attn_bv, L3_attn_gamma, L3_attn_beta, L3_ffn_attention_mask, L3_ffn_position_ids, L3_ffn_router_w, L3_ffn_router_b, L3_ffn_wq, L3_ffn_wk, L3_ffn_wv, L3_ffn_wo, L3_ffn_w1, L3_ffn_w2, L3_ffn_ln1, L3_ffn_ln2, L3_c, L3_wmod):

    def _L0_attn_ref(x, Wq, bq, Wk, bk, Wv, bv):
        import jax, jax.numpy as jnp
        import numpy as np
        EPS = 1e-06

        def _feature_map(x):
            return jax.nn.elu(x) + 1.0
        B, L, C = x.shape
        H = 8
        D = C // H
        q = x @ Wq + bq
        k = x @ Wk + bk
        v = x @ Wv + bv
        q = q.reshape(B, L, H, D)
        k = k.reshape(B, L, H, D)
        v = v.reshape(B, L, H, D)
        Q = _feature_map(q)
        K = _feature_map(k)
        v_len = jnp.asarray(L, v.dtype)
        v_scaled = v / v_len
        KV = jnp.einsum('nshd,nshv->nhdv', K, v_scaled)
        Z = 1.0 / (jnp.einsum('nlhd,nhd->nlh', Q, K.sum(axis=1)) + EPS)
        out = jnp.einsum('nlhd,nhdv,nlh->nlhv', Q, KV, Z) * v_len
        return out.reshape(B, L, C)

    def _L0_ffn_ref(x, controller, f1, f2, bias):
        import jax, jax.numpy as jnp
        import numpy as np
        DM, NE, ES, ESZ = (128, 16, 4, 64)
        BATCH, SEQ = (8, 256)
        ne = controller.shape[1]
        d = x.shape[-1]
        grouped = x.reshape(x.shape[:-2] + (-1, ne, d))
        logits = jnp.einsum('...btd,des->...btes', grouped, controller)
        tie = jnp.linspace(0.0, 1e-06, ne, dtype=logits.dtype).reshape(ne, 1, 1)
        logits = logits + tie
        perm = (logits == jnp.max(logits, axis=-3, keepdims=True)).astype(x.dtype)
        sel = jnp.einsum('...btd,...btes->...besd', grouped, perm)
        inner = jax.nn.relu(jnp.einsum('...besd,desf->...besf', sel, f1) + bias)
        inter = jnp.einsum('...besf,esfd->...besd', inner, f2)
        out = jnp.einsum('...besd,...btes->...btd', inter, perm)
        return out.reshape(x.shape)

    def _L1_attn_ref(x, time_maa_x, time_maa_w, time_maa_k, time_maa_v, time_maa_r, time_maa_g, time_maa_w1, time_maa_w2, time_decay, time_decay_w1, time_decay_w2, time_faaaa, Wr, Wk, Wv, Wg, Wo, ln_w, ln_b):
        import jax, jax.numpy as jnp
        import numpy as np
        B, T, C = (4, 128, 128)
        HEAD_SIZE = 64
        H = C // HEAD_SIZE
        N_LAYER, LAYER_ID = (24, 12)
        D_MIX_LORA, D_DECAY_LORA = (32, 64)
        HEAD_SIZE_DIVISOR = 8
        LN_EPS = 1e-05 * HEAD_SIZE_DIVISOR ** 2

        def _wkv6(r, k, v, w, u):

            def step(S, inp):
                r_t, k_t, v_t, w_t = inp
                y = jnp.einsum('bhj,bhji->bhi', r_t, S) + jnp.sum(r_t * u * k_t, axis=-1, keepdims=True) * v_t
                decay = jnp.exp(-jnp.exp(w_t))
                S = decay[..., None] * S + k_t[..., None] * v_t[..., None, :]
                return (S, y)
            to_t = lambda a: jnp.transpose(a, (1, 0, 2, 3))
            S0 = jnp.zeros(r.shape[:1] + (r.shape[2], r.shape[3], r.shape[3]), r.dtype)
            _, ys = jax.lax.scan(step, S0, (to_t(r), to_t(k), to_t(v), to_t(w)))
            return jnp.transpose(ys, (1, 0, 2, 3))
        b, t, c = x.shape
        h, n = (H, HEAD_SIZE)
        xx = jnp.concatenate([jnp.zeros_like(x[:, :1]), x[:, :-1]], axis=1) - x
        xxx = x + xx * time_maa_x
        mix = jnp.tanh(xxx @ time_maa_w1).reshape(b, t, 5, D_MIX_LORA)
        m = jnp.einsum('btsd,sdc->sbtc', mix, time_maa_w2)
        xw = x + xx * (time_maa_w + m[0])
        xk = x + xx * (time_maa_k + m[1])
        xv = x + xx * (time_maa_v + m[2])
        xr = x + xx * (time_maa_r + m[3])
        xg = x + xx * (time_maa_g + m[4])
        r = xr @ Wr
        k = xk @ Wk
        v = xv @ Wv
        g = jax.nn.silu(xg @ Wg)
        w = time_decay + jnp.tanh(xw @ time_decay_w1) @ time_decay_w2
        y = _wkv6(r.reshape(b, t, h, n), k.reshape(b, t, h, n), v.reshape(b, t, h, n), w.reshape(b, t, h, n), time_faaaa)
        mu = y.mean(-1, keepdims=True)
        var = y.var(-1, keepdims=True)
        yn = ((y - mu) / jnp.sqrt(var + LN_EPS)).reshape(b, t, c) * ln_w + ln_b
        return yn * g @ Wo

    def _L1_ffn_ref(x, gate_w, w1, w2, w3):
        import jax, jax.numpy as jnp
        import numpy as np
        TOP_K = 2
        B, S, D = x.shape
        E = gate_w.shape[1]
        xf = x.reshape(B * S, D)
        T = B * S
        logits = xf @ gate_w
        scores = jax.nn.softmax(logits, axis=-1)
        top_scores, top_idx = jax.lax.top_k(scores, TOP_K)
        scale = jnp.zeros((T, E), dtype=x.dtype).at[jnp.arange(T)[:, None], top_idx].set(top_scores)
        xs = scale.T[:, :, None] * xf[None, :, :]
        h = jax.nn.silu(jnp.einsum('etd,edh->eth', xs, w1)) * jnp.einsum('etd,edh->eth', xs, w3)
        y = jnp.einsum('eth,ehd->etd', h, w2)
        out = y.sum(axis=0)
        return out.reshape(B, S, D)

    def _L2_attn_ref(x, w_qkv, b_qkv, w_out, b_out):
        import jax, jax.numpy as jnp
        import numpy as np
        N_HEAD = 16
        B, T, C = x.shape
        H = N_HEAD
        D = C // H
        qkv = x @ w_qkv + b_qkv
        q, k, v = jnp.split(qkv, 3, axis=-1)
        q = q.reshape(B, T, H, D).transpose(0, 2, 1, 3)
        k = k.reshape(B, T, H, D).transpose(0, 2, 1, 3)
        v = v.reshape(B, T, H, D).transpose(0, 2, 1, 3)
        scale = 1.0 / np.sqrt(D).astype(np.float32)
        attn = jnp.einsum('bhqd,bhkd->bhqk', q, k) * scale
        causal = jnp.tril(jnp.ones((T, T), dtype=bool))
        attn = jnp.where(causal[None, None], attn, -jnp.inf)
        attn = jax.nn.softmax(attn, axis=-1)
        out = jnp.einsum('bhqk,bhkd->bhqd', attn, v)
        out = out.transpose(0, 2, 1, 3).reshape(B, T, C)
        return out @ w_out + b_out

    def _L2_ffn_ref(hidden_states, gate_w, w_gate, w_up, w_down, A1, B1, A3, B3, A2, B2):
        import jax, jax.numpy as jnp
        import numpy as np
        E = 8
        TOPK = 2
        SCALE = 2.0
        B, S, D = hidden_states.shape
        x = hidden_states.reshape(-1, D)
        N = x.shape[0]
        probs = jax.nn.softmax(x @ gate_w.T, axis=-1)
        vals, idx = jax.lax.top_k(probs, TOPK)
        rw = vals / jnp.sum(vals, axis=-1, keepdims=True)
        weight = jnp.zeros((N, E), x.dtype).at[jnp.arange(N)[:, None], idx].add(rw)
        common_w1 = x @ w_gate.T
        common_w3 = x @ w_up.T
        d1 = jnp.einsum('enr,efr->enf', jnp.einsum('nd,erd->enr', x, A1), B1) * SCALE
        d3 = jnp.einsum('enr,efr->enf', jnp.einsum('nd,erd->enr', x, A3), B3) * SCALE
        act = jax.nn.silu(common_w1[None] + d1) * (common_w3[None] + d3)
        out = jnp.einsum('ne,enf->nf', weight, act) @ w_down.T
        z = jnp.einsum('enf,erf->enr', act, A2)
        out = out + jnp.einsum('ne,enr,edr->nd', weight, z, B2) * SCALE
        return out.reshape(B, S, D)

    def _L3_attn_ref(x, Wq, bq, Wk, bk, Wv, bv, gamma, beta):
        import jax, jax.numpy as jnp
        import numpy as np
        H = 8
        LN_EPS = 1e-05
        B, S, D = x.shape
        dk = D // H
        mu = jnp.mean(x, axis=-1, keepdims=True)
        var = jnp.mean(jnp.square(x - mu), axis=-1, keepdims=True)
        xn = (x - mu) * jax.lax.rsqrt(var + LN_EPS) * gamma + beta
        q = (xn @ Wq + bq).reshape(B, S, H, dk).transpose(0, 2, 1, 3)
        k = (xn @ Wk + bk).reshape(B, S, H, dk).transpose(0, 2, 1, 3)
        v = (xn @ Wv + bv).reshape(B, S, H, D).transpose(0, 2, 1, 3)
        scores = jnp.einsum('bhsd,bhtd->bhst', q, k) / jnp.sqrt(jnp.asarray(dk, x.dtype))
        p = jax.nn.softmax(scores, axis=-1)
        att = jnp.einsum('bhst,bhtd->bhsd', p, v)
        out = att.reshape(S, B, D, H).sum(axis=-1).reshape(B, S, D)
        return out

    def _L3_ffn_ref(x, attention_mask, position_ids, router_w, router_b, wq, wk, wv, wo, w1, w2, ln1, ln2):
        import jax, jax.numpy as jnp
        import numpy as np
        B, S, D, H, F = (4, 512, 128, 16, 512)
        CAP = 0.125
        ROPE_BASE = 10000.0

        def rmsnorm(x, g):
            return x * jax.lax.rsqrt(jnp.mean(x * x, -1, keepdims=True) + 1e-06) * g

        def rope(t, pos):
            hd = t.shape[-1]
            inv = 1.0 / ROPE_BASE ** (jnp.arange(0, hd, 2, dtype=jnp.float32) / hd)
            f = pos[:, None, :, None].astype(jnp.float32) * inv
            emb = jnp.concatenate([f, f], axis=-1)
            cos, sin = (jnp.cos(emb), jnp.sin(emb))
            rot = jnp.concatenate([-t[..., hd // 2:], t[..., :hd // 2]], axis=-1)
            return t * cos + rot * sin
        b, s, d = x.shape
        hd = d // H
        weights = (x @ router_w)[..., 0] + router_b[0]
        k = int(CAP * s)
        topv, topi = jax.lax.top_k(weights, k)
        thr = topv[:, -1]
        sel_mask = (weights > thr[:, None]).astype(x.dtype)
        kc = k - 1
        sel_idx = jnp.sort(topi[:, :kc], axis=1)
        bidx = jnp.arange(b)[:, None]
        x_sel = x[bidx, sel_idx]
        pos_sel = position_ids[bidx, sel_idx]
        w_sel = weights[bidx, sel_idx]
        m = attention_mask[:, 0]
        m_sel = m[bidx[:, :, None], sel_idx[:, :, None], sel_idx[:, None, :]]
        hn = rmsnorm(x_sel, ln1)

        def heads(t):
            return t.reshape(b, kc, H, hd).transpose(0, 2, 1, 3)
        q = rope(heads(hn @ wq), pos_sel)
        kk = rope(heads(hn @ wk), pos_sel)
        v = heads(hn @ wv)
        sc = jnp.einsum('bhqd,bhkd->bhqk', q, kk) / np.sqrt(hd).astype(np.float32)
        sc = sc + m_sel[:, None]
        a = jax.nn.softmax(sc, axis=-1)
        o = jnp.einsum('bhqk,bhkd->bhqd', a, v).transpose(0, 2, 1, 3).reshape(b, kc, d) @ wo
        x1 = x_sel + o
        x2 = x1 + jax.nn.gelu(rmsnorm(x1, ln2) @ w1) @ w2
        proc = x2 * w_sel[..., None]
        out = jnp.zeros_like(x).at[bidx, sel_idx].set(proc)
        return out + x * (1.0 - sel_mask)[..., None]
    x = L0_attn_x
    mod = (_silu(L0_c) @ L0_wmod).reshape(L0_c.shape[0], 6, 1, -1)
    sa, ca, ga, sb, cb, gb = (mod[:, 0], mod[:, 1], mod[:, 2], mod[:, 3], mod[:, 4], mod[:, 5])
    ga = (2 * (ga >= 0) - 1) * jnp.maximum(jnp.abs(ga), 0.25)
    gb = (2 * (gb >= 0) - 1) * jnp.maximum(jnp.abs(gb), 0.25)
    h = _layernorm(x, axis=-1) * (1 + ca) + sa
    x = x + ga * _L0_attn_ref(h, L0_attn_Wq, L0_attn_bq, L0_attn_Wk, L0_attn_bk, L0_attn_Wv, L0_attn_bv)
    h = _layernorm(x, axis=-1) * (1 + cb) + sb
    x = x + gb * _L0_ffn_ref(h, L0_ffn_controller, L0_ffn_f1, L0_ffn_f2, L0_ffn_bias)
    mod = (_silu(L1_c) @ L1_wmod).reshape(L1_c.shape[0], 6, 1, -1)
    sa, ca, ga, sb, cb, gb = (mod[:, 0], mod[:, 1], mod[:, 2], mod[:, 3], mod[:, 4], mod[:, 5])
    ga = (2 * (ga >= 0) - 1) * jnp.maximum(jnp.abs(ga), 0.25)
    gb = (2 * (gb >= 0) - 1) * jnp.maximum(jnp.abs(gb), 0.25)
    h = _layernorm(x, axis=-1) * (1 + ca) + sa
    x = x + ga * _L1_attn_ref(h, L1_attn_time_maa_x, L1_attn_time_maa_w, L1_attn_time_maa_k, L1_attn_time_maa_v, L1_attn_time_maa_r, L1_attn_time_maa_g, L1_attn_time_maa_w1, L1_attn_time_maa_w2, L1_attn_time_decay, L1_attn_time_decay_w1, L1_attn_time_decay_w2, L1_attn_time_faaaa, L1_attn_Wr, L1_attn_Wk, L1_attn_Wv, L1_attn_Wg, L1_attn_Wo, L1_attn_ln_w, L1_attn_ln_b)
    h = _layernorm(x, axis=-1) * (1 + cb) + sb
    x = x + gb * _L1_ffn_ref(h, L1_ffn_gate_w, L1_ffn_w1, L1_ffn_w2, L1_ffn_w3)
    mod = (_silu(L2_c) @ L2_wmod).reshape(L2_c.shape[0], 6, 1, -1)
    sa, ca, ga, sb, cb, gb = (mod[:, 0], mod[:, 1], mod[:, 2], mod[:, 3], mod[:, 4], mod[:, 5])
    ga = (2 * (ga >= 0) - 1) * jnp.maximum(jnp.abs(ga), 0.25)
    gb = (2 * (gb >= 0) - 1) * jnp.maximum(jnp.abs(gb), 0.25)
    h = _layernorm(x, axis=-1) * (1 + ca) + sa
    x = x + ga * _L2_attn_ref(h, L2_attn_w_qkv, L2_attn_b_qkv, L2_attn_w_out, L2_attn_b_out)
    h = _layernorm(x, axis=-1) * (1 + cb) + sb
    x = x + gb * _L2_ffn_ref(h, L2_ffn_gate_w, L2_ffn_w_gate, L2_ffn_w_up, L2_ffn_w_down, L2_ffn_A1, L2_ffn_B1, L2_ffn_A3, L2_ffn_B3, L2_ffn_A2, L2_ffn_B2)
    mod = (_silu(L3_c) @ L3_wmod).reshape(L3_c.shape[0], 6, 1, -1)
    sa, ca, ga, sb, cb, gb = (mod[:, 0], mod[:, 1], mod[:, 2], mod[:, 3], mod[:, 4], mod[:, 5])
    ga = (2 * (ga >= 0) - 1) * jnp.maximum(jnp.abs(ga), 0.25)
    gb = (2 * (gb >= 0) - 1) * jnp.maximum(jnp.abs(gb), 0.25)
    h = _layernorm(x, axis=-1) * (1 + ca) + sa
    x = x + ga * _L3_attn_ref(h, L3_attn_Wq, L3_attn_bq, L3_attn_Wk, L3_attn_bk, L3_attn_Wv, L3_attn_bv, L3_attn_gamma, L3_attn_beta)
    h = _layernorm(x, axis=-1) * (1 + cb) + sb
    x = x + gb * _L3_ffn_ref(h, L3_ffn_attention_mask, L3_ffn_position_ids, L3_ffn_router_w, L3_ffn_router_b, L3_ffn_wq, L3_ffn_wk, L3_ffn_wv, L3_ffn_wo, L3_ffn_w1, L3_ffn_w2, L3_ffn_ln1, L3_ffn_ln2)
    return x

_drawn_inputs = setup_inputs


def setup_inputs(seed=0):
    import zlib

    import numpy as np

    out = dict(_drawn_inputs(seed))
    spreads = {'L0_attn_bq': (0.0, 0.8),
     'L0_attn_bk': (0.0, 0.8),
     'L0_attn_bv': (0.0, 0.1),
     'L1_attn_ln_w': (1.0, 0.565),
     'L1_attn_ln_b': (0.0, 0.514),
     'L2_attn_b_qkv': (0.0, 0.1),
     'L2_attn_b_out': (0.0, 0.1),
     'L3_attn_bq': (0.0, 2.0),
     'L3_attn_bk': (0.0, 2.0),
     'L3_attn_bv': (0.0, 0.637),
     'L3_attn_gamma': (1.0, 0.6),
     'L3_attn_beta': (0.0, 0.6),
     'L3_ffn_ln1': (1.0, 0.6),
     'L3_ffn_ln2': (1.0, 0.6)}
    factors = {'L0_attn_Wq': 7.196,
     'L0_attn_Wk': 7.119,
     'L0_attn_Wv': 3.192,
     'L0_ffn_controller': 3.695,
     'L0_ffn_f1': 3.996,
     'L0_ffn_f2': 3.64,
     'L0_ffn_bias': 8.0,
     'L1_attn_time_maa_x': 8.0,
     'L1_attn_time_maa_w': 8.0,
     'L1_attn_time_maa_w1': 8.0,
     'L1_attn_time_maa_w2': 8.0,
     'L1_attn_time_decay_w1': 8.0,
     'L1_attn_time_decay_w2': 8.0,
     'L1_attn_time_faaaa': 5.996,
     'L1_ffn_gate_w': 8.0,
     'L1_ffn_w1': 8.0,
     'L1_ffn_w2': 8.0,
     'L1_ffn_w3': 8.0,
     'L2_ffn_gate_w': 8.0,
     'L2_ffn_w_gate': 8.0,
     'L2_ffn_w_up': 8.0,
     'L2_ffn_w_down': 8.0,
     'L2_ffn_A1': 8.0,
     'L2_ffn_B1': 8.0,
     'L2_ffn_A3': 8.0,
     'L2_ffn_B3': 8.0,
     'L2_ffn_A2': 8.0,
     'L2_ffn_B2': 8.0,
     'L3_ffn_wq': 8.0,
     'L3_ffn_wk': 8.0,
     'L3_ffn_wv': 8.0,
     'L3_ffn_wo': 8.0,
     'L3_ffn_w1': 8.0,
     'L3_ffn_w2': 8.0,
     'L3_attn_Wq': 3.349,
     'L3_attn_Wk': 2.874}
    for name, (base, spread) in spreads.items():
        noise = np.random.default_rng([zlib.crc32(name.encode()), seed]).standard_normal(out[name].shape)
        drawn = base * np.exp(spread * noise) if base else spread * noise
        out[name] = jnp.asarray(drawn.astype(out[name].dtype))
    for name, factor in factors.items():
        out[name] = (out[name] * factor).astype(out[name].dtype)
    return out
```

```python
import numpy as np
import concourse.bass as bass
from concourse import mybir
from contextlib import ExitStack

F32 = mybir.dt.float32
BF16 = mybir.dt.bfloat16
I32 = mybir.dt.int32
ALU = mybir.AluOpType
ACT = mybir.ActivationFunctionType
AX = mybir.AxisListType

B, T, C = 8, 512, 128
NT = T // 128
LN_EPS = 1e-5

NE, NES, EW = 16, 64, 64
NG = T // NE
LORA, HS = 32, 64
LEVELS = (64, 32, 16, 8, 4, 2)
E1, H1 = 8, 64
E2, F2, R2 = 8, 512, 16
D16 = 16
H2N, H3N = 16, 8
MB = 4
KS = int(0.125 * T)
H4, HD4, F4 = 16, 8, 512
NEG = -1.0e30


def constant_table():
    p = np.arange(128)[:, None]
    t = np.arange(T)[None, :]
    c = np.arange(128)[None, :]
    parts = {
        "ident": (p == c),
        "mean": np.full((128, 128), 1.0 / C),
        "ones": np.ones((128, 128)),
        "same16": (p // D16 == c // D16),
        "same64": (p // HS == c // HS),
        "tie": np.broadcast_to(np.linspace(0.0, 1e-6, NE, dtype=np.float32)[np.arange(T) % NE][None], (128, T)),
        "restart": np.broadcast_to((t % 128 != 0), (128, T)),
        "half": (p // NES == (t // NE) % 2),
        "group8": (p // NE == np.arange(8)[None]),
        "head2": (p // D16 % 2 == np.arange(2)[None]) * 0.25,
        "head4": (p // HD4 % 4 == np.arange(4)[None]),
        "iota": np.broadcast_to(np.arange(2 * KS)[None] % KS, (128, 2 * KS)),
        "causal": np.where(c > p, NEG, 0.0),
        "row8": (p % 8 == np.arange(8)[None]),
        "oct16": (p // 8 == np.arange(16)[None]),
        "eps": np.broadcast_to(np.array([[LN_EPS, 64 * LN_EPS, 1e-6]], dtype=np.float32), (128, 3)),
        "index8": np.broadcast_to(np.arange(8)[None], (128, 8)),
        "freq": np.broadcast_to((1.0 / np.float32(10000.0) ** (np.arange(0, HD4, 2, dtype=np.float32) / np.float32(HD4)))[None], (128, 4)),
        "earlier": np.concatenate([(t < 128 * i + p) for i in range(NT)], axis=1),
    }
    q = np.arange(32)[None, :]
    s = p % 32
    lv = []
    for m in (16, 8, 4, 2, 1):
        lv.append((s // (2 * m) == q // (2 * m)) & (s // m % 2 == 0) & (q // m % 2 == 1))
    lv.append(s == q)
    parts["level"] = np.concatenate(lv, axis=1)
    parts["spread1"] = np.concatenate([(p == 2 * pr + c // H1) for pr in range(E1 // 2)], axis=1)
    parts["spread2"] = (p == c // R2) * 2.0
    parts["halves"] = np.full((128, 128), 0.5)
    at, off = {}, 0
    for k, v in parts.items():
        at[k] = (off, v.shape[1])
        off += v.shape[1]
    return np.concatenate([np.asarray(v, dtype=np.float32) for v in parts.values()], axis=1), at


CONST_AT = constant_table()[1]
CONST_W = sum(w for _, w in CONST_AT.values())

PER = {
    "ln_x": 8, "ln_mean": 9, "ln_xc": 9, "ln_sq": 9, "ln_var": 9, "ln_std": 9, "ln_h": 9,
    "att_s": 96, "att_max": 96, "att_exp": 96, "att_t": 96, "att_evA": 48, "att_evD": 48, "att_pv": 24,
    "x_in": 16, "x_out": 16, "mask_in": 16,
    "f0_sel": 4, "f0_up": 2, "f0_act": 2, "f0_down": 4, "f0_dev": 4, "f0_tr": 4, "f0_trev": 4,
    "a1_m": 5, "a1_x": 5, "a1_lvl": 6, "a1_q": 7, "a1_st": 3, "a1_st_new": 3,
    "f1_ab": 4, "f1_th": 4, "f1_hid": 4,
    "f0_selA": 2, "f0_selD": 2, "f0_up_b": 2, "a0_ek": 2, "a0_v": 2, "a1_a64": 2, "a1_a32": 4, "a1_diagA": 2, "a1_diagV": 2,
    "a1_lvl_e": 6, "a2_qkv": 5, "a3_qkv": 3, "f1_a": 4, "f1_y": 4, "f2_rows": 2, "f2_a": 2, "f2_z": 8, "f2_zc": 2,
    "f2_g": 8, "f2_th": 8, "f2_aw": 8,
}
SHARED = {
    "f0_tensor": ["f0_logit", "f0_ht", "f0_permt", "f0_sel", "f0_up", "f0_down", "f0_tr", "f0_out"],
    "a1_tensor": ["a1_mix", "a1_m", "a1_d1", "a1_k", "a1_v", "a1_w", "a1_r", "a1_g", "a1_kendt", "a1_s64",
                  "a1_st", "a1_sd", "a1_y", "a1_ynt", "a1_out"],
    "a1_scalar": ["a1_tanh", "a1_dt", "a1_kc", "a1_vc", "a1_ew", "a1_rc", "a1_gt", "a1_dend", "a1_kend_e", "a1_kendtok",
                  "a1_lvl_e", "a1_a64", "a1_a32", "a1_diagA", "a1_ysq", "a1_std"],
    "a1_vector": ["a1_xxx", "a1_x", "a1_kend_p", "a1_kend", "a1_lvl", "a1_q", "a1_st_new", "a1_dsum", "a1_diagV", "a1_yc", "a1_var", "a1_yn",
                  "a1_yg"],
    "f3_tensor": ["f3_ht", "f3_w", "f3_cnt", "f3_hott", "f3_xs", "f3_m1", "f3_msel", "f3_hnt", "f3_qkv", "f3_rot",
                  "f3_s", "f3_pt", "f3_o", "f3_ont", "f3_wo", "f3_h2t", "f3_u", "f3_d", "f3_back", "x_fint"],
    "f3_scalar": ["f3_htc", "f3_hottc", "f3_m1c", "f3_rt1", "f3_qkvc", "f3_p", "f3_ptc", "f3_ontc", "f3_rt2", "f3_th", "x_fin"],
    "f3_vector": ["f3_cge", "f3_hot", "f3_rope", "f3_ms1", "f3_hn", "f3_hntc", "f3_ro", "f3_qk", "f3_smx", "f3_on", "f3_ms2", "f3_h2",
                  "f3_h2tc", "f3_gu", "f3_g", "f3_proc", "x_done"],
}
PLACE = {}
for _sem, _names in SHARED.items():
    _n = 0
    for _name in _names:
        PLACE[_name] = (_sem, _n)
        _n += PER.get(_name, 1)
    for _name in _names:
        PLACE[_name] += (_n,)
STEPS = {"vector": 178, "scalar": 1}


def build(nc, d, out):
    with ExitStack() as ctx:
        def sb(name, shape, dt=F32):
            return ctx.enter_context(nc.sbuf_tensor(name, shape, dt))

        sems = {}

        def sem(name):
            name = PLACE.get(name, (name,))[0]
            if name not in sems:
                sems[name] = ctx.enter_context(nc.semaphore(name))
            return sems[name]

        ps = [ctx.enter_context(nc.psum_tensor(f"bank{i}", [128, 512], F32)) for i in range(8)]

        const = sb("const", [128, CONST_W])

        def k(name):
            o, w = CONST_AT[name]
            return const[:, o:o + w]

        ident, mean_m, ones = k("ident"), k("mean"), k("ones")
        identb = sb("identb", [128, 128], BF16)
        causalb = sb("causalb", [128, 128], BF16)

        vec_rows = sb("vec_rows", [20, 128])
        vecs = sb("vecs", [128, 20])
        VEC = ["L0_attn_bq", "L1_attn_time_maa_x", "L1_attn_time_maa_w", "L1_attn_time_maa_k",
               "L1_attn_time_maa_v", "L1_attn_time_maa_r", "L1_attn_time_maa_g", "L1_attn_time_decay",
               "L1_attn_time_faaaa", "L1_attn_ln_w", "L1_attn_ln_b", "L2_attn_b_out", "L3_attn_bq",
               "L3_attn_bk", "L3_attn_gamma", "L3_attn_beta", "L3_ffn_ln1", "L3_ffn_ln2", "bq2", "bk2"]

        def vec(name):
            i = VEC.index(name)
            return vecs[:, i:i + 1]

        bias_row = sb("bias_row", [1, 1409])
        wq0 = sb("wq0", [128, 128])
        wkv0 = sb("wkv0", [128, 256])
        ctl = sb("ctl", [128, 128])
        f1 = sb("f1", [128, NES, EW])
        f2 = sb("f2", [128, NES // 2, 128])
        bias0 = sb("bias0", [128, NES // 2])
        bias0_rows = sb("bias0_rows", [32, 128])
        wide = sb("wide", [128, 4, NT, 512])
        big = [wide[:, i] for i in range(4)]
        wmod = wide[:, 2:4].rearrange("p a b c -> p (a b c)")[:, 0:3072].rearrange("p (l n) -> p l n", l=4)
        wv3_wide = big[3][:, 2:4, :]
        c_rows = sb("c_rows", [32, 128])
        silu_c = sb("silu_c", [128, 32])
        silu_t = sb("silu_t", [128, 32])
        mods = sb("mods", [128, 24, 8])
        mtmp = sb("mtmp", [128, 4, 8])
        mod_now = sb("mod_now", [128, 24])
        w1mix = sb("w1mix", [128, 160])
        w2mix = sb("w2mix", [128, 128])
        w2mix4 = sb("w2mix4", [32, 128])
        dw1 = sb("dw1", [128, 64])
        dw2 = sb("dw2", [64, 128])
        w5 = sb("w5", [128, 5, 128])
        gw1 = sb("gw1", [128, 8])
        w1s = sb("w1s", [128, E1, H1])
        w3s = sb("w3s", [128, E1, H1])
        w2s = sb("w2s", [128, E1 // 2, 128])
        wqkv2 = sb("wqkv2", [128, 384])
        wout2 = sb("wout2", [128, 128])
        raw = wide[:, 0:2].rearrange("p a b c -> p (a b c)")[:, 0:27 * 128].rearrange("p (n c) -> p n c", c=128)
        gate2_rows = sb("gate2_rows", [8, 128])
        turned = sb("turned", [128, 27, 128])
        gate2 = sb("gate2", [128, 8])
        WG, WU, WD, B1, B3, A2, A1, A3, B2 = 0, 4, 8, 12, 16, 20, 24, 25, 26
        wqk3 = sb("wqk3", [128, 256])
        wv3 = sb("wv3", [128, 128])
        bv3 = sb("bv3", [1, 128])
        router = sb("router", [128, 1])
        router_bc = sb("router_bc", [128, 128])
        router_b = sb("router_b", [128, 1])
        wqkv4 = sb("wqkv4", [128, 384])
        wo4 = sb("wo4", [128, 128])
        w14 = sb("w14", [128, 512])
        w24 = sb("w24", [128, 4, 128])
        pos_i = sb("pos_i", [16, 128], I32)
        pos_f = sb("pos_f", [16, 128])
        pos_c = sb("pos_c", [128, 16])
        ang = sb("ang", [128, 16, 8])
        angt = sb("angt", [128, 16, 8])
        rope = sb("rope", [128, 8, NT, 8])

        x_tok = sb("x_tok", [128, NT, 128])
        x_fin = sb("x_fin", [128, NT, 128])
        X = sb("X", [128, T])
        xc = sb("xc", [128, T])
        sq = sb("sq", [128, T])
        rstd = sb("rstd", [128, T])
        hp = sb("hp", [128, T + 1])
        h = hp[:, 1:T + 1]
        w = [sb(f"tile{i}", [128, T]) for i in range(12)]
        xl = [big[1 + i // 4][:, i % 4, :] for i in range(len(LEVELS))]
        scoresT = sb("scoresT", [128, 8, 128])
        state = sb("state", [128, NT, 128])
        small = sb("small", [128, 512])
        v1 = sb("v1", [128, NT, 129])
        shifted = sb("shifted", [128, NT, 128])
        ksum = sb("ksum", [128, 1])

        seen = {"vector": 0, "scalar": 0}
        ahead = {"vector": 0, "scalar": 0}

        def at(it, name, n=None):
            n = PER.get(name, 1) if n is None else n
            before, per = PLACE[name][1:] if name in PLACE else (0, PER.get(name, 1))
            return it * per + before + n

        def step(it, engine):
            seen[engine] += 1
            return seen[engine] if it is None else it * STEPS[engine] + ahead[engine] + seen[engine]

        def enter(engine):
            ahead[engine], seen[engine] = seen[engine], 0

        def ln_pe(pe, it, n):
            if n == 8:
                pe.wait_ge(sem("ln_h"), at(it, "ln_h", 7))
            else:
                pe.wait_ge(sem("ln_x"), at(it, "ln_x", min(n, 8)))
            nc.tensor.matmul(ps[0][:], mean_m, h if n == 8 else X[:], start=True, stop=True).then_inc(sem("ln_mean"), 1)
            pe.wait_ge(sem("ln_sq"), at(it, "ln_sq", n))
            nc.tensor.matmul(ps[1][:], mean_m, sq[:], start=True, stop=True).then_inc(sem("ln_var"), 1)

        def ln_act(act, it, n):
            act.wait_ge(sem("ln_xc"), at(it, "ln_xc", n))
            nc.scalar.activation(sq[:], xc[:], ACT.Square).then_inc(sem("ln_sq"), 1)
            act.wait_ge(sem("ln_var"), at(it, "ln_var", n))
            nc.scalar.activation(rstd[:], ps[1][:], ACT.Sqrt, bias=k("eps")[:, 0:1]).then_inc(sem("ln_std"), 1)

        def ln_dve(dve, it, n, src, scale, bias):
            dve.wait_ge(sem("ln_mean"), at(it, "ln_mean", n))
            nc.vector.tensor_tensor(xc[:], src, ps[0][:], ALU.subtract).then_inc(sem("ln_xc"), 1)
            dve.wait_ge(sem("ln_xc"), at(it, "ln_xc", n))
            dve.wait_ge(sem("ln_std"), at(it, "ln_std", n))
            nc.vector.reciprocal(rstd[:], rstd[:]).then_inc(sem("vector_step"), 1)
            dve.wait_ge(sem("vector_step"), step(it, "vector"))
            nc.vector.tensor_tensor(xc[:], xc[:], rstd[:], ALU.mult).then_inc(sem("vector_step"), 1)
            dve.wait_ge(sem("vector_step"), step(it, "vector"))
            nc.vector.tensor_scalar(h, xc[:], scale, bias, ALU.mult, ALU.add).then_inc(sem("ln_h"), 1)
            dve.wait_ge(sem("ln_h"), at(it, "ln_h", n))

        def mod(layer, j):
            i = 6 * layer + j
            return mod_now[:, i:i + 1]

        Q0, K0, e0, t0 = w[0], w[1], w[2], w[3]
        kvm, ksm = w[4], w[5]

        def a0_pe(pe, it):
            pe.wait_ge(sem("ln_h"), at(it, "ln_h", 1))
            nc.tensor.matmul(ps[2][:], wq0[:], h, start=True, stop=True).then_inc(sem("a0_q"), 1)
            for t in range(NT):
                o = ps[3 + t // 2][:, t % 2 * 256:t % 2 * 256 + 256]
                nc.tensor.matmul(o, h[:, 128 * t:128 * t + 128], wkv0[:], start=True, stop=False)
                i = nc.tensor.matmul(o, ones[0:1, :], bias_row[0:1, 0:256], start=False, stop=True)
            i.then_inc(sem("a0_kv"), 1)
            pe.wait_ge(sem("a0_kf"), at(it, "a0_kf"))
            pe.wait_ge(sem("a0_v"), at(it, "a0_v"))
            for t in range(NT):
                i = nc.tensor.matmul(ps[5][:, 0:129], K0[:, 128 * t:128 * t + 128], v1[:, t, :],
                                     start=(t == 0), stop=(t == NT - 1))
            i.then_inc(sem("a0_outer"), 1)
            pe.wait_ge(sem("a0_kvm"), at(it, "a0_kvm"))
            nc.tensor.matmul(ps[6][:], kvm[:, 0:128], Q0[:], start=True, stop=True)
            nc.tensor.matmul(ps[7][:], ksm[:, 0:128], Q0[:], start=True, stop=True).then_inc(sem("a0_out"), 1)

        def a0_act(act, it):
            act.wait_ge(sem("a0_q"), at(it, "a0_q"))
            nc.scalar.activation(e0[:], ps[2][:], ACT.Exp, bias=vec("L0_attn_bq")).then_inc(sem("a0_eq"), 1)
            act.wait_ge(sem("a0_kv"), at(it, "a0_kv"))
            for half in range(2):
                kp = ps[3 + half][:].rearrange("p (t n) -> p t n", t=2)
                act.activation(sq[:, 256 * half:256 * half + 256].rearrange("p (t n) -> p t n", t=2),
                               kp[:, :, 0:128], ACT.Exp).then_inc(sem("a0_ek"), 1)
                act.activation(v1[:, 2 * half:2 * half + 2, 0:128], kp[:, :, 128:256], ACT.Copy).then_inc(sem("a0_v"), 1)

        def a0_dve(dve, it):
            dve.wait_ge(sem("a0_eq"), at(it, "a0_eq"))
            nc.vector.tensor_scalar(t0[:], ps[2][:], vec("L0_attn_bq"), 0.0, ALU.add, ALU.max).then_inc(sem("vector_step"), 1)
            dve.wait_ge(sem("vector_step"), step(it, "vector"))
            nc.vector.scalar_tensor_tensor(out=Q0[:], in0=e0[:], scalar=1.0, in1=t0[:], op0=ALU.min, op1=ALU.add).then_inc(sem("vector_step"), 1)
            dve.wait_ge(sem("vector_step"), step(it, "vector"))
            dve.wait_ge(sem("a0_ek"), at(it, "a0_ek"))
            dve.wait_ge(sem("a0_v"), at(it, "a0_v"))
            for half in range(2):
                kp = ps[3 + half][:].rearrange("p (t n) -> p t n", t=2)
                nc.vector.tensor_scalar(t0[:, 256 * half:256 * half + 256].rearrange("p (t n) -> p t n", t=2),
                                                kp[:, :, 0:128], 0.0, None, ALU.max).then_inc(sem("vector_step"), 1)
                dve.wait_ge(sem("vector_step"), step(it, "vector"))
            nc.vector.scalar_tensor_tensor(out=K0[:], in0=sq[:], scalar=1.0, in1=t0[:], op0=ALU.min, op1=ALU.add).then_inc(sem("a0_kf"), 1)
            dve.wait_ge(sem("a0_kf"), at(it, "a0_kf"))
            dve.wait_ge(sem("a0_outer"), at(it, "a0_outer"))
            nc.vector.tensor_copy(ksum[:], ps[5][:, 128:129]).then_inc(sem("vector_step"), 1)
            dve.wait_ge(sem("vector_step"), step(it, "vector"))
            nc.vector.tensor_tensor(kvm[:, 0:128], ps[5][:, 0:128], k("same16"), ALU.mult).then_inc(sem("vector_step"), 1)
            dve.wait_ge(sem("vector_step"), step(it, "vector"))
            nc.vector.tensor_scalar(ksm[:, 0:128], k("same16"), ksum[:, 0:1], None, ALU.mult).then_inc(sem("a0_kvm"), 1)
            dve.wait_ge(sem("a0_kvm"), at(it, "a0_kvm"))
            dve.wait_ge(sem("a0_out"), at(it, "a0_out"))
            nc.vector.tensor_scalar(t0[:], ps[7][:], 1e-6, None, ALU.add).then_inc(sem("vector_step"), 1)
            dve.wait_ge(sem("vector_step"), step(it, "vector"))
            nc.vector.reciprocal(e0[:], t0[:]).then_inc(sem("vector_step"), 1)
            dve.wait_ge(sem("vector_step"), step(it, "vector"))
            nc.vector.tensor_tensor(t0[:], ps[6][:], e0[:], ALU.mult).then_inc(sem("vector_step"), 1)
            dve.wait_ge(sem("vector_step"), step(it, "vector"))
            nc.vector.scalar_tensor_tensor(out=X[:], in0=t0[:], scalar=mod(0, 2), in1=X[:], op0=ALU.mult, op1=ALU.add).then_inc(sem("ln_x"), 1)
            dve.wait_ge(sem("ln_x"), at(it, "ln_x", 2))

        permT, permBD, lg = w[0], w[1], w[2]
        gmax = small[:, 0:NG]
        htok = w[3]
        bd = big[0]
        sel = big[1][:].rearrange("p a b -> p (a b)").rearrange("p (s g) -> p s g", s=NES)
        inner = big[2][:, 0:2, :].rearrange("p a b -> p (a b)").rearrange("p (q g) -> p q g", q=NES // 2)
        inter = big[3][:].rearrange("p a b -> p (a b)").rearrange("p (g s) -> p g s", g=NG)
        inter_tok = big[0][:].rearrange("p a b -> p (a b)").rearrange("p (n c) -> p n c", c=128)

        def f0_pe(pe, it):
            pe.wait_ge(sem("ln_h"), at(it, "ln_h", 2))
            nc.tensor.matmul(ps[2][:], ctl[:], h, start=True, stop=True).then_inc(sem("f0_logit"), 1)
            for t in range(NT):
                i = nc.tensor.transpose(ps[3][:, 128 * t:128 * t + 128], h[:, 128 * t:128 * t + 128], ident)
            i.then_inc(sem("f0_ht"), 1)
            pe.wait_ge(sem("f0_perm"), at(it, "f0_perm"))
            for t in range(NT):
                i = nc.tensor.transpose(ps[0][:, 128 * t:128 * t + 128], permT[:, 128 * t:128 * t + 128], ident)
            i.then_inc(sem("f0_permt"), 1)
            pe.wait_ge(sem("f0_htok"), at(it, "f0_htok"))
            for t in range(NT):
                pe.wait_ge(sem("f0_bd"), at(it, "f0_bd"))
                i = nc.tensor.matmul(ps[4 + t][:], htok[:, 128 * t:128 * t + 128], bd[:, t, :], start=True, stop=True)
                i.then_inc(sem("f0_sel"), 1)
            pe.wait_ge(sem("f0_selA"), at(it, "f0_selA"))
            pe.wait_ge(sem("f0_selD"), at(it, "f0_selD"))
            for half in range(2):
                for q in range(16 * half, 16 * half + 16):
                    for e in range(2):
                        i = nc.tensor.matmul(ps[half][64 * e:64 * e + 64, 32 * (q % 16):32 * (q % 16) + 32],
                                             f1[:, 2 * q + e, :], sel[:, 2 * q + e, :], start=True, stop=True,
                                             skip_group_check=True)
                i.then_inc(sem("f0_up"), 1)
            for half in range(2):
                pe.wait_ge(sem("f0_act"), at(it, "f0_act", half + 1))
                for e in range(2):
                    for q in range(16 * half, 16 * half + 16):
                        i = nc.tensor.matmul(ps[2 + 2 * half + e][:, 32 * (q % 16):32 * (q % 16) + 32],
                                             f2[64 * e:64 * e + 64, q, :], inner[64 * e:64 * e + 64, q, :],
                                             start=True, stop=True)
                    i.then_inc(sem("f0_down"), 1)
            pe.wait_ge(sem("f0_dev"), at(it, "f0_dev"))
            for n in range(4):
                for m in range(4):
                    i = nc.tensor.transpose(ps[n + (0 if n < 2 else 4)][:, 128 * m:128 * m + 128],
                                            inter[:, 2 * (4 * n + m):2 * (4 * n + m) + 2, :].rearrange("p g s -> p (g s)"), ident)
                i.then_inc(sem("f0_tr"), 1)
            pe.wait_ge(sem("f0_trev"), at(it, "f0_trev"))
            for n in range(NG // 2):
                i = nc.tensor.matmul(ps[2][:, 32 * n:32 * n + 32], inter_tok[:, n, :], permBD[:, 32 * n:32 * n + 32],
                                     start=True, stop=True)
            i.then_inc(sem("f0_out"), 1)

        def f0_act(act, it):
            act.wait_ge(sem("f0_ht"), at(it, "f0_ht"))
            nc.scalar.activation(htok[:], ps[3][:], ACT.Copy).then_inc(sem("f0_htok"), 1)
            for t in (0, 2):
                act.wait_ge(sem("f0_sel"), at(it, "f0_sel", t + 1))
                nc.scalar.activation(sel[:, :, 8 * t:8 * t + 8], ps[4 + t][:].rearrange("p (g s) -> p s g", g=8), ACT.Copy).then_inc(sem("f0_selA"), 1)
            for half in range(2):
                act.wait_ge(sem("f0_up_b"), at(it, "f0_up_b", half + 1))
                nc.scalar.activation(inner[:, 16 * half:16 * half + 16, :], inner[:, 16 * half:16 * half + 16, :], ACT.Relu).then_inc(sem("f0_act"), 1)
            for n in range(4):
                act.wait_ge(sem("f0_down"), at(it, "f0_down", n + 1))
                half, e = n // 2, n % 2
                o = inter.rearrange("p g (q e) -> p e q g", e=2)[:, e, 16 * half:16 * half + 16, :]
                nc.scalar.activation(o, ps[2 + n][:].rearrange("p (q g) -> p q g", q=16), ACT.Copy).then_inc(sem("f0_dev"), 1)
            for n in (0, 2):
                act.wait_ge(sem("f0_tr"), at(it, "f0_tr", n + 1))
                nc.scalar.activation(inter_tok[:, 4 * n:4 * n + 4, :].rearrange("p a b -> p (a b)"),
                                            ps[n + (0 if n < 2 else 4)][:], ACT.Copy).then_inc(sem("f0_trev"), 1)

        def f0_dve(dve, it):
            dve.wait_ge(sem("f0_logit"), at(it, "f0_logit"))
            nc.vector.tensor_tensor(lg[:], ps[2][:], k("tie"), ALU.add).then_inc(sem("vector_step"), 1)
            dve.wait_ge(sem("vector_step"), step(it, "vector"))
            nc.vector.tensor_reduce(gmax, lg[:].rearrange("p (g t) -> p g t", t=NE), AX.X, ALU.max).then_inc(sem("vector_step"), 1)
            dve.wait_ge(sem("vector_step"), step(it, "vector"))
            nc.vector.tensor_tensor(permT[:].rearrange("p (g t) -> p g t", t=NE), lg[:].rearrange("p (g t) -> p g t", t=NE),
                                             gmax.rearrange("p (g o) -> p g o", o=1).broadcast_to([128, NG, NE]), ALU.is_equal).then_inc(sem("f0_perm"), 1)
            dve.wait_ge(sem("f0_perm"), at(it, "f0_perm"))
            nc.vector.tensor_tensor(permBD[:], permT[:], k("half"), ALU.mult).then_inc(sem("vector_step"), 1)
            dve.wait_ge(sem("vector_step"), step(it, "vector"))
            dve.wait_ge(sem("f0_permt"), at(it, "f0_permt"))
            for t in range(NT):
                i = nc.vector.tensor_tensor(bd[:, t, :].rearrange("p (g s) -> p g s", g=8),
                                            ps[0][:, 128 * t:128 * t + 64].rearrange("p (o s) -> p o s", o=1).broadcast_to([128, 8, 64]),
                                            k("group8").rearrange("p (g o) -> p g o", o=1).broadcast_to([128, 8, 64]), ALU.mult)
            i.then_inc(sem("f0_bd"), 1)
            dve.wait_ge(sem("f0_bd"), at(it, "f0_bd"))
            for t in (1, 3):
                dve.wait_ge(sem("f0_sel"), at(it, "f0_sel", t + 1))
                nc.vector.tensor_copy(sel[:, :, 8 * t:8 * t + 8], ps[4 + t][:].rearrange("p (g s) -> p s g", g=8)).then_inc(sem("f0_selD"), 1)
            for half in range(2):
                dve.wait_ge(sem("f0_up"), at(it, "f0_up", half + 1))
                nc.vector.tensor_tensor(inner[:, 16 * half:16 * half + 16, :], ps[half][:].rearrange("p (q g) -> p q g", q=16),
                                               bias0[:, 16 * half:16 * half + 16].rearrange("p (q o) -> p q o", o=1).broadcast_to([128, 16, 32]), ALU.add).then_inc(sem("f0_up_b"), 1)
            for n in (1, 3):
                dve.wait_ge(sem("f0_tr"), at(it, "f0_tr", n + 1))
                nc.vector.tensor_copy(inter_tok[:, 4 * n:4 * n + 4, :].rearrange("p a b -> p (a b)"),
                                             ps[n + (0 if n < 2 else 4)][:]).then_inc(sem("f0_trev"), 1)
            dve.wait_ge(sem("f0_out"), at(it, "f0_out"))
            nc.vector.scalar_tensor_tensor(out=X[:], in0=ps[2][:], scalar=mod(0, 5), in1=X[:], op0=ALU.mult, op1=ALU.add).then_inc(sem("ln_x"), 1)
            dve.wait_ge(sem("ln_x"), at(it, "ln_x", 3))

        mix, mix4, xmix = w[0], w[1], [w[2], w[3], w[4], w[5], w[6]]
        xx, xt = w[7], w[8]
        rT, kT1, gs, ew, P1c = w[9], w[10], w[11], big[3][:, 0, :], big[3][:, 1, :]
        ku, r_in, k_end = big[3][:, 2, :], big[3][:, 3, :], w[0]
        ex, ex2 = w[7], w[8]
        vtok = v1[:, :, 0:128]
        kend_tok = w[1]
        diag = w[4]
        dmask = big[0][:, 0:3, :].rearrange("p a b -> p (a b)")
        yn, yt = w[5], w[6]
        dend = small[:, 64:68]
        st = small[:, 72:112]

        def a1_pe(pe, it):
            pe.wait_ge(sem("a1_xxx"), at(it, "a1_xxx"))
            nc.tensor.matmul(ps[2][:], w1mix[:, 0:128], xt[:], start=True, stop=True)
            nc.tensor.matmul(ps[3][0:32, :], w1mix[:, 128:160], xt[:], start=True, stop=True).then_inc(sem("a1_mix"), 1)
            pe.wait_ge(sem("a1_tanh"), at(it, "a1_tanh"))
            for s in range(5):
                b = (4, 5, 6, 7, 0)[s]
                lw, rh = (w2mix[32 * s:32 * s + 32, :], mix[32 * s:32 * s + 32, :]) if s < 4 else (w2mix4[:], mix4[0:32, :])
                nc.tensor.matmul(ps[b][:], lw, rh, start=True, stop=True).then_inc(sem("a1_m"), 1)
            pe.wait_ge(sem("a1_x"), at(it, "a1_x", 1))
            nc.tensor.matmul(ps[1][0:64, :], dw1[:], xmix[0][:], start=True, stop=True).then_inc(sem("a1_d1"), 1)
            pe.wait_ge(sem("a1_x"), at(it, "a1_x", 2))
            nc.tensor.matmul(ps[2][:], w5[:, 1, :], xmix[1][:], start=True, stop=True).then_inc(sem("a1_k"), 1)
            pe.wait_ge(sem("a1_x"), at(it, "a1_x", 3))
            for t in range(NT):
                i = nc.tensor.matmul(ps[3][:, 128 * t:128 * t + 128], xmix[2][:, 128 * t:128 * t + 128], w5[:, 2, :],
                                     start=True, stop=True)
            i.then_inc(sem("a1_v"), 1)
            pe.wait_ge(sem("a1_dt"), at(it, "a1_dt"))
            nc.tensor.matmul(ps[4][:], dw2[:], sq[0:64, :], start=True, stop=True).then_inc(sem("a1_w"), 1)
            pe.wait_ge(sem("a1_x"), at(it, "a1_x", 5))
            nc.tensor.matmul(ps[5][:], w5[:, 0, :], xmix[3][:], start=True, stop=True).then_inc(sem("a1_r"), 1)
            nc.tensor.matmul(ps[6][:], w5[:, 3, :], xmix[4][:], start=True, stop=True).then_inc(sem("a1_g"), 1)

            pe.wait_ge(sem("a1_kend"), at(it, "a1_kend"))
            for c in range(NT):
                i = nc.tensor.transpose(ps[7][:, 128 * c:128 * c + 128], k_end[:, 128 * c:128 * c + 128], ident)
            i.then_inc(sem("a1_kendt"), 1)
            def level(lv):
                kk, qq = (xl[2 + lv], xl[2 + lv]) if lv < 4 else ((kT1, rT) if lv == 4 else (ku, rT))
                for c in range(NT):
                    for hd in range(2):
                        q = slice(64 * hd, 64 * hd + 64)
                        bank = ps[(2, 4, 5, 7)[2 * hd + lv // 3]]
                        for b in range(4):
                            o = 128 * c + 32 * b
                            f = 128 * (lv % 3) + 32 * c
                            i = nc.tensor.matmul(bank[32 * b:32 * b + 32, f:f + 32], kk[q, o:o + 32], qq[q, o:o + 32],
                                                 start=True, stop=True, skip_group_check=True, tile_position=(q.start, 32 * b))
                return i

            for lv in range(4):
                pe.wait_ge(sem("a1_q"), at(it, "a1_q", 3 + lv))
                if lv == 3:
                    pe.wait_ge(sem("a1_kendtok"), at(it, "a1_kendtok"))
                c = slice(128 * lv, 128 * lv + 128)
                for hd in range(2):
                    q = slice(64 * hd, 64 * hd + 64)
                    nc.tensor.matmul(ps[hd][:, c.start:c.start + 64], xl[0][q, c], xl[0][q, c.start + 64:c.stop], start=True, stop=True)
                    i = nc.tensor.matmul(ps[hd][:, c.start + 64:c.stop], xl[1][q, c],
                                         xl[1][q, c].rearrange("p (b two t) -> p b two t", two=2, t=32)[:, :, 1, :], start=True, stop=True)
                if lv == 3:
                    i.then_inc(sem("a1_s64"), 1)
                level(lv)
            pe.wait_ge(sem("a1_kendtok"), at(it, "a1_kendtok"))
            pe.wait_ge(sem("a1_vc"), at(it, "a1_vc"))
            pe.wait_ge(sem("a1_q"), at(it, "a1_q"))
            for c in range(3):
                nc.tensor.matmul(ps[3][:, 128 * c:128 * c + 128], kend_tok[:, 128 * c:128 * c + 128], vtok[:, c, :],
                                        start=True, stop=True).then_inc(sem("a1_st"), 1)
            level(4)
            level(5).then_inc(sem("a1_sd"), 1)
            pe.wait_ge(sem("a1_st_new"), at(it, "a1_st_new"))
            pe.wait_ge(sem("a1_a64"), at(it, "a1_a64"))
            pe.wait_ge(sem("a1_a32"), at(it, "a1_a32"))
            pe.wait_ge(sem("a1_diagA"), at(it, "a1_diagA"))
            pe.wait_ge(sem("a1_diagV"), at(it, "a1_diagV"))
            for c in range(NT):
                y = ps[6][:, 128 * c:128 * c + 128]
                nc.tensor.matmul(y, r_in[:, 128 * c:128 * c + 128], state[:, c, :], start=True, stop=False, skip_group_check=True)
                for hd in range(2):
                    v = slice(64 * hd, 64 * hd + 64)
                    i = nc.tensor.matmul(y[:, v], scoresT[:, 4 * hd + c, :], vtok[:, c, v], start=False, stop=True, skip_group_check=True)
            i.then_inc(sem("a1_y"), 1)
            pe.wait_ge(sem("a1_yn"), at(it, "a1_yn"))
            for t in range(NT):
                i = nc.tensor.transpose(ps[7][:, 128 * t:128 * t + 128], yn[:, 128 * t:128 * t + 128], ident)
            i.then_inc(sem("a1_ynt"), 1)
            pe.wait_ge(sem("a1_yg"), at(it, "a1_yg"))
            nc.tensor.matmul(ps[2][:], w5[:, 4, :], yt[:], start=True, stop=True).then_inc(sem("a1_out"), 1)

        def a1_act(act, it):
            act.wait_ge(sem("a1_mix"), at(it, "a1_mix"))
            nc.scalar.activation(mix[:], ps[2][:], ACT.Tanh)
            nc.scalar.activation(mix4[0:32, :], ps[3][0:32, :], ACT.Tanh).then_inc(sem("a1_tanh"), 1)
            act.wait_ge(sem("a1_d1"), at(it, "a1_d1"))
            nc.scalar.activation(sq[0:64, :], ps[1][0:64, :], ACT.Tanh).then_inc(sem("a1_dt"), 1)
            act.wait_ge(sem("a1_k"), at(it, "a1_k"))
            nc.scalar.activation(kT1[:], ps[2][:], ACT.Copy).then_inc(sem("a1_kc"), 1)
            act.wait_ge(sem("a1_v"), at(it, "a1_v"))
            nc.scalar.activation(vtok, ps[3][:].rearrange("p (t n) -> p t n", t=NT), ACT.Copy).then_inc(sem("a1_vc"), 1)
            act.wait_ge(sem("a1_w"), at(it, "a1_w"))
            nc.scalar.activation(ew, ps[4][:], ACT.Exp, bias=vec("L1_attn_time_decay")).then_inc(sem("a1_ew"), 1)
            act.wait_ge(sem("a1_r"), at(it, "a1_r"))
            nc.scalar.activation(rT[:], ps[5][:], ACT.Copy).then_inc(sem("a1_rc"), 1)
            act.wait_ge(sem("a1_g"), at(it, "a1_g"))
            nc.scalar.activation(sq[:], ps[6][:], ACT.Tanh, scale=0.5).then_inc(sem("a1_gt"), 1)
            act.wait_ge(sem("a1_kend_p"), at(it, "a1_kend_p"))
            nc.scalar.activation(dend, P1c.rearrange("p (c t) -> p c t", t=128)[:, :, 127], ACT.Exp, scale=-1.0).then_inc(sem("a1_dend"), 1)
            nc.scalar.activation(ex[:], ex[:], ACT.Exp, scale=-1.0).then_inc(sem("scalar_step"), 1)
            act.wait_ge(sem("scalar_step"), step(it, "scalar"))
            nc.scalar.activation(r_in, shifted[:].rearrange("p a b -> p (a b)"), ACT.Exp, scale=-1.0).then_inc(sem("a1_kend_e"), 1)
            act.wait_ge(sem("a1_kendt"), at(it, "a1_kendt"))
            nc.scalar.activation(kend_tok[:], ps[7][:], ACT.Copy).then_inc(sem("a1_kendtok"), 1)
            for lv in range(6):
                act.wait_ge(sem("a1_lvl"), at(it, "a1_lvl", lv + 1))
                nc.scalar.activation(xl[lv][:], xl[lv][:], ACT.Exp, scale=-1.0).then_inc(sem("a1_lvl_e"), 1)
            act.wait_ge(sem("a1_s64"), at(it, "a1_s64"))
            for hd in range(2):
                nc.scalar.activation(scoresT[0:64, 4 * hd:4 * hd + 4, 64:128],
                                            ps[hd][0:64, :].rearrange("p (c n) -> p c n", c=4)[:, :, 0:64], ACT.Copy).then_inc(sem("a1_a64"), 1)
            for hd in range(2):
                for b in range(2):
                    r = slice(64 * b, 64 * b + 32)
                    nc.scalar.activation(scoresT[r, 4 * hd:4 * hd + 4, 64 * b + 32:64 * b + 64],
                                                ps[hd][r, :].rearrange("p (c n) -> p c n", c=4)[:, :, 64 + 32 * b:96 + 32 * b], ACT.Copy).then_inc(sem("a1_a32"), 1)
            act.wait_ge(sem("a1_dsum"), at(it, "a1_dsum"))
            for b in (0, 1):
                r = slice(32 * b, 32 * b + 32)
                nc.scalar.activation(scoresT[r, :, r], diag[r, 0:256].rearrange("p (u q) -> p u q", u=8), ACT.Copy).then_inc(sem("a1_diagA"), 1)
            act.wait_ge(sem("a1_yc"), at(it, "a1_yc"))
            nc.scalar.activation(yt[:], yn[:], ACT.Square).then_inc(sem("a1_ysq"), 1)
            act.wait_ge(sem("a1_var"), at(it, "a1_var"))
            nc.scalar.activation(st[:, 24:32], st[:, 16:24], ACT.Sqrt, bias=k("eps")[:, 1:2], scale=1.0 / HS).then_inc(sem("a1_std"), 1)

        def a1_dve(dve, it):
            nc.vector.tensor_tensor(xx[:], hp[:, 0:T], h, ALU.subtract).then_inc(sem("vector_step"), 1)
            dve.wait_ge(sem("vector_step"), step(it, "vector"))
            nc.vector.scalar_tensor_tensor(out=xt[:], in0=xx[:], scalar=vec("L1_attn_time_maa_x"), in1=h, op0=ALU.mult, op1=ALU.add).then_inc(sem("a1_xxx"), 1)
            dve.wait_ge(sem("a1_xxx"), at(it, "a1_xxx"))
            for s, n in enumerate("wkvrg"):
                b = (4, 5, 6, 7, 0)[s]
                dve.wait_ge(sem("a1_m"), at(it, "a1_m", s + 1))
                nc.vector.scalar_tensor_tensor(out=xmix[s][:], in0=ps[b][:], scalar=vec("L1_attn_time_maa_" + n), in1=xx[:], op0=ALU.add, op1=ALU.mult).then_inc(sem("vector_step"), 1)
                dve.wait_ge(sem("vector_step"), step(it, "vector"))
                nc.vector.tensor_tensor(xmix[s][:], xmix[s][:], h, ALU.add).then_inc(sem("a1_x"), 1)
            dve.wait_ge(sem("a1_ew"), at(it, "a1_ew"))
            nc.vector.tensor_tensor_scan(P1c, k("restart"), ew, 0.0, ALU.mult, ALU.add).then_inc(sem("vector_step"), 1)
            dve.wait_ge(sem("vector_step"), step(it, "vector"))
            c4 = P1c.rearrange("p (c t) -> p c t", t=128)
            nc.vector.tensor_copy(shifted[:, :, 1:128], c4[:, :, 0:127]).then_inc(sem("vector_step"), 1)
            dve.wait_ge(sem("vector_step"), step(it, "vector"))
            dve.wait_ge(sem("a1_x"), at(it, "a1_x", 5))
            nc.vector.tensor_tensor(ex[:].rearrange("p (c t) -> p c t", t=128), c4[:, :, 127:128].broadcast_to([128, NT, 128]), c4, ALU.subtract).then_inc(sem("a1_kend_p"), 1)
            dve.wait_ge(sem("a1_kend_p"), at(it, "a1_kend_p"))
            dve.wait_ge(sem("a1_kend_e"), at(it, "a1_kend_e"))
            dve.wait_ge(sem("a1_kc"), at(it, "a1_kc"))
            nc.vector.tensor_tensor(k_end[:], kT1[:], ex[:], ALU.mult).then_inc(sem("a1_kend"), 1)
            dve.wait_ge(sem("a1_kend"), at(it, "a1_kend"))
            dve.wait_ge(sem("a1_rc"), at(it, "a1_rc"))
            nc.vector.tensor_tensor(r_in, r_in, rT[:], ALU.mult).then_inc(sem("vector_step"), 1)
            dve.wait_ge(sem("vector_step"), step(it, "vector"))
            pprev = shifted[:].rearrange("p a b -> p (a b)")
            dve.wait_ge(sem("a1_g"), at(it, "a1_g"))
            dve.wait_ge(sem("a1_gt"), at(it, "a1_gt"))
            nc.vector.scalar_tensor_tensor(out=gs[:], in0=sq[:], scalar=1.0, in1=ps[6][:], op0=ALU.add, op1=ALU.mult).then_inc(sem("vector_step"), 1)
            dve.wait_ge(sem("vector_step"), step(it, "vector"))

            def halves(ap, m):
                return ap.rearrange("p (n two m) -> p two n m", two=2, m=m)

            for lv, m in enumerate(LEVELS):
                n = T // (2 * m)
                border = halves(P1c, m)[:, 0, :, m - 1:m].broadcast_to([128, n, m])
                nc.vector.tensor_tensor(halves(xl[lv][:], m)[:, 0], border, halves(P1c, m)[:, 0], ALU.subtract).then_inc(sem("vector_step"), 1)
                dve.wait_ge(sem("vector_step"), step(it, "vector"))
                nc.vector.tensor_tensor(halves(xl[lv][:], m)[:, 1], halves(pprev, m)[:, 1], border, ALU.subtract).then_inc(sem("a1_lvl"), 1)
            for lv, m in enumerate(LEVELS):
                dve.wait_ge(sem("a1_lvl_e"), at(it, "a1_lvl_e", lv + 1))
                nc.vector.tensor_tensor(halves(xl[lv][:], m)[:, 0], halves(xl[lv][:], m)[:, 0], halves(kT1[:], m)[:, 0], ALU.mult).then_inc(sem("vector_step"), 1)
                dve.wait_ge(sem("vector_step"), step(it, "vector"))
                nc.vector.tensor_tensor(halves(xl[lv][:], m)[:, 1], halves(xl[lv][:], m)[:, 1], halves(rT[:], m)[:, 1], ALU.mult).then_inc(sem("a1_q"), 1)
            nc.vector.tensor_scalar(ku, kT1[:], vec("L1_attn_time_faaaa"), None, ALU.mult).then_inc(sem("a1_q"), 1)
            dve.wait_ge(sem("a1_dend"), at(it, "a1_dend"))
            nc.vector.memset(state[:, 0, :], 0.0).then_inc(sem("vector_step"), 1)
            dve.wait_ge(sem("vector_step"), step(it, "vector"))
            for c in range(3):
                dve.wait_ge(sem("a1_st"), at(it, "a1_st"))
                nc.vector.tensor_tensor(state[:, c + 1, :], ps[3][:, 128 * c:128 * c + 128], k("same64"), ALU.mult).then_inc(sem("vector_step"), 1)
                dve.wait_ge(sem("vector_step"), step(it, "vector"))
                nc.vector.scalar_tensor_tensor(out=state[:, c + 1, :], in0=state[:, c, :], scalar=dend[:, c:c + 1], in1=state[:, c + 1, :],
                                                        op0=ALU.mult, op1=ALU.add).then_inc(sem("a1_st_new"), 1)
                dve.wait_ge(sem("a1_st_new"), at(it, "a1_st_new", c + 1))
            dve.wait_ge(sem("a1_sd"), at(it, "a1_sd"))
            for pr in range(4):
                nc.vector.tensor_tensor(
                    dmask[:, 384 * pr:384 * pr + 384].rearrange("p (l u q) -> p l u q", l=3, u=4),
                    ps[(2, 4, 5, 7)[pr]][:, 0:384].rearrange("p (l u q) -> p l u q", l=3, u=4),
                    k("level")[:, 96 * (pr % 2):96 * (pr % 2) + 96].rearrange("p (l o q) -> p l o q", l=3, o=1).broadcast_to([128, 3, 4, 32]), ALU.mult).then_inc(sem("vector_step"), 1)
                dve.wait_ge(sem("vector_step"), step(it, "vector"))
            nc.vector.tensor_reduce(diag[:, 0:256].rearrange("p (h u) -> p h u", h=2), dmask.rearrange("p (h l u) -> p h u l", h=2, l=6), AX.X, ALU.add).then_inc(sem("a1_dsum"), 1)
            dve.wait_ge(sem("a1_dsum"), at(it, "a1_dsum"))
            for b in (2, 3):
                r = slice(32 * b, 32 * b + 32)
                nc.vector.tensor_copy(scoresT[r, :, r], diag[r, 0:256].rearrange("p (u q) -> p u q", u=8)).then_inc(sem("a1_diagV"), 1)
            dve.wait_ge(sem("a1_y"), at(it, "a1_y"))
            nc.vector.tensor_reduce(st[:, 0:8], ps[6][:].rearrange("p (u i) -> p u i", u=8), AX.X, ALU.add).then_inc(sem("vector_step"), 1)
            dve.wait_ge(sem("vector_step"), step(it, "vector"))
            nc.vector.tensor_scalar(st[:, 8:16], st[:, 0:8], 1.0 / HS, None, ALU.mult).then_inc(sem("vector_step"), 1)
            dve.wait_ge(sem("vector_step"), step(it, "vector"))
            nc.vector.tensor_tensor(yn[:].rearrange("p (u i) -> p u i", u=8), ps[6][:].rearrange("p (u i) -> p u i", u=8),
                                             st[:, 8:16].rearrange("p (u o) -> p u o", o=1).broadcast_to([128, 8, 64]), ALU.subtract).then_inc(sem("a1_yc"), 1)
            dve.wait_ge(sem("a1_yc"), at(it, "a1_yc"))
            dve.wait_ge(sem("a1_ysq"), at(it, "a1_ysq"))
            nc.vector.tensor_reduce(st[:, 16:24], yt[:].rearrange("p (u i) -> p u i", u=8), AX.X, ALU.add).then_inc(sem("a1_var"), 1)
            dve.wait_ge(sem("a1_var"), at(it, "a1_var"))
            dve.wait_ge(sem("a1_std"), at(it, "a1_std"))
            nc.vector.reciprocal(st[:, 32:40], st[:, 24:32]).then_inc(sem("vector_step"), 1)
            dve.wait_ge(sem("vector_step"), step(it, "vector"))
            nc.vector.tensor_tensor(yn[:].rearrange("p (u i) -> p u i", u=8), yn[:].rearrange("p (u i) -> p u i", u=8),
                                             st[:, 32:40].rearrange("p (u o) -> p u o", o=1).broadcast_to([128, 8, 64]), ALU.mult).then_inc(sem("a1_yn"), 1)
            dve.wait_ge(sem("a1_yn"), at(it, "a1_yn"))
            dve.wait_ge(sem("a1_ynt"), at(it, "a1_ynt"))
            nc.vector.tensor_scalar(yt[:], ps[7][:], vec("L1_attn_ln_w"), vec("L1_attn_ln_b"), ALU.mult, ALU.add).then_inc(sem("vector_step"), 1)
            dve.wait_ge(sem("vector_step"), step(it, "vector"))
            nc.vector.scalar_tensor_tensor(out=yt[:], in0=yt[:], scalar=0.5, in1=gs[:], op0=ALU.mult, op1=ALU.mult).then_inc(sem("a1_yg"), 1)
            dve.wait_ge(sem("a1_yg"), at(it, "a1_yg"))
            dve.wait_ge(sem("a1_out"), at(it, "a1_out"))
            nc.vector.scalar_tensor_tensor(out=X[:], in0=ps[2][:], scalar=mod(1, 2), in1=X[:], op0=ALU.mult, op1=ALU.add).then_inc(sem("ln_x"), 1)
            dve.wait_ge(sem("ln_x"), at(it, "ln_x", 4))

        tk = [w[0][:, 32 * i:32 * i + 32] for i in range(10)]
        r4 = [w[0][:, 320 + 4 * i:324 + 4 * i] for i in range(8)]

        def per_tok(a):
            return a.rearrange("p (t o) -> p t o", o=1).broadcast_to([128, NT, 8])

        def v3(a):
            return a.rearrange("p (t e) -> p t e", t=NT)

        def top2(dve, it, logits, shifted_logits, exponentials):
            idx = k("index8").rearrange("p (o e) -> p o e", o=1).broadcast_to([128, NT, 8])
            nc.vector.tensor_reduce(r4[0], v3(logits), AX.X, ALU.max).then_inc(sem("vector_step"), 1)
            dve.wait_ge(sem("vector_step"), step(it, "vector"))
            nc.vector.tensor_tensor(v3(tk[0]), v3(logits), per_tok(r4[0]), ALU.subtract).then_inc(sem(shifted_logits), 1)
            dve.wait_ge(sem(shifted_logits), at(it, shifted_logits))
            dve.wait_ge(sem(exponentials), at(it, exponentials))
            nc.vector.tensor_reduce(r4[1], v3(tk[0]), AX.X, ALU.add).then_inc(sem("vector_step"), 1)
            dve.wait_ge(sem("vector_step"), step(it, "vector"))
            nc.vector.reciprocal(r4[2], r4[1]).then_inc(sem("vector_step"), 1)
            dve.wait_ge(sem("vector_step"), step(it, "vector"))
            nc.vector.tensor_tensor(v3(tk[1]), v3(tk[0]), per_tok(r4[2]), ALU.mult).then_inc(sem("vector_step"), 1)
            dve.wait_ge(sem("vector_step"), step(it, "vector"))
            src = tk[1]
            for j, (best, hot) in enumerate(((r4[3], tk[4]), (r4[4], tk[7]))):
                nc.vector.tensor_reduce(best, v3(src), AX.X, ALU.max).then_inc(sem("vector_step"), 1)
                dve.wait_ge(sem("vector_step"), step(it, "vector"))
                nc.vector.tensor_tensor(v3(tk[2]), v3(src), per_tok(best), ALU.is_lt).then_inc(sem("vector_step"), 1)
                dve.wait_ge(sem("vector_step"), step(it, "vector"))
                nc.vector.scalar_tensor_tensor(out=v3(tk[3]), in0=v3(tk[2]), scalar=100.0, in1=idx, op0=ALU.mult, op1=ALU.add).then_inc(sem("vector_step"), 1)
                dve.wait_ge(sem("vector_step"), step(it, "vector"))
                nc.vector.tensor_reduce(r4[5], v3(tk[3]), AX.X, ALU.min).then_inc(sem("vector_step"), 1)
                dve.wait_ge(sem("vector_step"), step(it, "vector"))
                nc.vector.tensor_tensor(v3(hot), idx, per_tok(r4[5]), ALU.is_equal).then_inc(sem("vector_step"), 1)
                dve.wait_ge(sem("vector_step"), step(it, "vector"))
                if j == 0:
                    nc.vector.scalar_tensor_tensor(out=tk[5], in0=hot, scalar=-4.0, in1=tk[1], op0=ALU.mult, op1=ALU.add).then_inc(sem("vector_step"), 1)
                    dve.wait_ge(sem("vector_step"), step(it, "vector"))
                    src = tk[5]

        scale_row, sc1, ga1, gb1, hid = w[1], w[2], w[3], w[4], w[5]

        def f1_pe(pe, it):
            pe.wait_ge(sem("ln_h"), at(it, "ln_h", 4))
            for t in range(NT):
                i = nc.tensor.matmul(ps[2][:, 8 * t:8 * t + 8], h[:, 128 * t:128 * t + 128], gw1[:], start=True, stop=True)
            i.then_inc(sem("f1_logit"), 1)
            pe.wait_ge(sem("f1_scale"), at(it, "f1_scale"))
            for t in range(NT):
                i = nc.tensor.transpose(ps[3][0:8, 128 * t:128 * t + 128], tk[8][:, 8 * t:8 * t + 8], ident)
            i.then_inc(sem("f1_scalet"), 1)
            pe.wait_ge(sem("f1_row"), at(it, "f1_row"))
            for pr in range(E1 // 2):
                if pr >= 1:
                    pe.wait_ge(sem("f1_hid"), at(it, "f1_hid", pr))
                nc.tensor.matmul(ps[4][:], w1s[:, 2 * pr:2 * pr + 2, :].rearrange("p a b -> p (a b)"), h, start=True, stop=True)
                nc.tensor.matmul(ps[5][:], w3s[:, 2 * pr:2 * pr + 2, :].rearrange("p a b -> p (a b)"), h, start=True, stop=True)
                nc.tensor.matmul(ps[6][:], k("spread1")[0:8, 128 * pr:128 * pr + 128], scale_row[0:8, :], start=True, stop=True).then_inc(sem("f1_ab"), 1)
                pe.wait_ge(sem("f1_hid"), at(it, "f1_hid", pr + 1))
                i = nc.tensor.matmul(ps[7][:], w2s[:, pr, :], hid[:], start=(pr == 0), stop=(pr == E1 // 2 - 1))
                i.then_inc(sem("f1_y"), 1)

        def f1_act(act, it):
            act.wait_ge(sem("f1_sm"), at(it, "f1_sm"))
            nc.scalar.activation(tk[0], tk[0], ACT.Exp).then_inc(sem("f1_sm_e"), 1)
            act.wait_ge(sem("f1_scalet"), at(it, "f1_scalet"))
            nc.scalar.activation(scale_row[0:8, :], ps[3][0:8, :], ACT.Copy).then_inc(sem("f1_row"), 1)
            for pr in range(E1 // 2):
                act.wait_ge(sem("f1_a"), at(it, "f1_a", pr + 1))
                nc.scalar.activation(gb1[:], ga1[:], ACT.Tanh, scale=0.5).then_inc(sem("f1_th"), 1)

        def f1_dve(dve, it):
            dve.wait_ge(sem("f1_logit"), at(it, "f1_logit"))
            top2(dve, it, ps[2][:, 0:32], "f1_sm", "f1_sm_e")
            nc.vector.tensor_tensor(tk[8], tk[4], tk[7], ALU.add).then_inc(sem("vector_step"), 1)
            dve.wait_ge(sem("vector_step"), step(it, "vector"))
            nc.vector.tensor_tensor(tk[8], tk[8], tk[1], ALU.mult).then_inc(sem("f1_scale"), 1)
            dve.wait_ge(sem("f1_scale"), at(it, "f1_scale"))
            for pr in range(E1 // 2):
                dve.wait_ge(sem("f1_ab"), at(it, "f1_ab", pr + 1))
                nc.vector.tensor_copy(sc1[:], ps[6][:]).then_inc(sem("vector_step"), 1)
                dve.wait_ge(sem("vector_step"), step(it, "vector"))
                nc.vector.tensor_tensor(ga1[:], ps[4][:], sc1[:], ALU.mult).then_inc(sem("f1_a"), 1)
                dve.wait_ge(sem("f1_a"), at(it, "f1_a", pr + 1))
                if pr >= 1:
                    dve.wait_ge(sem("f1_y"), at(it, "f1_y", pr))
                nc.vector.tensor_tensor(hid[:], ps[5][:], sc1[:], ALU.mult).then_inc(sem("vector_step"), 1)
                dve.wait_ge(sem("vector_step"), step(it, "vector"))
                dve.wait_ge(sem("f1_th"), at(it, "f1_th", pr + 1))
                nc.vector.scalar_tensor_tensor(out=gb1[:], in0=gb1[:], scalar=1.0, in1=ga1[:], op0=ALU.add, op1=ALU.mult).then_inc(sem("vector_step"), 1)
                dve.wait_ge(sem("vector_step"), step(it, "vector"))
                nc.vector.scalar_tensor_tensor(out=hid[:], in0=gb1[:], scalar=0.5, in1=hid[:], op0=ALU.mult, op1=ALU.mult).then_inc(sem("f1_hid"), 1)
                dve.wait_ge(sem("f1_hid"), at(it, "f1_hid", pr + 1))
            dve.wait_ge(sem("f1_y"), at(it, "f1_y"))
            nc.vector.scalar_tensor_tensor(out=X[:], in0=ps[7][:], scalar=mod(1, 5), in1=X[:], op0=ALU.mult, op1=ALU.add).then_inc(sem("ln_x"), 1)
            dve.wait_ge(sem("ln_x"), at(it, "ln_x", 5))

        q_of, kT, vA, o_tok = [w[0], w[1], w[5], w[6]], w[2], w[3], w[4]
        prob = [big[0], big[1]]
        turned_p = big[2]
        nmax, rsum, rrec = small[:, 128:136], small[:, 160:224], small[:, 224:288]

        def att_pe(pe, it, width, base, causal):
            NH, per = 128 // width, 32 // width
            for hh in range(NH + 1):
                if hh < NH:
                    g = slice(32 * (hh // per), 32 * (hh // per) + 32)
                    for i in range(NT):
                        L = 128 * (i + 1) if causal else T
                        if hh >= 1:
                            pe.wait_ge(sem("att_exp"), at(it, "att_exp", (base + hh - 1) * NT + i + 1))
                        ins = nc.tensor.matmul(ps[i][:, 0:L], q_of[hh % per][g, 128 * i:128 * i + 128], kT[g, 0:L],
                                               start=True, stop=not causal, tile_position=(g.start, 0))
                        if causal:
                            ins = nc.tensor.matmul(ps[i][:, 128 * i:128 * i + 128], identb[:], causalb[:], start=False, stop=True)
                        ins.then_inc(sem("att_s"), 1)
                if hh >= 1:
                    g = hh - 1
                    pe.wait_ge(sem("att_exp"), at(it, "att_exp", (base + g) * NT + NT))
                    for j in range(NT):
                        if j >= 2:
                            pe.wait_ge(sem(("att_evA", "att_evD")[j % 2]), at(it, ("att_evA", "att_evD")[j % 2], (base + g) * 2 + j // 2))
                        elif g >= 1:
                            pe.wait_ge(sem(("att_evA", "att_evD")[j % 2]), at(it, ("att_evA", "att_evD")[j % 2], (base + g) * 2))
                        for i in range(j if causal else 0, NT):
                            ins = nc.tensor.transpose(ps[4 + j % 2][:, 128 * i:128 * i + 128],
                                                      prob[g % 2][:, i, 128 * j:128 * j + 128], ident)
                        ins.then_inc(sem("att_t"), 1)
                    pe.wait_ge(sem("att_evA"), at(it, "att_evA", (base + g + 1) * 2))
                    pe.wait_ge(sem("att_evD"), at(it, "att_evD", (base + g + 1) * 2))
                    for i in range(NT):
                        last = i if causal else NT - 1
                        for j in range(last + 1):
                            ins = nc.tensor.matmul(ps[6][:, 128 * i + width * g:128 * i + width * g + width],
                                                   turned_p[:, j, 128 * i:128 * i + 128],
                                                   vA[:, 128 * j + width * g:128 * j + width * g + width],
                                                   start=(j == 0), stop=(j == last))
                    ins.then_inc(sem("att_pv"), 1)

        def att_act(act, it, width, base, causal):
            NH = 128 // width
            for hh in range(NH + 1):
                for i in range(NT):
                    if hh < NH:
                        L = 128 * (i + 1) if causal else T
                        act.wait_ge(sem("att_max"), at(it, "att_max", (base + hh) * NT + i + 1))
                        if hh >= 2:
                            act.wait_ge(sem("att_t"), at(it, "att_t", (base + hh - 1) * NT))
                        nc.scalar.activation(prob[hh % 2][:, i, 0:L], ps[i][:, 0:L], ACT.Exp,
                                                    bias=nmax[:, 4 * (hh % 2) + i:4 * (hh % 2) + i + 1],
                                                    accum_out=rsum[:, NH * i + hh:NH * i + hh + 1]).then_inc(sem("att_exp"), 1)
                if hh >= 1:
                    for j in (0, 2):
                        g = hh - 1
                        act.wait_ge(sem("att_t"), at(it, "att_t", (base + g) * NT + j + 1))
                        if g >= 1:
                            act.wait_ge(sem("att_pv"), at(it, "att_pv", base + g))
                        o = 128 * j if causal else 0
                        nc.scalar.activation(turned_p[:, j, o:T], ps[4][:, o:T], ACT.Copy).then_inc(sem("att_evA"), 1)

        def att_dve(dve, it, width, base, causal):
            NH = 128 // width
            for hh in range(NH + 1):
                for i in range(NT):
                    if hh < NH:
                        L = 128 * (i + 1) if causal else T
                        dve.wait_ge(sem("att_s"), at(it, "att_s", (base + hh) * NT + i + 1))
                        if hh >= 2:
                            dve.wait_ge(sem("att_exp"), at(it, "att_exp", (base + hh - 2) * NT + i + 1))
                        nc.vector.tensor_reduce(nmax[:, 4 * (hh % 2) + i:4 * (hh % 2) + i + 1], ps[i][:, 0:L], AX.X, ALU.max,
                                                       negate=True).then_inc(sem("att_max"), 1)
                if hh >= 1:
                    for j in (1, 3):
                        g = hh - 1
                        dve.wait_ge(sem("att_t"), at(it, "att_t", (base + g) * NT + j + 1))
                        if g >= 1:
                            dve.wait_ge(sem("att_pv"), at(it, "att_pv", base + g))
                        o = 128 * j if causal else 0
                        nc.vector.tensor_copy(turned_p[:, j, o:T], ps[5][:, o:T]).then_inc(sem("att_evD"), 1)
            dve.wait_ge(sem("att_pv"), at(it, "att_pv", base + NH))
            dve.wait_ge(sem("att_exp"), at(it, "att_exp", (base + NH) * NT))
            nc.vector.reciprocal(rrec[:, 0:NT * NH], rsum[:, 0:NT * NH]).then_inc(sem("vector_step"), 1)
            dve.wait_ge(sem("vector_step"), step(it, "vector"))
            ins = nc.vector.tensor_tensor(o_tok[:].rearrange("p (u d) -> p u d", d=width), ps[6][:].rearrange("p (u d) -> p u d", d=width),
                                          rrec[:, 0:NT * NH].rearrange("p (u o) -> p u o", o=1).broadcast_to([128, NT * NH, width]), ALU.mult)
            return ins

        def a2_pe(pe, it):
            pe.wait_ge(sem("ln_h"), at(it, "ln_h", 5))
            nc.tensor.matmul(ps[2][:], wqkv2[:, 0:128], h, start=True, stop=True).then_inc(sem("a2_q"), 1)
            nc.tensor.matmul(ps[3][:], wqkv2[:, 128:256], h, start=True, stop=True).then_inc(sem("a2_k"), 1)
            for t in range(NT):
                o = ps[7][:, 128 * t:128 * t + 128]
                nc.tensor.matmul(o, h[:, 128 * t:128 * t + 128], wqkv2[:, 256:384], start=True, stop=False)
                i = nc.tensor.matmul(o, ones[0:1, :], bias_row[0:1, 256:384], start=False, stop=True)
            i.then_inc(sem("a2_v"), 1)
            pe.wait_ge(sem("a2_qkv"), at(it, "a2_qkv"))
            pe.wait_ge(sem("a2_vc"), at(it, "a2_vc"))
            att_pe(pe, it, 8, 0, True)
            pe.wait_ge(sem("a2_o"), at(it, "a2_o"))
            for t in range(NT):
                i = nc.tensor.transpose(ps[7][:, 128 * t:128 * t + 128], o_tok[:, 128 * t:128 * t + 128], ident)
            i.then_inc(sem("a2_ot"), 1)
            pe.wait_ge(sem("a2_oc"), at(it, "a2_oc"))
            nc.tensor.matmul(ps[2][:], wout2[:], w[5][:], start=True, stop=True).then_inc(sem("a2_out"), 1)

        def a2_act(act, it):
            act.wait_ge(sem("a2_v"), at(it, "a2_v"))
            nc.scalar.activation(vA[:], ps[7][:], ACT.Copy).then_inc(sem("a2_vc"), 1)
            att_act(act, it, 8, 0, True)
            act.wait_ge(sem("a2_ot"), at(it, "a2_ot"))
            nc.scalar.activation(w[5][:], ps[7][:], ACT.Copy).then_inc(sem("a2_oc"), 1)

        def a2_dve(dve, it):
            dve.wait_ge(sem("a2_q"), at(it, "a2_q"))
            nc.vector.tensor_scalar(w[7][:], ps[2][:], vec("bq2"), 1.0 / np.sqrt(8.0), ALU.add, ALU.mult).then_inc(sem("vector_step"), 1)
            dve.wait_ge(sem("vector_step"), step(it, "vector"))
            for m in range(4):
                nc.vector.tensor_scalar(q_of[m][:], w[7][:], k("head4")[:, m:m + 1], None, ALU.mult).then_inc(sem("a2_qkv"), 1)
            dve.wait_ge(sem("a2_k"), at(it, "a2_k"))
            nc.vector.tensor_scalar(kT[:], ps[3][:], vec("bk2"), None, ALU.add).then_inc(sem("a2_qkv"), 1)
            att_dve(dve, it, 8, 0, True).then_inc(sem("a2_o"), 1)
            dve.wait_ge(sem("a2_o"), at(it, "a2_o"))
            dve.wait_ge(sem("a2_out"), at(it, "a2_out"))
            nc.vector.tensor_scalar(w[7][:], ps[2][:], vec("L2_attn_b_out"), None, ALU.add).then_inc(sem("vector_step"), 1)
            dve.wait_ge(sem("vector_step"), step(it, "vector"))
            nc.vector.scalar_tensor_tensor(out=X[:], in0=w[7][:], scalar=mod(2, 2), in1=X[:], op0=ALU.mult, op1=ALU.add).then_inc(sem("ln_x"), 1)
            dve.wait_ge(sem("ln_x"), at(it, "ln_x", 6))

        hot_row, wt_row = [big[0][:, 0, :], big[0][:, 1, :]], [big[0][:, 2, :], big[0][:, 3, :]]
        keep = [w[1], w[2]]
        a1x, a3x = w[3], w[4]
        in1, in3 = [w[5], w[6]], [w[7], w[8]]
        wt = [w[9], w[10]]
        aw = [big[1][:, 0, :], big[1][:, 1, :]]
        th = [big[1][:, 2, :], big[1][:, 3, :]]
        zw = [big[2][:, 0, :], big[2][:, 1, :]]

        def f2_pe(pe, it):
            pe.wait_ge(sem("ln_h"), at(it, "ln_h", 6))
            for t in range(NT):
                i = nc.tensor.matmul(ps[2][:, 8 * t:8 * t + 8], h[:, 128 * t:128 * t + 128], gate2[:], start=True, stop=True)
            i.then_inc(sem("f2_logit"), 1)
            nc.tensor.matmul(ps[3][:], turned[:, A1, :], h, start=True, stop=True).then_inc(sem("f2_a"), 1)
            nc.tensor.matmul(ps[4][:], turned[:, A3, :], h, start=True, stop=True).then_inc(sem("f2_a"), 1)
            pe.wait_ge(sem("f2_rows"), at(it, "f2_rows"))
            for j in range(2):
                for n, src in enumerate(((tk[4], tk[7])[j], (tk[8], tk[9])[j])):
                    for t in range(NT):
                        i = nc.tensor.transpose(ps[(5, 6, 7, 0)[2 * j + n]][0:8, 128 * t:128 * t + 128], src[:, 8 * t:8 * t + 8], ident)
            i.then_inc(sem("f2_rowst"), 1)
            pe.wait_ge(sem("f2_rowsc"), at(it, "f2_rowsc"))
            for j in range(2):
                nc.tensor.matmul(ps[(5, 6)[j]][:], k("spread2")[0:8, :], hot_row[j][0:8, :], start=True, stop=True)
                i = nc.tensor.matmul(ps[(7, 0)[j]][:], k("halves")[0:8, :], wt_row[j][0:8, :], start=True, stop=True)
            i.then_inc(sem("f2_spread"), 1)
            pe.wait_ge(sem("f2_in"), at(it, "f2_in"))

            def back(n):
                j, f = n // 4, n % 4
                pe.wait_ge(sem("f2_aw"), at(it, "f2_aw", n + 1))
                nc.tensor.matmul(ps[6][:], turned[:, WD + f, :], aw[n % 2], start=(n == 0), stop=False, skip_group_check=True)
                ins = nc.tensor.matmul(ps[7][:], turned[:, A2 + f, :], aw[n % 2], start=(f == 0), stop=(f == 3), skip_group_check=True)
                ins.then_inc(sem("f2_z"), 1)

            for n in range(8):
                j, f = n // 4, n % 4
                if n >= 2:
                    pe.wait_ge(sem("f2_aw"), at(it, "f2_aw", n - 1))
                a, b = ps[2 + 2 * (n % 2)], ps[3 + 2 * (n % 2)]
                nc.tensor.matmul(a[:], turned[:, WG + f, :], h, start=True, stop=False)
                nc.tensor.matmul(a[:], turned[:, B1 + f, :], in1[j][:], start=False, stop=True)
                nc.tensor.matmul(b[:], turned[:, WU + f, :], h, start=True, stop=False)
                nc.tensor.matmul(b[:], turned[:, B3 + f, :], in3[j][:], start=False, stop=True).then_inc(sem("f2_g"), 1)
                if n >= 1:
                    if n == 5:
                        pe.wait_ge(sem("f2_zc"), at(it, "f2_zc", 1))
                    back(n - 1)
            back(7)
            pe.wait_ge(sem("f2_zc"), at(it, "f2_zc", 1))
            nc.tensor.matmul(ps[6][:], turned[:, B2, :], zw[0], start=False, stop=False, skip_group_check=True)
            pe.wait_ge(sem("f2_zc"), at(it, "f2_zc", 2))
            nc.tensor.matmul(ps[6][:], turned[:, B2, :], zw[1], start=False, stop=True, skip_group_check=True).then_inc(sem("f2_out"), 1)

        def f2_act(act, it):
            act.wait_ge(sem("f2_sm"), at(it, "f2_sm"))
            nc.scalar.activation(tk[0], tk[0], ACT.Exp).then_inc(sem("f2_sm_e"), 1)
            act.wait_ge(sem("f2_rowst"), at(it, "f2_rowst"))
            for j in range(2):
                nc.scalar.activation(hot_row[j][0:8, :], ps[(5, 7)[j]][0:8, :], ACT.Copy)
                i = nc.scalar.activation(wt_row[j][0:8, :], ps[(6, 0)[j]][0:8, :], ACT.Copy)
            i.then_inc(sem("f2_rowsc"), 1)
            for n in range(8):
                act.wait_ge(sem("f2_g"), at(it, "f2_g", n + 1))
                if n >= 2:
                    act.wait_ge(sem("f2_aw"), at(it, "f2_aw", n - 1))
                nc.scalar.activation(th[n % 2], ps[2 + 2 * (n % 2)][:], ACT.Tanh, scale=0.5).then_inc(sem("f2_th"), 1)

        def f2_dve(dve, it):
            dve.wait_ge(sem("f2_logit"), at(it, "f2_logit"))
            top2(dve, it, ps[2][:, 0:32], "f2_sm", "f2_sm_e")
            nc.vector.tensor_tensor(r4[5], r4[3], r4[4], ALU.add).then_inc(sem("vector_step"), 1)
            dve.wait_ge(sem("vector_step"), step(it, "vector"))
            nc.vector.reciprocal(r4[6], r4[5]).then_inc(sem("vector_step"), 1)
            dve.wait_ge(sem("vector_step"), step(it, "vector"))
            for j in range(2):
                nc.vector.tensor_tensor(r4[7], r4[3 + j], r4[6], ALU.mult).then_inc(sem("vector_step"), 1)
                dve.wait_ge(sem("vector_step"), step(it, "vector"))
                i = nc.vector.tensor_tensor(v3(tk[8 + j]), v3((tk[4], tk[7])[j]), per_tok(r4[7]), ALU.mult)
                i.then_inc(sem("f2_rows"), 1)
                dve.wait_ge(sem("f2_rows"), at(it, "f2_rows", j + 1))
            dve.wait_ge(sem("f2_spread"), at(it, "f2_spread"))
            for j in range(2):
                nc.vector.tensor_copy(keep[j][:], ps[(5, 6)[j]][:])
                nc.vector.tensor_copy(wt[j][:], ps[(7, 0)[j]][:]).then_inc(sem("vector_step"), 1)
                dve.wait_ge(sem("vector_step"), step(it, "vector"))
            dve.wait_ge(sem("f2_a"), at(it, "f2_a"))
            for j in range(2):
                nc.vector.tensor_tensor(in1[j][:], ps[3][:], keep[j][:], ALU.mult)
                i = nc.vector.tensor_tensor(in3[j][:], ps[4][:], keep[j][:], ALU.mult)
            i.then_inc(sem("f2_in"), 1)
            dve.wait_ge(sem("f2_in"), at(it, "f2_in"))

            def z_part(j):
                nc.vector.tensor_tensor(zw[j], ps[7][:], keep[j][:], ALU.mult).then_inc(sem("f2_zc"), 1)

            for n in range(8):
                j, f = n // 4, n % 4
                dve.wait_ge(sem("f2_th"), at(it, "f2_th", n + 1))
                if n >= 2:
                    dve.wait_ge(sem("f2_z"), at(it, "f2_z", n - 1))
                nc.vector.scalar_tensor_tensor(out=aw[n % 2], in0=th[n % 2], scalar=1.0, in1=ps[2 + 2 * (n % 2)][:], op0=ALU.add, op1=ALU.mult).then_inc(sem("vector_step"), 1)
                dve.wait_ge(sem("vector_step"), step(it, "vector"))
                nc.vector.tensor_tensor(aw[n % 2], aw[n % 2], ps[3 + 2 * (n % 2)][:], ALU.mult).then_inc(sem("vector_step"), 1)
                dve.wait_ge(sem("vector_step"), step(it, "vector"))
                nc.vector.tensor_tensor(aw[n % 2], aw[n % 2], wt[j][:], ALU.mult).then_inc(sem("f2_aw"), 1)
                dve.wait_ge(sem("f2_aw"), at(it, "f2_aw", n + 1))
                if n == 3:
                    dve.wait_ge(sem("f2_z"), at(it, "f2_z", 4))
                    z_part(0)
            dve.wait_ge(sem("f2_z"), at(it, "f2_z", 8))
            z_part(1)
            dve.wait_ge(sem("f2_out"), at(it, "f2_out"))
            nc.vector.scalar_tensor_tensor(out=X[:], in0=ps[6][:], scalar=mod(2, 5), in1=X[:], op0=ALU.mult, op1=ALU.add).then_inc(sem("ln_x"), 1)
            dve.wait_ge(sem("ln_x"), at(it, "ln_x", 7))

        spread_o = big[0][:].rearrange("p a b -> p (a b)").rearrange("p (n c) -> p n c", c=128)
        spread_o2 = big[1][:].rearrange("p a b -> p (a b)").rearrange("p (n c) -> p n c", c=128)

        def a3_pe(pe, it):
            pe.wait_ge(sem("ln_h"), at(it, "ln_h", 8))
            nc.tensor.matmul(ps[2][:], wqk3[:, 0:128], h, start=True, stop=True).then_inc(sem("a3_q"), 1)
            nc.tensor.matmul(ps[3][:], wqk3[:, 128:256], h, start=True, stop=True).then_inc(sem("a3_k"), 1)
            for t in range(NT):
                o = ps[7][:, 128 * t:128 * t + 128]
                nc.tensor.matmul(o, h[:, 128 * t:128 * t + 128], wv3[:], start=True, stop=False)
                i = nc.tensor.matmul(o, ones[0:1, :], bv3[0:1, :], start=False, stop=True)
            i.then_inc(sem("a3_v"), 1)
            pe.wait_ge(sem("a3_qkv"), at(it, "a3_qkv"))
            pe.wait_ge(sem("a3_vc"), at(it, "a3_vc"))
            att_pe(pe, it, 16, H2N, False)
            pe.wait_ge(sem("a3_o"), at(it, "a3_o"))
            for n in range(NT * H3N):
                t, hd = n // H3N, n % H3N
                i = nc.tensor.matmul(ps[7][:, 64 * hd + 16 * t:64 * hd + 16 * t + 16],
                                     (spread_o if n < 16 else spread_o2)[:, n % 16, :], k("oct16"), start=True, stop=True)
            i.then_inc(sem("a3_out"), 1)

        def a3_act(act, it):
            act.wait_ge(sem("a3_v"), at(it, "a3_v"))
            nc.scalar.activation(vA[:], ps[7][:], ACT.Copy).then_inc(sem("a3_vc"), 1)
            att_act(act, it, 16, H2N, False)

        def a3_dve(dve, it):
            dve.wait_ge(sem("a3_q"), at(it, "a3_q"))
            nc.vector.tensor_scalar(w[7][:], ps[2][:], vec("L3_attn_bq"), None, ALU.add).then_inc(sem("vector_step"), 1)
            dve.wait_ge(sem("vector_step"), step(it, "vector"))
            for m in range(2):
                nc.vector.tensor_scalar(q_of[m][:], w[7][:], k("head2")[:, m:m + 1], None, ALU.mult).then_inc(sem("a3_qkv"), 1)
            dve.wait_ge(sem("a3_k"), at(it, "a3_k"))
            nc.vector.tensor_scalar(kT[:], ps[3][:], vec("L3_attn_bk"), None, ALU.add).then_inc(sem("a3_qkv"), 1)
            att_dve(dve, it, 16, H2N, False).then_inc(sem("vector_step"), 1)
            dve.wait_ge(sem("vector_step"), step(it, "vector"))
            for n in range(NT * H3N):
                i = nc.vector.tensor_tensor((spread_o if n < 16 else spread_o2)[:, n % 16, :].rearrange("p (r d) -> p r d", r=8),
                                            o_tok[:, 16 * n:16 * n + 16].rearrange("p (o d) -> p o d", o=1).broadcast_to([128, 8, 16]),
                                            k("row8").rearrange("p (r o) -> p r o", o=1).broadcast_to([128, 8, 16]), ALU.mult)
            i.then_inc(sem("a3_o"), 1)
            dve.wait_ge(sem("a3_o"), at(it, "a3_o"))
            dve.wait_ge(sem("a3_out"), at(it, "a3_out"))
            nc.vector.scalar_tensor_tensor(out=X[:], in0=ps[7][:], scalar=mod(3, 2), in1=X[:], op0=ALU.mult, op1=ALU.add).then_inc(sem("ln_x"), 1)
            dve.wait_ge(sem("ln_x"), at(it, "ln_x", 8))

        htok3, wrow, hot, hotT, notsel, selm, m1 = w[0], w[1], w[2], w[3], w[4], w[5], w[6]
        msk = big[3]
        R = slice(0, 2 * KS)
        xs, x1, x2n, proc = selm[R, 0:128], selm[R, 128:256], selm[R, 256:384], selm[R, 384:512]
        msel, osel = w[7][R, 0:64], w[7][R, 128:256]
        narrow = w[8]
        qkv4 = w[9]
        wcol, rank = small[:, 288:292], small[:, 292:296]
        cs, wsel, ssq = small[R, 300:308], small[R, 308:309], small[R, 309:312]
        smx, ssum, srec = small[R, 312:328], small[R, 328:344], small[R, 344:360]
        s4 = big[1][R, 0:2, :].rearrange("p a b -> p (a b)")
        q4, pT = big[2][:, 2, :], big[2][:, 0:2, :]
        RS8 = 1.0 / np.sqrt(8.0)

        def hot_i(i):
            return hot[:, 128 * i:128 * i + 128]

        def f3_pe(pe, it):
            pe.wait_ge(sem("ln_h"), at(it, "ln_h", 9))
            for t in range(NT):
                i = nc.tensor.transpose(ps[2][:, 128 * t:128 * t + 128], h[:, 128 * t:128 * t + 128], ident)
            i.then_inc(sem("f3_ht"), 1)
            nc.tensor.matmul(ps[3][:], router_bc[:], h, start=True, stop=True).then_inc(sem("f3_w"), 1)
            pe.wait_ge(sem("f3_cge"), at(it, "f3_cge"))
            for t in range(NT):
                i = nc.tensor.matmul(ps[4][:], onesb[:], cge[:, t, :], start=(t == 0), stop=(t == NT - 1))
            i.then_inc(sem("f3_cnt"), 1)
            pe.wait_ge(sem("f3_hot"), at(it, "f3_hot"))
            pe.wait_ge(sem("f3_htc"), at(it, "f3_htc"))
            pe.wait_ge(sem("f3_rope"), at(it, "f3_rope"))
            for t in range(NT):
                i = nc.tensor.transpose(ps[5][R, 128 * t:128 * t + 128], hot_i(t), ident)
            i.then_inc(sem("f3_hott"), 1)
            for o, wd, src in ((0, 128, lambda t: htok3[:, 128 * t:128 * t + 128]), (128, 1, lambda t: wcol[:, t:t + 1]),
                               (136, 8, lambda t: rope_now[:, t, :])):
                for t in range(NT):
                    i = nc.tensor.matmul(ps[6][R, o:o + wd], hot_i(t), src(t), start=(t == 0), stop=(t == NT - 1))
            i.then_inc(sem("f3_xs"), 1)
            pe.wait_ge(sem("mask_in"), at(it, "mask_in"))
            for j in range(NT):
                for t in range(NT):
                    i = nc.tensor.matmul(ps[7][:, 128 * j:128 * j + 128], msk[:, t, 128 * j:128 * j + 128], hot_i(t),
                                         start=(t == 0), stop=(t == NT - 1))
            i.then_inc(sem("f3_m1"), 1)
            pe.wait_ge(sem("f3_m1c"), at(it, "f3_m1c"))
            for j in range(NT):
                i = nc.tensor.matmul(ps[0][:, 0:64], m1[:, 128 * j:128 * j + 128], hot_i(j)[:, 0:64], start=(j == 0), stop=(j == NT - 1))
            i.then_inc(sem("f3_msel"), 1)
            pe.wait_ge(sem("f3_hn"), at(it, "f3_hn"))
            nc.tensor.transpose(ps[2][:, 0:128], osel, ident).then_inc(sem("f3_hnt"), 1)
            pe.wait_ge(sem("f3_hntc"), at(it, "f3_hntc"))
            nc.tensor.matmul(ps[3][:, 0:384], narrow[:, 0:128], wqkv4[:], start=True, stop=True).then_inc(sem("f3_qkv"), 1)
            pe.wait_ge(sem("f3_ro"), at(it, "f3_ro"))
            nc.tensor.transpose(ps[4][:, 0:128], w[11][:, 0:128], ident)
            nc.tensor.transpose(ps[4][:, 128:256], w[11][:, 128:256], ident).then_inc(sem("f3_rot"), 1)
            pe.wait_ge(sem("f3_qk"), at(it, "f3_qk"))
            for hd in range(H4):
                g = slice(32 * (hd // 4), 32 * (hd // 4) + 32)
                i = nc.tensor.matmul(ps[(0, 1, 2, 5)[hd // 4]][:, 64 * (hd % 4):64 * (hd % 4) + 64], q4[g, 128 * (hd % 4):128 * (hd % 4) + 128],
                                     narrow[g, 128:192], start=True, stop=True, tile_position=(g.start, 0))
            i.then_inc(sem("f3_s"), 1)
            pe.wait_ge(sem("f3_p"), at(it, "f3_p"))
            for n in range(8):
                i = nc.tensor.transpose(ps[(2, 5)[n // 4]][:, 128 * (n % 4):128 * (n % 4) + 128], s4[:, 128 * n:128 * n + 128], ident)
            i.then_inc(sem("f3_pt"), 1)
            pe.wait_ge(sem("f3_ptc"), at(it, "f3_ptc"))
            for hd in range(H4):
                a = 64 * (hd % 2)
                i = nc.tensor.matmul(ps[3 + hd % 2][R, 8 * (hd // 2):8 * (hd // 2) + 8], pT[a:a + 64, hd // 8, 128 * (hd // 2 % 4):128 * (hd // 2 % 4) + 128],
                                     qkv4[a:a + 64, 256 + 8 * hd:264 + 8 * hd], start=True, stop=True, tile_position=(a, 0))
            i.then_inc(sem("f3_o"), 1)
            pe.wait_ge(sem("f3_on"), at(it, "f3_on"))
            nc.tensor.transpose(ps[4][:, 0:128], osel, ident).then_inc(sem("f3_ont"), 1)
            pe.wait_ge(sem("f3_ontc"), at(it, "f3_ontc"))
            nc.tensor.matmul(ps[5][:, 0:128], narrow[:, 0:128], wo4[:], start=True, stop=True).then_inc(sem("f3_wo"), 1)
            pe.wait_ge(sem("f3_h2"), at(it, "f3_h2"))
            nc.tensor.transpose(ps[6][:, 0:128], x2n, ident).then_inc(sem("f3_h2t"), 1)
            pe.wait_ge(sem("f3_h2tc"), at(it, "f3_h2tc"))
            for f in range(4):
                i = nc.tensor.matmul(ps[7][:, 64 * f:64 * f + 64], w14[:, 128 * f:128 * f + 128], narrow[:, 0:64], start=True, stop=True)
            i.then_inc(sem("f3_u"), 1)
            pe.wait_ge(sem("f3_g"), at(it, "f3_g"))
            for f in range(4):
                i = nc.tensor.matmul(ps[2][0:KS, 0:128], w[11][:, 64 * f:64 * f + 64], w24[:, f, :], start=(f == 0), stop=(f == 3))
            i.then_inc(sem("f3_d"), 1)
            pe.wait_ge(sem("f3_proc"), at(it, "f3_proc"))
            nc.tensor.matmul(ps[3][:], proc[0:KS - 1, :], hotT[0:KS - 1, :], start=True, stop=True).then_inc(sem("f3_back"), 1)
            pe.wait_ge(sem("x_done"), at(it, "x_done"))
            for t in range(NT):
                i = nc.tensor.transpose(ps[4][:, 128 * t:128 * t + 128], X[:, 128 * t:128 * t + 128], ident)
            i.then_inc(sem("x_fint"), 1)

        def f3_act(act, it):
            act.wait_ge(sem("f3_ht"), at(it, "f3_ht"))
            nc.scalar.activation(htok3[:], ps[2][:], ACT.Copy).then_inc(sem("f3_htc"), 1)
            act.wait_ge(sem("f3_hott"), at(it, "f3_hott"))
            nc.scalar.activation(hotT[R, :], ps[5][R, :], ACT.Copy).then_inc(sem("f3_hottc"), 1)
            act.wait_ge(sem("f3_m1"), at(it, "f3_m1"))
            nc.scalar.activation(m1[:], ps[7][:], ACT.Copy).then_inc(sem("f3_m1c"), 1)
            act.wait_ge(sem("f3_ms1"), at(it, "f3_ms1"))
            nc.scalar.activation(ssq[:, 1:2], ssq[:, 0:1], ACT.Sqrt, bias=k("eps")[R, 2:3], scale=1.0 / C).then_inc(sem("f3_rt1"), 1)
            act.wait_ge(sem("f3_qkv"), at(it, "f3_qkv"))
            nc.scalar.activation(qkv4[:, 0:384], ps[3][:, 0:384], ACT.Copy).then_inc(sem("f3_qkvc"), 1)
            act.wait_ge(sem("f3_smx"), at(it, "f3_smx"))
            nc.scalar.activation(s4, s4, ACT.Exp).then_inc(sem("f3_p"), 1)
            act.wait_ge(sem("f3_pt"), at(it, "f3_pt"))
            nc.scalar.activation(pT[:, 0, :], ps[2][:], ACT.Copy)
            nc.scalar.activation(pT[:, 1, :], ps[5][:], ACT.Copy).then_inc(sem("f3_ptc"), 1)
            act.wait_ge(sem("f3_ont"), at(it, "f3_ont"))
            nc.scalar.activation(narrow[:, 0:128], ps[4][:, 0:128], ACT.Copy).then_inc(sem("f3_ontc"), 1)
            act.wait_ge(sem("f3_ms2"), at(it, "f3_ms2"))
            nc.scalar.activation(ssq[:, 1:2], ssq[:, 0:1], ACT.Sqrt, bias=k("eps")[R, 2:3], scale=1.0 / C).then_inc(sem("f3_rt2"), 1)
            act.wait_ge(sem("f3_gu"), at(it, "f3_gu"))
            nc.scalar.activation(w[11][:, 0:256], w[11][:, 0:256], ACT.Tanh, scale=0.7978845608028654).then_inc(sem("f3_th"), 1)
            act.wait_ge(sem("x_fint"), at(it, "x_fint"))
            act.wait_ge(sem("x_saved"), 16 * it + 16)
            nc.scalar.activation(x_fin[:].rearrange("p a b -> p (a b)"), ps[4][:], ACT.Copy).then_inc(sem("x_fin"), 1)

        def f3_dve(dve, it):
            dve.wait_ge(sem("f3_w"), at(it, "f3_w"))
            nc.vector.tensor_scalar(wrow[:], ps[3][:], router_b[:, 0:1], None, ALU.add).then_inc(sem("vector_step"), 1)
            dve.wait_ge(sem("vector_step"), step(it, "vector"))
            nc.vector.tensor_tensor(w[5][:].rearrange("p (t n) -> p t n", t=NT), wrow[:].rearrange("p (t n) -> p t n", t=NT),
                                            ident.rearrange("p (o n) -> p o n", o=1).broadcast_to([128, NT, 128]), ALU.mult).then_inc(sem("vector_step"), 1)
            dve.wait_ge(sem("vector_step"), step(it, "vector"))
            nc.vector.tensor_reduce(wcol, w[5][:].rearrange("p (t n) -> p t n", t=NT), AX.X, ALU.add).then_inc(sem("vector_step"), 1)
            dve.wait_ge(sem("vector_step"), step(it, "vector"))
            for t in range(NT):
                i = nc.vector.tensor_scalar(cge[:, t, :], wrow[:], wcol[:, t:t + 1], None, ALU.is_le)
            i.then_inc(sem("f3_cge"), 1)
            for t in range(NT):
                nc.vector.scalar_tensor_tensor(out=big[0][:, t, :], in0=wrow[:], scalar=wcol[:, t:t + 1],
                                                       in1=k("earlier")[:, T * t:T * t + T], op0=ALU.is_equal, op1=ALU.mult).then_inc(sem("vector_step"), 1)
                dve.wait_ge(sem("vector_step"), step(it, "vector"))
                nc.vector.scalar_tensor_tensor(out=big[0][:, t, :], in0=wrow[:], scalar=wcol[:, t:t + 1],
                                                       in1=big[0][:, t, :], op0=ALU.is_gt, op1=ALU.add).then_inc(sem("vector_step"), 1)
                dve.wait_ge(sem("vector_step"), step(it, "vector"))
            nc.vector.tensor_reduce(rank, big[0][:], AX.X, ALU.add).then_inc(sem("vector_step"), 1)
            dve.wait_ge(sem("vector_step"), step(it, "vector"))
            nc.vector.tensor_tensor(hot[:].rearrange("p (t r) -> p t r", t=NT), k("iota").rearrange("p (o r) -> p o r", o=1).broadcast_to([128, NT, 2 * KS]),
                                             rank.rearrange("p (t o) -> p t o", o=1).broadcast_to([128, NT, 2 * KS]), ALU.is_equal).then_inc(sem("f3_hot"), 1)
            dve.wait_ge(sem("f3_hot"), at(it, "f3_hot"))
            nc.vector.tensor_copy(rope_now[:].rearrange("p a b -> p (a b)"), rope[:, bass.ds(it, 1), :, :].rearrange("p o a b -> p (o a b)")).then_inc(sem("f3_rope"), 1)
            dve.wait_ge(sem("f3_rope"), at(it, "f3_rope"))
            dve.wait_ge(sem("f3_cnt"), at(it, "f3_cnt"))
            nc.vector.tensor_scalar(notsel[:], ps[4][:], KS - 0.5, None, ALU.is_ge).then_inc(sem("vector_step"), 1)
            dve.wait_ge(sem("vector_step"), step(it, "vector"))
            dve.wait_ge(sem("f3_xs"), at(it, "f3_xs"))
            nc.vector.tensor_copy(xs, ps[6][R, 0:128]).then_inc(sem("vector_step"), 1)
            dve.wait_ge(sem("vector_step"), step(it, "vector"))
            nc.vector.tensor_copy(wsel, ps[6][R, 128:129]).then_inc(sem("vector_step"), 1)
            dve.wait_ge(sem("vector_step"), step(it, "vector"))
            nc.vector.tensor_copy(cs, ps[6][R, 136:144]).then_inc(sem("vector_step"), 1)
            dve.wait_ge(sem("vector_step"), step(it, "vector"))

            def rms(src, tmp, dst, mean_sq, root, name):
                nc.vector.tensor_tensor(tmp, src, src, ALU.mult).then_inc(sem("vector_step"), 1)
                dve.wait_ge(sem("vector_step"), step(it, "vector"))
                nc.vector.tensor_reduce(ssq[:, 0:1], tmp, AX.X, ALU.add).then_inc(sem(mean_sq), 1)
                dve.wait_ge(sem(mean_sq), at(it, mean_sq))
                dve.wait_ge(sem(root), at(it, root))
                nc.vector.reciprocal(ssq[:, 2:3], ssq[:, 1:2]).then_inc(sem("vector_step"), 1)
                dve.wait_ge(sem("vector_step"), step(it, "vector"))
                nc.vector.tensor_scalar(dst, src, ssq[:, 2:3], None, ALU.mult).then_inc(sem(name), 1)
                dve.wait_ge(sem(name), at(it, name))

            rms(xs, osel, osel, "f3_ms1", "f3_rt1", "f3_hn")
            dve.wait_ge(sem("f3_hnt"), at(it, "f3_hnt"))
            nc.vector.tensor_scalar(narrow[:, 0:128], ps[2][:, 0:128], vec("L3_ffn_ln1"), None, ALU.mult).then_inc(sem("f3_hntc"), 1)
            dve.wait_ge(sem("f3_hntc"), at(it, "f3_hntc"))
            dve.wait_ge(sem("f3_msel"), at(it, "f3_msel"))
            nc.vector.tensor_copy(msel, ps[0][:, 0:64]).then_inc(sem("vector_step"), 1)
            dve.wait_ge(sem("vector_step"), step(it, "vector"))
            nc.vector.memset(msel[:, KS - 1:KS], NEG).then_inc(sem("vector_step"), 1)
            dve.wait_ge(sem("vector_step"), step(it, "vector"))
            dve.wait_ge(sem("f3_qkvc"), at(it, "f3_qkvc"))
            qk = qkv4[R, 0:256].rearrange("p (u two f) -> p u two f", two=2, f=4)
            cos = cs[:, 0:4].rearrange("p (a b f) -> p a b f", a=1, b=1).broadcast_to([128, 32, 2, 4])
            sin = cs[:, 4:8].rearrange("p (a f) -> p a f", a=1).broadcast_to([128, 32, 4])
            ra = w[10][R, 0:256].rearrange("p (u two f) -> p u two f", two=2, f=4)
            rb = w[10][R, 256:512].rearrange("p (u two f) -> p u two f", two=2, f=4)
            ro = w[11][R, 0:256].rearrange("p (u two f) -> p u two f", two=2, f=4)
            nc.vector.tensor_tensor(ra, qk, cos, ALU.mult).then_inc(sem("vector_step"), 1)
            dve.wait_ge(sem("vector_step"), step(it, "vector"))
            nc.vector.tensor_tensor(rb[:, :, 0], qk[:, :, 1], sin, ALU.mult).then_inc(sem("vector_step"), 1)
            dve.wait_ge(sem("vector_step"), step(it, "vector"))
            nc.vector.tensor_tensor(rb[:, :, 1], qk[:, :, 0], sin, ALU.mult).then_inc(sem("vector_step"), 1)
            dve.wait_ge(sem("vector_step"), step(it, "vector"))
            nc.vector.tensor_tensor(ro[:, :, 0], ra[:, :, 0], rb[:, :, 0], ALU.subtract).then_inc(sem("vector_step"), 1)
            dve.wait_ge(sem("vector_step"), step(it, "vector"))
            nc.vector.tensor_tensor(ro[:, :, 1], ra[:, :, 1], rb[:, :, 1], ALU.add).then_inc(sem("f3_ro"), 1)
            dve.wait_ge(sem("f3_ro"), at(it, "f3_ro"))
            dve.wait_ge(sem("f3_rot"), at(it, "f3_rot"))
            nc.vector.tensor_copy(narrow[:, 128:192], ps[4][:, 128:192]).then_inc(sem("vector_step"), 1)
            dve.wait_ge(sem("vector_step"), step(it, "vector"))
            for m in range(4):
                i = nc.vector.tensor_scalar(q4[:, 128 * m:128 * m + 128], ps[4][:, 0:128], k("head4")[:, m:m + 1], None, ALU.mult)
            i.then_inc(sem("f3_qk"), 1)
            dve.wait_ge(sem("f3_s"), at(it, "f3_s"))
            for g in range(4):
                nc.vector.scalar_tensor_tensor(out=s4[:, 256 * g:256 * g + 256].rearrange("p (u n) -> p u n", n=64),
                                                       in0=ps[(0, 1, 2, 5)[g]][R, 0:256].rearrange("p (u n) -> p u n", n=64), scalar=RS8,
                                                       in1=msel.rearrange("p (o n) -> p o n", o=1).broadcast_to([128, 4, 64]), op0=ALU.mult, op1=ALU.add).then_inc(sem("vector_step"), 1)
                dve.wait_ge(sem("vector_step"), step(it, "vector"))
            s4v = s4.rearrange("p (u n) -> p u n", n=64)
            nc.vector.tensor_reduce(smx, s4v, AX.X, ALU.max).then_inc(sem("vector_step"), 1)
            dve.wait_ge(sem("vector_step"), step(it, "vector"))
            nc.vector.tensor_tensor(s4v, s4v, smx.rearrange("p (u o) -> p u o", o=1).broadcast_to([128, 16, 64]), ALU.subtract).then_inc(sem("f3_smx"), 1)
            dve.wait_ge(sem("f3_smx"), at(it, "f3_smx"))
            dve.wait_ge(sem("f3_p"), at(it, "f3_p"))
            nc.vector.tensor_reduce(ssum, s4v, AX.X, ALU.add).then_inc(sem("vector_step"), 1)
            dve.wait_ge(sem("vector_step"), step(it, "vector"))
            nc.vector.reciprocal(srec, ssum).then_inc(sem("vector_step"), 1)
            dve.wait_ge(sem("vector_step"), step(it, "vector"))
            dve.wait_ge(sem("f3_o"), at(it, "f3_o"))
            for e in range(2):
                i = nc.vector.tensor_tensor(osel.rearrange("p (u e d) -> p e u d", e=2, d=HD4)[:, e], ps[3 + e][R, 0:64].rearrange("p (u d) -> p u d", d=HD4),
                                            srec.rearrange("p (u e o) -> p e u o", e=2, o=1)[:, e].broadcast_to([128, H4 // 2, HD4]), ALU.mult)
            i.then_inc(sem("f3_on"), 1)
            dve.wait_ge(sem("f3_on"), at(it, "f3_on"))
            dve.wait_ge(sem("f3_wo"), at(it, "f3_wo"))
            nc.vector.tensor_tensor(x1, xs, ps[5][R, 0:128], ALU.add).then_inc(sem("vector_step"), 1)
            dve.wait_ge(sem("vector_step"), step(it, "vector"))
            rms(x1, x2n, x2n, "f3_ms2", "f3_rt2", "f3_h2")
            dve.wait_ge(sem("f3_h2t"), at(it, "f3_h2t"))
            nc.vector.tensor_scalar(narrow[:, 0:128], ps[6][:, 0:128], vec("L3_ffn_ln2"), None, ALU.mult).then_inc(sem("f3_h2tc"), 1)
            dve.wait_ge(sem("f3_h2tc"), at(it, "f3_h2tc"))
            u, g, gg = w[10][:, 0:256], w[11][:, 0:256], w[11][:, 256:512]
            dve.wait_ge(sem("f3_u"), at(it, "f3_u"))
            nc.vector.tensor_copy(u, ps[7][:, 0:256]).then_inc(sem("vector_step"), 1)
            dve.wait_ge(sem("vector_step"), step(it, "vector"))
            nc.vector.tensor_tensor(gg, u, u, ALU.mult).then_inc(sem("vector_step"), 1)
            dve.wait_ge(sem("vector_step"), step(it, "vector"))
            nc.vector.tensor_scalar(gg, gg, 0.044715, 1.0, ALU.mult, ALU.add).then_inc(sem("vector_step"), 1)
            dve.wait_ge(sem("vector_step"), step(it, "vector"))
            nc.vector.tensor_tensor(g, gg, u, ALU.mult).then_inc(sem("f3_gu"), 1)
            dve.wait_ge(sem("f3_gu"), at(it, "f3_gu"))
            dve.wait_ge(sem("f3_th"), at(it, "f3_th"))
            nc.vector.tensor_scalar(g, g, 1.0, 0.5, ALU.add, ALU.mult).then_inc(sem("vector_step"), 1)
            dve.wait_ge(sem("vector_step"), step(it, "vector"))
            nc.vector.tensor_tensor(g, g, u, ALU.mult).then_inc(sem("f3_g"), 1)
            dve.wait_ge(sem("f3_g"), at(it, "f3_g"))
            dve.wait_ge(sem("f3_d"), at(it, "f3_d"))
            nc.vector.tensor_tensor(x2n[0:KS], x1[0:KS], ps[2][0:KS, 0:128], ALU.add).then_inc(sem("vector_step"), 1)
            dve.wait_ge(sem("vector_step"), step(it, "vector"))
            dve.wait_ge(sem("f3_hottc"), at(it, "f3_hottc"))
            nc.vector.tensor_scalar(proc[0:KS], x2n[0:KS], wsel[0:KS], None, ALU.mult).then_inc(sem("f3_proc"), 1)
            dve.wait_ge(sem("f3_proc"), at(it, "f3_proc"))
            nc.vector.tensor_tensor(notsel[:], notsel[:], h, ALU.mult).then_inc(sem("vector_step"), 1)
            dve.wait_ge(sem("vector_step"), step(it, "vector"))
            dve.wait_ge(sem("f3_back"), at(it, "f3_back"))
            nc.vector.tensor_tensor(notsel[:], notsel[:], ps[3][:], ALU.add).then_inc(sem("vector_step"), 1)
            dve.wait_ge(sem("vector_step"), step(it, "vector"))
            nc.vector.scalar_tensor_tensor(out=X[:], in0=notsel[:], scalar=mod(3, 5), in1=X[:], op0=ALU.mult, op1=ALU.add).then_inc(sem("x_done"), 1)
            dve.wait_ge(sem("x_done"), at(it, "x_done"))

        cge = sb("cge", [128, NT, T], BF16)
        mabs = sb("mabs", [128, 4, 8])
        onesb = sb("onesb", [128, 128], BF16)
        rope_now = sb("rope_now", [128, NT, 8])

        def flat(ap):
            return ap.rearrange("(a n) -> a n", a=1)

        loads = [(const[:], d["const"])]
        for i, n in enumerate(VEC):
            src = {"bq2": lambda: flat(d["L2_attn_b_qkv"][0:128]), "bk2": lambda: flat(d["L2_attn_b_qkv"][128:256]),
                   "L1_attn_time_faaaa": lambda: d[n].rearrange("(a h) n -> a (h n)", a=1)}.get(n, lambda: flat(d[n]))()
            loads.append((vec_rows[i:i + 1, :], src))
        loads += [
            (bias_row[0:1, 0:128], flat(d["L0_attn_bk"])), (bias_row[0:1, 128:256], flat(d["L0_attn_bv"])),
            (bias_row[0:1, 256:384], flat(d["L2_attn_b_qkv"][256:384])), (bias_row[0:1, 384:1408], flat(d["L3_attn_bv"])),
            (bias_row[0:1, 1408:1409], flat(d["L3_ffn_router_b"])),
            (wq0[:], d["L0_attn_Wq"]), (wkv0[:, 0:128], d["L0_attn_Wk"]), (wkv0[:, 128:256], d["L0_attn_Wv"]),
            (ctl[:, 0:64], d["L0_ffn_controller"].rearrange("d n s -> d (n s)")),
            (ctl[:, 64:128], d["L0_ffn_controller"].rearrange("d n s -> d (n s)")),
            (f1[:], d["L0_ffn_f1"].rearrange("d n s f -> d (n s) f")),
            (bias0_rows[:], d["L0_ffn_bias"].rearrange("n (a e) f -> (n a) (e f)", e=2)),
        ]
        f2v = d["L0_ffn_f2"].rearrange("n (a e) f d -> e f (n a) d", e=2)
        w2v = d["L1_ffn_w2"].rearrange("(q e) h d -> e h q d", e=2)
        for e in range(2):
            loads += [(f2[64 * e:64 * e + 64, :, :], f2v[e]), (w2s[64 * e:64 * e + 64, :, :], w2v[e])]
        for l in range(4):
            loads += [(wmod[:, l, :], d[f"L{l}_wmod"]), (c_rows[8 * l:8 * l + 8, :], d[f"L{l}_c"])]
        maw2 = d["L1_attn_time_maa_w2"]
        loads += [(w1mix[:], d["L1_attn_time_maa_w1"]), (w2mix[:], maw2[0:4].rearrange("s d c -> (s d) c")), (w2mix4[:], maw2[4]),
                  (dw1[:], d["L1_attn_time_decay_w1"]), (dw2[:], d["L1_attn_time_decay_w2"])]
        loads += [(w5[:, i, :], d["L1_attn_W" + n]) for i, n in enumerate("rkvgo")]
        loads += [(gw1[:], d["L1_ffn_gate_w"]), (w1s[:], d["L1_ffn_w1"].rearrange("e d h -> d e h")),
                  (w3s[:], d["L1_ffn_w3"].rearrange("e d h -> d e h")),
                  (wqkv2[:], d["L2_attn_w_qkv"]), (wout2[:], d["L2_attn_w_out"]), (gate2_rows[:], d["L2_ffn_gate_w"]),
                  (raw[:, WG:WG + 4, :], d["L2_ffn_w_gate"].rearrange("(f p) d -> p f d", p=128)),
                  (raw[:, WU:WU + 4, :], d["L2_ffn_w_up"].rearrange("(f p) d -> p f d", p=128)),
                  (raw[:, WD:WD + 4, :], d["L2_ffn_w_down"].rearrange("d (f q) -> d f q", q=128)),
                  (raw[:, A2:A2 + 4, :], d["L2_ffn_A2"].rearrange("e r (f q) -> (e r) f q", q=128)),
                  (raw[:, A1, :], d["L2_ffn_A1"].rearrange("e r d -> (e r) d")), (raw[:, A3, :], d["L2_ffn_A3"].rearrange("e r d -> (e r) d")),
                  (raw[:, B2, :].rearrange("p (e r) -> p e r", e=E2), d["L2_ffn_B2"].rearrange("e d r -> d e r"))]
        for name, first in (("B1", B1), ("B3", B3)):
            v = d["L2_ffn_" + name].rearrange("e (f p) r -> f p e r", p=128)
            loads += [(raw[:, first + f, :].rearrange("p (e r) -> p e r", e=E2), v[f]) for f in range(4)]
        loads += [(wqk3[:, 0:128], d["L3_attn_Wq"]), (wqk3[:, 128:256], d["L3_attn_Wk"]),
                  (wv3_wide.rearrange("p a b -> p (a b)"), d["L3_attn_Wv"]), (router[:], d["L3_ffn_router_w"]),
                  (wqkv4[:, 0:128], d["L3_ffn_wq"]), (wqkv4[:, 128:256], d["L3_ffn_wk"]), (wqkv4[:, 256:384], d["L3_ffn_wv"]),
                  (wo4[:], d["L3_ffn_wo"]), (w14[:], d["L3_ffn_w1"]), (w24[:], d["L3_ffn_w2"].rearrange("(f p) d -> p f d", p=128))]

        block = ctx.enter_context(nc.Block())

        @block.sync
        def _(sync):
            for dst, src in loads:
                sync.dma_start(dst, src).then_inc(sem("loaded"), 16)
            sync.dma_start(pos_i[:], d["L3_ffn_position_ids"].rearrange("b (t p) -> (b t) p", p=128)).then_inc(sem("x_saved"), 16)

            def load_x(b):
                sync.dma_start(x_tok[:], d["L0_attn_x"][bass.ds(b, 1)].rearrange("o (t p) c -> p (o t) c", p=128)).then_inc(sem("x_in"), 16)

            def one(it, row, more=True):
                if more:
                    following = sync.snap(it + 1)
                    sync.wait_ge(sem("x_used"), at(it, "x_used"))
                    load_x(following)
                sync.wait_ge(sem("ln_x"), at(it, "ln_x", 4))
                sync.dma_start(msk[:], d["L3_ffn_attention_mask"][bass.ds(row, 1)].rearrange("o u (t p) c -> p (o u t) c", p=128))\
                    .then_inc(sem("mask_in"), 16)
                sync.wait_ge(sem("x_fin"), at(it, "x_fin"))
                sync.dma_start(out[bass.ds(it, 1)].rearrange("o (t p) c -> p (o t) c", p=128), x_fin[:]).then_inc(sem("x_saved"), 16)

            load_x(0)
            with sync.Fori(0, MB) as it:
                one(it, it)
            with sync.Fori(MB, B - 1) as it:
                one(it, MB - 1)
            one(B - 1, MB - 1, more=False)
            sync.wait_ge(sem("x_saved"), 16 * (B + 1))

        @block.tensor
        def _(pe):
            pe.wait_ge(sem("loaded"), 16 * len(loads))
            pe.wait_ge(sem("pos"), 1)
            nc.tensor.transpose(ps[0][:, 0:20], vec_rows[:], ident[0:20, 0:20])
            nc.tensor.transpose(ps[0][:, 32:64], bias0_rows[:], ident[0:32, 0:32])
            nc.tensor.transpose(ps[0][:, 64:96], c_rows[:], ident[0:32, 0:32])
            nc.tensor.transpose(ps[0][:, 96:104], gate2_rows[:], ident[0:8, 0:8])
            nc.tensor.transpose(ps[0][:, 112:128], pos_f[:], ident[0:16, 0:16])
            nc.tensor.matmul(ps[0][:, 130:131], ones[0:1, :], bias_row[0:1, 1408:1409], start=True, stop=True)
            for n in range(27):
                i = nc.tensor.transpose(ps[1 + n // 4][:, 128 * (n % 4):128 * (n % 4) + 128], raw[:, n, :], ident)
            i.then_inc(sem("weights_turned"), 1)
            pe.wait_ge(sem("silu_c"), 1)
            for n in range(24):
                i = nc.tensor.matmul(ps[0][:, 8 * n:8 * n + 8], wmod[:, n // 6, 128 * (n % 6):128 * (n % 6) + 128],
                                     silu_c[:, 8 * (n // 6):8 * (n // 6) + 8], start=True, stop=True)
            i.then_inc(sem("mod"), 1)
            pe.wait_ge(sem("prepared"), 1)
            with pe.Fori(0, B) as it:
                pe.wait_ge(sem("x_in"), at(it, "x_in"))
                for t in range(NT):
                    i = nc.tensor.transpose(ps[5][:, 128 * t:128 * t + 128], x_tok[:, t, :], ident)
                i.then_inc(sem("x_used"), 1)
                for n, stage in enumerate((a0_pe, f0_pe, a1_pe, f1_pe, a2_pe, f2_pe, None, a3_pe, f3_pe)):
                    ln_pe(pe, it, n + 1)
                    if stage:
                        stage(pe, it)

        @block.scalar
        def _(act):
            act.wait_ge(sem("c_turned"), 1)
            act.activation(silu_t[:], silu_c[:], ACT.Tanh, scale=0.5).then_inc(sem("c_tanh"), 1)
            act.wait_ge(sem("angles"), 1)
            act.activation(ang[:].rearrange("p a b -> p (a b)"), angt[:].rearrange("p a b -> p (a b)"), ACT.Sin).then_inc(sem("sines"), 1)
            with act.Fori(0, B) as it:
                enter("scalar")
                for n, stage in enumerate((a0_act, f0_act, a1_act, f1_act, a2_act, f2_act, None, a3_act, f3_act)):
                    ln_act(act, it, n + 1)
                    if stage:
                        stage(act, it)

        @block.vector
        def _(dve):
            it = None
            dve.wait_ge(sem("loaded"), 16 * len(loads))
            dve.wait_ge(sem("x_saved"), 16)
            nc.vector.tensor_copy(pos_f[:], pos_i[:]).then_inc(sem("pos"), 1)
            nc.vector.tensor_copy(identb[:], ident)
            nc.vector.tensor_copy(causalb[:], k("causal"))
            nc.vector.tensor_copy(onesb[:], ones)
            nc.vector.memset(hp[:, 0:1], 0.0)
            nc.vector.memset(v1[:, :, 128:129], 1.0)
            nc.vector.memset(scoresT[:], 0.0)
            nc.vector.memset(shifted[:, :, 0:1], 0.0)
            nc.vector.tensor_reduce(wv3[:], wv3_wide.rearrange("p a (n r) -> p (a n) r", r=8), AX.X, ALU.add)
            nc.vector.tensor_reduce(bv3[:], bias_row[0:1, 384:1408].rearrange("p (n r) -> p n r", r=8), AX.X, ALU.add)
            nc.vector.tensor_copy(router_bc[:], router[:].broadcast_to([128, 128])).then_inc(sem("vector_step"), 1)
            dve.wait_ge(sem("vector_step"), step(it, "vector"))
            dve.wait_ge(sem("weights_turned"), 1)
            for n in range(7):
                m = 4 if n < 6 else 3
                nc.vector.tensor_copy(turned[:, 4 * n:4 * n + m, :].rearrange("p a b -> p (a b)"), ps[1 + n][:, 0:128 * m])
            nc.vector.tensor_copy(vecs[:], ps[0][:, 0:20])
            nc.vector.tensor_copy(bias0[:], ps[0][:, 32:64])
            nc.vector.tensor_copy(gate2[:], ps[0][:, 96:104])
            nc.vector.tensor_copy(pos_c[:], ps[0][:, 112:128])
            nc.vector.tensor_copy(router_b[:], ps[0][:, 130:131])
            nc.vector.tensor_copy(silu_c[:], ps[0][:, 64:96]).then_inc(sem("c_turned"), 1)
            dve.wait_ge(sem("c_tanh"), 1)
            nc.vector.scalar_tensor_tensor(out=silu_t[:], in0=silu_t[:], scalar=1.0, in1=silu_c[:], op0=ALU.add, op1=ALU.mult).then_inc(sem("vector_step"), 1)
            dve.wait_ge(sem("vector_step"), step(it, "vector"))
            nc.vector.tensor_scalar(silu_c[:], silu_t[:], 0.5, None, ALU.mult).then_inc(sem("silu_c"), 1)
            for half in range(2):
                nc.vector.tensor_tensor(ang[:, :, 4 * half:4 * half + 4], pos_c[:].rearrange("p (n o) -> p n o", o=1).broadcast_to([128, 16, 4]),
                                                k("freq").rearrange("p (o f) -> p o f", o=1).broadcast_to([128, 16, 4]), ALU.mult).then_inc(sem("vector_step"), 1)
                dve.wait_ge(sem("vector_step"), step(it, "vector"))
            a2 = ang[:].rearrange("p a b -> p (a b)")
            t2 = angt[:].rearrange("p a b -> p (a b)")
            q2 = small[:, 0:128]
            nc.vector.tensor_scalar(t2, a2, 1.0 / (2 * np.pi), None, ALU.mult).then_inc(sem("vector_step"), 1)
            dve.wait_ge(sem("vector_step"), step(it, "vector"))
            nc.vector.tensor_scalar(q2, t2, 12582912.0, None, ALU.add).then_inc(sem("vector_step"), 1)
            dve.wait_ge(sem("vector_step"), step(it, "vector"))
            nc.vector.tensor_scalar(q2, q2, -12582912.0, None, ALU.add).then_inc(sem("vector_step"), 1)
            dve.wait_ge(sem("vector_step"), step(it, "vector"))
            for part in (6.28125, 0.0019350051879882812, 3.019916050337359e-07):
                nc.vector.scalar_tensor_tensor(out=a2, in0=q2, scalar=-part, in1=a2, op0=ALU.mult, op1=ALU.add).then_inc(sem("vector_step"), 1)
                dve.wait_ge(sem("vector_step"), step(it, "vector"))
            nc.vector.tensor_scalar(ang[:, :, 0:4], ang[:, :, 0:4], np.pi / 2, None, ALU.add).then_inc(sem("vector_step"), 1)
            dve.wait_ge(sem("vector_step"), step(it, "vector"))
            nc.vector.tensor_scalar(t2, a2, np.pi, -2 * np.pi, ALU.is_gt, ALU.mult).then_inc(sem("vector_step"), 1)
            dve.wait_ge(sem("vector_step"), step(it, "vector"))
            nc.vector.tensor_tensor(t2, t2, a2, ALU.add).then_inc(sem("vector_step"), 1)
            dve.wait_ge(sem("vector_step"), step(it, "vector"))
            nc.vector.tensor_scalar(t2, t2, 3.1415925, -3.1415925, ALU.min, ALU.max).then_inc(sem("angles"), 1)
            dve.wait_ge(sem("mod"), 1)
            nc.vector.tensor_copy(mods[:].rearrange("p a b -> p (a b)"), ps[0][:, 0:192]).then_inc(sem("vector_step"), 1)
            dve.wait_ge(sem("vector_step"), step(it, "vector"))
            m4 = mods[:].rearrange("p (l j) b -> p l j b", l=4)
            for j in (1, 4):
                nc.vector.tensor_scalar(m4[:, :, j, :], m4[:, :, j, :], 1.0, None, ALU.add).then_inc(sem("vector_step"), 1)
                dve.wait_ge(sem("vector_step"), step(it, "vector"))
            for j in (2, 5):
                nc.vector.tensor_scalar(mtmp[:], m4[:, :, j, :], 0.0, 2.0, ALU.is_ge, ALU.mult).then_inc(sem("vector_step"), 1)
                dve.wait_ge(sem("vector_step"), step(it, "vector"))
                nc.vector.scalar_tensor_tensor(out=mabs[:], in0=m4[:, :, j, :], scalar=-1.0, in1=m4[:, :, j, :], op0=ALU.mult, op1=ALU.max).then_inc(sem("vector_step"), 1)
                dve.wait_ge(sem("vector_step"), step(it, "vector"))
                nc.vector.tensor_scalar(mabs[:], mabs[:], 0.25, None, ALU.max).then_inc(sem("vector_step"), 1)
                dve.wait_ge(sem("vector_step"), step(it, "vector"))
                nc.vector.scalar_tensor_tensor(out=m4[:, :, j, :], in0=mtmp[:], scalar=-1.0, in1=mabs[:], op0=ALU.add, op1=ALU.mult).then_inc(sem("vector_step"), 1)
                dve.wait_ge(sem("vector_step"), step(it, "vector"))
            dve.wait_ge(sem("sines"), 1)
            for b in range(B):
                i = nc.vector.tensor_copy(rope[:, b, :, :], ang[:, 4 * min(b, MB - 1):4 * min(b, MB - 1) + 4, :])
            i.then_inc(sem("vector_step"), 1)
            dve.wait_ge(sem("vector_step"), step(it, "vector"))
            nc.vector.memset(mtmp[:, 0, 0:1], 0.0).then_inc(sem("prepared"), 1)
            with dve.Fori(0, B) as it:
                enter("vector")
                nc.vector.tensor_copy(mod_now[:].rearrange("p (a o) -> p a o", o=1), mods[:, :, bass.ds(it, 1)]).then_inc(sem("vector_step"), 1)
                dve.wait_ge(sem("vector_step"), step(it, "vector"))
                dve.wait_ge(sem("x_used"), it + 1)
                nc.vector.tensor_copy(X[:], ps[5][:]).then_inc(sem("ln_x"), 1)
                dve.wait_ge(sem("ln_x"), at(it, "ln_x", 1))
                for n, stage in enumerate((a0_dve, f0_dve, a1_dve, f1_dve, a2_dve, f2_dve, None, a3_dve, f3_dve)):
                    l, j = (n // 2, n % 2) if n < 7 else ((3, 0) if n == 7 else (3, 1))
                    if n == 7:
                        ln_dve(dve, it, n + 1, h, vec("L3_attn_gamma"), vec("L3_attn_beta"))
                    else:
                        ln_dve(dve, it, n + 1, X[:], mod(l, 3 * j + 1), mod(l, 3 * j))
                    if stage is f3_dve:
                        f3_dve(dve, it)
                    elif stage:
                        stage(dve, it)
        assert {e: seen[e] for e in STEPS} == STEPS, seen


_INS = [
    'L0_attn_x', 'L0_attn_Wq', 'L0_attn_bq', 'L0_attn_Wk', 'L0_attn_bk', 'L0_attn_Wv', 'L0_attn_bv', 'L0_ffn_controller',
    'L0_ffn_f1', 'L0_ffn_f2', 'L0_ffn_bias', 'L0_c', 'L0_wmod', 'L1_attn_time_maa_x', 'L1_attn_time_maa_w',
    'L1_attn_time_maa_k', 'L1_attn_time_maa_v', 'L1_attn_time_maa_r', 'L1_attn_time_maa_g', 'L1_attn_time_maa_w1',
    'L1_attn_time_maa_w2', 'L1_attn_time_decay', 'L1_attn_time_decay_w1', 'L1_attn_time_decay_w2', 'L1_attn_time_faaaa',
    'L1_attn_Wr', 'L1_attn_Wk', 'L1_attn_Wv', 'L1_attn_Wg', 'L1_attn_Wo', 'L1_attn_ln_w', 'L1_attn_ln_b',
    'L1_ffn_gate_w', 'L1_ffn_w1', 'L1_ffn_w2', 'L1_ffn_w3', 'L1_c', 'L1_wmod', 'L2_attn_w_qkv', 'L2_attn_b_qkv',
    'L2_attn_w_out', 'L2_attn_b_out', 'L2_ffn_gate_w', 'L2_ffn_w_gate', 'L2_ffn_w_up', 'L2_ffn_w_down', 'L2_ffn_A1',
    'L2_ffn_B1', 'L2_ffn_A3', 'L2_ffn_B3', 'L2_ffn_A2', 'L2_ffn_B2', 'L2_c', 'L2_wmod', 'L3_attn_Wq', 'L3_attn_bq',
    'L3_attn_Wk', 'L3_attn_bk', 'L3_attn_Wv', 'L3_attn_bv', 'L3_attn_gamma', 'L3_attn_beta', 'L3_ffn_attention_mask',
    'L3_ffn_position_ids', 'L3_ffn_router_w', 'L3_ffn_router_b', 'L3_ffn_wq', 'L3_ffn_wk', 'L3_ffn_wv', 'L3_ffn_wo',
    'L3_ffn_w1', 'L3_ffn_w2', 'L3_ffn_ln1', 'L3_ffn_ln2', 'L3_c', 'L3_wmod']


def kernel(**inputs):
    import concourse.bacc as bacc
    from concourse.bass_utils import run_bass_kernel_spmd

    nc = bacc.Bacc("TRN2", target_bir_lowering=False, num_devices=1)
    arrays, aps = {}, {}
    for name in _INS:
        a = np.ascontiguousarray(inputs[name])
        arrays[f"in_{name}"] = a
        aps[name] = nc.dram_tensor(f"in_{name}", a.shape, mybir.dt.from_np(a.dtype), kind="ExternalInput").ap()
    arrays["in_const"] = constant_table()[0]
    aps["const"] = nc.dram_tensor("in_const", arrays["in_const"].shape, F32, kind="ExternalInput").ap()
    out = nc.dram_tensor("out", (B, T, C), F32, kind="ExternalOutput").ap()
    build(nc, aps, out)
    r = run_bass_kernel_spmd(nc, [arrays], core_ids=[0])
    return r.results[0]["out"]
```

```python
import numpy as np
import concourse.bass as bass
from concourse import mybir
from contextlib import ExitStack

F32 = mybir.dt.float32
BF16 = mybir.dt.bfloat16
I32 = mybir.dt.int32
ALU = mybir.AluOpType
ACT = mybir.ActivationFunctionType
AX = mybir.AxisListType

B, T, C = 8, 512, 128
NT = T // 128
LN_EPS = 1e-5

NE, NES, EW = 16, 64, 64
NG = T // NE
LORA, HS = 32, 64
LEVELS = (64, 32, 16, 8, 4, 2)
E1, H1 = 8, 64
E2, F2, R2 = 8, 512, 16
D16 = 16
H2N, H3N = 16, 8
MB = 4
KS = int(0.125 * T)
H4, HD4, F4 = 16, 8, 512
NEG = -1.0e30


def constant_table():
    p = np.arange(128)[:, None]
    t = np.arange(T)[None, :]
    c = np.arange(128)[None, :]
    parts = {
        "ident": (p == c),
        "mean": np.full((128, 128), 1.0 / C),
        "ones": np.ones((128, 128)),
        "same16": (p // D16 == c // D16),
        "same64": (p // HS == c // HS),
        "tie": np.broadcast_to(np.linspace(0.0, 1e-6, NE, dtype=np.float32)[np.arange(T) % NE][None], (128, T)),
        "restart": np.broadcast_to((t % 128 != 0), (128, T)),
        "half": (p // NES == (t // NE) % 2),
        "group8": (p // NE == np.arange(8)[None]),
        "head4": (p // HD4 % 4 == np.arange(4)[None]),
        "head8": np.broadcast_to((np.arange(32)[None] // HD4 == np.arange(4)[:, None]).reshape(1, 128), (128, 128)),
        "head16": np.broadcast_to((np.arange(32)[None] // D16 == np.arange(2)[:, None]).reshape(1, 64), (128, 64)),
        "iota": np.broadcast_to(np.arange(2 * KS)[None] % KS, (128, 2 * KS)),
        "causal": np.where(c > p, NEG, 0.0),
        "eps": np.broadcast_to(np.array([[LN_EPS, 64 * LN_EPS, 1e-6]], dtype=np.float32), (128, 3)),
        "index8": np.broadcast_to(np.arange(8)[None], (128, 8)),
        "freq": np.broadcast_to((1.0 / np.float32(10000.0) ** (np.arange(0, HD4, 2, dtype=np.float32) / np.float32(HD4)))[None], (128, 4)),
        "earlier": np.concatenate([(t < 128 * i + p) for i in range(NT)], axis=1),
    }
    q = np.arange(32)[None, :]
    s = p % 32
    lv = []
    for m in (16, 8, 4, 2, 1):
        lv.append((s // (2 * m) == q // (2 * m)) & (s // m % 2 == 0) & (q // m % 2 == 1))
    lv.append(s == q)
    parts["level"] = np.concatenate(lv, axis=1)
    parts["spread1"] = np.concatenate([(p == 2 * pr + c // H1) for pr in range(E1 // 2)], axis=1)
    parts["spread2"] = np.concatenate([(p == 8 * j + c // R2) * 2.0 for j in range(2)] + [(p // 8 == 2 + j + 0 * c) * 0.5 for j in range(2)], axis=1)
    at, off = {}, 0
    for k, v in parts.items():
        at[k] = (off, v.shape[1])
        off += v.shape[1]
    return np.concatenate([np.asarray(v, dtype=np.float32) for v in parts.values()], axis=1), at


def stack_table():
    p = np.arange(128)[:, None]
    c = np.arange(128)[None, :]
    products = (np.array([0, 0, 1, 1, 0, 2, 1, 2]), np.array([0, 1, 0, 1, 2, 0, 2, 1]))
    cols = []
    for width in (HD4, D16):
        head, term, dim = c // (8 * width), c // width % 8, c % width
        for which in range(2):
            for parity in range(2):
                cols.append((p % 32 == 16 * parity + width * head + dim) & (products[which][term] == p // 32))
    for m in range(4):
        cols.append((p % 4 == m) & (p < 12) & (c >= 0))
    return np.concatenate(cols, axis=1).astype(np.float32)


CONST_AT = constant_table()[1]
CONST_W = sum(w for _, w in CONST_AT.values())

PER = {
    "ln_x": 8, "ln_mean": 18, "ln_xc": 18, "ln_sq": 18, "ln_var": 18, "ln_std": 18, "ln_log": 18, "ln_h": 9,
    "att_s": 96, "att_max": 96, "att_exp": 96, "att_t": 96, "att_pv": 24, "att_parts": 6, "att_rowsA": 2, "att_rowsD": 2, "att_stack": 32, "att_stA": 16, "att_stD": 16,
    "att_pm": 8, "att_m": 8, "att_mrow": 8, "att_group": 8, "att_norm": 2,
    "x_in": 16, "x_out": 16, "mask_in": 16,
    "f0_sel": 4, "f0_up": 2, "f0_act": 2, "f0_down": 4, "f0_dev": 4, "f0_tr": 4, "f0_trev": 4,
    "a1_m": 5, "a1_x": 5, "a1_lvl": 6, "a1_q": 7, "a1_st": 3, "a1_st_new": 3,
    "f1_ab": 4, "f1_sp": 4, "f1_sc": 4, "f1_th": 4, "f1_hid": 4,
    "f0_selA": 2, "f0_selD": 2, "f0_up_b": 2, "a0_ek": 2, "a0_v": 2, "a1_a64": 2, "a1_a32": 4, "a1_diagA": 2, "a1_diagV": 2,
    "a1_lvl_e": 6, "f1_a": 4, "f1_y": 4, "f2_rows": 2, "f2_sum": 4, "f2_z": 8, "f2_zc": 2,
    "f2_g": 8, "f2_th": 8, "f2_aw": 8,
}
SHARED = {
    "f0_tensor": ["f0_logit", "f0_ht", "f0_permt", "f0_sel", "f0_up", "f0_down", "f0_tr", "f0_out"],
    "a1_tensor": ["a1_mix", "a1_m", "a1_d1", "a1_k", "a1_v", "a1_w", "a1_r", "a1_g", "a1_kendt", "a1_s64",
                  "a1_st", "a1_sd", "a1_y", "a1_ynt", "a1_out"],
    "a1_scalar": ["a1_tanh", "a1_dt", "a1_kc", "a1_vc", "a1_ew", "a1_rc", "a1_gt", "a1_dend", "a1_kend_e", "a1_kendtok",
                  "a1_lvl_e", "a1_a64", "a1_a32", "a1_diagA", "a1_ysq", "a1_std"],
    "a1_vector": ["a1_xxx", "a1_x", "a1_kend_p", "a1_kend", "a1_lvl", "a1_q", "a1_st_new", "a1_dsum", "a1_diagV", "a1_yc", "a1_var", "a1_yn",
                  "a1_yg"],
    "f3_tensor": ["f3_ht", "f3_w", "f3_cnt", "f3_hott", "f3_xs", "f3_m1", "f3_msel", "f3_hnt", "f3_qkv", "f3_rot",
                  "f3_s", "f3_pt", "f3_o", "f3_ont", "f3_wo", "f3_h2t", "f3_u", "f3_d", "f3_back", "x_fint"],
    "f3_scalar": ["f3_htc", "f3_hottc", "f3_m1c", "f3_rt1", "f3_qkvc", "f3_p", "f3_ptc", "f3_ontc", "f3_rt2", "f3_th", "x_fin"],
    "f3_vector": ["f3_cge", "f3_hot", "f3_rope", "f3_ms1", "f3_hn", "f3_hntc", "f3_ro", "f3_qk", "f3_smx", "f3_on", "f3_ms2", "f3_h2",
                  "f3_h2tc", "f3_gu", "f3_g", "f3_proc", "x_done"],
}
PLACE = {}
for _sem, _names in SHARED.items():
    _n = 0
    for _name in _names:
        PLACE[_name] = (_sem, _n)
        _n += PER.get(_name, 1)
    for _name in _names:
        PLACE[_name] += (_n,)
STEPS = {"vector": 209, "scalar": 1}


def build(nc, d, out):
    with ExitStack() as ctx:
        def sb(name, shape, dt=F32):
            return ctx.enter_context(nc.sbuf_tensor(name, shape, dt))

        sems = {}

        def sem(name):
            name = PLACE.get(name, (name,))[0]
            if name not in sems:
                sems[name] = ctx.enter_context(nc.semaphore(name))
            return sems[name]

        ps = [ctx.enter_context(nc.psum_tensor(f"bank{i}", [128, 512], F32)) for i in range(8)]

        const = sb("const", [128, CONST_W])

        def k(name):
            o, w = CONST_AT[name]
            return const[:, o:o + w]

        ident, mean_m, ones = k("ident"), k("mean"), k("ones")
        identb = sb("identb", [128, 128], BF16)
        causalb = sb("causalb", [128, 128], BF16)
        stack_rows = sb("stack_rows", [128, 2, 2, 2, 128], BF16)
        hot_max = sb("hot_max", [128, 4, 128], BF16)
        max_part = sb("max_part", [128, 2, NT, 32], BF16)
        max_rows = sb("max_rows", [128, 2, T], BF16)

        vec_rows = sb("vec_rows", [20, 128])
        vecs = sb("vecs", [128, 20])
        VEC = ["L0_attn_bq", "L1_attn_time_maa_x", "L1_attn_time_maa_w", "L1_attn_time_maa_k",
               "L1_attn_time_maa_v", "L1_attn_time_maa_r", "L1_attn_time_maa_g", "L1_attn_time_decay",
               "L1_attn_time_faaaa", "L1_attn_ln_w", "L1_attn_ln_b", "L2_attn_b_out", "L3_attn_bq",
               "L3_attn_bk", "L3_attn_gamma", "L3_attn_beta", "L3_ffn_ln1", "L3_ffn_ln2", "bq2", "bk2"]

        def vec(name):
            i = VEC.index(name)
            return vecs[:, i:i + 1]

        bias_row = sb("bias_row", [1, 1409])
        wq0 = sb("wq0", [128, 128])
        wkv0 = sb("wkv0", [128, 256])
        ctl = sb("ctl", [128, 128])
        f1 = sb("f1", [128, NES, EW])
        f2 = sb("f2", [128, NES // 2, 128])
        bias0 = sb("bias0", [128, NES // 2])
        bias0_rows = sb("bias0_rows", [32, 128])
        wide = sb("wide", [128, 4, NT, 512])
        big = [wide[:, i] for i in range(4)]
        wmod = wide[:, 2:4].rearrange("p a b c -> p (a b c)")[:, 0:3072].rearrange("p (l n) -> p l n", l=4)
        wv3_wide = big[3][:, 2:4, :]
        c_rows = sb("c_rows", [32, 128])
        silu_c = sb("silu_c", [128, 32])
        silu_t = sb("silu_t", [128, 32])
        mods = sb("mods", [128, 24, 8])
        mtmp = sb("mtmp", [128, 4, 8])
        mod_now = sb("mod_now", [128, 24])
        w1mix = sb("w1mix", [128, 160])
        w2mix = sb("w2mix", [128, 128])
        w2mix4 = sb("w2mix4", [32, 128])
        dw1 = sb("dw1", [128, 64])
        dw2 = sb("dw2", [64, 128])
        w5 = sb("w5", [128, 5, 128])
        gw1 = sb("gw1", [128, 8])
        w1s = sb("w1s", [128, E1, H1])
        w3s = sb("w3s", [128, E1, H1])
        w2s = sb("w2s", [128, E1 // 2, 128])
        wqkv2 = sb("wqkv2", [128, 384])
        wout2 = sb("wout2", [128, 128])
        raw = wide[:, 0:2].rearrange("p a b c -> p (a b c)")[:, 0:27 * 128].rearrange("p (n c) -> p n c", c=128)
        gate2_rows = sb("gate2_rows", [8, 128])
        turned = sb("turned", [128, 27, 128])
        gate2 = sb("gate2", [128, 8])
        WG, WU, WD, B1, B3, A2, A1, A3, B2 = 0, 4, 8, 12, 16, 20, 24, 25, 26
        wqk3 = sb("wqk3", [128, 256])
        wv3 = sb("wv3", [128, 128])
        bv3 = sb("bv3", [1, 128])
        router = sb("router", [128, 1])
        router_bc = sb("router_bc", [128, 128])
        router_b = sb("router_b", [128, 1])
        wqkv4 = sb("wqkv4", [128, 384])
        wo4 = sb("wo4", [128, 128])
        w14 = sb("w14", [128, 512])
        w24 = sb("w24", [128, 4, 128])
        pos_i = sb("pos_i", [16, 128], I32)
        pos_f = sb("pos_f", [16, 128])
        pos_c = sb("pos_c", [128, 16])
        ang = sb("ang", [128, 16, 8])
        angt = sb("angt", [128, 16, 8])
        rope = sb("rope", [128, 8, NT, 8])

        x_tok = sb("x_tok", [128, NT, 128])
        x_fin = sb("x_fin", [128, NT, 128])
        X = sb("X", [128, T])
        xc = sb("xc", [128, T])
        sq = sb("sq", [128, T])
        rstd = sb("rstd", [128, T])
        hp = sb("hp", [128, T + 1])
        h = hp[:, 1:T + 1]
        w = [sb(f"tile{i}", [128, T]) for i in range(12)]

        def bf_view(tile):
            return tile[:].bitcast(BF16).rearrange("p (a t) -> p a t", a=2)

        xl = [big[1 + i // 4][:, i % 4, :] for i in range(len(LEVELS))]
        scoresT = sb("scoresT", [128, 8, 128])
        state = sb("state", [128, NT, 128])
        small = sb("small", [128, 512])
        v1 = sb("v1", [128, NT, 129])
        shifted = sb("shifted", [128, NT, 128])
        ksum = sb("ksum", [128, 1])

        seen = {"vector": 0, "scalar": 0}
        ahead = {"vector": 0, "scalar": 0}

        def at(it, name, n=None):
            n = PER.get(name, 1) if n is None else n
            before, per = PLACE[name][1:] if name in PLACE else (0, PER.get(name, 1))
            return it * per + before + n

        def step(it, engine):
            seen[engine] += 1
            return seen[engine] if it is None else it * STEPS[engine] + ahead[engine] + seen[engine]

        def enter(engine):
            ahead[engine], seen[engine] = seen[engine], 0

        def half_of(v):
            return slice(v * (T // 2), v * (T // 2) + T // 2)

        def ln_pe(pe, it, n):
            if n == 8:
                pe.wait_ge(sem("ln_h"), at(it, "ln_h", 7))
            else:
                pe.wait_ge(sem("ln_x"), at(it, "ln_x", min(n, 8)))
            for v in range(2):
                nc.tensor.matmul(ps[(0, 2)[v]][:, 0:T // 2], mean_m, (h if n == 8 else X[:])[:, half_of(v)], start=True, stop=True).then_inc(sem("ln_mean"), 1)
            for v in range(2):
                pe.wait_ge(sem("ln_sq"), at(it, "ln_sq", 2 * n - 1 + v))
                nc.tensor.matmul(ps[(1, 3)[v]][:, 0:T // 2], mean_m, sq[:, half_of(v)], start=True, stop=True).then_inc(sem("ln_var"), 1)

        def ln_act(act, it, n):
            for v in range(2):
                act.wait_ge(sem("ln_xc"), at(it, "ln_xc", 2 * n - 1 + v))
                nc.scalar.activation(sq[:, half_of(v)], xc[:, half_of(v)], ACT.Square).then_inc(sem("ln_sq"), 1)
            for v in range(2):
                act.wait_ge(sem("ln_var"), at(it, "ln_var", 2 * n - 1 + v))
                nc.scalar.activation(rstd[:, half_of(v)], ps[(1, 3)[v]][:, 0:T // 2], ACT.Ln, bias=k("eps")[:, 0:1]).then_inc(sem("ln_log"), 1)
            for v in range(2):
                act.wait_ge(sem("ln_log"), at(it, "ln_log", 2 * n - 1 + v))
                nc.scalar.activation(rstd[:, half_of(v)], rstd[:, half_of(v)], ACT.Exp, scale=-0.5).then_inc(sem("ln_std"), 1)

        def ln_dve(dve, it, n, src, scale, bias):
            for v in range(2):
                dve.wait_ge(sem("ln_mean"), at(it, "ln_mean", 2 * n - 1 + v))
                nc.vector.tensor_tensor(xc[:, half_of(v)], src[:, half_of(v)], ps[(0, 2)[v]][:, 0:T // 2], ALU.subtract).then_inc(sem("ln_xc"), 1)
            for v in range(2):
                dve.wait_ge(sem("ln_xc"), at(it, "ln_xc", 2 * n - 1 + v))
                dve.wait_ge(sem("ln_std"), at(it, "ln_std", 2 * n - 1 + v))
                nc.vector.tensor_tensor(xc[:, half_of(v)], xc[:, half_of(v)], rstd[:, half_of(v)], ALU.mult).then_inc(sem("vector_step"), 1)
                dve.wait_ge(sem("vector_step"), step(it, "vector"))
                i = nc.vector.tensor_scalar(h[:, half_of(v)], xc[:, half_of(v)], scale, bias, ALU.mult, ALU.add)
            i.then_inc(sem("ln_h"), 1)
            dve.wait_ge(sem("ln_h"), at(it, "ln_h", n))

        def mod(layer, j):
            i = 6 * layer + j
            return mod_now[:, i:i + 1]

        Q0, K0, e0, t0 = w[0], w[1], w[2], w[3]
        kvm, ksm = w[4], w[5]

        def a0_pe(pe, it):
            pe.wait_ge(sem("ln_h"), at(it, "ln_h", 1))
            nc.tensor.matmul(ps[2][:], wq0[:], h, start=True, stop=True).then_inc(sem("a0_q"), 1)
            for t in range(NT):
                o = ps[3 + t // 2][:, t % 2 * 256:t % 2 * 256 + 256]
                nc.tensor.matmul(o, h[:, 128 * t:128 * t + 128], wkv0[:], start=True, stop=False)
                i = nc.tensor.matmul(o, ones[0:1, :], bias_row[0:1, 0:256], start=False, stop=True)
            i.then_inc(sem("a0_kv"), 1)
            pe.wait_ge(sem("a0_kf"), at(it, "a0_kf"))
            pe.wait_ge(sem("a0_v"), at(it, "a0_v"))
            for t in range(NT):
                i = nc.tensor.matmul(ps[5][:, 0:129], K0[:, 128 * t:128 * t + 128], v1[:, t, :],
                                     start=(t == 0), stop=(t == NT - 1))
            i.then_inc(sem("a0_outer"), 1)
            pe.wait_ge(sem("a0_kvm"), at(it, "a0_kvm"))
            nc.tensor.matmul(ps[6][:], kvm[:, 0:128], Q0[:], start=True, stop=True)
            nc.tensor.matmul(ps[7][:], ksm[:, 0:128], Q0[:], start=True, stop=True).then_inc(sem("a0_out"), 1)

        def a0_act(act, it):
            act.wait_ge(sem("a0_q"), at(it, "a0_q"))
            nc.scalar.activation(e0[:], ps[2][:], ACT.Exp, bias=vec("L0_attn_bq")).then_inc(sem("a0_eq"), 1)
            act.wait_ge(sem("a0_kv"), at(it, "a0_kv"))
            for half in range(2):
                kp = ps[3 + half][:].rearrange("p (t n) -> p t n", t=2)
                act.activation(sq[:, 256 * half:256 * half + 256].rearrange("p (t n) -> p t n", t=2),
                               kp[:, :, 0:128], ACT.Exp).then_inc(sem("a0_ek"), 1)
                act.activation(v1[:, 2 * half:2 * half + 2, 0:128], kp[:, :, 128:256], ACT.Copy).then_inc(sem("a0_v"), 1)

        def a0_dve(dve, it):
            dve.wait_ge(sem("a0_eq"), at(it, "a0_eq"))
            nc.vector.tensor_scalar(t0[:], ps[2][:], vec("L0_attn_bq"), 0.0, ALU.add, ALU.max).then_inc(sem("vector_step"), 1)
            dve.wait_ge(sem("vector_step"), step(it, "vector"))
            nc.vector.scalar_tensor_tensor(out=Q0[:], in0=e0[:], scalar=1.0, in1=t0[:], op0=ALU.min, op1=ALU.add).then_inc(sem("vector_step"), 1)
            dve.wait_ge(sem("vector_step"), step(it, "vector"))
            dve.wait_ge(sem("a0_ek"), at(it, "a0_ek"))
            dve.wait_ge(sem("a0_v"), at(it, "a0_v"))
            for half in range(2):
                kp = ps[3 + half][:].rearrange("p (t n) -> p t n", t=2)
                nc.vector.tensor_scalar(t0[:, 256 * half:256 * half + 256].rearrange("p (t n) -> p t n", t=2),
                                                kp[:, :, 0:128], 0.0, None, ALU.max).then_inc(sem("vector_step"), 1)
                dve.wait_ge(sem("vector_step"), step(it, "vector"))
            nc.vector.scalar_tensor_tensor(out=K0[:], in0=sq[:], scalar=1.0, in1=t0[:], op0=ALU.min, op1=ALU.add).then_inc(sem("a0_kf"), 1)
            dve.wait_ge(sem("a0_kf"), at(it, "a0_kf"))
            dve.wait_ge(sem("a0_outer"), at(it, "a0_outer"))
            nc.vector.tensor_copy(ksum[:], ps[5][:, 128:129]).then_inc(sem("vector_step"), 1)
            dve.wait_ge(sem("vector_step"), step(it, "vector"))
            nc.vector.tensor_tensor(kvm[:, 0:128], ps[5][:, 0:128], k("same16"), ALU.mult).then_inc(sem("vector_step"), 1)
            dve.wait_ge(sem("vector_step"), step(it, "vector"))
            nc.vector.tensor_scalar(ksm[:, 0:128], k("same16"), ksum[:, 0:1], None, ALU.mult).then_inc(sem("a0_kvm"), 1)
            dve.wait_ge(sem("a0_kvm"), at(it, "a0_kvm"))
            dve.wait_ge(sem("a0_out"), at(it, "a0_out"))
            nc.vector.tensor_scalar(t0[:], ps[7][:], 1e-6, None, ALU.add).then_inc(sem("vector_step"), 1)
            dve.wait_ge(sem("vector_step"), step(it, "vector"))
            nc.vector.reciprocal(e0[:], t0[:]).then_inc(sem("vector_step"), 1)
            dve.wait_ge(sem("vector_step"), step(it, "vector"))
            nc.vector.tensor_tensor(t0[:], ps[6][:], e0[:], ALU.mult).then_inc(sem("vector_step"), 1)
            dve.wait_ge(sem("vector_step"), step(it, "vector"))
            nc.vector.scalar_tensor_tensor(out=X[:], in0=t0[:], scalar=mod(0, 2), in1=X[:], op0=ALU.mult, op1=ALU.add).then_inc(sem("ln_x"), 1)
            dve.wait_ge(sem("ln_x"), at(it, "ln_x", 2))

        permT, permBD, lg = w[0], w[1], w[2]
        gmax = small[:, 0:NG]
        htok = w[3]
        bd = big[0]
        sel = big[1][:].rearrange("p a b -> p (a b)").rearrange("p (s g) -> p s g", s=NES)
        inner = big[2][:, 0:2, :].rearrange("p a b -> p (a b)").rearrange("p (q g) -> p q g", q=NES // 2)
        inter = big[3][:].rearrange("p a b -> p (a b)").rearrange("p (g s) -> p g s", g=NG)
        inter_tok = big[0][:].rearrange("p a b -> p (a b)").rearrange("p (n c) -> p n c", c=128)

        def f0_pe(pe, it):
            pe.wait_ge(sem("ln_h"), at(it, "ln_h", 2))
            nc.tensor.matmul(ps[2][:], ctl[:], h, start=True, stop=True).then_inc(sem("f0_logit"), 1)
            for t in range(NT):
                i = nc.tensor.transpose(ps[3][:, 128 * t:128 * t + 128], h[:, 128 * t:128 * t + 128], ident)
            i.then_inc(sem("f0_ht"), 1)
            pe.wait_ge(sem("f0_perm"), at(it, "f0_perm"))
            for t in range(NT):
                i = nc.tensor.transpose(ps[0][:, 128 * t:128 * t + 128], permT[:, 128 * t:128 * t + 128], ident)
            i.then_inc(sem("f0_permt"), 1)
            pe.wait_ge(sem("f0_htok"), at(it, "f0_htok"))
            for t in range(NT):
                pe.wait_ge(sem("f0_bd"), at(it, "f0_bd"))
                i = nc.tensor.matmul(ps[4 + t][:], htok[:, 128 * t:128 * t + 128], bd[:, t, :], start=True, stop=True)
                i.then_inc(sem("f0_sel"), 1)
            pe.wait_ge(sem("f0_selA"), at(it, "f0_selA"))
            pe.wait_ge(sem("f0_selD"), at(it, "f0_selD"))
            for half in range(2):
                for q in range(16 * half, 16 * half + 16):
                    for e in range(2):
                        i = nc.tensor.matmul(ps[half][64 * e:64 * e + 64, 32 * (q % 16):32 * (q % 16) + 32],
                                             f1[:, 2 * q + e, :], sel[:, 2 * q + e, :], start=True, stop=True,
                                             skip_group_check=True)
                i.then_inc(sem("f0_up"), 1)
            for half in range(2):
                pe.wait_ge(sem("f0_act"), at(it, "f0_act", half + 1))
                for e in range(2):
                    for q in range(16 * half, 16 * half + 16):
                        i = nc.tensor.matmul(ps[2 + 2 * half + e][:, 32 * (q % 16):32 * (q % 16) + 32],
                                             f2[64 * e:64 * e + 64, q, :], inner[64 * e:64 * e + 64, q, :],
                                             start=True, stop=True)
                    i.then_inc(sem("f0_down"), 1)
            pe.wait_ge(sem("f0_dev"), at(it, "f0_dev"))
            for n in range(4):
                for m in range(4):
                    i = nc.tensor.transpose(ps[n + (0 if n < 2 else 4)][:, 128 * m:128 * m + 128],
                                            inter[:, 2 * (4 * n + m):2 * (4 * n + m) + 2, :].rearrange("p g s -> p (g s)"), ident)
                i.then_inc(sem("f0_tr"), 1)
            pe.wait_ge(sem("f0_trev"), at(it, "f0_trev"))
            for n in range(NG // 2):
                i = nc.tensor.matmul(ps[2][:, 32 * n:32 * n + 32], inter_tok[:, n, :], permBD[:, 32 * n:32 * n + 32],
                                     start=True, stop=True)
            i.then_inc(sem("f0_out"), 1)

        def f0_act(act, it):
            act.wait_ge(sem("f0_ht"), at(it, "f0_ht"))
            nc.scalar.activation(htok[:], ps[3][:], ACT.Copy).then_inc(sem("f0_htok"), 1)
            for t in (0, 2):
                act.wait_ge(sem("f0_sel"), at(it, "f0_sel", t + 1))
                nc.scalar.activation(sel[:, :, 8 * t:8 * t + 8], ps[4 + t][:].rearrange("p (g s) -> p s g", g=8), ACT.Copy).then_inc(sem("f0_selA"), 1)
            for half in range(2):
                act.wait_ge(sem("f0_up_b"), at(it, "f0_up_b", half + 1))
                nc.scalar.activation(inner[:, 16 * half:16 * half + 16, :], inner[:, 16 * half:16 * half + 16, :], ACT.Relu).then_inc(sem("f0_act"), 1)
            for n in range(4):
                act.wait_ge(sem("f0_down"), at(it, "f0_down", n + 1))
                half, e = n // 2, n % 2
                o = inter.rearrange("p g (q e) -> p e q g", e=2)[:, e, 16 * half:16 * half + 16, :]
                nc.scalar.activation(o, ps[2 + n][:].rearrange("p (q g) -> p q g", q=16), ACT.Copy).then_inc(sem("f0_dev"), 1)
            for n in (0, 2):
                act.wait_ge(sem("f0_tr"), at(it, "f0_tr", n + 1))
                nc.scalar.activation(inter_tok[:, 4 * n:4 * n + 4, :].rearrange("p a b -> p (a b)"),
                                            ps[n + (0 if n < 2 else 4)][:], ACT.Copy).then_inc(sem("f0_trev"), 1)

        def f0_dve(dve, it):
            dve.wait_ge(sem("f0_logit"), at(it, "f0_logit"))
            nc.vector.tensor_tensor(lg[:], ps[2][:], k("tie"), ALU.add).then_inc(sem("vector_step"), 1)
            dve.wait_ge(sem("vector_step"), step(it, "vector"))
            nc.vector.tensor_reduce(gmax, lg[:].rearrange("p (g t) -> p g t", t=NE), AX.X, ALU.max).then_inc(sem("vector_step"), 1)
            dve.wait_ge(sem("vector_step"), step(it, "vector"))
            nc.vector.tensor_tensor(permT[:].rearrange("p (g t) -> p g t", t=NE), lg[:].rearrange("p (g t) -> p g t", t=NE),
                                             gmax.rearrange("p (g o) -> p g o", o=1).broadcast_to([128, NG, NE]), ALU.is_equal).then_inc(sem("f0_perm"), 1)
            dve.wait_ge(sem("f0_perm"), at(it, "f0_perm"))
            nc.vector.tensor_tensor(permBD[:], permT[:], k("half"), ALU.mult).then_inc(sem("vector_step"), 1)
            dve.wait_ge(sem("vector_step"), step(it, "vector"))
            dve.wait_ge(sem("f0_permt"), at(it, "f0_permt"))
            for t in range(NT):
                i = nc.vector.tensor_tensor(bd[:, t, :].rearrange("p (g s) -> p g s", g=8),
                                            ps[0][:, 128 * t:128 * t + 64].rearrange("p (o s) -> p o s", o=1).broadcast_to([128, 8, 64]),
                                            k("group8").rearrange("p (g o) -> p g o", o=1).broadcast_to([128, 8, 64]), ALU.mult)
            i.then_inc(sem("f0_bd"), 1)
            dve.wait_ge(sem("f0_bd"), at(it, "f0_bd"))
            for t in (1, 3):
                dve.wait_ge(sem("f0_sel"), at(it, "f0_sel", t + 1))
                nc.vector.tensor_copy(sel[:, :, 8 * t:8 * t + 8], ps[4 + t][:].rearrange("p (g s) -> p s g", g=8)).then_inc(sem("f0_selD"), 1)
            for half in range(2):
                dve.wait_ge(sem("f0_up"), at(it, "f0_up", half + 1))
                nc.vector.tensor_tensor(inner[:, 16 * half:16 * half + 16, :], ps[half][:].rearrange("p (q g) -> p q g", q=16),
                                               bias0[:, 16 * half:16 * half + 16].rearrange("p (q o) -> p q o", o=1).broadcast_to([128, 16, 32]), ALU.add).then_inc(sem("f0_up_b"), 1)
            for n in (1, 3):
                dve.wait_ge(sem("f0_tr"), at(it, "f0_tr", n + 1))
                nc.vector.tensor_copy(inter_tok[:, 4 * n:4 * n + 4, :].rearrange("p a b -> p (a b)"),
                                             ps[n + (0 if n < 2 else 4)][:]).then_inc(sem("f0_trev"), 1)
            dve.wait_ge(sem("f0_out"), at(it, "f0_out"))
            nc.vector.scalar_tensor_tensor(out=X[:], in0=ps[2][:], scalar=mod(0, 5), in1=X[:], op0=ALU.mult, op1=ALU.add).then_inc(sem("ln_x"), 1)
            dve.wait_ge(sem("ln_x"), at(it, "ln_x", 3))

        mix, mix4, xmix = w[0], w[1], [w[2], w[3], w[4], w[5], w[6]]
        xx, xt = w[7], w[8]
        rT, kT1, gs, ew, P1c = w[9], w[10], w[11], big[3][:, 0, :], big[3][:, 1, :]
        ku, r_in, k_end = big[3][:, 2, :], big[3][:, 3, :], w[0]
        ex, ex2 = w[7], w[8]
        vtok = v1[:, :, 0:128]
        kend_tok = w[1]
        diag = w[4]
        dmask = big[0][:, 0:3, :].rearrange("p a b -> p (a b)")
        yn, yt = w[5], w[6]
        dend = small[:, 64:68]
        st = small[:, 72:112]

        def a1_pe(pe, it):
            pe.wait_ge(sem("a1_xxx"), at(it, "a1_xxx"))
            nc.tensor.matmul(ps[2][:], w1mix[:, 0:128], xt[:], start=True, stop=True)
            nc.tensor.matmul(ps[3][0:32, :], w1mix[:, 128:160], xt[:], start=True, stop=True).then_inc(sem("a1_mix"), 1)
            pe.wait_ge(sem("a1_tanh"), at(it, "a1_tanh"))
            for s in range(5):
                b = (4, 5, 6, 7, 0)[s]
                lw, rh = (w2mix[32 * s:32 * s + 32, :], mix[32 * s:32 * s + 32, :]) if s < 4 else (w2mix4[:], mix4[0:32, :])
                nc.tensor.matmul(ps[b][:], lw, rh, start=True, stop=True).then_inc(sem("a1_m"), 1)
            pe.wait_ge(sem("a1_x"), at(it, "a1_x", 1))
            nc.tensor.matmul(ps[1][0:64, :], dw1[:], xmix[0][:], start=True, stop=True).then_inc(sem("a1_d1"), 1)
            pe.wait_ge(sem("a1_x"), at(it, "a1_x", 2))
            nc.tensor.matmul(ps[2][:], w5[:, 1, :], xmix[1][:], start=True, stop=True).then_inc(sem("a1_k"), 1)
            pe.wait_ge(sem("a1_x"), at(it, "a1_x", 3))
            for t in range(NT):
                i = nc.tensor.matmul(ps[3][:, 128 * t:128 * t + 128], xmix[2][:, 128 * t:128 * t + 128], w5[:, 2, :],
                                     start=True, stop=True)
            i.then_inc(sem("a1_v"), 1)
            pe.wait_ge(sem("a1_dt"), at(it, "a1_dt"))
            nc.tensor.matmul(ps[4][:], dw2[:], sq[0:64, :], start=True, stop=True).then_inc(sem("a1_w"), 1)
            pe.wait_ge(sem("a1_x"), at(it, "a1_x", 5))
            nc.tensor.matmul(ps[5][:], w5[:, 0, :], xmix[3][:], start=True, stop=True).then_inc(sem("a1_r"), 1)
            nc.tensor.matmul(ps[6][:], w5[:, 3, :], xmix[4][:], start=True, stop=True).then_inc(sem("a1_g"), 1)

            pe.wait_ge(sem("a1_kend"), at(it, "a1_kend"))
            for c in range(NT):
                i = nc.tensor.transpose(ps[7][:, 128 * c:128 * c + 128], k_end[:, 128 * c:128 * c + 128], ident)
            i.then_inc(sem("a1_kendt"), 1)
            def level(lv):
                kk, qq = (xl[2 + lv], xl[2 + lv]) if lv < 4 else ((kT1, rT) if lv == 4 else (ku, rT))
                for c in range(NT):
                    for hd in range(2):
                        q = slice(64 * hd, 64 * hd + 64)
                        bank = ps[(2, 4, 5, 7)[2 * hd + lv // 3]]
                        for b in range(4):
                            o = 128 * c + 32 * b
                            f = 128 * (lv % 3) + 32 * c
                            i = nc.tensor.matmul(bank[32 * b:32 * b + 32, f:f + 32], kk[q, o:o + 32], qq[q, o:o + 32],
                                                 start=True, stop=True, skip_group_check=True, tile_position=(q.start, 32 * b))
                return i

            for lv in range(4):
                pe.wait_ge(sem("a1_q"), at(it, "a1_q", 3 + lv))
                if lv == 3:
                    pe.wait_ge(sem("a1_kendtok"), at(it, "a1_kendtok"))
                c = slice(128 * lv, 128 * lv + 128)
                for hd in range(2):
                    q = slice(64 * hd, 64 * hd + 64)
                    nc.tensor.matmul(ps[hd][:, c.start:c.start + 64], xl[0][q, c], xl[0][q, c.start + 64:c.stop], start=True, stop=True)
                    i = nc.tensor.matmul(ps[hd][:, c.start + 64:c.stop], xl[1][q, c],
                                         xl[1][q, c].rearrange("p (b two t) -> p b two t", two=2, t=32)[:, :, 1, :], start=True, stop=True)
                if lv == 3:
                    i.then_inc(sem("a1_s64"), 1)
                level(lv)
            pe.wait_ge(sem("a1_kendtok"), at(it, "a1_kendtok"))
            pe.wait_ge(sem("a1_vc"), at(it, "a1_vc"))
            pe.wait_ge(sem("a1_q"), at(it, "a1_q"))
            for c in range(3):
                nc.tensor.matmul(ps[3][:, 128 * c:128 * c + 128], kend_tok[:, 128 * c:128 * c + 128], vtok[:, c, :],
                                        start=True, stop=True).then_inc(sem("a1_st"), 1)
            level(4)
            level(5).then_inc(sem("a1_sd"), 1)
            pe.wait_ge(sem("a1_st_new"), at(it, "a1_st_new"))
            pe.wait_ge(sem("a1_a64"), at(it, "a1_a64"))
            pe.wait_ge(sem("a1_a32"), at(it, "a1_a32"))
            pe.wait_ge(sem("a1_diagA"), at(it, "a1_diagA"))
            pe.wait_ge(sem("a1_diagV"), at(it, "a1_diagV"))
            for c in range(NT):
                y = ps[6][:, 128 * c:128 * c + 128]
                nc.tensor.matmul(y, r_in[:, 128 * c:128 * c + 128], state[:, c, :], start=True, stop=False, skip_group_check=True)
                for hd in range(2):
                    v = slice(64 * hd, 64 * hd + 64)
                    i = nc.tensor.matmul(y[:, v], scoresT[:, 4 * hd + c, :], vtok[:, c, v], start=False, stop=True, skip_group_check=True)
            i.then_inc(sem("a1_y"), 1)
            pe.wait_ge(sem("a1_yn"), at(it, "a1_yn"))
            for t in range(NT):
                i = nc.tensor.transpose(ps[7][:, 128 * t:128 * t + 128], yn[:, 128 * t:128 * t + 128], ident)
            i.then_inc(sem("a1_ynt"), 1)
            pe.wait_ge(sem("a1_yg"), at(it, "a1_yg"))
            nc.tensor.matmul(ps[2][:], w5[:, 4, :], yt[:], start=True, stop=True).then_inc(sem("a1_out"), 1)

        def a1_act(act, it):
            act.wait_ge(sem("a1_mix"), at(it, "a1_mix"))
            nc.scalar.activation(mix[:], ps[2][:], ACT.Tanh)
            nc.scalar.activation(mix4[0:32, :], ps[3][0:32, :], ACT.Tanh).then_inc(sem("a1_tanh"), 1)
            act.wait_ge(sem("a1_d1"), at(it, "a1_d1"))
            nc.scalar.activation(sq[0:64, :], ps[1][0:64, :], ACT.Tanh).then_inc(sem("a1_dt"), 1)
            act.wait_ge(sem("a1_k"), at(it, "a1_k"))
            nc.scalar.activation(kT1[:], ps[2][:], ACT.Copy).then_inc(sem("a1_kc"), 1)
            act.wait_ge(sem("a1_v"), at(it, "a1_v"))
            nc.scalar.activation(vtok, ps[3][:].rearrange("p (t n) -> p t n", t=NT), ACT.Copy).then_inc(sem("a1_vc"), 1)
            act.wait_ge(sem("a1_w"), at(it, "a1_w"))
            nc.scalar.activation(ew, ps[4][:], ACT.Exp, bias=vec("L1_attn_time_decay")).then_inc(sem("a1_ew"), 1)
            act.wait_ge(sem("a1_r"), at(it, "a1_r"))
            nc.scalar.activation(rT[:], ps[5][:], ACT.Copy).then_inc(sem("a1_rc"), 1)
            act.wait_ge(sem("a1_g"), at(it, "a1_g"))
            nc.scalar.activation(sq[:], ps[6][:], ACT.Tanh, scale=0.5).then_inc(sem("a1_gt"), 1)
            act.wait_ge(sem("a1_kend_p"), at(it, "a1_kend_p"))
            nc.scalar.activation(dend, P1c.rearrange("p (c t) -> p c t", t=128)[:, :, 127], ACT.Exp, scale=-1.0).then_inc(sem("a1_dend"), 1)
            nc.scalar.activation(ex[:], ex[:], ACT.Exp, scale=-1.0).then_inc(sem("scalar_step"), 1)
            act.wait_ge(sem("scalar_step"), step(it, "scalar"))
            nc.scalar.activation(r_in, shifted[:].rearrange("p a b -> p (a b)"), ACT.Exp, scale=-1.0).then_inc(sem("a1_kend_e"), 1)
            act.wait_ge(sem("a1_kendt"), at(it, "a1_kendt"))
            nc.scalar.activation(kend_tok[:], ps[7][:], ACT.Copy).then_inc(sem("a1_kendtok"), 1)
            for lv in range(6):
                act.wait_ge(sem("a1_lvl"), at(it, "a1_lvl", lv + 1))
                nc.scalar.activation(xl[lv][:], xl[lv][:], ACT.Exp, scale=-1.0).then_inc(sem("a1_lvl_e"), 1)
            act.wait_ge(sem("a1_s64"), at(it, "a1_s64"))
            for hd in range(2):
                nc.scalar.activation(scoresT[0:64, 4 * hd:4 * hd + 4, 64:128],
                                            ps[hd][0:64, :].rearrange("p (c n) -> p c n", c=4)[:, :, 0:64], ACT.Copy).then_inc(sem("a1_a64"), 1)
            for hd in range(2):
                for b in range(2):
                    r = slice(64 * b, 64 * b + 32)
                    nc.scalar.activation(scoresT[r, 4 * hd:4 * hd + 4, 64 * b + 32:64 * b + 64],
                                                ps[hd][r, :].rearrange("p (c n) -> p c n", c=4)[:, :, 64 + 32 * b:96 + 32 * b], ACT.Copy).then_inc(sem("a1_a32"), 1)
            act.wait_ge(sem("a1_dsum"), at(it, "a1_dsum"))
            for b in (0, 1):
                r = slice(32 * b, 32 * b + 32)
                nc.scalar.activation(scoresT[r, :, r], diag[r, 0:256].rearrange("p (u q) -> p u q", u=8), ACT.Copy).then_inc(sem("a1_diagA"), 1)
            act.wait_ge(sem("a1_yc"), at(it, "a1_yc"))
            nc.scalar.activation(yt[:], yn[:], ACT.Square).then_inc(sem("a1_ysq"), 1)
            act.wait_ge(sem("a1_var"), at(it, "a1_var"))
            nc.scalar.activation(st[:, 24:32], st[:, 16:24], ACT.Sqrt, bias=k("eps")[:, 1:2], scale=1.0 / HS).then_inc(sem("a1_std"), 1)

        def a1_dve(dve, it):
            nc.vector.tensor_tensor(xx[:], hp[:, 0:T], h, ALU.subtract).then_inc(sem("vector_step"), 1)
            dve.wait_ge(sem("vector_step"), step(it, "vector"))
            nc.vector.scalar_tensor_tensor(out=xt[:], in0=xx[:], scalar=vec("L1_attn_time_maa_x"), in1=h, op0=ALU.mult, op1=ALU.add).then_inc(sem("a1_xxx"), 1)
            dve.wait_ge(sem("a1_xxx"), at(it, "a1_xxx"))
            for s, n in enumerate("wkvrg"):
                b = (4, 5, 6, 7, 0)[s]
                dve.wait_ge(sem("a1_m"), at(it, "a1_m", s + 1))
                nc.vector.scalar_tensor_tensor(out=xmix[s][:], in0=ps[b][:], scalar=vec("L1_attn_time_maa_" + n), in1=xx[:], op0=ALU.add, op1=ALU.mult).then_inc(sem("vector_step"), 1)
                dve.wait_ge(sem("vector_step"), step(it, "vector"))
                nc.vector.tensor_tensor(xmix[s][:], xmix[s][:], h, ALU.add).then_inc(sem("a1_x"), 1)
            dve.wait_ge(sem("a1_ew"), at(it, "a1_ew"))
            nc.vector.tensor_tensor_scan(P1c, k("restart"), ew, 0.0, ALU.mult, ALU.add).then_inc(sem("vector_step"), 1)
            dve.wait_ge(sem("vector_step"), step(it, "vector"))
            c4 = P1c.rearrange("p (c t) -> p c t", t=128)
            nc.vector.tensor_copy(shifted[:, :, 1:128], c4[:, :, 0:127]).then_inc(sem("vector_step"), 1)
            dve.wait_ge(sem("vector_step"), step(it, "vector"))
            dve.wait_ge(sem("a1_x"), at(it, "a1_x", 5))
            nc.vector.tensor_tensor(ex[:].rearrange("p (c t) -> p c t", t=128), c4[:, :, 127:128].broadcast_to([128, NT, 128]), c4, ALU.subtract).then_inc(sem("a1_kend_p"), 1)
            dve.wait_ge(sem("a1_kend_p"), at(it, "a1_kend_p"))
            dve.wait_ge(sem("a1_kend_e"), at(it, "a1_kend_e"))
            dve.wait_ge(sem("a1_kc"), at(it, "a1_kc"))
            nc.vector.tensor_tensor(k_end[:], kT1[:], ex[:], ALU.mult).then_inc(sem("a1_kend"), 1)
            dve.wait_ge(sem("a1_kend"), at(it, "a1_kend"))
            dve.wait_ge(sem("a1_rc"), at(it, "a1_rc"))
            nc.vector.tensor_tensor(r_in, r_in, rT[:], ALU.mult).then_inc(sem("vector_step"), 1)
            dve.wait_ge(sem("vector_step"), step(it, "vector"))
            pprev = shifted[:].rearrange("p a b -> p (a b)")
            dve.wait_ge(sem("a1_g"), at(it, "a1_g"))
            dve.wait_ge(sem("a1_gt"), at(it, "a1_gt"))
            nc.vector.scalar_tensor_tensor(out=gs[:], in0=sq[:], scalar=1.0, in1=ps[6][:], op0=ALU.add, op1=ALU.mult).then_inc(sem("vector_step"), 1)
            dve.wait_ge(sem("vector_step"), step(it, "vector"))

            def halves(ap, m):
                return ap.rearrange("p (n two m) -> p two n m", two=2, m=m)

            for lv, m in enumerate(LEVELS):
                n = T // (2 * m)
                border = halves(P1c, m)[:, 0, :, m - 1:m].broadcast_to([128, n, m])
                nc.vector.tensor_tensor(halves(xl[lv][:], m)[:, 0], border, halves(P1c, m)[:, 0], ALU.subtract).then_inc(sem("vector_step"), 1)
                dve.wait_ge(sem("vector_step"), step(it, "vector"))
                nc.vector.tensor_tensor(halves(xl[lv][:], m)[:, 1], halves(pprev, m)[:, 1], border, ALU.subtract).then_inc(sem("a1_lvl"), 1)
            for lv, m in enumerate(LEVELS):
                dve.wait_ge(sem("a1_lvl_e"), at(it, "a1_lvl_e", lv + 1))
                nc.vector.tensor_tensor(halves(xl[lv][:], m)[:, 0], halves(xl[lv][:], m)[:, 0], halves(kT1[:], m)[:, 0], ALU.mult).then_inc(sem("vector_step"), 1)
                dve.wait_ge(sem("vector_step"), step(it, "vector"))
                nc.vector.tensor_tensor(halves(xl[lv][:], m)[:, 1], halves(xl[lv][:], m)[:, 1], halves(rT[:], m)[:, 1], ALU.mult).then_inc(sem("a1_q"), 1)
            nc.vector.tensor_scalar(ku, kT1[:], vec("L1_attn_time_faaaa"), None, ALU.mult).then_inc(sem("a1_q"), 1)
            dve.wait_ge(sem("a1_dend"), at(it, "a1_dend"))
            nc.vector.memset(state[:, 0, :], 0.0).then_inc(sem("vector_step"), 1)
            dve.wait_ge(sem("vector_step"), step(it, "vector"))
            for c in range(3):
                dve.wait_ge(sem("a1_st"), at(it, "a1_st"))
                nc.vector.tensor_tensor(state[:, c + 1, :], ps[3][:, 128 * c:128 * c + 128], k("same64"), ALU.mult).then_inc(sem("vector_step"), 1)
                dve.wait_ge(sem("vector_step"), step(it, "vector"))
                nc.vector.scalar_tensor_tensor(out=state[:, c + 1, :], in0=state[:, c, :], scalar=dend[:, c:c + 1], in1=state[:, c + 1, :],
                                                        op0=ALU.mult, op1=ALU.add).then_inc(sem("a1_st_new"), 1)
                dve.wait_ge(sem("a1_st_new"), at(it, "a1_st_new", c + 1))
            dve.wait_ge(sem("a1_sd"), at(it, "a1_sd"))
            for pr in range(4):
                nc.vector.tensor_tensor(
                    dmask[:, 384 * pr:384 * pr + 384].rearrange("p (l u q) -> p l u q", l=3, u=4),
                    ps[(2, 4, 5, 7)[pr]][:, 0:384].rearrange("p (l u q) -> p l u q", l=3, u=4),
                    k("level")[:, 96 * (pr % 2):96 * (pr % 2) + 96].rearrange("p (l o q) -> p l o q", l=3, o=1).broadcast_to([128, 3, 4, 32]), ALU.mult).then_inc(sem("vector_step"), 1)
                dve.wait_ge(sem("vector_step"), step(it, "vector"))
            nc.vector.tensor_reduce(diag[:, 0:256].rearrange("p (h u) -> p h u", h=2), dmask.rearrange("p (h l u) -> p h u l", h=2, l=6), AX.X, ALU.add).then_inc(sem("a1_dsum"), 1)
            dve.wait_ge(sem("a1_dsum"), at(it, "a1_dsum"))
            for b in (2, 3):
                r = slice(32 * b, 32 * b + 32)
                nc.vector.tensor_copy(scoresT[r, :, r], diag[r, 0:256].rearrange("p (u q) -> p u q", u=8)).then_inc(sem("a1_diagV"), 1)
            dve.wait_ge(sem("a1_y"), at(it, "a1_y"))
            nc.vector.tensor_reduce(st[:, 0:8], ps[6][:].rearrange("p (u i) -> p u i", u=8), AX.X, ALU.add).then_inc(sem("vector_step"), 1)
            dve.wait_ge(sem("vector_step"), step(it, "vector"))
            nc.vector.tensor_scalar(st[:, 8:16], st[:, 0:8], 1.0 / HS, None, ALU.mult).then_inc(sem("vector_step"), 1)
            dve.wait_ge(sem("vector_step"), step(it, "vector"))
            nc.vector.tensor_tensor(yn[:].rearrange("p (u i) -> p u i", u=8), ps[6][:].rearrange("p (u i) -> p u i", u=8),
                                             st[:, 8:16].rearrange("p (u o) -> p u o", o=1).broadcast_to([128, 8, 64]), ALU.subtract).then_inc(sem("a1_yc"), 1)
            dve.wait_ge(sem("a1_yc"), at(it, "a1_yc"))
            dve.wait_ge(sem("a1_ysq"), at(it, "a1_ysq"))
            nc.vector.tensor_reduce(st[:, 16:24], yt[:].rearrange("p (u i) -> p u i", u=8), AX.X, ALU.add).then_inc(sem("a1_var"), 1)
            dve.wait_ge(sem("a1_var"), at(it, "a1_var"))
            dve.wait_ge(sem("a1_std"), at(it, "a1_std"))
            nc.vector.reciprocal(st[:, 32:40], st[:, 24:32]).then_inc(sem("vector_step"), 1)
            dve.wait_ge(sem("vector_step"), step(it, "vector"))
            nc.vector.tensor_tensor(yn[:].rearrange("p (u i) -> p u i", u=8), yn[:].rearrange("p (u i) -> p u i", u=8),
                                             st[:, 32:40].rearrange("p (u o) -> p u o", o=1).broadcast_to([128, 8, 64]), ALU.mult).then_inc(sem("a1_yn"), 1)
            dve.wait_ge(sem("a1_yn"), at(it, "a1_yn"))
            dve.wait_ge(sem("a1_ynt"), at(it, "a1_ynt"))
            nc.vector.tensor_scalar(yt[:], ps[7][:], vec("L1_attn_ln_w"), vec("L1_attn_ln_b"), ALU.mult, ALU.add).then_inc(sem("vector_step"), 1)
            dve.wait_ge(sem("vector_step"), step(it, "vector"))
            nc.vector.scalar_tensor_tensor(out=yt[:], in0=yt[:], scalar=0.5, in1=gs[:], op0=ALU.mult, op1=ALU.mult).then_inc(sem("a1_yg"), 1)
            dve.wait_ge(sem("a1_yg"), at(it, "a1_yg"))
            dve.wait_ge(sem("a1_out"), at(it, "a1_out"))
            nc.vector.scalar_tensor_tensor(out=X[:], in0=ps[2][:], scalar=mod(1, 2), in1=X[:], op0=ALU.mult, op1=ALU.add).then_inc(sem("ln_x"), 1)
            dve.wait_ge(sem("ln_x"), at(it, "ln_x", 4))

        tk = [w[0][:, 32 * i:32 * i + 32] for i in range(10)]
        r4 = [w[0][:, 320 + 4 * i:324 + 4 * i] for i in range(8)]

        def per_tok(a):
            return a.rearrange("p (t o) -> p t o", o=1).broadcast_to([128, NT, 8])

        def v3(a):
            return a.rearrange("p (t e) -> p t e", t=NT)

        def top2(dve, it, logits, shifted_logits, exponentials):
            idx = k("index8").rearrange("p (o e) -> p o e", o=1).broadcast_to([128, NT, 8])
            nc.vector.tensor_reduce(r4[0], v3(logits), AX.X, ALU.max).then_inc(sem("vector_step"), 1)
            dve.wait_ge(sem("vector_step"), step(it, "vector"))
            nc.vector.tensor_tensor(v3(tk[0]), v3(logits), per_tok(r4[0]), ALU.subtract).then_inc(sem(shifted_logits), 1)
            dve.wait_ge(sem(shifted_logits), at(it, shifted_logits))
            dve.wait_ge(sem(exponentials), at(it, exponentials))
            nc.vector.tensor_reduce(r4[1], v3(tk[0]), AX.X, ALU.add).then_inc(sem("vector_step"), 1)
            dve.wait_ge(sem("vector_step"), step(it, "vector"))
            nc.vector.reciprocal(r4[2], r4[1]).then_inc(sem("vector_step"), 1)
            dve.wait_ge(sem("vector_step"), step(it, "vector"))
            nc.vector.tensor_tensor(v3(tk[1]), v3(tk[0]), per_tok(r4[2]), ALU.mult).then_inc(sem("vector_step"), 1)
            dve.wait_ge(sem("vector_step"), step(it, "vector"))
            src = tk[1]
            for j, (best, hot) in enumerate(((r4[3], tk[4]), (r4[4], tk[7]))):
                nc.vector.tensor_reduce(best, v3(src), AX.X, ALU.max).then_inc(sem("vector_step"), 1)
                dve.wait_ge(sem("vector_step"), step(it, "vector"))
                nc.vector.tensor_tensor(v3(tk[2]), v3(src), per_tok(best), ALU.is_lt).then_inc(sem("vector_step"), 1)
                dve.wait_ge(sem("vector_step"), step(it, "vector"))
                nc.vector.scalar_tensor_tensor(out=v3(tk[3]), in0=v3(tk[2]), scalar=100.0, in1=idx, op0=ALU.mult, op1=ALU.add).then_inc(sem("vector_step"), 1)
                dve.wait_ge(sem("vector_step"), step(it, "vector"))
                nc.vector.tensor_reduce(r4[5], v3(tk[3]), AX.X, ALU.min).then_inc(sem("vector_step"), 1)
                dve.wait_ge(sem("vector_step"), step(it, "vector"))
                nc.vector.tensor_tensor(v3(hot), idx, per_tok(r4[5]), ALU.is_equal).then_inc(sem("vector_step"), 1)
                dve.wait_ge(sem("vector_step"), step(it, "vector"))
                if j == 0:
                    nc.vector.scalar_tensor_tensor(out=tk[5], in0=hot, scalar=-4.0, in1=tk[1], op0=ALU.mult, op1=ALU.add).then_inc(sem("vector_step"), 1)
                    dve.wait_ge(sem("vector_step"), step(it, "vector"))
                    src = tk[5]

        scale_row = w[1]
        sc1, ga1, gb1, hid = [w[2], w[6]], [w[3], w[7]], [w[4], w[8]], [w[5], w[9]]

        def f1_pe(pe, it):
            pe.wait_ge(sem("ln_h"), at(it, "ln_h", 4))
            for t in range(NT):
                i = nc.tensor.matmul(ps[1][:, 8 * t:8 * t + 8], h[:, 128 * t:128 * t + 128], gw1[:], start=True, stop=True)
            i.then_inc(sem("f1_logit"), 1)

            def up(pr):
                nc.tensor.matmul(ps[(4, 2)[pr % 2]][:], w1s[:, 2 * pr:2 * pr + 2, :].rearrange("p a b -> p (a b)"), h, start=True, stop=True)
                nc.tensor.matmul(ps[(5, 3)[pr % 2]][:], w3s[:, 2 * pr:2 * pr + 2, :].rearrange("p a b -> p (a b)"), h,
                                 start=True, stop=True).then_inc(sem("f1_ab"), 1)

            def spread(pr):
                nc.tensor.matmul(ps[(6, 0)[pr % 2]][:], k("spread1")[0:8, 128 * pr:128 * pr + 128], scale_row[0:8, :],
                                 start=True, stop=True).then_inc(sem("f1_sp"), 1)

            up(0)
            up(1)
            pe.wait_ge(sem("f1_scale"), at(it, "f1_scale"))
            for t in range(NT):
                i = nc.tensor.transpose(ps[1][0:8, 128 * t:128 * t + 128], tk[8][:, 8 * t:8 * t + 8], ident)
            i.then_inc(sem("f1_scalet"), 1)
            pe.wait_ge(sem("f1_row"), at(it, "f1_row"))
            spread(0)
            spread(1)
            for pr in range(E1 // 2):
                pe.wait_ge(sem("f1_hid"), at(it, "f1_hid", pr + 1))
                i = nc.tensor.matmul(ps[7][:], w2s[:, pr, :], hid[pr % 2][:], start=(pr == 0), stop=(pr == E1 // 2 - 1), skip_group_check=True)
                i.then_inc(sem("f1_y"), 1)
                if pr + 2 < E1 // 2:
                    spread(pr + 2)
                    up(pr + 2)

        def f1_act(act, it):
            act.wait_ge(sem("f1_sm"), at(it, "f1_sm"))
            nc.scalar.activation(tk[0], tk[0], ACT.Exp).then_inc(sem("f1_sm_e"), 1)
            act.wait_ge(sem("f1_scalet"), at(it, "f1_scalet"))
            nc.scalar.activation(scale_row[0:8, :], ps[1][0:8, :], ACT.Copy).then_inc(sem("f1_row"), 1)

            def spread_copy(pr):
                act.wait_ge(sem("f1_sp"), at(it, "f1_sp", pr + 1))
                nc.scalar.activation(sc1[pr % 2][:], ps[(6, 0)[pr % 2]][:], ACT.Copy).then_inc(sem("f1_sc"), 1)

            spread_copy(0)
            for pr in range(E1 // 2):
                if pr == 0:
                    spread_copy(1)
                act.wait_ge(sem("f1_a"), at(it, "f1_a", pr + 1))
                nc.scalar.activation(gb1[pr % 2][:], ga1[pr % 2][:], ACT.Tanh, scale=0.5).then_inc(sem("f1_th"), 1)
                if 1 <= pr < E1 // 2 - 1:
                    spread_copy(pr + 1)

        def f1_dve(dve, it):
            dve.wait_ge(sem("f1_logit"), at(it, "f1_logit"))
            top2(dve, it, ps[1][:, 0:32], "f1_sm", "f1_sm_e")
            nc.vector.tensor_tensor(tk[8], tk[4], tk[7], ALU.add).then_inc(sem("vector_step"), 1)
            dve.wait_ge(sem("vector_step"), step(it, "vector"))
            nc.vector.tensor_tensor(tk[8], tk[8], tk[1], ALU.mult).then_inc(sem("f1_scale"), 1)
            dve.wait_ge(sem("f1_scale"), at(it, "f1_scale"))

            def scaled(pr):
                dve.wait_ge(sem("f1_sc"), at(it, "f1_sc", pr + 1))
                dve.wait_ge(sem("f1_ab"), at(it, "f1_ab", pr + 1))
                nc.vector.tensor_tensor(ga1[pr % 2][:], ps[(4, 2)[pr % 2]][:], sc1[pr % 2][:], ALU.mult).then_inc(sem("f1_a"), 1)
                nc.vector.tensor_tensor(hid[pr % 2][:], ps[(5, 3)[pr % 2]][:], sc1[pr % 2][:], ALU.mult).then_inc(sem("vector_step"), 1)
                dve.wait_ge(sem("f1_a"), at(it, "f1_a", pr + 1))
                dve.wait_ge(sem("vector_step"), step(it, "vector"))

            def gated(pr):
                dve.wait_ge(sem("f1_th"), at(it, "f1_th", pr + 1))
                nc.vector.scalar_tensor_tensor(out=gb1[pr % 2][:], in0=gb1[pr % 2][:], scalar=1.0, in1=ga1[pr % 2][:], op0=ALU.add, op1=ALU.mult)\
                    .then_inc(sem("vector_step"), 1)
                dve.wait_ge(sem("vector_step"), step(it, "vector"))
                nc.vector.scalar_tensor_tensor(out=hid[pr % 2][:], in0=gb1[pr % 2][:], scalar=0.5, in1=hid[pr % 2][:], op0=ALU.mult, op1=ALU.mult)\
                    .then_inc(sem("f1_hid"), 1)
                dve.wait_ge(sem("f1_hid"), at(it, "f1_hid", pr + 1))

            scaled(0)
            scaled(1)
            gated(0)
            gated(1)
            for pr in range(2, E1 // 2):
                scaled(pr)
                gated(pr)
            dve.wait_ge(sem("f1_y"), at(it, "f1_y"))
            nc.vector.scalar_tensor_tensor(out=X[:], in0=ps[7][:], scalar=mod(1, 5), in1=X[:], op0=ALU.mult, op1=ALU.add).then_inc(sem("ln_x"), 1)
            dve.wait_ge(sem("ln_x"), at(it, "ln_x", 5))

        q_part = [bf_view(w[8])[:, 0, :], bf_view(w[8])[:, 1, :], bf_view(w[9])[:, 0, :]]
        k_part = [bf_view(w[10])[:, 0, :], bf_view(w[10])[:, 1, :], bf_view(w[11])[:, 0, :]]
        q_stack = [bf_view(w[p // 2])[:, p % 2, :] for p in range(8)]
        k_stack = [bf_view(w[4 + p // 2])[:, p % 2, :] for p in range(8)]
        exps = [big[0], big[1]]
        values = wide[:, 2:4].rearrange("p a b c -> p (a b c)")
        oT, sums = w[8], xc
        nmax, nrest = [small[:, 128:144], small[:, 144:160]], small[:, 160:176]
        spread_o = big[0][:].rearrange("p a b -> p (a b)")[0:64, 0:1024]

        def by_head(ap, per):
            return ap.rearrange("p (i m) -> p i m", m=4)[:, :, 0:per]

        part_rows = [[bf_view(big[which][:, g, :])[0:96, 0, :] for g in range(4)] for which in range(2)]

        def att_stacks_pe(pe, it, sel, base):
            pe.wait_ge(sem("att_rowsA"), at(it, "att_rowsA", base // H2N + 1))
            pe.wait_ge(sem("att_rowsD"), at(it, "att_rowsD", base // H2N + 1))
            for n in range(16):
                p, which = n // 2, n % 2
                if n >= 4:
                    if which == 0:
                        pe.wait_ge(sem("att_stA"), at(it, "att_stA", base // 2 + p - 1))
                    else:
                        pe.wait_ge(sem("att_stD"), at(it, "att_stD", base // 2 + p - 1))
                nc.tensor.matmul(ps[n % 4][:], sel[0:96, which, p % 2, :], part_rows[which][p // 2], start=True, stop=True)\
                    .then_inc(sem("att_stack"), 1)
            pe.wait_ge(sem("att_stA"), at(it, "att_stA", base // 2 + 8))
            pe.wait_ge(sem("att_stD"), at(it, "att_stD", base // 2 + 8))

        def att_stacks_act(act, it, base):
            for j in range(3):
                act.wait_ge(sem("att_parts"), at(it, "att_parts", 3 * (base // H2N) + j + 1))
                for g in range(4):
                    i = nc.scalar.activation(part_rows[0][g][32 * j:32 * j + 32], q_part[j][32 * g:32 * g + 32], ACT.Copy)
            i.then_inc(sem("att_rowsA"), 1)
            for p in range(8):
                act.wait_ge(sem("att_stack"), at(it, "att_stack", base + 2 * p + 1))
                nc.scalar.activation(q_stack[p], ps[2 * p % 4][:], ACT.Copy).then_inc(sem("att_stA"), 1)

        def att_stacks_dve(dve, it, base):
            for p in range(8):
                dve.wait_ge(sem("att_stack"), at(it, "att_stack", base + 2 * p + 2))
                nc.vector.tensor_copy(k_stack[p], ps[(2 * p + 1) % 4][:]).then_inc(sem("att_stD"), 1)

        def att_parts_dve(dve, it, base, qf, kf):
            for j in range(3):
                nc.vector.tensor_copy(q_part[j], qf)
                nc.vector.tensor_copy(k_part[j], kf).then_inc(sem("att_parts"), 1)
                dve.wait_ge(sem("att_parts"), at(it, "att_parts", 3 * (base // H2N) + j + 1))
                if j < 2:
                    nc.vector.tensor_tensor(qf, qf, q_part[j], ALU.subtract)
                    nc.vector.tensor_tensor(kf, kf, k_part[j], ALU.subtract).then_inc(sem("vector_step"), 1)
                for g in range(4):
                    i = nc.vector.tensor_copy(part_rows[1][g][32 * j:32 * j + 32], k_part[j][32 * g:32 * g + 32])
                if j < 2:
                    dve.wait_ge(sem("vector_step"), step(it, "vector"))
            i.then_inc(sem("att_rowsD"), 1)

        def att_pe(pe, it, width, base, causal):
            NH, per, gb = 128 // width, 32 // width, base // 4

            def rows(hd):
                return (hd // 2, slice(64 * (hd % 2), 64 * (hd % 2) + 64)) if width == 8 else (hd, slice(0, 128))

            for hh in range(NH + per + 2):
                h2, h3 = hh - per - 1, hh - per - 2
                for i in range(NT):
                    if i == 2 and hh % per == 0 and 0 < hh <= NH:
                        g = hh // per - 1
                        pe.wait_ge(sem("att_pm"), at(it, "att_pm", gb + g + 1))
                        for t in range(NT):
                            ins = nc.tensor.matmul(ps[7][0:32, 128 * t:128 * t + 128], max_part[:, g % 2, t, :], identb[:], start=True, stop=True)
                        ins.then_inc(sem("att_m"), 1)
                    if hh < NH:
                        L = 128 * (i + 1) if causal else T
                        p, r = rows(hh)
                        if 4 * hh + i >= 2:
                            pe.wait_ge(sem("att_max"), at(it, "att_max", (base + hh) * NT + i - 1))
                        ins = nc.tensor.matmul(ps[i % 2][:, 0:L], q_stack[p][r, 128 * i:128 * i + 128], k_stack[p][r, 0:L],
                                               start=True, stop=not causal, tile_position=(r.start, 0))
                        if causal:
                            ins = nc.tensor.matmul(ps[i % 2][:, 128 * i:128 * i + 128], identb[:], causalb[:], start=False, stop=True)
                        ins.then_inc(sem("att_s"), 1)
                    if 0 <= h2 < NH:
                        g, m, j, o = h2 // per, h2 % per, i, (128 * i if causal else 0)
                        p, r = rows(h2)
                        s = ps[2 + (4 * h2 + j) % 3]
                        if m == 0 and j == 0:
                            pe.wait_ge(sem("att_mrow"), at(it, "att_mrow", gb + g + 1))
                        if 4 * h2 + j >= 3:
                            pe.wait_ge(sem("att_exp"), at(it, "att_exp", (base + h2) * NT + j - 2))
                        nc.tensor.matmul(s[:, o:T], k_stack[p][r, 128 * j:128 * j + 128], q_stack[p][r, o:T],
                                         start=True, stop=False, tile_position=(r.start, 0))
                        if causal:
                            nc.tensor.matmul(s[:, o:o + 128], causalb[:], identb[:], start=False, stop=False)
                        nc.tensor.matmul(s[:, o:T], hot_max[:, m, :], max_rows[:, g % 2, o:T], start=False, stop=True).then_inc(sem("att_t"), 1)
                    if 0 <= h3 < NH:
                        g, m, j, o = h3 // per, h3 % per, i, (128 * i if causal else 0)
                        if g >= 2 and m == 0 and j == 0:
                            pe.wait_ge(sem("att_group"), at(it, "att_group", gb + g - 1))
                        pe.wait_ge(sem("att_exp"), at(it, "att_exp", (base + h3) * NT + j + 1))
                        c = 64 * ((4 * j + g) * per + m)
                        ins = nc.tensor.matmul(ps[5 + g % 2][0:64, o:T], values[:, c:c + 64], exps[h3 % 2][:, j, o:T],
                                               start=(m == 0 and j == 0), stop=(m == per - 1 and j == NT - 1), skip_group_check=True)
                        if j == NT - 1:
                            ins.then_inc(sem("att_pv"), 1)

        def att_act(act, it, width, base, causal):
            NH, per, gb = 128 // width, 32 // width, base // 4
            for hh in range(NH + per + 2):
                h2, h3 = hh - per - 1, hh - per - 2
                for j in range(NT):
                    if j == 2 and hh % per == 0 and 0 < hh <= NH:
                        g = hh // per - 1
                        act.wait_ge(sem("att_m"), at(it, "att_m", gb + g + 1))
                        if g >= 2:
                            act.wait_ge(sem("att_t"), at(it, "att_t", (base + per * (g - 1)) * NT))
                        nc.scalar.activation(max_rows[0:32, g % 2, :], ps[7][0:32, :], ACT.Copy).then_inc(sem("att_mrow"), 1)
                    if 0 <= h2 < NH:
                        o = 128 * j if causal else 0
                        act.wait_ge(sem("att_t"), at(it, "att_t", (base + h2) * NT + j + 1))
                        if h2 >= 2 and j == 0:
                            act.wait_ge(sem("att_pv"), at(it, "att_pv", base + h2 - 1))
                        nc.scalar.activation(exps[h2 % 2][:, j, o:T], ps[2 + (4 * h2 + j) % 3][:, o:T], ACT.Exp).then_inc(sem("att_exp"), 1)
                if h3 >= 0 and h3 % per == per - 1:
                    g = h3 // per
                    act.wait_ge(sem("att_pv"), at(it, "att_pv", base + h3 + 1))
                    nc.scalar.activation(sums[32 * g:32 * g + 32, :], ps[5 + g % 2][32:64, :], ACT.Copy)
                    nc.scalar.activation(oT[32 * g:32 * g + 32, :], ps[5 + g % 2][0:32, :], ACT.Copy).then_inc(sem("att_group"), 1)

        def att_dve(dve, it, width, base, causal):
            NH, per, gb = 128 // width, 32 // width, base // 4
            for hh in range(NH):
                g, m = hh // per, hh % per
                for i in range(NT):
                    L = 128 * (i + 1) if causal else T
                    dve.wait_ge(sem("att_s"), at(it, "att_s", (base + hh) * NT + i + 1))
                    nc.vector.tensor_reduce(nmax[g % 2][:, 4 * i + m:4 * i + m + 1], ps[i % 2][:, 0:L], AX.X, ALU.max,
                                            negate=True).then_inc(sem("att_max"), 1)
                if m == per - 1:
                    dve.wait_ge(sem("att_max"), at(it, "att_max", (base + hh + 1) * NT))
                    if g >= 2:
                        dve.wait_ge(sem("att_m"), at(it, "att_m", gb + g - 1))
                    rest = by_head(nmax[g % 2], per)
                    for j in range(3):
                        part = max_part[:, g % 2, :, 4 * j:4 * j + per]
                        i = nc.vector.tensor_copy(part, rest)
                        if j == 2:
                            i.then_inc(sem("att_pm"), 1)
                            break
                        i.then_inc(sem("vector_step"), 1)
                        dve.wait_ge(sem("vector_step"), step(it, "vector"))
                        nc.vector.tensor_tensor(by_head(nrest, per), rest, part, ALU.subtract).then_inc(sem("vector_step"), 1)
                        dve.wait_ge(sem("vector_step"), step(it, "vector"))
                        rest = by_head(nrest, per)
            dve.wait_ge(sem("att_group"), at(it, "att_group", gb + 4))
            nc.vector.reciprocal(sums[:], sums[:]).then_inc(sem("vector_step"), 1)
            dve.wait_ge(sem("vector_step"), step(it, "vector"))
            nc.vector.tensor_tensor(oT[:], oT[:], sums[:], ALU.mult).then_inc(sem("att_norm"), 1)

        def att_values_dve(dve, it, per, mask):
            n = NT * 4
            return nc.vector.tensor_tensor(
                values[:, 0:n * per * 64].rearrange("p (n m c) -> p n m c", n=n, m=per)[:, :, :, 0:32],
                ps[7][:].rearrange("p (n o c) -> p n o c", n=n, o=1).broadcast_to([128, n, per, 32]),
                mask.rearrange("p (o m c) -> p o m c", o=1, m=per).broadcast_to([128, n, per, 32]), ALU.mult)

        def att_ones_act(act, it, per, mask):
            n = NT * 4
            return nc.scalar.activation(
                values[:, 0:n * per * 64].rearrange("p (n m c) -> p n m c", n=n, m=per)[:, :, :, 32:64],
                mask.rearrange("p (o m c) -> p o m c", o=1, m=per).broadcast_to([128, n, per, 32]), ACT.Copy)

        def a2_pe(pe, it):
            pe.wait_ge(sem("ln_h"), at(it, "ln_h", 5))
            nc.tensor.matmul(ps[2][:], wqkv2[:, 0:128], h, start=True, stop=True).then_inc(sem("a2_q"), 1)
            nc.tensor.matmul(ps[3][:], wqkv2[:, 128:256], h, start=True, stop=True).then_inc(sem("a2_k"), 1)
            for t in range(NT):
                o = ps[7][:, 128 * t:128 * t + 128]
                nc.tensor.matmul(o, h[:, 128 * t:128 * t + 128], wqkv2[:, 256:384], start=True, stop=False)
                i = nc.tensor.matmul(o, ones[0:1, :], bias_row[0:1, 256:384], start=False, stop=True)
            i.then_inc(sem("a2_v"), 1)
            att_stacks_pe(pe, it, stack_rows[:, 0], 0)
            pe.wait_ge(sem("a2_ones"), at(it, "a2_ones"))
            pe.wait_ge(sem("a2_vc"), at(it, "a2_vc"))
            att_pe(pe, it, 8, 0, True)
            pe.wait_ge(sem("att_norm"), at(it, "att_norm", 1))
            nc.tensor.matmul(ps[2][:], wout2[:], oT[:], start=True, stop=True).then_inc(sem("a2_out"), 1)

        def a2_act(act, it):
            act.wait_ge(sem("ln_h"), at(it, "ln_h", 5))
            att_ones_act(act, it, 4, k("head8")).then_inc(sem("a2_ones"), 1)
            att_stacks_act(act, it, 0)
            att_act(act, it, 8, 0, True)

        def a2_dve(dve, it):
            dve.wait_ge(sem("a2_q"), at(it, "a2_q"))
            nc.vector.tensor_scalar(sq[:], ps[2][:], vec("bq2"), 1.0 / np.sqrt(8.0), ALU.add, ALU.mult)
            dve.wait_ge(sem("a2_k"), at(it, "a2_k"))
            nc.vector.tensor_scalar(rstd[:], ps[3][:], vec("bk2"), None, ALU.add).then_inc(sem("vector_step"), 1)
            dve.wait_ge(sem("vector_step"), step(it, "vector"))
            att_parts_dve(dve, it, 0, sq[:], rstd[:])
            dve.wait_ge(sem("a2_v"), at(it, "a2_v"))
            att_values_dve(dve, it, 4, k("head8")).then_inc(sem("a2_vc"), 1)
            att_stacks_dve(dve, it, 0)
            att_dve(dve, it, 8, 0, True)
            dve.wait_ge(sem("a2_out"), at(it, "a2_out"))
            nc.vector.tensor_scalar(w[7][:], ps[2][:], vec("L2_attn_b_out"), None, ALU.add).then_inc(sem("vector_step"), 1)
            dve.wait_ge(sem("vector_step"), step(it, "vector"))
            nc.vector.scalar_tensor_tensor(out=X[:], in0=w[7][:], scalar=mod(2, 2), in1=X[:], op0=ALU.mult, op1=ALU.add).then_inc(sem("ln_x"), 1)
            dve.wait_ge(sem("ln_x"), at(it, "ln_x", 6))

        slot_row = small[:, 160:288]
        slot_rows = big[0][:, 0, :]
        keep, keep_d = [w[1], w[2]], w[0]
        in1, in3 = [w[5], w[6]], [w[7], w[8]]
        wt = [w[9], w[10]]
        aw = [[big[1][:, 2 * f + j, :] for j in range(2)] for f in range(2)]
        aw_sum = [w[3], w[4]]
        th = [big[2][:, 0, :], big[2][:, 1, :]]
        zw = [big[2][:, 2, :], big[2][:, 3, :]]
        F2_ORDER = [(0, 0), (1, 0), (0, 1), (1, 1), (2, 0), (3, 0), (2, 1), (3, 1)]

        def f2_pe(pe, it):
            pe.wait_ge(sem("ln_h"), at(it, "ln_h", 6))
            for t in range(NT):
                i = nc.tensor.matmul(ps[1][:, 8 * t:8 * t + 8], h[:, 128 * t:128 * t + 128], gate2[:], start=True, stop=True)
            i.then_inc(sem("f2_logit"), 1)

            def dense(f):
                nc.tensor.matmul(ps[2 + 2 * (f % 2)][:], turned[:, WG + f, :], h, start=True, stop=False, skip_group_check=True)
                nc.tensor.matmul(ps[3 + 2 * (f % 2)][:], turned[:, WU + f, :], h, start=True, stop=False, skip_group_check=True)

            def low_rank(f, j):
                nc.tensor.matmul(ps[2 + 2 * (f % 2)][:], turned[:, B1 + f, :], in1[j][:], start=False, stop=(j == 1), skip_group_check=True)
                nc.tensor.matmul(ps[3 + 2 * (f % 2)][:], turned[:, B3 + f, :], in3[j][:], start=False, stop=(j == 1), skip_group_check=True)\
                    .then_inc(sem("f2_g"), 1)

            nc.tensor.matmul(ps[6][:], turned[:, A1, :], h, start=True, stop=True)
            nc.tensor.matmul(ps[7][:], turned[:, A3, :], h, start=True, stop=True).then_inc(sem("f2_a"), 1)
            dense(0)
            dense(1)
            pe.wait_ge(sem("f2_rows"), at(it, "f2_rows"))
            for t in range(NT):
                i = nc.tensor.transpose(ps[0][0:32, 128 * t:128 * t + 128], slot_row[:, 32 * t:32 * t + 32], ident)
            i.then_inc(sem("f2_rowst"), 1)
            pe.wait_ge(sem("f2_rowsc"), at(it, "f2_rowsc"))
            for j in range(2):
                i = nc.tensor.matmul(ps[j][:], k("spread2")[0:32, 128 * j:128 * j + 128], slot_rows[0:32, :], start=True, stop=True)
            i.then_inc(sem("f2_spread"), 1)
            pe.wait_ge(sem("f2_in"), at(it, "f2_in"))
            for j in range(2):
                i = nc.tensor.matmul(ps[j][:], k("spread2")[0:32, 256 + 128 * j:384 + 128 * j], slot_rows[0:32, :], start=True, stop=True)
            i.then_inc(sem("f2_weight"), 1)

            def back(n):
                f, j = F2_ORDER[n]
                pe.wait_ge(sem("f2_aw"), at(it, "f2_aw", n + 1))
                if n == 2:
                    pe.wait_ge(sem("f2_wt"), at(it, "f2_wt"))
                ins = nc.tensor.matmul(ps[(7, 1)[j]][:], turned[:, A2 + f, :], aw[f % 2][j], start=(f == 0), stop=(f == 3), skip_group_check=True)
                if j == 1:
                    pe.wait_ge(sem("f2_sum"), at(it, "f2_sum", f + 1))
                    ins = nc.tensor.matmul(ps[6][:], turned[:, WD + f, :], aw_sum[f % 2][:], start=(f == 0), stop=False, skip_group_check=True)
                ins.then_inc(sem("f2_z"), 1)

            for n, (f, j) in enumerate(F2_ORDER):
                if n >= 2:
                    pe.wait_ge(sem("f2_aw"), at(it, "f2_aw", n - 1))
                if n >= 2 and j == 0:
                    dense(f)
                low_rank(f, j)
                if n >= 1:
                    back(n - 1)
            back(7)
            pe.wait_ge(sem("f2_zc"), at(it, "f2_zc", 1))
            nc.tensor.matmul(ps[6][:], turned[:, B2, :], zw[0], start=False, stop=False, skip_group_check=True)
            pe.wait_ge(sem("f2_zc"), at(it, "f2_zc", 2))
            nc.tensor.matmul(ps[6][:], turned[:, B2, :], zw[1], start=False, stop=True, skip_group_check=True).then_inc(sem("f2_out"), 1)

        def f2_act(act, it):
            act.wait_ge(sem("f2_sm"), at(it, "f2_sm"))
            nc.scalar.activation(tk[0], tk[0], ACT.Exp).then_inc(sem("f2_sm_e"), 1)
            act.wait_ge(sem("f2_rowst"), at(it, "f2_rowst"))
            nc.scalar.activation(slot_rows[0:32, :], ps[0][0:32, :], ACT.Copy).then_inc(sem("f2_rowsc"), 1)
            act.wait_ge(sem("f2_weight"), at(it, "f2_weight"))
            for j in range(2):
                i = nc.scalar.activation(wt[j][:], ps[j][:], ACT.Copy)
            i.then_inc(sem("f2_wt"), 1)
            for n, (f, j) in enumerate(F2_ORDER):
                act.wait_ge(sem("f2_g"), at(it, "f2_g", n + 1))
                if n >= 2:
                    act.wait_ge(sem("f2_aw"), at(it, "f2_aw", n - 1))
                nc.scalar.activation(th[n % 2], ps[2 + 2 * (f % 2)][:], ACT.Tanh, scale=0.5).then_inc(sem("f2_th"), 1)

        def f2_dve(dve, it):
            dve.wait_ge(sem("f2_logit"), at(it, "f2_logit"))
            top2(dve, it, ps[1][:, 0:32], "f2_sm", "f2_sm_e")
            nc.vector.tensor_tensor(r4[5], r4[3], r4[4], ALU.add).then_inc(sem("vector_step"), 1)
            dve.wait_ge(sem("vector_step"), step(it, "vector"))
            nc.vector.reciprocal(r4[6], r4[5]).then_inc(sem("vector_step"), 1)
            dve.wait_ge(sem("vector_step"), step(it, "vector"))
            rows = slot_row.rearrange("p (t s e) -> p s t e", s=4, e=E2)
            for j in range(2):
                nc.vector.tensor_copy(rows[:, j], v3((tk[4], tk[7])[j]))
                nc.vector.tensor_tensor(r4[7], r4[3 + j], r4[6], ALU.mult).then_inc(sem("vector_step"), 1)
                dve.wait_ge(sem("vector_step"), step(it, "vector"))
                i = nc.vector.tensor_tensor(rows[:, 2 + j], v3((tk[4], tk[7])[j]), per_tok(r4[7]), ALU.mult)
                i.then_inc(sem("f2_rows"), 1)
                dve.wait_ge(sem("f2_rows"), at(it, "f2_rows", j + 1))
            dve.wait_ge(sem("f2_spread"), at(it, "f2_spread"))
            nc.vector.tensor_copy(keep[0][:], ps[0][:])
            nc.vector.tensor_copy(keep[1][:], ps[1][:]).then_inc(sem("vector_step"), 1)
            dve.wait_ge(sem("vector_step"), step(it, "vector"))
            nc.vector.tensor_tensor(keep_d[:], keep[1][:], keep[0][:], ALU.subtract).then_inc(sem("vector_step"), 1)
            dve.wait_ge(sem("f2_a"), at(it, "f2_a"))
            nc.vector.tensor_tensor(in1[0][:], ps[6][:], keep[0][:], ALU.mult)
            nc.vector.tensor_tensor(in3[0][:], ps[7][:], keep[0][:], ALU.mult)
            dve.wait_ge(sem("vector_step"), step(it, "vector"))
            nc.vector.tensor_tensor(in1[1][:], ps[6][:], keep_d[:], ALU.mult)
            nc.vector.tensor_tensor(in3[1][:], ps[7][:], keep_d[:], ALU.mult).then_inc(sem("f2_in"), 1)
            dve.wait_ge(sem("f2_in"), at(it, "f2_in"))
            dve.wait_ge(sem("f2_wt"), at(it, "f2_wt"))
            for n, (f, j) in enumerate(F2_ORDER):
                v = aw[f % 2][j]
                dve.wait_ge(sem("f2_th"), at(it, "f2_th", n + 1))
                if n >= 4:
                    dve.wait_ge(sem("f2_z"), at(it, "f2_z", n - 3))
                nc.vector.scalar_tensor_tensor(out=v, in0=th[n % 2], scalar=1.0, in1=ps[2 + 2 * (f % 2)][:], op0=ALU.add, op1=ALU.mult).then_inc(sem("vector_step"), 1)
                dve.wait_ge(sem("vector_step"), step(it, "vector"))
                nc.vector.tensor_tensor(v, v, ps[3 + 2 * (f % 2)][:], ALU.mult).then_inc(sem("vector_step"), 1)
                dve.wait_ge(sem("vector_step"), step(it, "vector"))
                nc.vector.tensor_tensor(v, v, wt[j][:], ALU.mult).then_inc(sem("f2_aw"), 1)
                dve.wait_ge(sem("f2_aw"), at(it, "f2_aw", n + 1))
                if j == 1:
                    nc.vector.tensor_tensor(aw_sum[f % 2][:], aw[f % 2][0], v, ALU.add).then_inc(sem("f2_sum"), 1)
            for j in range(2):
                dve.wait_ge(sem("f2_z"), at(it, "f2_z", 7 + j))
                nc.vector.tensor_tensor(zw[j], ps[(7, 1)[j]][:], keep[j][:], ALU.mult).then_inc(sem("f2_zc"), 1)
            dve.wait_ge(sem("f2_out"), at(it, "f2_out"))
            nc.vector.scalar_tensor_tensor(out=X[:], in0=ps[6][:], scalar=mod(2, 5), in1=X[:], op0=ALU.mult, op1=ALU.add).then_inc(sem("ln_x"), 1)
            dve.wait_ge(sem("ln_x"), at(it, "ln_x", 7))

        def a3_pe(pe, it):
            pe.wait_ge(sem("ln_h"), at(it, "ln_h", 8))
            nc.tensor.matmul(ps[2][:], wqk3[:, 0:128], h, start=True, stop=True).then_inc(sem("a3_q"), 1)
            nc.tensor.matmul(ps[3][:], wqk3[:, 128:256], h, start=True, stop=True).then_inc(sem("a3_k"), 1)
            for t in range(NT):
                o = ps[7][:, 128 * t:128 * t + 128]
                nc.tensor.matmul(o, h[:, 128 * t:128 * t + 128], wv3[:], start=True, stop=False)
                i = nc.tensor.matmul(o, ones[0:1, :], bv3[0:1, :], start=False, stop=True)
            i.then_inc(sem("a3_v"), 1)
            att_stacks_pe(pe, it, stack_rows[:, 1], H2N)
            pe.wait_ge(sem("a3_ones"), at(it, "a3_ones"))
            pe.wait_ge(sem("a3_vc"), at(it, "a3_vc"))
            att_pe(pe, it, 16, H2N, False)
            pe.wait_ge(sem("att_norm"), at(it, "att_norm", 2))
            for r in range(8):
                i = nc.tensor.matmul(ps[r // 4][0:64, 128 * (r % 4):128 * (r % 4) + 128],
                                     oT[:].rearrange("p (a r) -> p r a", r=8)[:, r, :], ident, start=True, stop=True)
            i.then_inc(sem("a3_ot"), 1)
            pe.wait_ge(sem("a3_soA"), at(it, "a3_soA"))
            pe.wait_ge(sem("a3_soD"), at(it, "a3_soD"))
            for hd in range(H3N):
                i = nc.tensor.matmul(ps[7][:, 64 * hd:64 * hd + 64], spread_o[:, 128 * hd:128 * hd + 128], ident[0:64, 0:64], start=True, stop=True)
            i.then_inc(sem("a3_out"), 1)

        def spread_half(n):
            return (spread_o.rearrange("p (h r d) -> p r h d", h=H3N, r=8)[:, 4 * n:4 * n + 4],
                    ps[n][0:64, :].rearrange("p (r h d) -> p r h d", r=4, h=H3N))

        def a3_act(act, it):
            act.wait_ge(sem("ln_h"), at(it, "ln_h", 8))
            att_ones_act(act, it, 2, k("head16")).then_inc(sem("a3_ones"), 1)
            att_stacks_act(act, it, H2N)
            att_act(act, it, 16, H2N, False)
            act.wait_ge(sem("a3_ot"), at(it, "a3_ot"))
            o, i = spread_half(0)
            nc.scalar.activation(o, i, ACT.Copy).then_inc(sem("a3_soA"), 1)

        def a3_dve(dve, it):
            dve.wait_ge(sem("a3_q"), at(it, "a3_q"))
            nc.vector.tensor_scalar(sq[:], ps[2][:], vec("L3_attn_bq"), 0.25, ALU.add, ALU.mult)
            dve.wait_ge(sem("a3_k"), at(it, "a3_k"))
            nc.vector.tensor_scalar(rstd[:], ps[3][:], vec("L3_attn_bk"), None, ALU.add).then_inc(sem("vector_step"), 1)
            dve.wait_ge(sem("vector_step"), step(it, "vector"))
            att_parts_dve(dve, it, H2N, sq[:], rstd[:])
            dve.wait_ge(sem("a3_v"), at(it, "a3_v"))
            att_values_dve(dve, it, 2, k("head16")).then_inc(sem("a3_vc"), 1)
            att_stacks_dve(dve, it, H2N)
            att_dve(dve, it, 16, H2N, False)
            dve.wait_ge(sem("a3_ot"), at(it, "a3_ot"))
            o, i = spread_half(1)
            nc.vector.tensor_copy(o, i).then_inc(sem("a3_soD"), 1)
            dve.wait_ge(sem("a3_out"), at(it, "a3_out"))
            nc.vector.scalar_tensor_tensor(out=X[:], in0=ps[7][:], scalar=mod(3, 2), in1=X[:], op0=ALU.mult, op1=ALU.add).then_inc(sem("ln_x"), 1)
            dve.wait_ge(sem("ln_x"), at(it, "ln_x", 8))
        htok3, wrow, hot, hotT, notsel, selm, m1 = w[0], w[1], w[2], w[3], w[4], w[5], w[6]
        msk = big[3]
        R = slice(0, 2 * KS)
        xs, x1, x2n, proc = selm[R, 0:128], selm[R, 128:256], selm[R, 256:384], selm[R, 384:512]
        msel, osel = w[7][R, 0:64], w[7][R, 128:256]
        narrow = w[8]
        qkv4 = w[9]
        wcol, rank = small[:, 288:292], small[:, 292:296]
        cs, wsel, ssq = small[R, 300:308], small[R, 308:309], small[R, 309:312]
        smx, ssum, srec = small[R, 312:328], small[R, 328:344], small[R, 344:360]
        s4 = big[1][R, 0:2, :].rearrange("p a b -> p (a b)")
        q4, pT = big[2][:, 2, :], big[2][:, 0:2, :]
        RS8 = 1.0 / np.sqrt(8.0)

        def hot_i(i):
            return hot[:, 128 * i:128 * i + 128]

        def f3_pe(pe, it):
            pe.wait_ge(sem("ln_h"), at(it, "ln_h", 9))
            for t in range(NT):
                i = nc.tensor.transpose(ps[2][:, 128 * t:128 * t + 128], h[:, 128 * t:128 * t + 128], ident)
            i.then_inc(sem("f3_ht"), 1)
            nc.tensor.matmul(ps[3][:], router_bc[:], h, start=True, stop=True).then_inc(sem("f3_w"), 1)
            pe.wait_ge(sem("f3_cge"), at(it, "f3_cge"))
            for t in range(NT):
                i = nc.tensor.matmul(ps[4][:], onesb[:], cge[:, t, :], start=(t == 0), stop=(t == NT - 1))
            i.then_inc(sem("f3_cnt"), 1)
            pe.wait_ge(sem("f3_hot"), at(it, "f3_hot"))
            pe.wait_ge(sem("f3_htc"), at(it, "f3_htc"))
            pe.wait_ge(sem("f3_rope"), at(it, "f3_rope"))
            for t in range(NT):
                i = nc.tensor.transpose(ps[5][R, 128 * t:128 * t + 128], hot_i(t), ident)
            i.then_inc(sem("f3_hott"), 1)
            for o, wd, src in ((0, 128, lambda t: htok3[:, 128 * t:128 * t + 128]), (128, 1, lambda t: wcol[:, t:t + 1]),
                               (136, 8, lambda t: rope_now[:, t, :])):
                for t in range(NT):
                    i = nc.tensor.matmul(ps[6][R, o:o + wd], hot_i(t), src(t), start=(t == 0), stop=(t == NT - 1))
            i.then_inc(sem("f3_xs"), 1)
            pe.wait_ge(sem("mask_in"), at(it, "mask_in"))
            for j in range(NT):
                for t in range(NT):
                    i = nc.tensor.matmul(ps[7][:, 128 * j:128 * j + 128], msk[:, t, 128 * j:128 * j + 128], hot_i(t),
                                         start=(t == 0), stop=(t == NT - 1))
            i.then_inc(sem("f3_m1"), 1)
            pe.wait_ge(sem("f3_m1c"), at(it, "f3_m1c"))
            for j in range(NT):
                i = nc.tensor.matmul(ps[0][:, 0:64], m1[:, 128 * j:128 * j + 128], hot_i(j)[:, 0:64], start=(j == 0), stop=(j == NT - 1))
            i.then_inc(sem("f3_msel"), 1)
            pe.wait_ge(sem("f3_hn"), at(it, "f3_hn"))
            nc.tensor.transpose(ps[2][:, 0:128], osel, ident).then_inc(sem("f3_hnt"), 1)
            pe.wait_ge(sem("f3_hntc"), at(it, "f3_hntc"))
            nc.tensor.matmul(ps[3][:, 0:384], narrow[:, 0:128], wqkv4[:], start=True, stop=True).then_inc(sem("f3_qkv"), 1)
            pe.wait_ge(sem("f3_ro"), at(it, "f3_ro"))
            nc.tensor.transpose(ps[4][:, 0:128], w[11][:, 0:128], ident)
            nc.tensor.transpose(ps[4][:, 128:256], w[11][:, 128:256], ident).then_inc(sem("f3_rot"), 1)
            pe.wait_ge(sem("f3_qk"), at(it, "f3_qk"))
            for hd in range(H4):
                g = slice(32 * (hd // 4), 32 * (hd // 4) + 32)
                i = nc.tensor.matmul(ps[(0, 1, 2, 5)[hd // 4]][:, 64 * (hd % 4):64 * (hd % 4) + 64], q4[g, 128 * (hd % 4):128 * (hd % 4) + 128],
                                     narrow[g, 128:192], start=True, stop=True, tile_position=(g.start, 0))
            i.then_inc(sem("f3_s"), 1)
            pe.wait_ge(sem("f3_p"), at(it, "f3_p"))
            for n in range(8):
                i = nc.tensor.transpose(ps[(2, 5)[n // 4]][:, 128 * (n % 4):128 * (n % 4) + 128], s4[:, 128 * n:128 * n + 128], ident)
            i.then_inc(sem("f3_pt"), 1)
            pe.wait_ge(sem("f3_ptc"), at(it, "f3_ptc"))
            for hd in range(H4):
                a = 64 * (hd % 2)
                i = nc.tensor.matmul(ps[3 + hd % 2][R, 8 * (hd // 2):8 * (hd // 2) + 8], pT[a:a + 64, hd // 8, 128 * (hd // 2 % 4):128 * (hd // 2 % 4) + 128],
                                     qkv4[a:a + 64, 256 + 8 * hd:264 + 8 * hd], start=True, stop=True, tile_position=(a, 0))
            i.then_inc(sem("f3_o"), 1)
            pe.wait_ge(sem("f3_on"), at(it, "f3_on"))
            nc.tensor.transpose(ps[4][:, 0:128], osel, ident).then_inc(sem("f3_ont"), 1)
            pe.wait_ge(sem("f3_ontc"), at(it, "f3_ontc"))
            nc.tensor.matmul(ps[5][:, 0:128], narrow[:, 0:128], wo4[:], start=True, stop=True).then_inc(sem("f3_wo"), 1)
            pe.wait_ge(sem("f3_h2"), at(it, "f3_h2"))
            nc.tensor.transpose(ps[6][:, 0:128], x2n, ident).then_inc(sem("f3_h2t"), 1)
            pe.wait_ge(sem("f3_h2tc"), at(it, "f3_h2tc"))
            for f in range(4):
                i = nc.tensor.matmul(ps[7][:, 64 * f:64 * f + 64], w14[:, 128 * f:128 * f + 128], narrow[:, 0:64], start=True, stop=True)
            i.then_inc(sem("f3_u"), 1)
            pe.wait_ge(sem("f3_g"), at(it, "f3_g"))
            for f in range(4):
                i = nc.tensor.matmul(ps[2][0:KS, 0:128], w[11][:, 64 * f:64 * f + 64], w24[:, f, :], start=(f == 0), stop=(f == 3))
            i.then_inc(sem("f3_d"), 1)
            pe.wait_ge(sem("f3_proc"), at(it, "f3_proc"))
            nc.tensor.matmul(ps[3][:], proc[0:KS - 1, :], hotT[0:KS - 1, :], start=True, stop=True).then_inc(sem("f3_back"), 1)
            pe.wait_ge(sem("x_done"), at(it, "x_done"))
            for t in range(NT):
                i = nc.tensor.transpose(ps[4][:, 128 * t:128 * t + 128], X[:, 128 * t:128 * t + 128], ident)
            i.then_inc(sem("x_fint"), 1)

        def f3_act(act, it):
            act.wait_ge(sem("f3_ht"), at(it, "f3_ht"))
            nc.scalar.activation(htok3[:], ps[2][:], ACT.Copy).then_inc(sem("f3_htc"), 1)
            act.wait_ge(sem("f3_hott"), at(it, "f3_hott"))
            nc.scalar.activation(hotT[R, :], ps[5][R, :], ACT.Copy).then_inc(sem("f3_hottc"), 1)
            act.wait_ge(sem("f3_m1"), at(it, "f3_m1"))
            nc.scalar.activation(m1[:], ps[7][:], ACT.Copy).then_inc(sem("f3_m1c"), 1)
            act.wait_ge(sem("f3_ms1"), at(it, "f3_ms1"))
            nc.scalar.activation(ssq[:, 1:2], ssq[:, 0:1], ACT.Sqrt, bias=k("eps")[R, 2:3], scale=1.0 / C).then_inc(sem("f3_rt1"), 1)
            act.wait_ge(sem("f3_qkv"), at(it, "f3_qkv"))
            nc.scalar.activation(qkv4[:, 0:384], ps[3][:, 0:384], ACT.Copy).then_inc(sem("f3_qkvc"), 1)
            act.wait_ge(sem("f3_smx"), at(it, "f3_smx"))
            nc.scalar.activation(s4, s4, ACT.Exp).then_inc(sem("f3_p"), 1)
            act.wait_ge(sem("f3_pt"), at(it, "f3_pt"))
            nc.scalar.activation(pT[:, 0, :], ps[2][:], ACT.Copy)
            nc.scalar.activation(pT[:, 1, :], ps[5][:], ACT.Copy).then_inc(sem("f3_ptc"), 1)
            act.wait_ge(sem("f3_ont"), at(it, "f3_ont"))
            nc.scalar.activation(narrow[:, 0:128], ps[4][:, 0:128], ACT.Copy).then_inc(sem("f3_ontc"), 1)
            act.wait_ge(sem("f3_ms2"), at(it, "f3_ms2"))
            nc.scalar.activation(ssq[:, 1:2], ssq[:, 0:1], ACT.Sqrt, bias=k("eps")[R, 2:3], scale=1.0 / C).then_inc(sem("f3_rt2"), 1)
            act.wait_ge(sem("f3_gu"), at(it, "f3_gu"))
            nc.scalar.activation(w[11][:, 0:256], w[11][:, 0:256], ACT.Tanh, scale=0.7978845608028654).then_inc(sem("f3_th"), 1)
            act.wait_ge(sem("x_fint"), at(it, "x_fint"))
            act.wait_ge(sem("x_saved"), 16 * it + 16)
            nc.scalar.activation(x_fin[:].rearrange("p a b -> p (a b)"), ps[4][:], ACT.Copy).then_inc(sem("x_fin"), 1)

        def f3_dve(dve, it):
            dve.wait_ge(sem("f3_w"), at(it, "f3_w"))
            nc.vector.tensor_scalar(wrow[:], ps[3][:], router_b[:, 0:1], None, ALU.add).then_inc(sem("vector_step"), 1)
            dve.wait_ge(sem("vector_step"), step(it, "vector"))
            nc.vector.tensor_tensor(w[5][:].rearrange("p (t n) -> p t n", t=NT), wrow[:].rearrange("p (t n) -> p t n", t=NT),
                                            ident.rearrange("p (o n) -> p o n", o=1).broadcast_to([128, NT, 128]), ALU.mult).then_inc(sem("vector_step"), 1)
            dve.wait_ge(sem("vector_step"), step(it, "vector"))
            nc.vector.tensor_reduce(wcol, w[5][:].rearrange("p (t n) -> p t n", t=NT), AX.X, ALU.add).then_inc(sem("vector_step"), 1)
            dve.wait_ge(sem("vector_step"), step(it, "vector"))
            for t in range(NT):
                i = nc.vector.tensor_scalar(cge[:, t, :], wrow[:], wcol[:, t:t + 1], None, ALU.is_le)
            i.then_inc(sem("f3_cge"), 1)
            for t in range(NT):
                nc.vector.scalar_tensor_tensor(out=big[0][:, t, :], in0=wrow[:], scalar=wcol[:, t:t + 1],
                                                       in1=k("earlier")[:, T * t:T * t + T], op0=ALU.is_equal, op1=ALU.mult).then_inc(sem("vector_step"), 1)
                dve.wait_ge(sem("vector_step"), step(it, "vector"))
                nc.vector.scalar_tensor_tensor(out=big[0][:, t, :], in0=wrow[:], scalar=wcol[:, t:t + 1],
                                                       in1=big[0][:, t, :], op0=ALU.is_gt, op1=ALU.add).then_inc(sem("vector_step"), 1)
                dve.wait_ge(sem("vector_step"), step(it, "vector"))
            nc.vector.tensor_reduce(rank, big[0][:], AX.X, ALU.add).then_inc(sem("vector_step"), 1)
            dve.wait_ge(sem("vector_step"), step(it, "vector"))
            nc.vector.tensor_tensor(hot[:].rearrange("p (t r) -> p t r", t=NT), k("iota").rearrange("p (o r) -> p o r", o=1).broadcast_to([128, NT, 2 * KS]),
                                             rank.rearrange("p (t o) -> p t o", o=1).broadcast_to([128, NT, 2 * KS]), ALU.is_equal).then_inc(sem("f3_hot"), 1)
            dve.wait_ge(sem("f3_hot"), at(it, "f3_hot"))
            nc.vector.tensor_copy(rope_now[:].rearrange("p a b -> p (a b)"), rope[:, bass.ds(it, 1), :, :].rearrange("p o a b -> p (o a b)")).then_inc(sem("f3_rope"), 1)
            dve.wait_ge(sem("f3_rope"), at(it, "f3_rope"))
            dve.wait_ge(sem("f3_cnt"), at(it, "f3_cnt"))
            nc.vector.tensor_scalar(notsel[:], ps[4][:], KS - 0.5, None, ALU.is_ge).then_inc(sem("vector_step"), 1)
            dve.wait_ge(sem("vector_step"), step(it, "vector"))
            dve.wait_ge(sem("f3_xs"), at(it, "f3_xs"))
            nc.vector.tensor_copy(xs, ps[6][R, 0:128]).then_inc(sem("vector_step"), 1)
            dve.wait_ge(sem("vector_step"), step(it, "vector"))
            nc.vector.tensor_copy(wsel, ps[6][R, 128:129]).then_inc(sem("vector_step"), 1)
            dve.wait_ge(sem("vector_step"), step(it, "vector"))
            nc.vector.tensor_copy(cs, ps[6][R, 136:144]).then_inc(sem("vector_step"), 1)
            dve.wait_ge(sem("vector_step"), step(it, "vector"))

            def rms(src, tmp, dst, mean_sq, root, name):
                nc.vector.tensor_tensor(tmp, src, src, ALU.mult).then_inc(sem("vector_step"), 1)
                dve.wait_ge(sem("vector_step"), step(it, "vector"))
                nc.vector.tensor_reduce(ssq[:, 0:1], tmp, AX.X, ALU.add).then_inc(sem(mean_sq), 1)
                dve.wait_ge(sem(mean_sq), at(it, mean_sq))
                dve.wait_ge(sem(root), at(it, root))
                nc.vector.reciprocal(ssq[:, 2:3], ssq[:, 1:2]).then_inc(sem("vector_step"), 1)
                dve.wait_ge(sem("vector_step"), step(it, "vector"))
                nc.vector.tensor_scalar(dst, src, ssq[:, 2:3], None, ALU.mult).then_inc(sem(name), 1)
                dve.wait_ge(sem(name), at(it, name))

            rms(xs, osel, osel, "f3_ms1", "f3_rt1", "f3_hn")
            dve.wait_ge(sem("f3_hnt"), at(it, "f3_hnt"))
            nc.vector.tensor_scalar(narrow[:, 0:128], ps[2][:, 0:128], vec("L3_ffn_ln1"), None, ALU.mult).then_inc(sem("f3_hntc"), 1)
            dve.wait_ge(sem("f3_hntc"), at(it, "f3_hntc"))
            dve.wait_ge(sem("f3_msel"), at(it, "f3_msel"))
            nc.vector.tensor_copy(msel, ps[0][:, 0:64]).then_inc(sem("vector_step"), 1)
            dve.wait_ge(sem("vector_step"), step(it, "vector"))
            nc.vector.memset(msel[:, KS - 1:KS], NEG).then_inc(sem("vector_step"), 1)
            dve.wait_ge(sem("vector_step"), step(it, "vector"))
            dve.wait_ge(sem("f3_qkvc"), at(it, "f3_qkvc"))
            qk = qkv4[R, 0:256].rearrange("p (u two f) -> p u two f", two=2, f=4)
            cos = cs[:, 0:4].rearrange("p (a b f) -> p a b f", a=1, b=1).broadcast_to([128, 32, 2, 4])
            sin = cs[:, 4:8].rearrange("p (a f) -> p a f", a=1).broadcast_to([128, 32, 4])
            ra = w[10][R, 0:256].rearrange("p (u two f) -> p u two f", two=2, f=4)
            rb = w[10][R, 256:512].rearrange("p (u two f) -> p u two f", two=2, f=4)
            ro = w[11][R, 0:256].rearrange("p (u two f) -> p u two f", two=2, f=4)
            nc.vector.tensor_tensor(ra, qk, cos, ALU.mult).then_inc(sem("vector_step"), 1)
            dve.wait_ge(sem("vector_step"), step(it, "vector"))
            nc.vector.tensor_tensor(rb[:, :, 0], qk[:, :, 1], sin, ALU.mult).then_inc(sem("vector_step"), 1)
            dve.wait_ge(sem("vector_step"), step(it, "vector"))
            nc.vector.tensor_tensor(rb[:, :, 1], qk[:, :, 0], sin, ALU.mult).then_inc(sem("vector_step"), 1)
            dve.wait_ge(sem("vector_step"), step(it, "vector"))
            nc.vector.tensor_tensor(ro[:, :, 0], ra[:, :, 0], rb[:, :, 0], ALU.subtract).then_inc(sem("vector_step"), 1)
            dve.wait_ge(sem("vector_step"), step(it, "vector"))
            nc.vector.tensor_tensor(ro[:, :, 1], ra[:, :, 1], rb[:, :, 1], ALU.add).then_inc(sem("f3_ro"), 1)
            dve.wait_ge(sem("f3_ro"), at(it, "f3_ro"))
            dve.wait_ge(sem("f3_rot"), at(it, "f3_rot"))
            nc.vector.tensor_copy(narrow[:, 128:192], ps[4][:, 128:192]).then_inc(sem("vector_step"), 1)
            dve.wait_ge(sem("vector_step"), step(it, "vector"))
            for m in range(4):
                i = nc.vector.tensor_scalar(q4[:, 128 * m:128 * m + 128], ps[4][:, 0:128], k("head4")[:, m:m + 1], None, ALU.mult)
            i.then_inc(sem("f3_qk"), 1)
            dve.wait_ge(sem("f3_s"), at(it, "f3_s"))
            for g in range(4):
                nc.vector.scalar_tensor_tensor(out=s4[:, 256 * g:256 * g + 256].rearrange("p (u n) -> p u n", n=64),
                                                       in0=ps[(0, 1, 2, 5)[g]][R, 0:256].rearrange("p (u n) -> p u n", n=64), scalar=RS8,
                                                       in1=msel.rearrange("p (o n) -> p o n", o=1).broadcast_to([128, 4, 64]), op0=ALU.mult, op1=ALU.add).then_inc(sem("vector_step"), 1)
                dve.wait_ge(sem("vector_step"), step(it, "vector"))
            s4v = s4.rearrange("p (u n) -> p u n", n=64)
            nc.vector.tensor_reduce(smx, s4v, AX.X, ALU.max).then_inc(sem("vector_step"), 1)
            dve.wait_ge(sem("vector_step"), step(it, "vector"))
            nc.vector.tensor_tensor(s4v, s4v, smx.rearrange("p (u o) -> p u o", o=1).broadcast_to([128, 16, 64]), ALU.subtract).then_inc(sem("f3_smx"), 1)
            dve.wait_ge(sem("f3_smx"), at(it, "f3_smx"))
            dve.wait_ge(sem("f3_p"), at(it, "f3_p"))
            nc.vector.tensor_reduce(ssum, s4v, AX.X, ALU.add).then_inc(sem("vector_step"), 1)
            dve.wait_ge(sem("vector_step"), step(it, "vector"))
            nc.vector.reciprocal(srec, ssum).then_inc(sem("vector_step"), 1)
            dve.wait_ge(sem("vector_step"), step(it, "vector"))
            dve.wait_ge(sem("f3_o"), at(it, "f3_o"))
            for e in range(2):
                i = nc.vector.tensor_tensor(osel.rearrange("p (u e d) -> p e u d", e=2, d=HD4)[:, e], ps[3 + e][R, 0:64].rearrange("p (u d) -> p u d", d=HD4),
                                            srec.rearrange("p (u e o) -> p e u o", e=2, o=1)[:, e].broadcast_to([128, H4 // 2, HD4]), ALU.mult)
            i.then_inc(sem("f3_on"), 1)
            dve.wait_ge(sem("f3_on"), at(it, "f3_on"))
            dve.wait_ge(sem("f3_wo"), at(it, "f3_wo"))
            nc.vector.tensor_tensor(x1, xs, ps[5][R, 0:128], ALU.add).then_inc(sem("vector_step"), 1)
            dve.wait_ge(sem("vector_step"), step(it, "vector"))
            rms(x1, x2n, x2n, "f3_ms2", "f3_rt2", "f3_h2")
            dve.wait_ge(sem("f3_h2t"), at(it, "f3_h2t"))
            nc.vector.tensor_scalar(narrow[:, 0:128], ps[6][:, 0:128], vec("L3_ffn_ln2"), None, ALU.mult).then_inc(sem("f3_h2tc"), 1)
            dve.wait_ge(sem("f3_h2tc"), at(it, "f3_h2tc"))
            u, g, gg = w[10][:, 0:256], w[11][:, 0:256], w[11][:, 256:512]
            dve.wait_ge(sem("f3_u"), at(it, "f3_u"))
            nc.vector.tensor_copy(u, ps[7][:, 0:256]).then_inc(sem("vector_step"), 1)
            dve.wait_ge(sem("vector_step"), step(it, "vector"))
            nc.vector.tensor_tensor(gg, u, u, ALU.mult).then_inc(sem("vector_step"), 1)
            dve.wait_ge(sem("vector_step"), step(it, "vector"))
            nc.vector.tensor_scalar(gg, gg, 0.044715, 1.0, ALU.mult, ALU.add).then_inc(sem("vector_step"), 1)
            dve.wait_ge(sem("vector_step"), step(it, "vector"))
            nc.vector.tensor_tensor(g, gg, u, ALU.mult).then_inc(sem("f3_gu"), 1)
            dve.wait_ge(sem("f3_gu"), at(it, "f3_gu"))
            dve.wait_ge(sem("f3_th"), at(it, "f3_th"))
            nc.vector.tensor_scalar(g, g, 1.0, 0.5, ALU.add, ALU.mult).then_inc(sem("vector_step"), 1)
            dve.wait_ge(sem("vector_step"), step(it, "vector"))
            nc.vector.tensor_tensor(g, g, u, ALU.mult).then_inc(sem("f3_g"), 1)
            dve.wait_ge(sem("f3_g"), at(it, "f3_g"))
            dve.wait_ge(sem("f3_d"), at(it, "f3_d"))
            nc.vector.tensor_tensor(x2n[0:KS], x1[0:KS], ps[2][0:KS, 0:128], ALU.add).then_inc(sem("vector_step"), 1)
            dve.wait_ge(sem("vector_step"), step(it, "vector"))
            dve.wait_ge(sem("f3_hottc"), at(it, "f3_hottc"))
            nc.vector.tensor_scalar(proc[0:KS], x2n[0:KS], wsel[0:KS], None, ALU.mult).then_inc(sem("f3_proc"), 1)
            dve.wait_ge(sem("f3_proc"), at(it, "f3_proc"))
            nc.vector.tensor_tensor(notsel[:], notsel[:], h, ALU.mult).then_inc(sem("vector_step"), 1)
            dve.wait_ge(sem("vector_step"), step(it, "vector"))
            dve.wait_ge(sem("f3_back"), at(it, "f3_back"))
            nc.vector.tensor_tensor(notsel[:], notsel[:], ps[3][:], ALU.add).then_inc(sem("vector_step"), 1)
            dve.wait_ge(sem("vector_step"), step(it, "vector"))
            nc.vector.scalar_tensor_tensor(out=X[:], in0=notsel[:], scalar=mod(3, 5), in1=X[:], op0=ALU.mult, op1=ALU.add).then_inc(sem("x_done"), 1)
            dve.wait_ge(sem("x_done"), at(it, "x_done"))

        cge = sb("cge", [128, NT, T], BF16)
        mabs = sb("mabs", [128, 4, 8])
        onesb = sb("onesb", [128, 128], BF16)
        rope_now = sb("rope_now", [128, NT, 8])

        def flat(ap):
            return ap.rearrange("(a n) -> a n", a=1)

        loads = [(const[:], d["const"])]
        loads += [(w[i][:], d["stack_const"][:, 512 * i:512 * i + 512]) for i in range(3)]
        for i, n in enumerate(VEC):
            src = {"bq2": lambda: flat(d["L2_attn_b_qkv"][0:128]), "bk2": lambda: flat(d["L2_attn_b_qkv"][128:256]),
                   "L1_attn_time_faaaa": lambda: d[n].rearrange("(a h) n -> a (h n)", a=1)}.get(n, lambda: flat(d[n]))()
            loads.append((vec_rows[i:i + 1, :], src))
        loads += [
            (bias_row[0:1, 0:128], flat(d["L0_attn_bk"])), (bias_row[0:1, 128:256], flat(d["L0_attn_bv"])),
            (bias_row[0:1, 256:384], flat(d["L2_attn_b_qkv"][256:384])), (bias_row[0:1, 384:1408], flat(d["L3_attn_bv"])),
            (bias_row[0:1, 1408:1409], flat(d["L3_ffn_router_b"])),
            (wq0[:], d["L0_attn_Wq"]), (wkv0[:, 0:128], d["L0_attn_Wk"]), (wkv0[:, 128:256], d["L0_attn_Wv"]),
            (ctl[:, 0:64], d["L0_ffn_controller"].rearrange("d n s -> d (n s)")),
            (ctl[:, 64:128], d["L0_ffn_controller"].rearrange("d n s -> d (n s)")),
            (f1[:], d["L0_ffn_f1"].rearrange("d n s f -> d (n s) f")),
            (bias0_rows[:], d["L0_ffn_bias"].rearrange("n (a e) f -> (n a) (e f)", e=2)),
        ]
        f2v = d["L0_ffn_f2"].rearrange("n (a e) f d -> e f (n a) d", e=2)
        w2v = d["L1_ffn_w2"].rearrange("(q e) h d -> e h q d", e=2)
        for e in range(2):
            loads += [(f2[64 * e:64 * e + 64, :, :], f2v[e]), (w2s[64 * e:64 * e + 64, :, :], w2v[e])]
        for l in range(4):
            loads += [(wmod[:, l, :], d[f"L{l}_wmod"]), (c_rows[8 * l:8 * l + 8, :], d[f"L{l}_c"])]
        maw2 = d["L1_attn_time_maa_w2"]
        loads += [(w1mix[:], d["L1_attn_time_maa_w1"]), (w2mix[:], maw2[0:4].rearrange("s d c -> (s d) c")), (w2mix4[:], maw2[4]),
                  (dw1[:], d["L1_attn_time_decay_w1"]), (dw2[:], d["L1_attn_time_decay_w2"])]
        loads += [(w5[:, i, :], d["L1_attn_W" + n]) for i, n in enumerate("rkvgo")]
        loads += [(gw1[:], d["L1_ffn_gate_w"]), (w1s[:], d["L1_ffn_w1"].rearrange("e d h -> d e h")),
                  (w3s[:], d["L1_ffn_w3"].rearrange("e d h -> d e h")),
                  (wqkv2[:], d["L2_attn_w_qkv"]), (wout2[:], d["L2_attn_w_out"]), (gate2_rows[:], d["L2_ffn_gate_w"]),
                  (raw[:, WG:WG + 4, :], d["L2_ffn_w_gate"].rearrange("(f p) d -> p f d", p=128)),
                  (raw[:, WU:WU + 4, :], d["L2_ffn_w_up"].rearrange("(f p) d -> p f d", p=128)),
                  (raw[:, WD:WD + 4, :], d["L2_ffn_w_down"].rearrange("d (f q) -> d f q", q=128)),
                  (raw[:, A2:A2 + 4, :], d["L2_ffn_A2"].rearrange("e r (f q) -> (e r) f q", q=128)),
                  (raw[:, A1, :], d["L2_ffn_A1"].rearrange("e r d -> (e r) d")), (raw[:, A3, :], d["L2_ffn_A3"].rearrange("e r d -> (e r) d")),
                  (raw[:, B2, :].rearrange("p (e r) -> p e r", e=E2), d["L2_ffn_B2"].rearrange("e d r -> d e r"))]
        for name, first in (("B1", B1), ("B3", B3)):
            v = d["L2_ffn_" + name].rearrange("e (f p) r -> f p e r", p=128)
            loads += [(raw[:, first + f, :].rearrange("p (e r) -> p e r", e=E2), v[f]) for f in range(4)]
        loads += [(wqk3[:, 0:128], d["L3_attn_Wq"]), (wqk3[:, 128:256], d["L3_attn_Wk"]),
                  (wv3_wide.rearrange("p a b -> p (a b)"), d["L3_attn_Wv"]), (router[:], d["L3_ffn_router_w"]),
                  (wqkv4[:, 0:128], d["L3_ffn_wq"]), (wqkv4[:, 128:256], d["L3_ffn_wk"]), (wqkv4[:, 256:384], d["L3_ffn_wv"]),
                  (wo4[:], d["L3_ffn_wo"]), (w14[:], d["L3_ffn_w1"]), (w24[:], d["L3_ffn_w2"].rearrange("(f p) d -> p f d", p=128))]

        block = ctx.enter_context(nc.Block())

        @block.sync
        def _(sync):
            for dst, src in loads:
                sync.dma_start(dst, src).then_inc(sem("loaded"), 16)
            sync.dma_start(pos_i[:], d["L3_ffn_position_ids"].rearrange("b (t p) -> (b t) p", p=128)).then_inc(sem("x_saved"), 16)

            def load_x(b):
                sync.dma_start(x_tok[:], d["L0_attn_x"][bass.ds(b, 1)].rearrange("o (t p) c -> p (o t) c", p=128)).then_inc(sem("x_in"), 16)

            def one(it, row, more=True):
                if more:
                    following = sync.snap(it + 1)
                    sync.wait_ge(sem("x_used"), at(it, "x_used"))
                    load_x(following)
                sync.wait_ge(sem("ln_x"), at(it, "ln_x", 6))
                sync.dma_start(msk[:], d["L3_ffn_attention_mask"][bass.ds(row, 1)].rearrange("o u (t p) c -> p (o u t) c", p=128))\
                    .then_inc(sem("mask_in"), 16)
                sync.wait_ge(sem("x_fin"), at(it, "x_fin"))
                sync.dma_start(out[bass.ds(it, 1)].rearrange("o (t p) c -> p (o t) c", p=128), x_fin[:]).then_inc(sem("x_saved"), 16)

            load_x(0)
            with sync.Fori(0, MB) as it:
                one(it, it)
            with sync.Fori(MB, B - 1) as it:
                one(it, MB - 1)
            one(B - 1, MB - 1, more=False)
            sync.wait_ge(sem("x_saved"), 16 * (B + 1))

        @block.tensor
        def _(pe):
            pe.wait_ge(sem("loaded"), 16 * len(loads))
            pe.wait_ge(sem("pos"), 1)
            nc.tensor.transpose(ps[0][:, 0:20], vec_rows[:], ident[0:20, 0:20])
            nc.tensor.transpose(ps[0][:, 32:64], bias0_rows[:], ident[0:32, 0:32])
            nc.tensor.transpose(ps[0][:, 64:96], c_rows[:], ident[0:32, 0:32])
            nc.tensor.transpose(ps[0][:, 96:104], gate2_rows[:], ident[0:8, 0:8])
            nc.tensor.transpose(ps[0][:, 112:128], pos_f[:], ident[0:16, 0:16])
            nc.tensor.matmul(ps[0][:, 130:131], ones[0:1, :], bias_row[0:1, 1408:1409], start=True, stop=True)
            for n in range(27):
                i = nc.tensor.transpose(ps[1 + n // 4][:, 128 * (n % 4):128 * (n % 4) + 128], raw[:, n, :], ident)
            i.then_inc(sem("weights_turned"), 1)
            pe.wait_ge(sem("silu_c"), 1)
            for n in range(24):
                i = nc.tensor.matmul(ps[0][:, 8 * n:8 * n + 8], wmod[:, n // 6, 128 * (n % 6):128 * (n % 6) + 128],
                                     silu_c[:, 8 * (n // 6):8 * (n // 6) + 8], start=True, stop=True)
            i.then_inc(sem("mod"), 1)
            pe.wait_ge(sem("prepared"), 1)
            with pe.Fori(0, B) as it:
                pe.wait_ge(sem("x_in"), at(it, "x_in"))
                for t in range(NT):
                    i = nc.tensor.transpose(ps[5][:, 128 * t:128 * t + 128], x_tok[:, t, :], ident)
                i.then_inc(sem("x_used"), 1)
                for n, stage in enumerate((a0_pe, f0_pe, a1_pe, f1_pe, a2_pe, f2_pe, None, a3_pe, f3_pe)):
                    ln_pe(pe, it, n + 1)
                    if stage:
                        stage(pe, it)

        @block.scalar
        def _(act):
            act.wait_ge(sem("c_turned"), 1)
            act.activation(silu_t[:], silu_c[:], ACT.Tanh, scale=0.5).then_inc(sem("c_tanh"), 1)
            act.wait_ge(sem("angles"), 1)
            act.activation(ang[:].rearrange("p a b -> p (a b)"), angt[:].rearrange("p a b -> p (a b)"), ACT.Sin).then_inc(sem("sines"), 1)
            with act.Fori(0, B) as it:
                enter("scalar")
                for n, stage in enumerate((a0_act, f0_act, a1_act, f1_act, a2_act, f2_act, None, a3_act, f3_act)):
                    ln_act(act, it, n + 1)
                    if stage:
                        stage(act, it)

        @block.vector
        def _(dve):
            it = None
            dve.wait_ge(sem("loaded"), 16 * len(loads))
            dve.wait_ge(sem("x_saved"), 16)
            nc.vector.tensor_copy(pos_f[:], pos_i[:]).then_inc(sem("pos"), 1)
            nc.vector.tensor_copy(identb[:], ident)
            nc.vector.tensor_copy(causalb[:], k("causal"))
            nc.vector.tensor_copy(onesb[:], ones)
            for i in range(2):
                nc.vector.tensor_copy(stack_rows[:].rearrange("p a b c e -> p (a b c e)")[:, 512 * i:512 * i + 512], w[i][:])
            nc.vector.tensor_copy(hot_max[:].rearrange("p a b -> p (a b)"), w[2][:])
            nc.vector.memset(max_part[:], 0.0)
            nc.vector.memset(max_rows[:], 0.0)
            nc.vector.memset(hp[:, 0:1], 0.0)
            nc.vector.memset(v1[:, :, 128:129], 1.0)
            nc.vector.memset(scoresT[:], 0.0)
            nc.vector.memset(shifted[:, :, 0:1], 0.0)
            nc.vector.tensor_reduce(wv3[:], wv3_wide.rearrange("p a (n r) -> p (a n) r", r=8), AX.X, ALU.add)
            nc.vector.tensor_reduce(bv3[:], bias_row[0:1, 384:1408].rearrange("p (n r) -> p n r", r=8), AX.X, ALU.add)
            nc.vector.tensor_copy(router_bc[:], router[:].broadcast_to([128, 128])).then_inc(sem("vector_step"), 1)
            dve.wait_ge(sem("vector_step"), step(it, "vector"))
            dve.wait_ge(sem("weights_turned"), 1)
            for n in range(7):
                m = 4 if n < 6 else 3
                nc.vector.tensor_copy(turned[:, 4 * n:4 * n + m, :].rearrange("p a b -> p (a b)"), ps[1 + n][:, 0:128 * m])
            nc.vector.tensor_copy(vecs[:], ps[0][:, 0:20])
            nc.vector.tensor_copy(bias0[:], ps[0][:, 32:64])
            nc.vector.tensor_copy(gate2[:], ps[0][:, 96:104])
            nc.vector.tensor_copy(pos_c[:], ps[0][:, 112:128])
            nc.vector.tensor_copy(router_b[:], ps[0][:, 130:131])
            nc.vector.tensor_copy(silu_c[:], ps[0][:, 64:96]).then_inc(sem("c_turned"), 1)
            dve.wait_ge(sem("c_tanh"), 1)
            nc.vector.scalar_tensor_tensor(out=silu_t[:], in0=silu_t[:], scalar=1.0, in1=silu_c[:], op0=ALU.add, op1=ALU.mult).then_inc(sem("vector_step"), 1)
            dve.wait_ge(sem("vector_step"), step(it, "vector"))
            nc.vector.tensor_scalar(silu_c[:], silu_t[:], 0.5, None, ALU.mult).then_inc(sem("silu_c"), 1)
            for half in range(2):
                nc.vector.tensor_tensor(ang[:, :, 4 * half:4 * half + 4], pos_c[:].rearrange("p (n o) -> p n o", o=1).broadcast_to([128, 16, 4]),
                                                k("freq").rearrange("p (o f) -> p o f", o=1).broadcast_to([128, 16, 4]), ALU.mult).then_inc(sem("vector_step"), 1)
                dve.wait_ge(sem("vector_step"), step(it, "vector"))
            a2 = ang[:].rearrange("p a b -> p (a b)")
            t2 = angt[:].rearrange("p a b -> p (a b)")
            q2 = small[:, 0:128]
            nc.vector.tensor_scalar(t2, a2, 1.0 / (2 * np.pi), None, ALU.mult).then_inc(sem("vector_step"), 1)
            dve.wait_ge(sem("vector_step"), step(it, "vector"))
            nc.vector.tensor_scalar(q2, t2, 12582912.0, None, ALU.add).then_inc(sem("vector_step"), 1)
            dve.wait_ge(sem("vector_step"), step(it, "vector"))
            nc.vector.tensor_scalar(q2, q2, -12582912.0, None, ALU.add).then_inc(sem("vector_step"), 1)
            dve.wait_ge(sem("vector_step"), step(it, "vector"))
            for part in (6.28125, 0.0019350051879882812, 3.019916050337359e-07):
                nc.vector.scalar_tensor_tensor(out=a2, in0=q2, scalar=-part, in1=a2, op0=ALU.mult, op1=ALU.add).then_inc(sem("vector_step"), 1)
                dve.wait_ge(sem("vector_step"), step(it, "vector"))
            nc.vector.tensor_scalar(ang[:, :, 0:4], ang[:, :, 0:4], np.pi / 2, None, ALU.add).then_inc(sem("vector_step"), 1)
            dve.wait_ge(sem("vector_step"), step(it, "vector"))
            nc.vector.tensor_scalar(t2, a2, np.pi, -2 * np.pi, ALU.is_gt, ALU.mult).then_inc(sem("vector_step"), 1)
            dve.wait_ge(sem("vector_step"), step(it, "vector"))
            nc.vector.tensor_tensor(t2, t2, a2, ALU.add).then_inc(sem("vector_step"), 1)
            dve.wait_ge(sem("vector_step"), step(it, "vector"))
            nc.vector.tensor_scalar(t2, t2, 3.1415925, -3.1415925, ALU.min, ALU.max).then_inc(sem("angles"), 1)
            dve.wait_ge(sem("mod"), 1)
            nc.vector.tensor_copy(mods[:].rearrange("p a b -> p (a b)"), ps[0][:, 0:192]).then_inc(sem("vector_step"), 1)
            dve.wait_ge(sem("vector_step"), step(it, "vector"))
            m4 = mods[:].rearrange("p (l j) b -> p l j b", l=4)
            for j in (1, 4):
                nc.vector.tensor_scalar(m4[:, :, j, :], m4[:, :, j, :], 1.0, None, ALU.add).then_inc(sem("vector_step"), 1)
                dve.wait_ge(sem("vector_step"), step(it, "vector"))
            for j in (2, 5):
                nc.vector.tensor_scalar(mtmp[:], m4[:, :, j, :], 0.0, 2.0, ALU.is_ge, ALU.mult).then_inc(sem("vector_step"), 1)
                dve.wait_ge(sem("vector_step"), step(it, "vector"))
                nc.vector.scalar_tensor_tensor(out=mabs[:], in0=m4[:, :, j, :], scalar=-1.0, in1=m4[:, :, j, :], op0=ALU.mult, op1=ALU.max).then_inc(sem("vector_step"), 1)
                dve.wait_ge(sem("vector_step"), step(it, "vector"))
                nc.vector.tensor_scalar(mabs[:], mabs[:], 0.25, None, ALU.max).then_inc(sem("vector_step"), 1)
                dve.wait_ge(sem("vector_step"), step(it, "vector"))
                nc.vector.scalar_tensor_tensor(out=m4[:, :, j, :], in0=mtmp[:], scalar=-1.0, in1=mabs[:], op0=ALU.add, op1=ALU.mult).then_inc(sem("vector_step"), 1)
                dve.wait_ge(sem("vector_step"), step(it, "vector"))
            dve.wait_ge(sem("sines"), 1)
            for b in range(B):
                i = nc.vector.tensor_copy(rope[:, b, :, :], ang[:, 4 * min(b, MB - 1):4 * min(b, MB - 1) + 4, :])
            i.then_inc(sem("vector_step"), 1)
            dve.wait_ge(sem("vector_step"), step(it, "vector"))
            nc.vector.memset(mtmp[:, 0, 0:1], 0.0).then_inc(sem("prepared"), 1)
            with dve.Fori(0, B) as it:
                enter("vector")
                nc.vector.tensor_copy(mod_now[:].rearrange("p (a o) -> p a o", o=1), mods[:, :, bass.ds(it, 1)]).then_inc(sem("vector_step"), 1)
                dve.wait_ge(sem("vector_step"), step(it, "vector"))
                dve.wait_ge(sem("x_used"), it + 1)
                nc.vector.tensor_copy(X[:], ps[5][:]).then_inc(sem("ln_x"), 1)
                dve.wait_ge(sem("ln_x"), at(it, "ln_x", 1))
                for n, stage in enumerate((a0_dve, f0_dve, a1_dve, f1_dve, a2_dve, f2_dve, None, a3_dve, f3_dve)):
                    l, j = (n // 2, n % 2) if n < 7 else ((3, 0) if n == 7 else (3, 1))
                    if n == 7:
                        ln_dve(dve, it, n + 1, h, vec("L3_attn_gamma"), vec("L3_attn_beta"))
                    else:
                        ln_dve(dve, it, n + 1, X[:], mod(l, 3 * j + 1), mod(l, 3 * j))
                    if stage is f3_dve:
                        f3_dve(dve, it)
                    elif stage:
                        stage(dve, it)
        assert {e: seen[e] for e in STEPS} == STEPS, seen


_INS = [
    'L0_attn_x', 'L0_attn_Wq', 'L0_attn_bq', 'L0_attn_Wk', 'L0_attn_bk', 'L0_attn_Wv', 'L0_attn_bv', 'L0_ffn_controller',
    'L0_ffn_f1', 'L0_ffn_f2', 'L0_ffn_bias', 'L0_c', 'L0_wmod', 'L1_attn_time_maa_x', 'L1_attn_time_maa_w',
    'L1_attn_time_maa_k', 'L1_attn_time_maa_v', 'L1_attn_time_maa_r', 'L1_attn_time_maa_g', 'L1_attn_time_maa_w1',
    'L1_attn_time_maa_w2', 'L1_attn_time_decay', 'L1_attn_time_decay_w1', 'L1_attn_time_decay_w2', 'L1_attn_time_faaaa',
    'L1_attn_Wr', 'L1_attn_Wk', 'L1_attn_Wv', 'L1_attn_Wg', 'L1_attn_Wo', 'L1_attn_ln_w', 'L1_attn_ln_b',
    'L1_ffn_gate_w', 'L1_ffn_w1', 'L1_ffn_w2', 'L1_ffn_w3', 'L1_c', 'L1_wmod', 'L2_attn_w_qkv', 'L2_attn_b_qkv',
    'L2_attn_w_out', 'L2_attn_b_out', 'L2_ffn_gate_w', 'L2_ffn_w_gate', 'L2_ffn_w_up', 'L2_ffn_w_down', 'L2_ffn_A1',
    'L2_ffn_B1', 'L2_ffn_A3', 'L2_ffn_B3', 'L2_ffn_A2', 'L2_ffn_B2', 'L2_c', 'L2_wmod', 'L3_attn_Wq', 'L3_attn_bq',
    'L3_attn_Wk', 'L3_attn_bk', 'L3_attn_Wv', 'L3_attn_bv', 'L3_attn_gamma', 'L3_attn_beta', 'L3_ffn_attention_mask',
    'L3_ffn_position_ids', 'L3_ffn_router_w', 'L3_ffn_router_b', 'L3_ffn_wq', 'L3_ffn_wk', 'L3_ffn_wv', 'L3_ffn_wo',
    'L3_ffn_w1', 'L3_ffn_w2', 'L3_ffn_ln1', 'L3_ffn_ln2', 'L3_c', 'L3_wmod']


def kernel(**inputs):
    import concourse.bacc as bacc
    from concourse.bass_utils import run_bass_kernel_spmd

    nc = bacc.Bacc("TRN2", target_bir_lowering=False, num_devices=1)
    arrays, aps = {}, {}
    for name in _INS:
        a = np.ascontiguousarray(inputs[name])
        arrays[f"in_{name}"] = a
        aps[name] = nc.dram_tensor(f"in_{name}", a.shape, mybir.dt.from_np(a.dtype), kind="ExternalInput").ap()
    arrays["in_const"] = constant_table()[0]
    aps["const"] = nc.dram_tensor("in_const", arrays["in_const"].shape, F32, kind="ExternalInput").ap()
    arrays["in_stack_const"] = stack_table()
    aps["stack_const"] = nc.dram_tensor("in_stack_const", arrays["in_stack_const"].shape, F32, kind="ExternalInput").ap()
    out = nc.dram_tensor("out", (B, T, C), F32, kind="ExternalOutput").ap()
    build(nc, aps, out)
    r = run_bass_kernel_spmd(nc, [arrays], core_ids=[0])
    return r.results[0]["out"]
```

```python
import numpy as np
import concourse.bass as bass
from concourse import mybir
from contextlib import ExitStack

F32 = mybir.dt.float32
BF16 = mybir.dt.bfloat16
I32 = mybir.dt.int32
ALU = mybir.AluOpType
ACT = mybir.ActivationFunctionType
AX = mybir.AxisListType

B, T, C = 8, 512, 128
NT = T // 128
LN_EPS = 1e-5

NE, NES, EW = 16, 64, 64
NG = T // NE
LORA, HS = 32, 64
LEVELS = (64, 32, 16, 8, 4, 2)
E1, H1 = 8, 64
E2, F2, R2 = 8, 512, 16
D16 = 16
H2N, H3N = 16, 8
MB = 4
KS = int(0.125 * T)
H4, HD4, F4 = 16, 8, 512
NEG = -1.0e30


def constant_table():
    p = np.arange(128)[:, None]
    t = np.arange(T)[None, :]
    c = np.arange(128)[None, :]
    parts = {
        "ident": (p == c),
        "mean": np.full((128, 128), 1.0 / C),
        "ones": np.ones((128, 128)),
        "same16": (p // D16 == c // D16),
        "same64": (p // HS == c // HS),
        "tie": np.broadcast_to(np.linspace(0.0, 1e-6, NE, dtype=np.float32)[np.arange(T) % NE][None], (128, T)),
        "restart": np.broadcast_to((t % 128 != 0), (128, T)),
        "half": (p // NES == (t // NE) % 2),
        "group8": (p // NE == np.arange(8)[None]),
        "head4": (p // HD4 % 4 == np.arange(4)[None]),
        "head8": np.broadcast_to((np.arange(32)[None] // HD4 == np.arange(4)[:, None]).reshape(1, 128), (128, 128)),
        "head16": np.broadcast_to((np.arange(32)[None] // D16 == np.arange(2)[:, None]).reshape(1, 64), (128, 64)),
        "iota": np.broadcast_to(np.arange(2 * KS)[None] % KS, (128, 2 * KS)),
        "causal": np.where(c > p, NEG, 0.0),
        "eps": np.broadcast_to(np.array([[LN_EPS, 64 * LN_EPS, 1e-6]], dtype=np.float32), (128, 3)),
        "index8": np.broadcast_to(np.arange(8)[None], (128, 8)),
        "freq": np.broadcast_to((1.0 / np.float32(10000.0) ** (np.arange(0, HD4, 2, dtype=np.float32) / np.float32(HD4)))[None], (128, 4)),
        "earlier": np.concatenate([(t < 128 * i + p) for i in range(NT)], axis=1),
    }
    q = np.arange(32)[None, :]
    s = p % 32
    lv = []
    for m in (16, 8, 4, 2, 1):
        lv.append((s // (2 * m) == q // (2 * m)) & (s // m % 2 == 0) & (q // m % 2 == 1))
    lv.append(s == q)
    parts["level"] = np.concatenate(lv, axis=1)
    parts["spread1"] = np.concatenate([(p == 2 * pr + c // H1) for pr in range(E1 // 2)], axis=1)
    parts["spread2"] = np.concatenate([(p == 8 * j + c // R2) * 2.0 for j in range(2)] + [(p // 8 == 2 + j + 0 * c) * 0.5 for j in range(2)], axis=1)
    at, off = {}, 0
    for k, v in parts.items():
        at[k] = (off, v.shape[1])
        off += v.shape[1]
    return np.concatenate([np.asarray(v, dtype=np.float32) for v in parts.values()], axis=1), at


def stack_table():
    p = np.arange(128)[:, None]
    c = np.arange(128)[None, :]
    products = (np.array([0, 0, 1, 1, 0, 2, 1, 2]), np.array([0, 1, 0, 1, 2, 0, 2, 1]))
    cols = []
    for width in (HD4, D16):
        head, term, dim = c // (8 * width), c // width % 8, c % width
        for which in range(2):
            for parity in range(2):
                cols.append((p % 32 == 16 * parity + width * head + dim) & (products[which][term] == p // 32))
    for m in range(4):
        cols.append((p % 4 == m) & (p < 12) & (c >= 0))
    return np.concatenate(cols, axis=1).astype(np.float32)


CONST_AT = constant_table()[1]
CONST_W = sum(w for _, w in CONST_AT.values())

PER = {
    "ln_x": 8, "ln_mean": 18, "ln_xc": 18, "ln_sq": 18, "ln_var": 18, "ln_std": 18, "ln_log": 18, "ln_h": 9,
    "att_s": 96, "att_max": 96, "att_exp": 96, "att_t": 96, "att_pv": 24, "att_parts": 6, "att_rowsA": 2, "att_rowsD": 2, "att_stack": 32, "att_st": 32,
    "att_pm": 8, "att_m": 8, "att_mrow": 8, "att_group": 8, "att_norm": 2,
    "x_in": 16, "x_out": 16, "mask_in": 16,
    "f0_sel": 4, "f0_up": 2, "f0_act": 2, "f0_down": 4, "f0_dev": 4, "f0_tr": 4, "f0_trev": 4,
    "a1_m": 5, "a1_x": 5, "a1_lvl": 6, "a1_q": 7, "a1_st": 3, "a1_st_new": 3,
    "f1_ab": 4, "f1_sp": 4, "f1_sc": 4, "f1_th": 4, "f1_hid": 4,
    "f0_selA": 2, "f0_selD": 2, "f0_up_b": 2, "a0_ek": 2, "a0_v": 2, "a1_a64": 2, "a1_a32": 4, "a1_diagA": 2, "a1_diagV": 2,
    "a1_lvl_e": 6, "f1_a": 4, "f1_y": 4, "f2_rows": 2, "f2_sum": 4, "f2_z": 8, "f2_zc": 2,
    "f3_s": 4, "f3_p": 4, "f3_smx": 4, "f3_pt": 2, "f3_ptc": 2, "f0_bd": 4, "f2_g": 8, "f2_th": 8, "f2_aw": 8,
}
SHARED = {
    "f0_tensor": ["f0_logit", "f0_ht", "f0_permt", "f0_sel", "f0_up", "f0_down", "f0_tr", "f0_out"],
    "a1_tensor": ["a1_mix", "a1_m", "a1_d1", "a1_k", "a1_v", "a1_w", "a1_r", "a1_g", "a1_kendt", "a1_sd0", "a1_s64",
                  "a1_st", "a1_sd", "a1_y", "a1_ynt", "a1_out"],
    "a1_scalar": ["a1_tanh", "a1_dt", "a1_kc", "a1_vc", "a1_ew", "a1_rc", "a1_gt", "a1_dend", "a1_kend_e", "a1_kendtok",
                  "a1_lvl_e", "a1_a64", "a1_a32", "a1_diagA", "a1_ysq", "a1_std"],
    "a1_vector": ["a1_xxx", "a1_x", "a1_kend_p", "a1_kend", "a1_lvl", "a1_q", "a1_st_new", "a1_dsum", "a1_diagV", "a1_yc", "a1_var", "a1_yn",
                  "a1_yg"],
    "f3_tensor": ["f3_ht", "f3_w", "f3_hott", "f3_xs", "f3_cnt", "f3_hnt", "f3_qkv", "f3_m1", "f3_msel", "f3_rot",
                  "f3_s", "f3_pt", "f3_o", "f3_ont", "f3_wo", "f3_h2t", "f3_u", "f3_d", "f3_back", "x_fint"],
    "f3_scalar": ["f3_htc", "f3_hottc", "f3_rt1", "f3_qkvc", "f3_m1c", "f3_p", "f3_ptc", "f3_ontc", "f3_rt2", "f3_th", "x_fin"],
    "f3_vector": ["f3_rope", "f3_hot", "f3_cge", "f3_ms1", "f3_hn", "f3_hntc", "f3_ro", "f3_qk", "f3_smx", "f3_on", "f3_ms2", "f3_h2",
                  "f3_h2tc", "f3_gu", "f3_g", "f3_proc", "x_done"],
}
PLACE = {}
for _sem, _names in SHARED.items():
    _n = 0
    for _name in _names:
        PLACE[_name] = (_sem, _n)
        _n += PER.get(_name, 1)
    for _name in _names:
        PLACE[_name] += (_n,)
STEPS = {"vector": 194, "scalar": 1}


def build(nc, d, out):
    with ExitStack() as ctx:
        def sb(name, shape, dt=F32):
            return ctx.enter_context(nc.sbuf_tensor(name, shape, dt))

        sems = {}

        def sem(name):
            name = PLACE.get(name, (name,))[0]
            if name not in sems:
                sems[name] = ctx.enter_context(nc.semaphore(name))
            return sems[name]

        ps = [ctx.enter_context(nc.psum_tensor(f"bank{i}", [128, 512], F32)) for i in range(8)]

        const = sb("const", [128, CONST_W])

        def k(name):
            o, w = CONST_AT[name]
            return const[:, o:o + w]

        ident, mean_m, ones = k("ident"), k("mean"), k("ones")
        identb = sb("identb", [128, 128], BF16)
        causalb = sb("causalb", [128, 128], BF16)
        stack_rows = sb("stack_rows", [128, 2, 2, 2, 128], BF16)
        hot_max = sb("hot_max", [128, 4, 128], BF16)
        max_part = sb("max_part", [128, 2, NT, 32], BF16)
        max_rows = sb("max_rows", [128, 2, T], BF16)

        vec_rows = sb("vec_rows", [20, 128])
        vecs = sb("vecs", [128, 20])
        VEC = ["L0_attn_bq", "L1_attn_time_maa_x", "L1_attn_time_maa_w", "L1_attn_time_maa_k",
               "L1_attn_time_maa_v", "L1_attn_time_maa_r", "L1_attn_time_maa_g", "L1_attn_time_decay",
               "L1_attn_time_faaaa", "L1_attn_ln_w", "L1_attn_ln_b", "L2_attn_b_out", "L3_attn_bq",
               "L3_attn_bk", "L3_attn_gamma", "L3_attn_beta", "L3_ffn_ln1", "L3_ffn_ln2", "bq2", "bk2"]

        def vec(name):
            i = VEC.index(name)
            return vecs[:, i:i + 1]

        bias_row = sb("bias_row", [1, 1409])
        wq0 = sb("wq0", [128, 128])
        wkv0 = sb("wkv0", [128, 256])
        ctl = sb("ctl", [128, 128])
        f1 = sb("f1", [128, NES, EW])
        f2 = sb("f2", [128, NES // 2, 128])
        bias0 = sb("bias0", [128, NES // 2])
        bias0_rows = sb("bias0_rows", [32, 128])
        wide = sb("wide", [128, 4, NT, 512])
        big = [wide[:, i] for i in range(4)]
        wmod = wide[:, 2:4].rearrange("p a b c -> p (a b c)")[:, 0:3072].rearrange("p (l n) -> p l n", l=4)
        wv3_wide = big[3][:, 2:4, :]
        c_rows = sb("c_rows", [32, 128])
        silu_c = sb("silu_c", [128, 32])
        silu_t = sb("silu_t", [128, 32])
        mods = sb("mods", [128, 24, 8])
        mtmp = sb("mtmp", [128, 4, 8])
        mod_now = sb("mod_now", [128, 24])
        w1mix = sb("w1mix", [128, 160])
        w2mix = sb("w2mix", [128, 128])
        w2mix4 = sb("w2mix4", [32, 128])
        dw1 = sb("dw1", [128, 64])
        dw2 = sb("dw2", [64, 128])
        w5 = sb("w5", [128, 5, 128])
        gw1 = sb("gw1", [128, 8])
        w1s = sb("w1s", [128, E1, H1])
        w3s = sb("w3s", [128, E1, H1])
        w2s = sb("w2s", [128, E1 // 2, 128])
        wqkv2 = sb("wqkv2", [128, 384])
        wout2 = sb("wout2", [128, 128])
        raw = wide[:, 0:2].rearrange("p a b c -> p (a b c)")[:, 0:27 * 128].rearrange("p (n c) -> p n c", c=128)
        gate2_rows = sb("gate2_rows", [8, 128])
        turned = sb("turned", [128, 27, 128])
        gate2 = sb("gate2", [128, 8])
        WG, WU, WD, B1, B3, A2, A1, A3, B2 = 0, 4, 8, 12, 16, 20, 24, 25, 26
        wqk3 = sb("wqk3", [128, 256])
        wv3 = sb("wv3", [128, 128])
        bv3 = sb("bv3", [1, 128])
        router = sb("router", [128, 1])
        router_bc = sb("router_bc", [128, 128])
        router_b = sb("router_b", [128, 1])
        wqkv4 = sb("wqkv4", [128, 384])
        wo4 = sb("wo4", [128, 128])
        w14 = sb("w14", [128, 512])
        w24 = sb("w24", [128, 4, 128])
        pos_i = sb("pos_i", [16, 128], I32)
        pos_f = sb("pos_f", [16, 128])
        pos_c = sb("pos_c", [128, 16])
        ang = sb("ang", [128, 16, 8])
        angt = sb("angt", [128, 16, 8])
        rope = sb("rope", [128, 8, NT, 8])

        x_tok = sb("x_tok", [128, NT, 128])
        x_fin = sb("x_fin", [128, NT, 128])
        X = sb("X", [128, T])
        xc = sb("xc", [128, T])
        sq = sb("sq", [128, T])
        rstd = sb("rstd", [128, T])
        hp = sb("hp", [128, T + 1])
        h = hp[:, 1:T + 1]
        w = [sb(f"tile{i}", [128, T]) for i in range(12)]

        def bf_view(tile):
            return tile[:].bitcast(BF16).rearrange("p (a t) -> p a t", a=2)

        xl = [big[1 + i // 4][:, i % 4, :] for i in range(len(LEVELS))]
        scoresT = sb("scoresT", [128, 8, 128])
        state = sb("state", [128, NT, 128])
        small = sb("small", [128, 512])
        v1 = sb("v1", [128, NT, 129])
        shifted = sb("shifted", [128, NT, 128])
        ksum = sb("ksum", [128, 1])
        cge = sb("cge", [128, NT, T], BF16)

        seen = {"vector": 0, "scalar": 0}
        ahead = {"vector": 0, "scalar": 0}

        def at(it, name, n=None):
            n = PER.get(name, 1) if n is None else n
            before, per = PLACE[name][1:] if name in PLACE else (0, PER.get(name, 1))
            return it * per + before + n

        def step(it, engine):
            seen[engine] += 1
            return seen[engine] if it is None else it * STEPS[engine] + ahead[engine] + seen[engine]

        def enter(engine):
            ahead[engine], seen[engine] = seen[engine], 0

        def half_of(v):
            return slice(v * (T // 2), v * (T // 2) + T // 2)

        def ln_pe(pe, it, n):
            if n == 8:
                pe.wait_ge(sem("ln_h"), at(it, "ln_h", 7))
            else:
                pe.wait_ge(sem("ln_x"), at(it, "ln_x", min(n, 8)))
            for v in range(2):
                nc.tensor.matmul(ps[(0, 2)[v]][:, 0:T // 2], mean_m, (h if n == 8 else X[:])[:, half_of(v)], start=True, stop=True).then_inc(sem("ln_mean"), 1)
            for v in range(2):
                pe.wait_ge(sem("ln_sq"), at(it, "ln_sq", 2 * n - 1 + v))
                nc.tensor.matmul(ps[(1, 3)[v]][:, 0:T // 2], mean_m, sq[:, half_of(v)], start=True, stop=True).then_inc(sem("ln_var"), 1)

        def ln_act(act, it, n):
            for v in range(2):
                act.wait_ge(sem("ln_xc"), at(it, "ln_xc", 2 * n - 1 + v))
                nc.scalar.activation(sq[:, half_of(v)], xc[:, half_of(v)], ACT.Square).then_inc(sem("ln_sq"), 1)
            for v in range(2):
                act.wait_ge(sem("ln_var"), at(it, "ln_var", 2 * n - 1 + v))
                nc.scalar.activation(rstd[:, half_of(v)], ps[(1, 3)[v]][:, 0:T // 2], ACT.Ln, bias=k("eps")[:, 0:1]).then_inc(sem("ln_log"), 1)
            for v in range(2):
                act.wait_ge(sem("ln_log"), at(it, "ln_log", 2 * n - 1 + v))
                nc.scalar.activation(rstd[:, half_of(v)], rstd[:, half_of(v)], ACT.Exp, scale=-0.5).then_inc(sem("ln_std"), 1)

        def ln_dve(dve, it, n, src, scale, bias):
            for v in range(2):
                dve.wait_ge(sem("ln_mean"), at(it, "ln_mean", 2 * n - 1 + v))
                nc.vector.tensor_tensor(xc[:, half_of(v)], src[:, half_of(v)], ps[(0, 2)[v]][:, 0:T // 2], ALU.subtract).then_inc(sem("ln_xc"), 1)
            for v in range(2):
                dve.wait_ge(sem("ln_xc"), at(it, "ln_xc", 2 * n - 1 + v))
                dve.wait_ge(sem("ln_std"), at(it, "ln_std", 2 * n - 1 + v))
                nc.vector.tensor_tensor(xc[:, half_of(v)], xc[:, half_of(v)], rstd[:, half_of(v)], ALU.mult).then_inc(sem("vector_step"), 1)
                dve.wait_ge(sem("vector_step"), step(it, "vector"))
                i = nc.vector.tensor_scalar(h[:, half_of(v)], xc[:, half_of(v)], scale, bias, ALU.mult, ALU.add)
            i.then_inc(sem("ln_h"), 1)
            dve.wait_ge(sem("ln_h"), at(it, "ln_h", n))

        def mod(layer, j):
            i = 6 * layer + j
            return mod_now[:, i:i + 1]

        Q0, K0, e0, t0 = w[0], w[1], w[2], w[3]
        kvm, ksm = w[4], w[5]

        def a0_pe(pe, it):
            pe.wait_ge(sem("ln_h"), at(it, "ln_h", 1))
            nc.tensor.matmul(ps[2][:], wq0[:], h, start=True, stop=True).then_inc(sem("a0_q"), 1)
            for t in range(NT):
                o = ps[3 + t // 2][:, t % 2 * 256:t % 2 * 256 + 256]
                nc.tensor.matmul(o, h[:, 128 * t:128 * t + 128], wkv0[:], start=True, stop=False)
                i = nc.tensor.matmul(o, ones[0:1, :], bias_row[0:1, 0:256], start=False, stop=True)
            i.then_inc(sem("a0_kv"), 1)
            pe.wait_ge(sem("a0_kf"), at(it, "a0_kf"))
            pe.wait_ge(sem("a0_v"), at(it, "a0_v"))
            for t in range(NT):
                i = nc.tensor.matmul(ps[5][:, 0:129], K0[:, 128 * t:128 * t + 128], v1[:, t, :],
                                     start=(t == 0), stop=(t == NT - 1))
            i.then_inc(sem("a0_outer"), 1)
            pe.wait_ge(sem("a0_kvm"), at(it, "a0_kvm"))
            nc.tensor.matmul(ps[6][:], kvm[:, 0:128], Q0[:], start=True, stop=True)
            nc.tensor.matmul(ps[7][:], ksm[:, 0:128], Q0[:], start=True, stop=True).then_inc(sem("a0_out"), 1)

        def a0_act(act, it):
            act.wait_ge(sem("a0_q"), at(it, "a0_q"))
            nc.scalar.activation(e0[:], ps[2][:], ACT.Exp, bias=vec("L0_attn_bq")).then_inc(sem("a0_eq"), 1)
            act.wait_ge(sem("a0_kv"), at(it, "a0_kv"))
            for half in range(2):
                kp = ps[3 + half][:].rearrange("p (t n) -> p t n", t=2)
                act.activation(sq[:, 256 * half:256 * half + 256].rearrange("p (t n) -> p t n", t=2),
                               kp[:, :, 0:128], ACT.Exp).then_inc(sem("a0_ek"), 1)
                act.activation(v1[:, 2 * half:2 * half + 2, 0:128], kp[:, :, 128:256], ACT.Copy).then_inc(sem("a0_v"), 1)

        def a0_dve(dve, it):
            dve.wait_ge(sem("a0_eq"), at(it, "a0_eq"))
            nc.vector.tensor_scalar(t0[:], ps[2][:], vec("L0_attn_bq"), 0.0, ALU.add, ALU.max).then_inc(sem("vector_step"), 1)
            dve.wait_ge(sem("vector_step"), step(it, "vector"))
            nc.vector.scalar_tensor_tensor(out=Q0[:], in0=e0[:], scalar=1.0, in1=t0[:], op0=ALU.min, op1=ALU.add).then_inc(sem("vector_step"), 1)
            dve.wait_ge(sem("vector_step"), step(it, "vector"))
            dve.wait_ge(sem("a0_ek"), at(it, "a0_ek"))
            dve.wait_ge(sem("a0_v"), at(it, "a0_v"))
            for half in range(2):
                kp = ps[3 + half][:].rearrange("p (t n) -> p t n", t=2)
                nc.vector.tensor_scalar(t0[:, 256 * half:256 * half + 256].rearrange("p (t n) -> p t n", t=2),
                                                kp[:, :, 0:128], 0.0, None, ALU.max).then_inc(sem("vector_step"), 1)
                dve.wait_ge(sem("vector_step"), step(it, "vector"))
            nc.vector.scalar_tensor_tensor(out=K0[:], in0=sq[:], scalar=1.0, in1=t0[:], op0=ALU.min, op1=ALU.add).then_inc(sem("a0_kf"), 1)
            dve.wait_ge(sem("a0_kf"), at(it, "a0_kf"))
            dve.wait_ge(sem("a0_outer"), at(it, "a0_outer"))
            nc.vector.tensor_copy(ksum[:], ps[5][:, 128:129]).then_inc(sem("vector_step"), 1)
            dve.wait_ge(sem("vector_step"), step(it, "vector"))
            nc.vector.tensor_tensor(kvm[:, 0:128], ps[5][:, 0:128], k("same16"), ALU.mult).then_inc(sem("vector_step"), 1)
            dve.wait_ge(sem("vector_step"), step(it, "vector"))
            nc.vector.tensor_scalar(ksm[:, 0:128], k("same16"), ksum[:, 0:1], None, ALU.mult).then_inc(sem("a0_kvm"), 1)
            dve.wait_ge(sem("a0_kvm"), at(it, "a0_kvm"))
            dve.wait_ge(sem("a0_out"), at(it, "a0_out"))
            nc.vector.tensor_scalar(t0[:], ps[7][:], 1e-6, None, ALU.add).then_inc(sem("vector_step"), 1)
            dve.wait_ge(sem("vector_step"), step(it, "vector"))
            nc.vector.reciprocal(e0[:], t0[:]).then_inc(sem("vector_step"), 1)
            dve.wait_ge(sem("vector_step"), step(it, "vector"))
            nc.vector.tensor_tensor(t0[:], ps[6][:], e0[:], ALU.mult).then_inc(sem("vector_step"), 1)
            dve.wait_ge(sem("vector_step"), step(it, "vector"))
            nc.vector.scalar_tensor_tensor(out=X[:], in0=t0[:], scalar=mod(0, 2), in1=X[:], op0=ALU.mult, op1=ALU.add).then_inc(sem("ln_x"), 1)
            dve.wait_ge(sem("ln_x"), at(it, "ln_x", 2))

        permT, permBD, lg = w[0], w[1], w[2]
        gmax = small[:, 0:NG]
        htok = w[3]
        bd = big[0]
        sel = big[1][:].rearrange("p a b -> p (a b)").rearrange("p (s g) -> p s g", s=NES)
        biased = [w[4 + half][:].rearrange("p (q g) -> p q g", g=NG) for half in range(2)]
        inner = big[2][:].rearrange("p a b -> p (a b)").rearrange("p (q g) -> p q g", q=NES // 2)
        inter = big[3][:].rearrange("p a b -> p (a b)").rearrange("p (g s) -> p g s", g=NG)
        inter_tok = big[0][:].rearrange("p a b -> p (a b)").rearrange("p (n c) -> p n c", c=128)

        def f0_pe(pe, it):
            pe.wait_ge(sem("ln_h"), at(it, "ln_h", 2))
            nc.tensor.matmul(ps[2][:], ctl[:], h, start=True, stop=True).then_inc(sem("f0_logit"), 1)
            for t in range(NT):
                i = nc.tensor.transpose(ps[3][:, 128 * t:128 * t + 128], h[:, 128 * t:128 * t + 128], ident)
            i.then_inc(sem("f0_ht"), 1)
            pe.wait_ge(sem("f0_perm"), at(it, "f0_perm"))
            for t in range(NT):
                i = nc.tensor.transpose(ps[0][:, 128 * t:128 * t + 128], permT[:, 128 * t:128 * t + 128], ident)
            i.then_inc(sem("f0_permt"), 1)
            pe.wait_ge(sem("f0_htok"), at(it, "f0_htok"))
            for t in range(NT):
                pe.wait_ge(sem("f0_bd"), at(it, "f0_bd", t + 1))
                i = nc.tensor.matmul(ps[4 + t][:], htok[:, 128 * t:128 * t + 128], bd[:, t, :], start=True, stop=True)
                i.then_inc(sem("f0_sel"), 1)
            pe.wait_ge(sem("f0_selA"), at(it, "f0_selA"))
            pe.wait_ge(sem("f0_selD"), at(it, "f0_selD"))
            for half in range(2):
                for q in range(16 * half, 16 * half + 16):
                    for e in range(2):
                        i = nc.tensor.matmul(ps[half][64 * e:64 * e + 64, 32 * (q % 16):32 * (q % 16) + 32],
                                             f1[:, 2 * q + e, :], sel[:, 2 * q + e, :], start=True, stop=True,
                                             skip_group_check=True)
                i.then_inc(sem("f0_up"), 1)
            for half in range(2):
                pe.wait_ge(sem("f0_act"), at(it, "f0_act", half + 1))
                for n in (2 * half, 2 * half + 1):
                    for q in range(8 * n, 8 * n + 8):
                        i = nc.tensor.matmul(ps[2 + n][:, 64 * (q % 8):64 * (q % 8) + 64], f2[:, q, :], inner[:, q, :], start=True, stop=True)
                    i.then_inc(sem("f0_down"), 1)
            pe.wait_ge(sem("f0_dev"), at(it, "f0_dev"))
            for n in range(4):
                for m in range(4):
                    i = nc.tensor.transpose(ps[n + (0 if n < 2 else 4)][:, 128 * m:128 * m + 128],
                                            inter[:, 2 * (4 * n + m):2 * (4 * n + m) + 2, :].rearrange("p g s -> p (g s)"), ident)
                i.then_inc(sem("f0_tr"), 1)
            pe.wait_ge(sem("f0_trev"), at(it, "f0_trev"))
            for n in range(NG // 2):
                i = nc.tensor.matmul(ps[2][:, 32 * n:32 * n + 32], inter_tok[:, n, :], permBD[:, 32 * n:32 * n + 32],
                                     start=True, stop=True)
            i.then_inc(sem("f0_out"), 1)

        def f0_act(act, it):
            act.wait_ge(sem("f0_ht"), at(it, "f0_ht"))
            nc.scalar.activation(htok[:], ps[3][:], ACT.Copy).then_inc(sem("f0_htok"), 1)
            for t in (0, 2):
                act.wait_ge(sem("f0_sel"), at(it, "f0_sel", t + 1))
                nc.scalar.activation(sel[:, :, 8 * t:8 * t + 8], ps[4 + t][:].rearrange("p (g s) -> p s g", g=8), ACT.Copy).then_inc(sem("f0_selA"), 1)
            for half in range(2):
                act.wait_ge(sem("f0_up_b"), at(it, "f0_up_b", half + 1))
                for e in range(2):
                    r = slice(64 * e, 64 * e + 64)
                    i = nc.scalar.activation(inner[r, 16 * half:16 * half + 16, NG * e:NG * e + NG], biased[half][r], ACT.Relu)
                i.then_inc(sem("f0_act"), 1)
            for n in range(4):
                act.wait_ge(sem("f0_down"), at(it, "f0_down", n + 1))
                nc.scalar.activation(inter.rearrange("p g s -> p s g")[:, 16 * n:16 * n + 16, :],
                                     ps[2 + n][:].rearrange("p (s g) -> p s g", s=16), ACT.Copy).then_inc(sem("f0_dev"), 1)
            for n in (0, 2):
                act.wait_ge(sem("f0_tr"), at(it, "f0_tr", n + 1))
                nc.scalar.activation(inter_tok[:, 4 * n:4 * n + 4, :].rearrange("p a b -> p (a b)"),
                                            ps[n + (0 if n < 2 else 4)][:], ACT.Copy).then_inc(sem("f0_trev"), 1)

        def f0_dve(dve, it):
            dve.wait_ge(sem("f0_logit"), at(it, "f0_logit"))
            nc.vector.tensor_tensor(lg[:], ps[2][:], k("tie"), ALU.add).then_inc(sem("vector_step"), 1)
            dve.wait_ge(sem("vector_step"), step(it, "vector"))
            nc.vector.tensor_reduce(gmax, lg[:].rearrange("p (g t) -> p g t", t=NE), AX.X, ALU.max).then_inc(sem("vector_step"), 1)
            dve.wait_ge(sem("vector_step"), step(it, "vector"))
            nc.vector.tensor_tensor(permT[:].rearrange("p (g t) -> p g t", t=NE), lg[:].rearrange("p (g t) -> p g t", t=NE),
                                             gmax.rearrange("p (g o) -> p g o", o=1).broadcast_to([128, NG, NE]), ALU.is_equal).then_inc(sem("f0_perm"), 1)
            dve.wait_ge(sem("f0_perm"), at(it, "f0_perm"))
            dve.wait_ge(sem("f0_permt"), at(it, "f0_permt"))
            for t in range(NT):
                i = nc.vector.tensor_tensor(bd[:, t, :].rearrange("p (g s) -> p g s", g=8),
                                            ps[0][:, 128 * t:128 * t + 64].rearrange("p (o s) -> p o s", o=1).broadcast_to([128, 8, 64]),
                                            k("group8").rearrange("p (g o) -> p g o", o=1).broadcast_to([128, 8, 64]), ALU.mult)
                i.then_inc(sem("f0_bd"), 1)
            dve.wait_ge(sem("f0_bd"), at(it, "f0_bd"))
            nc.vector.tensor_tensor(permBD[:], permT[:], k("half"), ALU.mult).then_inc(sem("vector_step"), 1)
            dve.wait_ge(sem("vector_step"), step(it, "vector"))
            for e in range(2):
                nc.vector.memset(inner[64 * e:64 * e + 64, :, NG * (1 - e):NG * (1 - e) + NG], 0.0)
            for t in (1, 3):
                dve.wait_ge(sem("f0_sel"), at(it, "f0_sel", t + 1))
                nc.vector.tensor_copy(sel[:, :, 8 * t:8 * t + 8], ps[4 + t][:].rearrange("p (g s) -> p s g", g=8)).then_inc(sem("f0_selD"), 1)
            for half in range(2):
                dve.wait_ge(sem("f0_up"), at(it, "f0_up", half + 1))
                nc.vector.tensor_tensor(biased[half], ps[half][:].rearrange("p (q g) -> p q g", q=16),
                                               bias0[:, 16 * half:16 * half + 16].rearrange("p (q o) -> p q o", o=1).broadcast_to([128, 16, 32]), ALU.add).then_inc(sem("f0_up_b"), 1)
            for n in (1, 3):
                dve.wait_ge(sem("f0_tr"), at(it, "f0_tr", n + 1))
                nc.vector.tensor_copy(inter_tok[:, 4 * n:4 * n + 4, :].rearrange("p a b -> p (a b)"),
                                             ps[n + (0 if n < 2 else 4)][:]).then_inc(sem("f0_trev"), 1)
            dve.wait_ge(sem("f0_out"), at(it, "f0_out"))
            nc.vector.scalar_tensor_tensor(out=X[:], in0=ps[2][:], scalar=mod(0, 5), in1=X[:], op0=ALU.mult, op1=ALU.add).then_inc(sem("ln_x"), 1)
            dve.wait_ge(sem("ln_x"), at(it, "ln_x", 3))

        mix, mix4, xmix = w[0], w[1], [w[2], w[3], w[4], w[5], w[6]]
        xx, xt = w[7], w[8]
        rT, kT1, gs, ew, P1c = w[9], w[10], w[11], big[3][:, 0, :], big[3][:, 1, :]
        ku, r_in, k_end = big[3][:, 2, :], big[3][:, 3, :], w[0]
        ex, ex2 = w[7], w[8]
        vtok = v1[:, :, 0:128]
        kend_tok = w[1]
        diag = w[4]
        dmask = big[0][:, 0:3, :].rearrange("p a b -> p (a b)")
        yn, yt = w[5], w[6]
        dend = small[:, 64:68]
        st = small[:, 72:112]

        def a1_pe(pe, it):
            pe.wait_ge(sem("a1_xxx"), at(it, "a1_xxx"))
            nc.tensor.matmul(ps[2][:], w1mix[:, 0:128], xt[:], start=True, stop=True)
            nc.tensor.matmul(ps[3][0:32, :], w1mix[:, 128:160], xt[:], start=True, stop=True).then_inc(sem("a1_mix"), 1)
            pe.wait_ge(sem("a1_tanh"), at(it, "a1_tanh"))
            for s in range(5):
                b = (4, 5, 6, 7, 0)[s]
                lw, rh = (w2mix[32 * s:32 * s + 32, :], mix[32 * s:32 * s + 32, :]) if s < 4 else (w2mix4[:], mix4[0:32, :])
                nc.tensor.matmul(ps[b][:], lw, rh, start=True, stop=True).then_inc(sem("a1_m"), 1)
            pe.wait_ge(sem("a1_x"), at(it, "a1_x", 1))
            nc.tensor.matmul(ps[1][0:64, :], dw1[:], xmix[0][:], start=True, stop=True).then_inc(sem("a1_d1"), 1)
            pe.wait_ge(sem("a1_x"), at(it, "a1_x", 2))
            nc.tensor.matmul(ps[2][:], w5[:, 1, :], xmix[1][:], start=True, stop=True).then_inc(sem("a1_k"), 1)
            pe.wait_ge(sem("a1_x"), at(it, "a1_x", 3))
            for t in range(NT):
                i = nc.tensor.matmul(ps[3][:, 128 * t:128 * t + 128], xmix[2][:, 128 * t:128 * t + 128], w5[:, 2, :],
                                     start=True, stop=True)
            i.then_inc(sem("a1_v"), 1)
            pe.wait_ge(sem("a1_dt"), at(it, "a1_dt"))
            nc.tensor.matmul(ps[4][:], dw2[:], sq[0:64, :], start=True, stop=True).then_inc(sem("a1_w"), 1)
            pe.wait_ge(sem("a1_x"), at(it, "a1_x", 5))
            nc.tensor.matmul(ps[5][:], w5[:, 0, :], xmix[3][:], start=True, stop=True).then_inc(sem("a1_r"), 1)
            nc.tensor.matmul(ps[6][:], w5[:, 3, :], xmix[4][:], start=True, stop=True).then_inc(sem("a1_g"), 1)

            pe.wait_ge(sem("a1_kend"), at(it, "a1_kend"))
            for c in range(NT):
                i = nc.tensor.transpose(ps[7][:, 128 * c:128 * c + 128], k_end[:, 128 * c:128 * c + 128], ident)
            i.then_inc(sem("a1_kendt"), 1)
            def level(lv):
                kk, qq = (xl[2 + lv], xl[2 + lv]) if lv < 4 else ((kT1, rT) if lv == 4 else (ku, rT))
                for c in range(NT):
                    for hd in range(2):
                        q = slice(64 * hd, 64 * hd + 64)
                        bank = ps[(2, 4, 5, 7)[2 * hd + lv // 3]]
                        for b in range(4):
                            o = 128 * c + 32 * b
                            f = 128 * (lv % 3) + 32 * c
                            i = nc.tensor.matmul(bank[32 * b:32 * b + 32, f:f + 32], kk[q, o:o + 32], qq[q, o:o + 32],
                                                 start=True, stop=True, skip_group_check=True, tile_position=(q.start, 32 * b))
                return i

            for lv in range(4):
                pe.wait_ge(sem("a1_q"), at(it, "a1_q", 3 + lv))
                if lv == 3:
                    pe.wait_ge(sem("a1_kendtok"), at(it, "a1_kendtok"))
                c = slice(128 * lv, 128 * lv + 128)
                for hd in range(2):
                    q = slice(64 * hd, 64 * hd + 64)
                    nc.tensor.matmul(ps[hd][:, c.start:c.start + 64], xl[0][q, c], xl[0][q, c.start + 64:c.stop], start=True, stop=True)
                    i = nc.tensor.matmul(ps[hd][:, c.start + 64:c.stop], xl[1][q, c],
                                         xl[1][q, c].rearrange("p (b two t) -> p b two t", two=2, t=32)[:, :, 1, :], start=True, stop=True)
                if lv == 3:
                    i.then_inc(sem("a1_s64"), 1)
                if lv == 2:
                    level(lv).then_inc(sem("a1_sd0"), 1)
                else:
                    level(lv)
            pe.wait_ge(sem("a1_kendtok"), at(it, "a1_kendtok"))
            pe.wait_ge(sem("a1_vc"), at(it, "a1_vc"))
            pe.wait_ge(sem("a1_q"), at(it, "a1_q"))
            for c in range(3):
                nc.tensor.matmul(ps[3][:, 128 * c:128 * c + 128], kend_tok[:, 128 * c:128 * c + 128], vtok[:, c, :],
                                        start=True, stop=True).then_inc(sem("a1_st"), 1)
            level(4)
            level(5).then_inc(sem("a1_sd"), 1)
            pe.wait_ge(sem("a1_st_new"), at(it, "a1_st_new"))
            pe.wait_ge(sem("a1_a64"), at(it, "a1_a64"))
            pe.wait_ge(sem("a1_a32"), at(it, "a1_a32"))
            pe.wait_ge(sem("a1_diagA"), at(it, "a1_diagA"))
            pe.wait_ge(sem("a1_diagV"), at(it, "a1_diagV"))
            for c in range(NT):
                y = ps[6][:, 128 * c:128 * c + 128]
                nc.tensor.matmul(y, r_in[:, 128 * c:128 * c + 128], state[:, c, :], start=True, stop=False, skip_group_check=True)
                for hd in range(2):
                    v = slice(64 * hd, 64 * hd + 64)
                    i = nc.tensor.matmul(y[:, v], scoresT[:, 4 * hd + c, :], vtok[:, c, v], start=False, stop=True, skip_group_check=True)
            i.then_inc(sem("a1_y"), 1)
            pe.wait_ge(sem("a1_yn"), at(it, "a1_yn"))
            for t in range(NT):
                i = nc.tensor.transpose(ps[7][:, 128 * t:128 * t + 128], yn[:, 128 * t:128 * t + 128], ident)
            i.then_inc(sem("a1_ynt"), 1)
            pe.wait_ge(sem("a1_yg"), at(it, "a1_yg"))
            nc.tensor.matmul(ps[2][:], w5[:, 4, :], yt[:], start=True, stop=True).then_inc(sem("a1_out"), 1)

        def a1_act(act, it):
            act.wait_ge(sem("a1_mix"), at(it, "a1_mix"))
            nc.scalar.activation(mix[:], ps[2][:], ACT.Tanh)
            nc.scalar.activation(mix4[0:32, :], ps[3][0:32, :], ACT.Tanh).then_inc(sem("a1_tanh"), 1)
            act.wait_ge(sem("a1_d1"), at(it, "a1_d1"))
            nc.scalar.activation(sq[0:64, :], ps[1][0:64, :], ACT.Tanh).then_inc(sem("a1_dt"), 1)
            act.wait_ge(sem("a1_k"), at(it, "a1_k"))
            nc.scalar.activation(kT1[:], ps[2][:], ACT.Copy).then_inc(sem("a1_kc"), 1)
            act.wait_ge(sem("a1_v"), at(it, "a1_v"))
            nc.scalar.activation(vtok, ps[3][:].rearrange("p (t n) -> p t n", t=NT), ACT.Copy).then_inc(sem("a1_vc"), 1)
            act.wait_ge(sem("a1_w"), at(it, "a1_w"))
            nc.scalar.activation(ew, ps[4][:], ACT.Exp, bias=vec("L1_attn_time_decay")).then_inc(sem("a1_ew"), 1)
            act.wait_ge(sem("a1_r"), at(it, "a1_r"))
            nc.scalar.activation(rT[:], ps[5][:], ACT.Copy).then_inc(sem("a1_rc"), 1)
            act.wait_ge(sem("a1_g"), at(it, "a1_g"))
            nc.scalar.activation(sq[:], ps[6][:], ACT.Tanh, scale=0.5).then_inc(sem("a1_gt"), 1)
            act.wait_ge(sem("a1_kend_p"), at(it, "a1_kend_p"))
            nc.scalar.activation(dend, P1c.rearrange("p (c t) -> p c t", t=128)[:, :, 127], ACT.Exp, scale=-1.0).then_inc(sem("a1_dend"), 1)
            nc.scalar.activation(ex[:], ex[:], ACT.Exp, scale=-1.0).then_inc(sem("scalar_step"), 1)
            act.wait_ge(sem("scalar_step"), step(it, "scalar"))
            nc.scalar.activation(r_in, shifted[:].rearrange("p a b -> p (a b)"), ACT.Exp, scale=-1.0).then_inc(sem("a1_kend_e"), 1)
            act.wait_ge(sem("a1_kendt"), at(it, "a1_kendt"))
            nc.scalar.activation(kend_tok[:], ps[7][:], ACT.Copy).then_inc(sem("a1_kendtok"), 1)
            for lv in range(6):
                act.wait_ge(sem("a1_lvl"), at(it, "a1_lvl", lv + 1))
                nc.scalar.activation(xl[lv][:], xl[lv][:], ACT.Exp, scale=-1.0).then_inc(sem("a1_lvl_e"), 1)
            act.wait_ge(sem("a1_s64"), at(it, "a1_s64"))
            for hd in range(2):
                nc.scalar.activation(scoresT[0:64, 4 * hd:4 * hd + 4, 64:128],
                                            ps[hd][0:64, :].rearrange("p (c n) -> p c n", c=4)[:, :, 0:64], ACT.Copy).then_inc(sem("a1_a64"), 1)
            for hd in range(2):
                for b in range(2):
                    r = slice(64 * b, 64 * b + 32)
                    nc.scalar.activation(scoresT[r, 4 * hd:4 * hd + 4, 64 * b + 32:64 * b + 64],
                                                ps[hd][r, :].rearrange("p (c n) -> p c n", c=4)[:, :, 64 + 32 * b:96 + 32 * b], ACT.Copy).then_inc(sem("a1_a32"), 1)
            act.wait_ge(sem("a1_dsum"), at(it, "a1_dsum"))
            for b in (0, 1):
                r = slice(32 * b, 32 * b + 32)
                nc.scalar.activation(scoresT[r, :, r], diag[r, 0:256].rearrange("p (u q) -> p u q", u=8), ACT.Copy).then_inc(sem("a1_diagA"), 1)
            act.wait_ge(sem("a1_yc"), at(it, "a1_yc"))
            nc.scalar.activation(yt[:], yn[:], ACT.Square).then_inc(sem("a1_ysq"), 1)
            act.wait_ge(sem("a1_var"), at(it, "a1_var"))
            nc.scalar.activation(st[:, 24:32], st[:, 16:24], ACT.Sqrt, bias=k("eps")[:, 1:2], scale=1.0 / HS).then_inc(sem("a1_std"), 1)

        def a1_dve(dve, it):
            nc.vector.tensor_tensor(xx[:], hp[:, 0:T], h, ALU.subtract).then_inc(sem("vector_step"), 1)
            dve.wait_ge(sem("vector_step"), step(it, "vector"))
            nc.vector.scalar_tensor_tensor(out=xt[:], in0=xx[:], scalar=vec("L1_attn_time_maa_x"), in1=h, op0=ALU.mult, op1=ALU.add).then_inc(sem("a1_xxx"), 1)
            dve.wait_ge(sem("a1_xxx"), at(it, "a1_xxx"))
            for s, n in enumerate("wkvrg"):
                b = (4, 5, 6, 7, 0)[s]
                dve.wait_ge(sem("a1_m"), at(it, "a1_m", s + 1))
                nc.vector.scalar_tensor_tensor(out=xmix[s][:], in0=ps[b][:], scalar=vec("L1_attn_time_maa_" + n), in1=xx[:], op0=ALU.add, op1=ALU.mult).then_inc(sem("vector_step"), 1)
                dve.wait_ge(sem("vector_step"), step(it, "vector"))
                nc.vector.tensor_tensor(xmix[s][:], xmix[s][:], h, ALU.add).then_inc(sem("a1_x"), 1)
            dve.wait_ge(sem("a1_ew"), at(it, "a1_ew"))
            nc.vector.tensor_tensor_scan(P1c, k("restart"), ew, 0.0, ALU.mult, ALU.add).then_inc(sem("vector_step"), 1)
            dve.wait_ge(sem("vector_step"), step(it, "vector"))
            c4 = P1c.rearrange("p (c t) -> p c t", t=128)
            nc.vector.tensor_copy(shifted[:, :, 1:128], c4[:, :, 0:127]).then_inc(sem("vector_step"), 1)
            dve.wait_ge(sem("vector_step"), step(it, "vector"))
            dve.wait_ge(sem("a1_x"), at(it, "a1_x", 5))
            nc.vector.tensor_tensor(ex[:].rearrange("p (c t) -> p c t", t=128), c4[:, :, 127:128].broadcast_to([128, NT, 128]), c4, ALU.subtract).then_inc(sem("a1_kend_p"), 1)
            dve.wait_ge(sem("a1_kend_p"), at(it, "a1_kend_p"))
            dve.wait_ge(sem("a1_kend_e"), at(it, "a1_kend_e"))
            dve.wait_ge(sem("a1_kc"), at(it, "a1_kc"))
            nc.vector.tensor_tensor(k_end[:], kT1[:], ex[:], ALU.mult).then_inc(sem("a1_kend"), 1)
            dve.wait_ge(sem("a1_kend"), at(it, "a1_kend"))
            dve.wait_ge(sem("a1_rc"), at(it, "a1_rc"))
            nc.vector.tensor_tensor(r_in, r_in, rT[:], ALU.mult).then_inc(sem("vector_step"), 1)
            dve.wait_ge(sem("vector_step"), step(it, "vector"))
            pprev = shifted[:].rearrange("p a b -> p (a b)")
            dve.wait_ge(sem("a1_g"), at(it, "a1_g"))
            dve.wait_ge(sem("a1_gt"), at(it, "a1_gt"))
            nc.vector.scalar_tensor_tensor(out=gs[:], in0=sq[:], scalar=1.0, in1=ps[6][:], op0=ALU.add, op1=ALU.mult).then_inc(sem("vector_step"), 1)
            dve.wait_ge(sem("vector_step"), step(it, "vector"))

            def halves(ap, m):
                return ap.rearrange("p (n two m) -> p two n m", two=2, m=m)

            for lv, m in enumerate(LEVELS):
                n = T // (2 * m)
                border = halves(P1c, m)[:, 0, :, m - 1:m].broadcast_to([128, n, m])
                nc.vector.tensor_tensor(halves(xl[lv][:], m)[:, 0], border, halves(P1c, m)[:, 0], ALU.subtract).then_inc(sem("vector_step"), 1)
                dve.wait_ge(sem("vector_step"), step(it, "vector"))
                nc.vector.tensor_tensor(halves(xl[lv][:], m)[:, 1], halves(pprev, m)[:, 1], border, ALU.subtract).then_inc(sem("a1_lvl"), 1)
            for lv, m in enumerate(LEVELS):
                dve.wait_ge(sem("a1_lvl_e"), at(it, "a1_lvl_e", lv + 1))
                nc.vector.tensor_tensor(halves(xl[lv][:], m)[:, 0], halves(xl[lv][:], m)[:, 0], halves(kT1[:], m)[:, 0], ALU.mult)
                nc.vector.tensor_tensor(halves(xl[lv][:], m)[:, 1], halves(xl[lv][:], m)[:, 1], halves(rT[:], m)[:, 1], ALU.mult).then_inc(sem("a1_q"), 1)
            nc.vector.tensor_scalar(ku, kT1[:], vec("L1_attn_time_faaaa"), None, ALU.mult).then_inc(sem("a1_q"), 1)
            dve.wait_ge(sem("a1_dend"), at(it, "a1_dend"))
            nc.vector.memset(state[:, 0, :], 0.0).then_inc(sem("vector_step"), 1)
            dve.wait_ge(sem("vector_step"), step(it, "vector"))
            for c in range(3):
                dve.wait_ge(sem("a1_st"), at(it, "a1_st"))
                nc.vector.tensor_tensor(state[:, c + 1, :], ps[3][:, 128 * c:128 * c + 128], k("same64"), ALU.mult).then_inc(sem("vector_step"), 1)
                dve.wait_ge(sem("vector_step"), step(it, "vector"))
                nc.vector.scalar_tensor_tensor(out=state[:, c + 1, :], in0=state[:, c, :], scalar=dend[:, c:c + 1], in1=state[:, c + 1, :],
                                                        op0=ALU.mult, op1=ALU.add).then_inc(sem("a1_st_new"), 1)
                dve.wait_ge(sem("a1_st_new"), at(it, "a1_st_new", c + 1))
            for part in range(2):
                dve.wait_ge(sem(("a1_sd0", "a1_sd")[part]), at(it, ("a1_sd0", "a1_sd")[part]))
                for hd in range(2):
                    pr = 2 * hd + part
                    i = nc.vector.tensor_tensor(
                        dmask[:, 384 * pr:384 * pr + 384].rearrange("p (l u q) -> p l u q", l=3, u=4),
                        ps[(2, 4, 5, 7)[pr]][:, 0:384].rearrange("p (l u q) -> p l u q", l=3, u=4),
                        k("level")[:, 96 * part:96 * part + 96].rearrange("p (l o q) -> p l o q", l=3, o=1).broadcast_to([128, 3, 4, 32]), ALU.mult)
                i.then_inc(sem("vector_step"), 1)
                dve.wait_ge(sem("vector_step"), step(it, "vector"))
                nc.vector.tensor_reduce(diag[:, 256 * part:256 * part + 256].rearrange("p (h u) -> p h u", h=2),
                                        dmask.rearrange("p (h l u) -> p h u l", h=2, l=6)[:, :, :, 3 * part:3 * part + 3], AX.X, ALU.add)\
                    .then_inc(sem("vector_step"), 1)
                dve.wait_ge(sem("vector_step"), step(it, "vector"))
            nc.vector.tensor_tensor(diag[:, 0:256], diag[:, 0:256], diag[:, 256:512], ALU.add).then_inc(sem("a1_dsum"), 1)
            dve.wait_ge(sem("a1_dsum"), at(it, "a1_dsum"))
            for b in (2, 3):
                r = slice(32 * b, 32 * b + 32)
                nc.vector.tensor_copy(scoresT[r, :, r], diag[r, 0:256].rearrange("p (u q) -> p u q", u=8)).then_inc(sem("a1_diagV"), 1)
            dve.wait_ge(sem("a1_y"), at(it, "a1_y"))
            nc.vector.tensor_reduce(st[:, 0:8], ps[6][:].rearrange("p (u i) -> p u i", u=8), AX.X, ALU.add).then_inc(sem("vector_step"), 1)
            dve.wait_ge(sem("vector_step"), step(it, "vector"))
            nc.vector.tensor_scalar(st[:, 8:16], st[:, 0:8], 1.0 / HS, None, ALU.mult).then_inc(sem("vector_step"), 1)
            dve.wait_ge(sem("vector_step"), step(it, "vector"))
            nc.vector.tensor_tensor(yn[:].rearrange("p (u i) -> p u i", u=8), ps[6][:].rearrange("p (u i) -> p u i", u=8),
                                             st[:, 8:16].rearrange("p (u o) -> p u o", o=1).broadcast_to([128, 8, 64]), ALU.subtract).then_inc(sem("a1_yc"), 1)
            dve.wait_ge(sem("a1_yc"), at(it, "a1_yc"))
            dve.wait_ge(sem("a1_ysq"), at(it, "a1_ysq"))
            nc.vector.tensor_reduce(st[:, 16:24], yt[:].rearrange("p (u i) -> p u i", u=8), AX.X, ALU.add).then_inc(sem("a1_var"), 1)
            dve.wait_ge(sem("a1_var"), at(it, "a1_var"))
            dve.wait_ge(sem("a1_std"), at(it, "a1_std"))
            nc.vector.reciprocal(st[:, 32:40], st[:, 24:32]).then_inc(sem("vector_step"), 1)
            dve.wait_ge(sem("vector_step"), step(it, "vector"))
            nc.vector.tensor_tensor(yn[:].rearrange("p (u i) -> p u i", u=8), yn[:].rearrange("p (u i) -> p u i", u=8),
                                             st[:, 32:40].rearrange("p (u o) -> p u o", o=1).broadcast_to([128, 8, 64]), ALU.mult).then_inc(sem("a1_yn"), 1)
            dve.wait_ge(sem("a1_yn"), at(it, "a1_yn"))
            dve.wait_ge(sem("a1_ynt"), at(it, "a1_ynt"))
            nc.vector.tensor_scalar(yt[:], ps[7][:], vec("L1_attn_ln_w"), vec("L1_attn_ln_b"), ALU.mult, ALU.add).then_inc(sem("vector_step"), 1)
            dve.wait_ge(sem("vector_step"), step(it, "vector"))
            nc.vector.scalar_tensor_tensor(out=yt[:], in0=yt[:], scalar=0.5, in1=gs[:], op0=ALU.mult, op1=ALU.mult).then_inc(sem("a1_yg"), 1)
            dve.wait_ge(sem("a1_yg"), at(it, "a1_yg"))
            dve.wait_ge(sem("a1_out"), at(it, "a1_out"))
            nc.vector.scalar_tensor_tensor(out=X[:], in0=ps[2][:], scalar=mod(1, 2), in1=X[:], op0=ALU.mult, op1=ALU.add).then_inc(sem("ln_x"), 1)
            dve.wait_ge(sem("ln_x"), at(it, "ln_x", 4))

        tk = [w[0][:, 32 * i:32 * i + 32] for i in range(10)]
        r4 = [w[0][:, 320 + 4 * i:324 + 4 * i] for i in range(8)]

        def per_tok(a):
            return a.rearrange("p (t o) -> p t o", o=1).broadcast_to([128, NT, 8])

        def v3(a):
            return a.rearrange("p (t e) -> p t e", t=NT)

        def top2(dve, it, logits, shifted_logits, exponentials):
            idx = k("index8").rearrange("p (o e) -> p o e", o=1).broadcast_to([128, NT, 8])
            nc.vector.tensor_reduce(r4[0], v3(logits), AX.X, ALU.max).then_inc(sem("vector_step"), 1)
            dve.wait_ge(sem("vector_step"), step(it, "vector"))
            nc.vector.tensor_tensor(v3(tk[0]), v3(logits), per_tok(r4[0]), ALU.subtract).then_inc(sem(shifted_logits), 1)
            dve.wait_ge(sem(shifted_logits), at(it, shifted_logits))
            dve.wait_ge(sem(exponentials), at(it, exponentials))
            nc.vector.tensor_reduce(r4[1], v3(tk[0]), AX.X, ALU.add).then_inc(sem("vector_step"), 1)
            dve.wait_ge(sem("vector_step"), step(it, "vector"))
            nc.vector.reciprocal(r4[2], r4[1]).then_inc(sem("vector_step"), 1)
            dve.wait_ge(sem("vector_step"), step(it, "vector"))
            nc.vector.tensor_tensor(v3(tk[1]), v3(tk[0]), per_tok(r4[2]), ALU.mult).then_inc(sem("vector_step"), 1)
            dve.wait_ge(sem("vector_step"), step(it, "vector"))
            src = tk[1]
            for j, (best, hot) in enumerate(((r4[3], tk[4]), (r4[4], tk[7]))):
                nc.vector.tensor_reduce(best, v3(src), AX.X, ALU.max).then_inc(sem("vector_step"), 1)
                dve.wait_ge(sem("vector_step"), step(it, "vector"))
                nc.vector.tensor_tensor(v3(tk[2]), v3(src), per_tok(best), ALU.is_lt).then_inc(sem("vector_step"), 1)
                dve.wait_ge(sem("vector_step"), step(it, "vector"))
                nc.vector.scalar_tensor_tensor(out=v3(tk[3]), in0=v3(tk[2]), scalar=100.0, in1=idx, op0=ALU.mult, op1=ALU.add).then_inc(sem("vector_step"), 1)
                dve.wait_ge(sem("vector_step"), step(it, "vector"))
                nc.vector.tensor_reduce(r4[5], v3(tk[3]), AX.X, ALU.min).then_inc(sem("vector_step"), 1)
                dve.wait_ge(sem("vector_step"), step(it, "vector"))
                nc.vector.tensor_tensor(v3(hot), idx, per_tok(r4[5]), ALU.is_equal).then_inc(sem("vector_step"), 1)
                dve.wait_ge(sem("vector_step"), step(it, "vector"))
                if j == 0:
                    nc.vector.scalar_tensor_tensor(out=tk[5], in0=hot, scalar=-4.0, in1=tk[1], op0=ALU.mult, op1=ALU.add).then_inc(sem("vector_step"), 1)
                    dve.wait_ge(sem("vector_step"), step(it, "vector"))
                    src = tk[5]

        scale_row = w[1]
        sc1, ga1, gb1, hid = [w[2], w[6]], [w[3], w[7]], [w[4], w[8]], [w[5], w[9]]

        def f1_pe(pe, it):
            pe.wait_ge(sem("ln_h"), at(it, "ln_h", 4))
            for t in range(NT):
                i = nc.tensor.matmul(ps[1][:, 8 * t:8 * t + 8], h[:, 128 * t:128 * t + 128], gw1[:], start=True, stop=True)
            i.then_inc(sem("f1_logit"), 1)

            def up(pr):
                nc.tensor.matmul(ps[(4, 2)[pr % 2]][:], w1s[:, 2 * pr:2 * pr + 2, :].rearrange("p a b -> p (a b)"), h, start=True, stop=True)
                nc.tensor.matmul(ps[(5, 3)[pr % 2]][:], w3s[:, 2 * pr:2 * pr + 2, :].rearrange("p a b -> p (a b)"), h,
                                 start=True, stop=True).then_inc(sem("f1_ab"), 1)

            def spread(pr):
                nc.tensor.matmul(ps[(6, 0)[pr % 2]][:], k("spread1")[0:8, 128 * pr:128 * pr + 128], scale_row[0:8, :],
                                 start=True, stop=True).then_inc(sem("f1_sp"), 1)

            up(0)
            up(1)
            pe.wait_ge(sem("f1_scale"), at(it, "f1_scale"))
            for t in range(NT):
                i = nc.tensor.transpose(ps[1][0:8, 128 * t:128 * t + 128], tk[8][:, 8 * t:8 * t + 8], ident)
            i.then_inc(sem("f1_scalet"), 1)
            pe.wait_ge(sem("f1_row"), at(it, "f1_row"))
            spread(0)
            spread(1)
            for pr in range(E1 // 2):
                pe.wait_ge(sem("f1_hid"), at(it, "f1_hid", pr + 1))
                i = nc.tensor.matmul(ps[7][:], w2s[:, pr, :], hid[pr % 2][:], start=(pr == 0), stop=(pr == E1 // 2 - 1), skip_group_check=True)
                i.then_inc(sem("f1_y"), 1)
                if pr + 2 < E1 // 2:
                    spread(pr + 2)
                    up(pr + 2)

        def f1_act(act, it):
            act.wait_ge(sem("f1_sm"), at(it, "f1_sm"))
            nc.scalar.activation(tk[0], tk[0], ACT.Exp).then_inc(sem("f1_sm_e"), 1)
            act.wait_ge(sem("f1_scalet"), at(it, "f1_scalet"))
            nc.scalar.activation(scale_row[0:8, :], ps[1][0:8, :], ACT.Copy).then_inc(sem("f1_row"), 1)

            def spread_copy(pr):
                act.wait_ge(sem("f1_sp"), at(it, "f1_sp", pr + 1))
                nc.scalar.activation(sc1[pr % 2][:], ps[(6, 0)[pr % 2]][:], ACT.Copy).then_inc(sem("f1_sc"), 1)

            spread_copy(0)
            for pr in range(E1 // 2):
                if pr == 0:
                    spread_copy(1)
                act.wait_ge(sem("f1_a"), at(it, "f1_a", pr + 1))
                nc.scalar.activation(gb1[pr % 2][:], ga1[pr % 2][:], ACT.Tanh, scale=0.5).then_inc(sem("f1_th"), 1)
                if 1 <= pr < E1 // 2 - 1:
                    spread_copy(pr + 1)

        def f1_dve(dve, it):
            dve.wait_ge(sem("f1_logit"), at(it, "f1_logit"))
            top2(dve, it, ps[1][:, 0:32], "f1_sm", "f1_sm_e")
            nc.vector.tensor_tensor(tk[8], tk[4], tk[7], ALU.add).then_inc(sem("vector_step"), 1)
            dve.wait_ge(sem("vector_step"), step(it, "vector"))
            nc.vector.tensor_tensor(tk[8], tk[8], tk[1], ALU.mult).then_inc(sem("f1_scale"), 1)
            dve.wait_ge(sem("f1_scale"), at(it, "f1_scale"))

            def scaled(pr):
                dve.wait_ge(sem("f1_sc"), at(it, "f1_sc", pr + 1))
                dve.wait_ge(sem("f1_ab"), at(it, "f1_ab", pr + 1))
                nc.vector.tensor_tensor(ga1[pr % 2][:], ps[(4, 2)[pr % 2]][:], sc1[pr % 2][:], ALU.mult).then_inc(sem("f1_a"), 1)
                nc.vector.tensor_tensor(hid[pr % 2][:], ps[(5, 3)[pr % 2]][:], sc1[pr % 2][:], ALU.mult).then_inc(sem("vector_step"), 1)
                dve.wait_ge(sem("f1_a"), at(it, "f1_a", pr + 1))
                dve.wait_ge(sem("vector_step"), step(it, "vector"))

            def gated(pr):
                dve.wait_ge(sem("f1_th"), at(it, "f1_th", pr + 1))
                nc.vector.scalar_tensor_tensor(out=gb1[pr % 2][:], in0=gb1[pr % 2][:], scalar=1.0, in1=ga1[pr % 2][:], op0=ALU.add, op1=ALU.mult)\
                    .then_inc(sem("vector_step"), 1)
                dve.wait_ge(sem("vector_step"), step(it, "vector"))
                nc.vector.scalar_tensor_tensor(out=hid[pr % 2][:], in0=gb1[pr % 2][:], scalar=0.5, in1=hid[pr % 2][:], op0=ALU.mult, op1=ALU.mult)\
                    .then_inc(sem("f1_hid"), 1)
                dve.wait_ge(sem("f1_hid"), at(it, "f1_hid", pr + 1))

            scaled(0)
            scaled(1)
            gated(0)
            gated(1)
            for pr in range(2, E1 // 2):
                scaled(pr)
                gated(pr)
            dve.wait_ge(sem("f1_y"), at(it, "f1_y"))
            nc.vector.scalar_tensor_tensor(out=X[:], in0=ps[7][:], scalar=mod(1, 5), in1=X[:], op0=ALU.mult, op1=ALU.add).then_inc(sem("ln_x"), 1)
            dve.wait_ge(sem("ln_x"), at(it, "ln_x", 5))

        q_part = [bf_view(w[8])[:, 0, :], bf_view(w[8])[:, 1, :], bf_view(w[9])[:, 0, :]]
        k_part = [bf_view(w[10])[:, 0, :], bf_view(w[10])[:, 1, :], bf_view(w[11])[:, 0, :]]
        q_stack = [bf_view(w[p // 2])[:, p % 2, :] for p in range(8)]
        k_stack = [bf_view(w[4 + p // 2])[:, p % 2, :] for p in range(8)]
        exps = [big[0], big[1]]
        values = wide[:, 2:4].rearrange("p a b c -> p (a b c)")
        oT, sums = w[8], w[10]
        state_bf = state[:].rearrange("p a b -> p (a b)").bitcast(BF16).rearrange("p (a t) -> p a t", a=2)
        part_rows = [[cge[0:96, g, :] for g in range(4)],
                     [state_bf[0:96, 0, :], state_bf[0:96, 1, :], bf_view(xc)[0:96, 0, :], bf_view(xc)[0:96, 1, :]]]
        nmax, nrest = [small[:, 128:144], small[:, 144:160]], small[:, 160:176]
        spread_o = big[0][:].rearrange("p a b -> p (a b)")[0:64, 0:1024]

        def by_head(ap, per):
            return ap.rearrange("p (i m) -> p i m", m=4)[:, :, 0:per]

        def next_stack(hh, width):
            heads = 2 if width == 8 else 1
            p = (hh + 1) // heads
            return p if (hh + 1) % heads == 0 and p < 8 else None

        def stack_pe(pe, it, width, base, p, hh):
            if p >= 1:
                pe.wait_ge(sem("att_st"), at(it, "att_st", base + 2 * p))
                rows_out = min((hh - 1) * width // 32, 4) if hh >= 1 else 0
                if rows_out >= 1:
                    pe.wait_ge(sem("att_mrow"), at(it, "att_mrow", base // 4 + rows_out))
            for which in range(2):
                nc.tensor.matmul(ps[(4, 7)[which]][:], stack_rows[0:96, 0 if width == 8 else 1, which, p % 2, :], part_rows[which][p // 2],
                                 start=True, stop=True).then_inc(sem("att_stack"), 1)

        def stack_act(act, it, base, p):
            for which in range(2):
                act.wait_ge(sem("att_stack"), at(it, "att_stack", base + 2 * p + which + 1))
                nc.scalar.activation((q_stack, k_stack)[which][p], ps[(4, 7)[which]][:], ACT.Copy).then_inc(sem("att_st"), 1)

        def att_rows_act(act, it, base):
            for j in range(2):
                act.wait_ge(sem("att_parts"), at(it, "att_parts", 3 * (base // H2N) + j + 1))
                for g in range(4):
                    i = nc.scalar.activation(part_rows[0][g][32 * j:32 * j + 32], q_part[j][32 * g:32 * g + 32], ACT.Copy)
            i.then_inc(sem("att_rowsA"), 1)

        def att_parts_dve(dve, it, base, qf, kf):
            for j in range(3):
                nc.vector.tensor_copy(q_part[j], qf)
                nc.vector.tensor_copy(k_part[j], kf).then_inc(sem("att_parts"), 1)
                dve.wait_ge(sem("att_parts"), at(it, "att_parts", 3 * (base // H2N) + j + 1))
                if j < 2:
                    nc.vector.tensor_tensor(qf, qf, q_part[j], ALU.subtract)
                    nc.vector.tensor_tensor(kf, kf, k_part[j], ALU.subtract).then_inc(sem("vector_step"), 1)
                for g in range(4):
                    if j == 2:
                        nc.vector.tensor_copy(part_rows[0][g][32 * j:32 * j + 32], q_part[j][32 * g:32 * g + 32])
                    i = nc.vector.tensor_copy(part_rows[1][g][32 * j:32 * j + 32], k_part[j][32 * g:32 * g + 32])
                if j < 2:
                    dve.wait_ge(sem("vector_step"), step(it, "vector"))
            i.then_inc(sem("att_rowsD"), 1)

        def att_pe(pe, it, width, base, causal, value_copy):
            NH, per, gb = 128 // width, 32 // width, base // 4

            def rows(hd):
                return (hd // 2, slice(64 * (hd % 2), 64 * (hd % 2) + 64)) if width == 8 else (hd, slice(0, 128))

            pe.wait_ge(sem("att_rowsA"), at(it, "att_rowsA", base // H2N + 1))
            pe.wait_ge(sem("att_rowsD"), at(it, "att_rowsD", base // H2N + 1))
            stack_pe(pe, it, width, base, 0, 0)
            for hh in range(NH + per + 2):
                h2, h3 = hh - per - 1, hh - per - 2
                if next_stack(hh, width) is not None:
                    stack_pe(pe, it, width, base, next_stack(hh, width), hh)
                for i in range(NT):
                    if i == 2 and hh % per == 0 and 0 < hh <= NH:
                        g = hh // per - 1
                        pe.wait_ge(sem("att_pm"), at(it, "att_pm", gb + g + 1))
                        made = min((hh + 1) * width // 16 + 1, 8)
                        pe.wait_ge(sem("att_st"), at(it, "att_st", base + 2 * made))
                        for t in range(NT):
                            ins = nc.tensor.matmul(ps[7][0:32, 128 * t:128 * t + 128], max_part[:, g % 2, t, :], identb[:], start=True, stop=True)
                        ins.then_inc(sem("att_m"), 1)
                    if hh < NH:
                        L = 128 * (i + 1) if causal else T
                        p, r = rows(hh)
                        if i == 0:
                            pe.wait_ge(sem("att_st"), at(it, "att_st", base + 2 * p + 2))
                        if 4 * hh + i >= 2:
                            pe.wait_ge(sem("att_max"), at(it, "att_max", (base + hh) * NT + i - 1))
                        ins = nc.tensor.matmul(ps[i % 2][:, 0:L], q_stack[p][r, 128 * i:128 * i + 128], k_stack[p][r, 0:L],
                                               start=True, stop=not causal, tile_position=(r.start, 0))
                        if causal:
                            ins = nc.tensor.matmul(ps[i % 2][:, 128 * i:128 * i + 128], identb[:], causalb[:], start=False, stop=True)
                        ins.then_inc(sem("att_s"), 1)
                    if 0 <= h2 < NH:
                        g, m, j, o = h2 // per, h2 % per, i, (128 * i if causal else 0)
                        p, r = rows(h2)
                        s = ps[2 + j % 2]
                        if m == 0 and j == 0:
                            pe.wait_ge(sem("att_mrow"), at(it, "att_mrow", gb + g + 1))
                        if 4 * h2 + j >= 2:
                            pe.wait_ge(sem("att_exp"), at(it, "att_exp", (base + h2) * NT + j - 1))
                        nc.tensor.matmul(s[:, o:T], k_stack[p][r, 128 * j:128 * j + 128], q_stack[p][r, o:T],
                                         start=True, stop=False, tile_position=(r.start, 0))
                        if causal:
                            nc.tensor.matmul(s[:, o:o + 128], causalb[:], identb[:], start=False, stop=False)
                        nc.tensor.matmul(s[:, o:T], hot_max[:, m, :], max_rows[:, g % 2, o:T], start=False, stop=True).then_inc(sem("att_t"), 1)
                    if 0 <= h3 < NH:
                        g, m, j, o = h3 // per, h3 % per, i, (128 * i if causal else 0)
                        if h3 == 0 and j == 0:
                            pe.wait_ge(sem(value_copy), at(it, value_copy))
                        if g >= 2 and m == 0 and j == 0:
                            pe.wait_ge(sem("att_group"), at(it, "att_group", gb + g - 1))
                        pe.wait_ge(sem("att_exp"), at(it, "att_exp", (base + h3) * NT + j + 1))
                        c = 64 * ((4 * j + g) * per + m)
                        ins = nc.tensor.matmul(ps[5 + g % 2][0:64, o:T], values[:, c:c + 64], exps[h3 % 2][:, j, o:T],
                                               start=(m == 0 and j == 0), stop=(m == per - 1 and j == NT - 1), skip_group_check=True)
                        if j == NT - 1:
                            ins.then_inc(sem("att_pv"), 1)

        def att_act(act, it, width, base, causal):
            NH, per, gb = 128 // width, 32 // width, base // 4
            stack_act(act, it, base, 0)
            for hh in range(NH + per + 2):
                h2, h3 = hh - per - 1, hh - per - 2
                if next_stack(hh, width) is not None:
                    stack_act(act, it, base, next_stack(hh, width))
                for j in range(NT):
                    if j == 2 and hh % per == 0 and 0 < hh <= NH:
                        g = hh // per - 1
                        act.wait_ge(sem("att_m"), at(it, "att_m", gb + g + 1))
                        if g >= 2:
                            act.wait_ge(sem("att_t"), at(it, "att_t", (base + per * (g - 1)) * NT))
                        nc.scalar.activation(max_rows[0:32, g % 2, :], ps[7][0:32, :], ACT.Copy).then_inc(sem("att_mrow"), 1)
                    if 0 <= h2 < NH:
                        o = 128 * j if causal else 0
                        act.wait_ge(sem("att_t"), at(it, "att_t", (base + h2) * NT + j + 1))
                        if h2 >= 2 and j == 0:
                            act.wait_ge(sem("att_pv"), at(it, "att_pv", base + h2 - 1))
                        nc.scalar.activation(exps[h2 % 2][:, j, o:T], ps[2 + j % 2][:, o:T], ACT.Exp).then_inc(sem("att_exp"), 1)
                if h3 >= 0 and h3 % per == per - 1:
                    g = h3 // per
                    act.wait_ge(sem("att_pv"), at(it, "att_pv", base + h3 + 1))
                    nc.scalar.activation(sums[32 * g:32 * g + 32, :], ps[5 + g % 2][32:64, :], ACT.Copy)
                    nc.scalar.activation(oT[32 * g:32 * g + 32, :], ps[5 + g % 2][0:32, :], ACT.Copy).then_inc(sem("att_group"), 1)

        def att_dve(dve, it, width, base, causal, mask, value, value_copy):
            NH, per, gb = 128 // width, 32 // width, base // 4
            for hh in range(NH):
                g, m = hh // per, hh % per
                for i in range(NT):
                    L = 128 * (i + 1) if causal else T
                    dve.wait_ge(sem("att_s"), at(it, "att_s", (base + hh) * NT + i + 1))
                    nc.vector.tensor_reduce(nmax[g % 2][:, 4 * i + m:4 * i + m + 1], ps[i % 2][:, 0:L], AX.X, ALU.max,
                                            negate=True).then_inc(sem("att_max"), 1)
                if hh < NT:
                    if hh == 0:
                        dve.wait_ge(sem(value), at(it, value))
                    i = att_values_dve(dve, it, per, mask, hh)
                    if hh == NT - 1:
                        i.then_inc(sem(value_copy), 1)
                if m == per - 1:
                    dve.wait_ge(sem("att_max"), at(it, "att_max", (base + hh + 1) * NT))
                    if g >= 2:
                        dve.wait_ge(sem("att_m"), at(it, "att_m", gb + g - 1))
                    rest = by_head(nmax[g % 2], per)
                    for j in range(3):
                        part = max_part[:, g % 2, :, 4 * j:4 * j + per]
                        i = nc.vector.tensor_copy(part, rest)
                        if j == 2:
                            i.then_inc(sem("att_pm"), 1)
                            break
                        i.then_inc(sem("vector_step"), 1)
                        dve.wait_ge(sem("vector_step"), step(it, "vector"))
                        nc.vector.tensor_tensor(by_head(nrest, per), rest, part, ALU.subtract).then_inc(sem("vector_step"), 1)
                        dve.wait_ge(sem("vector_step"), step(it, "vector"))
                        rest = by_head(nrest, per)
            dve.wait_ge(sem("att_group"), at(it, "att_group", gb + 4))
            nc.vector.reciprocal(sums[:], sums[:]).then_inc(sem("vector_step"), 1)
            dve.wait_ge(sem("vector_step"), step(it, "vector"))
            nc.vector.tensor_tensor(oT[:], oT[:], sums[:], ALU.mult).then_inc(sem("att_norm"), 1)

        def att_values_dve(dve, it, per, mask, t):
            return nc.vector.tensor_tensor(
                values[:, 256 * per * t:256 * per * (t + 1)].rearrange("p (n m c) -> p n m c", n=4, m=per)[:, :, :, 0:32],
                ps[5][:, 128 * t:128 * t + 128].rearrange("p (n o c) -> p n o c", n=4, o=1).broadcast_to([128, 4, per, 32]),
                mask.rearrange("p (o m c) -> p o m c", o=1, m=per).broadcast_to([128, 4, per, 32]), ALU.mult)

        def att_ones_act(act, it, per, mask):
            n = NT * 4
            return nc.scalar.activation(
                values[:, 0:n * per * 64].rearrange("p (n m c) -> p n m c", n=n, m=per)[:, :, :, 32:64],
                mask.rearrange("p (o m c) -> p o m c", o=1, m=per).broadcast_to([128, n, per, 32]), ACT.Copy)

        def a2_pe(pe, it):
            pe.wait_ge(sem("ln_h"), at(it, "ln_h", 5))
            nc.tensor.matmul(ps[2][:], wqkv2[:, 0:128], h, start=True, stop=True).then_inc(sem("a2_q"), 1)
            nc.tensor.matmul(ps[3][:], wqkv2[:, 128:256], h, start=True, stop=True).then_inc(sem("a2_k"), 1)
            for t in range(NT):
                o = ps[5][:, 128 * t:128 * t + 128]
                nc.tensor.matmul(o, h[:, 128 * t:128 * t + 128], wqkv2[:, 256:384], start=True, stop=False)
                i = nc.tensor.matmul(o, ones[0:1, :], bias_row[0:1, 256:384], start=False, stop=True)
            i.then_inc(sem("a2_v"), 1)
            pe.wait_ge(sem("a2_ones"), at(it, "a2_ones"))
            att_pe(pe, it, 8, 0, True, "a2_vc")
            pe.wait_ge(sem("att_norm"), at(it, "att_norm", 1))
            nc.tensor.matmul(ps[2][:], wout2[:], oT[:], start=True, stop=True).then_inc(sem("a2_out"), 1)

        def a2_act(act, it):
            act.wait_ge(sem("ln_h"), at(it, "ln_h", 5))
            att_ones_act(act, it, 4, k("head8")).then_inc(sem("a2_ones"), 1)
            att_rows_act(act, it, 0)
            att_act(act, it, 8, 0, True)

        def a2_dve(dve, it):
            dve.wait_ge(sem("a2_q"), at(it, "a2_q"))
            nc.vector.tensor_scalar(sq[:], ps[2][:], vec("bq2"), 1.0 / np.sqrt(8.0), ALU.add, ALU.mult)
            dve.wait_ge(sem("a2_k"), at(it, "a2_k"))
            nc.vector.tensor_scalar(rstd[:], ps[3][:], vec("bk2"), None, ALU.add).then_inc(sem("vector_step"), 1)
            dve.wait_ge(sem("vector_step"), step(it, "vector"))
            att_parts_dve(dve, it, 0, sq[:], rstd[:])
            att_dve(dve, it, 8, 0, True, k("head8"), "a2_v", "a2_vc")
            dve.wait_ge(sem("a2_out"), at(it, "a2_out"))
            nc.vector.tensor_scalar(w[7][:], ps[2][:], vec("L2_attn_b_out"), None, ALU.add).then_inc(sem("vector_step"), 1)
            dve.wait_ge(sem("vector_step"), step(it, "vector"))
            nc.vector.scalar_tensor_tensor(out=X[:], in0=w[7][:], scalar=mod(2, 2), in1=X[:], op0=ALU.mult, op1=ALU.add).then_inc(sem("ln_x"), 1)
            dve.wait_ge(sem("ln_x"), at(it, "ln_x", 6))

        slot_row = small[:, 160:288]
        slot_rows = big[0][:, 0, :]
        keep, keep_d = [w[1], w[2]], w[0]
        in1, in3 = [w[5], w[6]], [w[7], w[8]]
        wt = [w[9], w[10]]
        aw = [[big[1][:, 2 * f + j, :] for j in range(2)] for f in range(2)]
        aw_sum = [w[3], w[4]]
        th = [big[2][:, 0, :], big[2][:, 1, :]]
        zw = [big[2][:, 2, :], big[2][:, 3, :]]
        F2_ORDER = [(0, 0), (1, 0), (0, 1), (1, 1), (2, 0), (3, 0), (2, 1), (3, 1)]

        def f2_pe(pe, it):
            pe.wait_ge(sem("ln_h"), at(it, "ln_h", 6))
            for t in range(NT):
                i = nc.tensor.matmul(ps[1][:, 8 * t:8 * t + 8], h[:, 128 * t:128 * t + 128], gate2[:], start=True, stop=True)
            i.then_inc(sem("f2_logit"), 1)

            def dense(f):
                nc.tensor.matmul(ps[2 + 2 * (f % 2)][:], turned[:, WG + f, :], h, start=True, stop=False, skip_group_check=True)
                nc.tensor.matmul(ps[3 + 2 * (f % 2)][:], turned[:, WU + f, :], h, start=True, stop=False, skip_group_check=True)

            def low_rank(f, j):
                nc.tensor.matmul(ps[2 + 2 * (f % 2)][:], turned[:, B1 + f, :], in1[j][:], start=False, stop=(j == 1), skip_group_check=True)
                nc.tensor.matmul(ps[3 + 2 * (f % 2)][:], turned[:, B3 + f, :], in3[j][:], start=False, stop=(j == 1), skip_group_check=True)\
                    .then_inc(sem("f2_g"), 1)

            nc.tensor.matmul(ps[6][:], turned[:, A1, :], h, start=True, stop=True)
            nc.tensor.matmul(ps[7][:], turned[:, A3, :], h, start=True, stop=True).then_inc(sem("f2_a"), 1)
            dense(0)
            dense(1)
            pe.wait_ge(sem("f2_rows"), at(it, "f2_rows"))
            for t in range(NT):
                i = nc.tensor.transpose(ps[0][0:32, 128 * t:128 * t + 128], slot_row[:, 32 * t:32 * t + 32], ident)
            i.then_inc(sem("f2_rowst"), 1)
            pe.wait_ge(sem("f2_rowsc"), at(it, "f2_rowsc"))
            for j in range(2):
                i = nc.tensor.matmul(ps[j][:], k("spread2")[0:32, 128 * j:128 * j + 128], slot_rows[0:32, :], start=True, stop=True)
            i.then_inc(sem("f2_spread"), 1)
            pe.wait_ge(sem("f2_in"), at(it, "f2_in"))
            for j in range(2):
                i = nc.tensor.matmul(ps[j][:], k("spread2")[0:32, 256 + 128 * j:384 + 128 * j], slot_rows[0:32, :], start=True, stop=True)
            i.then_inc(sem("f2_weight"), 1)

            def back(n):
                f, j = F2_ORDER[n]
                pe.wait_ge(sem("f2_aw"), at(it, "f2_aw", n + 1))
                if n == 2:
                    pe.wait_ge(sem("f2_wt"), at(it, "f2_wt"))
                ins = nc.tensor.matmul(ps[(7, 1)[j]][:], turned[:, A2 + f, :], aw[f % 2][j], start=(f == 0), stop=(f == 3), skip_group_check=True)
                if j == 1:
                    pe.wait_ge(sem("f2_sum"), at(it, "f2_sum", f + 1))
                    ins = nc.tensor.matmul(ps[6][:], turned[:, WD + f, :], aw_sum[f % 2][:], start=(f == 0), stop=False, skip_group_check=True)
                ins.then_inc(sem("f2_z"), 1)

            for n, (f, j) in enumerate(F2_ORDER):
                if n >= 2:
                    pe.wait_ge(sem("f2_aw"), at(it, "f2_aw", n - 1))
                if n >= 2 and j == 0:
                    dense(f)
                low_rank(f, j)
                if n >= 1:
                    back(n - 1)
            back(7)
            pe.wait_ge(sem("f2_zc"), at(it, "f2_zc", 1))
            nc.tensor.matmul(ps[6][:], turned[:, B2, :], zw[0], start=False, stop=False, skip_group_check=True)
            pe.wait_ge(sem("f2_zc"), at(it, "f2_zc", 2))
            nc.tensor.matmul(ps[6][:], turned[:, B2, :], zw[1], start=False, stop=True, skip_group_check=True).then_inc(sem("f2_out"), 1)

        def f2_act(act, it):
            act.wait_ge(sem("f2_sm"), at(it, "f2_sm"))
            nc.scalar.activation(tk[0], tk[0], ACT.Exp).then_inc(sem("f2_sm_e"), 1)
            act.wait_ge(sem("f2_rowst"), at(it, "f2_rowst"))
            nc.scalar.activation(slot_rows[0:32, :], ps[0][0:32, :], ACT.Copy).then_inc(sem("f2_rowsc"), 1)
            act.wait_ge(sem("f2_weight"), at(it, "f2_weight"))
            for j in range(2):
                i = nc.scalar.activation(wt[j][:], ps[j][:], ACT.Copy)
            i.then_inc(sem("f2_wt"), 1)
            for n, (f, j) in enumerate(F2_ORDER):
                act.wait_ge(sem("f2_g"), at(it, "f2_g", n + 1))
                if n >= 2:
                    act.wait_ge(sem("f2_aw"), at(it, "f2_aw", n - 1))
                nc.scalar.activation(th[n % 2], ps[2 + 2 * (f % 2)][:], ACT.Tanh, scale=0.5).then_inc(sem("f2_th"), 1)

        def f2_dve(dve, it):
            dve.wait_ge(sem("f2_logit"), at(it, "f2_logit"))
            top2(dve, it, ps[1][:, 0:32], "f2_sm", "f2_sm_e")
            nc.vector.tensor_tensor(r4[5], r4[3], r4[4], ALU.add).then_inc(sem("vector_step"), 1)
            dve.wait_ge(sem("vector_step"), step(it, "vector"))
            nc.vector.reciprocal(r4[6], r4[5]).then_inc(sem("vector_step"), 1)
            dve.wait_ge(sem("vector_step"), step(it, "vector"))
            rows = slot_row.rearrange("p (t s e) -> p s t e", s=4, e=E2)
            for j in range(2):
                nc.vector.tensor_copy(rows[:, j], v3((tk[4], tk[7])[j]))
                nc.vector.tensor_tensor(r4[7], r4[3 + j], r4[6], ALU.mult).then_inc(sem("vector_step"), 1)
                dve.wait_ge(sem("vector_step"), step(it, "vector"))
                i = nc.vector.tensor_tensor(rows[:, 2 + j], v3((tk[4], tk[7])[j]), per_tok(r4[7]), ALU.mult)
                i.then_inc(sem("f2_rows"), 1)
                dve.wait_ge(sem("f2_rows"), at(it, "f2_rows", j + 1))
            dve.wait_ge(sem("f2_spread"), at(it, "f2_spread"))
            nc.vector.tensor_copy(keep[0][:], ps[0][:])
            nc.vector.tensor_copy(keep[1][:], ps[1][:]).then_inc(sem("vector_step"), 1)
            dve.wait_ge(sem("vector_step"), step(it, "vector"))
            nc.vector.tensor_tensor(keep_d[:], keep[1][:], keep[0][:], ALU.subtract).then_inc(sem("vector_step"), 1)
            dve.wait_ge(sem("f2_a"), at(it, "f2_a"))
            nc.vector.tensor_tensor(in1[0][:], ps[6][:], keep[0][:], ALU.mult)
            nc.vector.tensor_tensor(in3[0][:], ps[7][:], keep[0][:], ALU.mult)
            dve.wait_ge(sem("vector_step"), step(it, "vector"))
            nc.vector.tensor_tensor(in1[1][:], ps[6][:], keep_d[:], ALU.mult)
            nc.vector.tensor_tensor(in3[1][:], ps[7][:], keep_d[:], ALU.mult).then_inc(sem("f2_in"), 1)
            dve.wait_ge(sem("f2_in"), at(it, "f2_in"))
            dve.wait_ge(sem("f2_wt"), at(it, "f2_wt"))
            for n, (f, j) in enumerate(F2_ORDER):
                v = aw[f % 2][j]
                dve.wait_ge(sem("f2_th"), at(it, "f2_th", n + 1))
                if n >= 4:
                    dve.wait_ge(sem("f2_z"), at(it, "f2_z", n - 3))
                nc.vector.scalar_tensor_tensor(out=v, in0=th[n % 2], scalar=1.0, in1=ps[2 + 2 * (f % 2)][:], op0=ALU.add, op1=ALU.mult).then_inc(sem("vector_step"), 1)
                dve.wait_ge(sem("vector_step"), step(it, "vector"))
                nc.vector.tensor_tensor(v, v, ps[3 + 2 * (f % 2)][:], ALU.mult).then_inc(sem("vector_step"), 1)
                dve.wait_ge(sem("vector_step"), step(it, "vector"))
                nc.vector.tensor_tensor(v, v, wt[j][:], ALU.mult).then_inc(sem("f2_aw"), 1)
                dve.wait_ge(sem("f2_aw"), at(it, "f2_aw", n + 1))
                if j == 1:
                    nc.vector.tensor_tensor(aw_sum[f % 2][:], aw[f % 2][0], v, ALU.add).then_inc(sem("f2_sum"), 1)
            for j in range(2):
                dve.wait_ge(sem("f2_z"), at(it, "f2_z", 7 + j))
                nc.vector.tensor_tensor(zw[j], ps[(7, 1)[j]][:], keep[j][:], ALU.mult).then_inc(sem("f2_zc"), 1)
            dve.wait_ge(sem("f2_out"), at(it, "f2_out"))
            nc.vector.scalar_tensor_tensor(out=X[:], in0=ps[6][:], scalar=mod(2, 5), in1=X[:], op0=ALU.mult, op1=ALU.add).then_inc(sem("ln_x"), 1)
            dve.wait_ge(sem("ln_x"), at(it, "ln_x", 7))

        def a3_pe(pe, it):
            pe.wait_ge(sem("ln_h"), at(it, "ln_h", 8))
            nc.tensor.matmul(ps[2][:], wqk3[:, 0:128], h, start=True, stop=True).then_inc(sem("a3_q"), 1)
            nc.tensor.matmul(ps[3][:], wqk3[:, 128:256], h, start=True, stop=True).then_inc(sem("a3_k"), 1)
            for t in range(NT):
                o = ps[5][:, 128 * t:128 * t + 128]
                nc.tensor.matmul(o, h[:, 128 * t:128 * t + 128], wv3[:], start=True, stop=False)
                i = nc.tensor.matmul(o, ones[0:1, :], bv3[0:1, :], start=False, stop=True)
            i.then_inc(sem("a3_v"), 1)
            pe.wait_ge(sem("a3_ones"), at(it, "a3_ones"))
            att_pe(pe, it, 16, H2N, False, "a3_vc")
            pe.wait_ge(sem("att_norm"), at(it, "att_norm", 2))
            for r in range(8):
                i = nc.tensor.matmul(ps[r // 4][0:64, 128 * (r % 4):128 * (r % 4) + 128],
                                     oT[:].rearrange("p (a r) -> p r a", r=8)[:, r, :], ident, start=True, stop=True)
            i.then_inc(sem("a3_ot"), 1)
            pe.wait_ge(sem("a3_soA"), at(it, "a3_soA"))
            pe.wait_ge(sem("a3_soD"), at(it, "a3_soD"))
            for hd in range(H3N):
                i = nc.tensor.matmul(ps[7][:, 64 * hd:64 * hd + 64], spread_o[:, 128 * hd:128 * hd + 128], ident[0:64, 0:64], start=True, stop=True)
            i.then_inc(sem("a3_out"), 1)

        def spread_half(n):
            return (spread_o.rearrange("p (h r d) -> p r h d", h=H3N, r=8)[:, 4 * n:4 * n + 4],
                    ps[n][0:64, :].rearrange("p (r h d) -> p r h d", r=4, h=H3N))

        def a3_act(act, it):
            act.wait_ge(sem("ln_h"), at(it, "ln_h", 8))
            att_ones_act(act, it, 2, k("head16")).then_inc(sem("a3_ones"), 1)
            att_rows_act(act, it, H2N)
            att_act(act, it, 16, H2N, False)
            act.wait_ge(sem("a3_ot"), at(it, "a3_ot"))
            o, i = spread_half(0)
            nc.scalar.activation(o, i, ACT.Copy).then_inc(sem("a3_soA"), 1)

        def a3_dve(dve, it):
            dve.wait_ge(sem("a3_q"), at(it, "a3_q"))
            nc.vector.tensor_scalar(sq[:], ps[2][:], vec("L3_attn_bq"), 0.25, ALU.add, ALU.mult)
            dve.wait_ge(sem("a3_k"), at(it, "a3_k"))
            nc.vector.tensor_scalar(rstd[:], ps[3][:], vec("L3_attn_bk"), None, ALU.add).then_inc(sem("vector_step"), 1)
            dve.wait_ge(sem("vector_step"), step(it, "vector"))
            att_parts_dve(dve, it, H2N, sq[:], rstd[:])
            att_dve(dve, it, 16, H2N, False, k("head16"), "a3_v", "a3_vc")
            dve.wait_ge(sem("a3_ot"), at(it, "a3_ot"))
            o, i = spread_half(1)
            nc.vector.tensor_copy(o, i).then_inc(sem("a3_soD"), 1)
            dve.wait_ge(sem("a3_out"), at(it, "a3_out"))
            nc.vector.scalar_tensor_tensor(out=X[:], in0=ps[7][:], scalar=mod(3, 2), in1=X[:], op0=ALU.mult, op1=ALU.add).then_inc(sem("ln_x"), 1)
            dve.wait_ge(sem("ln_x"), at(it, "ln_x", 8))
        wrow, hot, hotT, notsel, selm, m1 = w[1], w[2], w[3], w[4], w[5], w[6]
        msk = big[3]
        R = slice(0, 2 * KS)
        xs, x1, x2n, proc = selm[R, 0:128], selm[R, 128:256], selm[R, 256:384], selm[R, 384:512]
        msel, osel = w[7][R, 0:64], w[7][R, 128:256]
        narrow = w[8]
        qkv4 = w[9]
        rank = small[:, 292:296]
        cs, wsel, ssq = small[R, 300:308], small[R, 308:309], small[R, 309:312]
        smx, ssum, srec = small[R, 312:328], small[R, 328:344], small[R, 344:360]
        s4 = big[1][R, 0:2, :].rearrange("p a b -> p (a b)")
        q4, pT = big[2][:, 2, :], big[2][:, 0:2, :]
        RS8 = 1.0 / np.sqrt(8.0)

        def hot_i(i):
            return hot[:, 128 * i:128 * i + 128]

        def f3_pe(pe, it):
            pe.wait_ge(sem("ln_h"), at(it, "ln_h", 9))
            for t in range(NT):
                i = nc.tensor.transpose(ps[2][:, 128 * t:128 * t + 128], h[:, 128 * t:128 * t + 128], ident)
            i.then_inc(sem("f3_ht"), 1)
            nc.tensor.matmul(ps[3][:], router_bc[:], h, start=True, stop=True).then_inc(sem("f3_w"), 1)
            pe.wait_ge(sem("f3_hot"), at(it, "f3_hot"))
            pe.wait_ge(sem("f3_htc"), at(it, "f3_htc"))
            pe.wait_ge(sem("f3_rope"), at(it, "f3_rope"))
            for t in range(NT):
                i = nc.tensor.transpose(ps[5][R, 128 * t:128 * t + 128], hot_i(t), ident)
            i.then_inc(sem("f3_hott"), 1)
            for t in range(NT):
                i = nc.tensor.matmul(ps[6][R, 0:137], hot_i(t), to_gather[:, t, :], start=(t == 0), stop=(t == NT - 1))
            i.then_inc(sem("f3_xs"), 1)
            pe.wait_ge(sem("f3_cge"), at(it, "f3_cge"))
            for t in range(NT):
                i = nc.tensor.matmul(ps[4][:], onesb[:], cge[:, t, :], start=(t == 0), stop=(t == NT - 1))
            i.then_inc(sem("f3_cnt"), 1)
            pe.wait_ge(sem("f3_hn"), at(it, "f3_hn"))
            nc.tensor.transpose(ps[2][:, 0:128], osel, ident).then_inc(sem("f3_hnt"), 1)
            pe.wait_ge(sem("f3_hntc"), at(it, "f3_hntc"))
            nc.tensor.matmul(ps[3][:, 0:384], narrow[:, 0:128], wqkv4[:], start=True, stop=True).then_inc(sem("f3_qkv"), 1)
            pe.wait_ge(sem("mask_in"), at(it, "mask_in"))
            for j in range(NT):
                for t in range(NT):
                    i = nc.tensor.matmul(ps[7][:, 128 * j:128 * j + 128], msk[:, t, 128 * j:128 * j + 128], hot_i(t),
                                         start=(t == 0), stop=(t == NT - 1))
            i.then_inc(sem("f3_m1"), 1)
            pe.wait_ge(sem("f3_m1c"), at(it, "f3_m1c"))
            for j in range(NT):
                i = nc.tensor.matmul(ps[0][:, 0:64], m1[:, 128 * j:128 * j + 128], hot_i(j)[:, 0:64], start=(j == 0), stop=(j == NT - 1))
            i.then_inc(sem("f3_msel"), 1)
            pe.wait_ge(sem("f3_ro"), at(it, "f3_ro"))
            nc.tensor.transpose(ps[4][:, 0:128], w[11][:, 0:128], ident)
            nc.tensor.transpose(ps[4][:, 128:256], w[11][:, 128:256], ident).then_inc(sem("f3_rot"), 1)
            pe.wait_ge(sem("f3_qk"), at(it, "f3_qk"))
            for hd in range(H4):
                g = slice(32 * (hd // 4), 32 * (hd // 4) + 32)
                i = nc.tensor.matmul(ps[(0, 1, 2, 5)[hd // 4]][:, 64 * (hd % 4):64 * (hd % 4) + 64], q4[g, 128 * (hd % 4):128 * (hd % 4) + 128],
                                     narrow[g, 128:192], start=True, stop=True, tile_position=(g.start, 0))
                if hd % 4 == 3:
                    i.then_inc(sem("f3_s"), 1)
            for n in range(8):
                if n % 2 == 0:
                    pe.wait_ge(sem("f3_p"), at(it, "f3_p", n // 2 + 1))
                i = nc.tensor.transpose(ps[(6, 7)[n // 4]][:, 128 * (n % 4):128 * (n % 4) + 128], s4[:, 128 * n:128 * n + 128], ident)
                if n % 4 == 3:
                    i.then_inc(sem("f3_pt"), 1)
            for hd in range(H4):
                if hd % 8 == 0:
                    pe.wait_ge(sem("f3_ptc"), at(it, "f3_ptc", hd // 8 + 1))
                a = 64 * (hd % 2)
                i = nc.tensor.matmul(ps[3 + hd % 2][R, 8 * (hd // 2):8 * (hd // 2) + 8], pT[a:a + 64, hd // 8, 128 * (hd // 2 % 4):128 * (hd // 2 % 4) + 128],
                                     qkv4[a:a + 64, 256 + 8 * hd:264 + 8 * hd], start=True, stop=True, tile_position=(a, 0))
            i.then_inc(sem("f3_o"), 1)
            pe.wait_ge(sem("f3_on"), at(it, "f3_on"))
            nc.tensor.transpose(ps[4][:, 0:128], osel, ident).then_inc(sem("f3_ont"), 1)
            pe.wait_ge(sem("f3_ontc"), at(it, "f3_ontc"))
            nc.tensor.matmul(ps[5][:, 0:128], narrow[:, 0:128], wo4[:], start=True, stop=True).then_inc(sem("f3_wo"), 1)
            pe.wait_ge(sem("f3_h2"), at(it, "f3_h2"))
            nc.tensor.transpose(ps[6][:, 0:128], x2n, ident).then_inc(sem("f3_h2t"), 1)
            pe.wait_ge(sem("f3_h2tc"), at(it, "f3_h2tc"))
            for f in range(4):
                i = nc.tensor.matmul(ps[7][:, 64 * f:64 * f + 64], w14[:, 128 * f:128 * f + 128], narrow[:, 0:64], start=True, stop=True)
            i.then_inc(sem("f3_u"), 1)
            pe.wait_ge(sem("f3_g"), at(it, "f3_g"))
            for f in range(4):
                i = nc.tensor.matmul(ps[2][0:KS, 0:128], w[11][:, 64 * f:64 * f + 64], w24[:, f, :], start=(f == 0), stop=(f == 3))
            i.then_inc(sem("f3_d"), 1)
            pe.wait_ge(sem("f3_proc"), at(it, "f3_proc"))
            nc.tensor.matmul(ps[3][:], proc[0:KS - 1, :], hotT[0:KS - 1, :], start=True, stop=True).then_inc(sem("f3_back"), 1)
            pe.wait_ge(sem("x_done"), at(it, "x_done"))
            for t in range(NT):
                i = nc.tensor.transpose(ps[4][:, 128 * t:128 * t + 128], X[:, 128 * t:128 * t + 128], ident)
            i.then_inc(sem("x_fint"), 1)

        def f3_act(act, it):
            act.wait_ge(sem("f3_ht"), at(it, "f3_ht"))
            nc.scalar.activation(to_gather[:, :, 0:128], ps[2][:].rearrange("p (t c) -> p t c", t=NT), ACT.Copy).then_inc(sem("f3_htc"), 1)
            act.wait_ge(sem("f3_hott"), at(it, "f3_hott"))
            nc.scalar.activation(hotT[R, :], ps[5][R, :], ACT.Copy).then_inc(sem("f3_hottc"), 1)
            act.wait_ge(sem("f3_ms1"), at(it, "f3_ms1"))
            nc.scalar.activation(ssq[:, 1:2], ssq[:, 0:1], ACT.Sqrt, bias=k("eps")[R, 2:3], scale=1.0 / C).then_inc(sem("f3_rt1"), 1)
            act.wait_ge(sem("f3_qkv"), at(it, "f3_qkv"))
            nc.scalar.activation(qkv4[:, 0:384], ps[3][:, 0:384], ACT.Copy).then_inc(sem("f3_qkvc"), 1)
            act.wait_ge(sem("f3_m1"), at(it, "f3_m1"))
            nc.scalar.activation(m1[:], ps[7][:], ACT.Copy).then_inc(sem("f3_m1c"), 1)
            for g in range(4):
                act.wait_ge(sem("f3_smx"), at(it, "f3_smx", g + 1))
                nc.scalar.activation(s4[:, 256 * g:256 * g + 256], s4[:, 256 * g:256 * g + 256], ACT.Exp).then_inc(sem("f3_p"), 1)
            for n in range(2):
                act.wait_ge(sem("f3_pt"), at(it, "f3_pt", n + 1))
                nc.scalar.activation(pT[:, n, :], ps[6 + n][:], ACT.Copy).then_inc(sem("f3_ptc"), 1)
            act.wait_ge(sem("f3_ont"), at(it, "f3_ont"))
            nc.scalar.activation(narrow[:, 0:128], ps[4][:, 0:128], ACT.Copy).then_inc(sem("f3_ontc"), 1)
            act.wait_ge(sem("f3_ms2"), at(it, "f3_ms2"))
            nc.scalar.activation(ssq[:, 1:2], ssq[:, 0:1], ACT.Sqrt, bias=k("eps")[R, 2:3], scale=1.0 / C).then_inc(sem("f3_rt2"), 1)
            act.wait_ge(sem("f3_gu"), at(it, "f3_gu"))
            nc.scalar.activation(w[11][:, 0:256], w[11][:, 0:256], ACT.Tanh, scale=0.7978845608028654).then_inc(sem("f3_th"), 1)
            act.wait_ge(sem("x_fint"), at(it, "x_fint"))
            act.wait_ge(sem("x_saved"), 16 * it + 16)
            nc.scalar.activation(x_fin[:].rearrange("p a b -> p (a b)"), ps[4][:], ACT.Copy).then_inc(sem("x_fin"), 1)

        def f3_dve(dve, it):
            nc.vector.tensor_copy(rope_now, rope[:, bass.ds(it, 1), :, :].rearrange("p o a b -> p (o a) b")).then_inc(sem("f3_rope"), 1)
            dve.wait_ge(sem("f3_rope"), at(it, "f3_rope"))
            dve.wait_ge(sem("f3_w"), at(it, "f3_w"))
            nc.vector.tensor_scalar(wrow[:], ps[3][:], router_b[:, 0:1], None, ALU.add).then_inc(sem("vector_step"), 1)
            dve.wait_ge(sem("vector_step"), step(it, "vector"))
            nc.vector.tensor_tensor(w[5][:].rearrange("p (t n) -> p t n", t=NT), wrow[:].rearrange("p (t n) -> p t n", t=NT),
                                            ident.rearrange("p (o n) -> p o n", o=1).broadcast_to([128, NT, 128]), ALU.mult).then_inc(sem("vector_step"), 1)
            dve.wait_ge(sem("vector_step"), step(it, "vector"))
            nc.vector.tensor_reduce(to_gather[:, :, 128], w[5][:].rearrange("p (t n) -> p t n", t=NT), AX.X, ALU.add).then_inc(sem("vector_step"), 1)
            dve.wait_ge(sem("vector_step"), step(it, "vector"))
            for t in range(NT):
                i = nc.vector.scalar_tensor_tensor(out=big[0][:, t, :], in0=wrow[:], scalar=to_gather[:, t, 128:129],
                                                   in1=k("earlier")[:, T * t:T * t + T], op0=ALU.is_equal, op1=ALU.mult)
            i.then_inc(sem("vector_step"), 1)
            dve.wait_ge(sem("vector_step"), step(it, "vector"))
            for t in range(NT):
                i = nc.vector.scalar_tensor_tensor(out=big[0][:, t, :], in0=wrow[:], scalar=to_gather[:, t, 128:129],
                                                   in1=big[0][:, t, :], op0=ALU.is_gt, op1=ALU.add, accum_out=rank[:, t:t + 1])
            i.then_inc(sem("vector_step"), 1)
            dve.wait_ge(sem("vector_step"), step(it, "vector"))
            nc.vector.tensor_tensor(hot[:].rearrange("p (t r) -> p t r", t=NT), k("iota").rearrange("p (o r) -> p o r", o=1).broadcast_to([128, NT, 2 * KS]),
                                             rank.rearrange("p (t o) -> p t o", o=1).broadcast_to([128, NT, 2 * KS]), ALU.is_equal).then_inc(sem("f3_hot"), 1)
            dve.wait_ge(sem("f3_hot"), at(it, "f3_hot"))
            for t in range(NT):
                i = nc.vector.tensor_scalar(cge[:, t, :], wrow[:], to_gather[:, t, 128:129], None, ALU.is_le)
            i.then_inc(sem("f3_cge"), 1)
            dve.wait_ge(sem("f3_cge"), at(it, "f3_cge"))
            dve.wait_ge(sem("f3_xs"), at(it, "f3_xs"))
            nc.vector.tensor_copy(xs, ps[6][R, 0:128])
            nc.vector.tensor_copy(wsel, ps[6][R, 128:129])
            nc.vector.tensor_copy(cs, ps[6][R, 129:137]).then_inc(sem("vector_step"), 1)
            dve.wait_ge(sem("vector_step"), step(it, "vector"))

            def rms(src, tmp, dst, mean_sq, root, name):
                nc.vector.tensor_tensor(tmp, src, src, ALU.mult).then_inc(sem("vector_step"), 1)
                dve.wait_ge(sem("vector_step"), step(it, "vector"))
                nc.vector.tensor_reduce(ssq[:, 0:1], tmp, AX.X, ALU.add).then_inc(sem(mean_sq), 1)
                dve.wait_ge(sem(mean_sq), at(it, mean_sq))
                dve.wait_ge(sem(root), at(it, root))
                nc.vector.reciprocal(ssq[:, 2:3], ssq[:, 1:2]).then_inc(sem("vector_step"), 1)
                dve.wait_ge(sem("vector_step"), step(it, "vector"))
                nc.vector.tensor_scalar(dst, src, ssq[:, 2:3], None, ALU.mult).then_inc(sem(name), 1)
                dve.wait_ge(sem(name), at(it, name))

            rms(xs, osel, osel, "f3_ms1", "f3_rt1", "f3_hn")
            dve.wait_ge(sem("f3_hnt"), at(it, "f3_hnt"))
            nc.vector.tensor_scalar(narrow[:, 0:128], ps[2][:, 0:128], vec("L3_ffn_ln1"), None, ALU.mult).then_inc(sem("f3_hntc"), 1)
            dve.wait_ge(sem("f3_hntc"), at(it, "f3_hntc"))
            dve.wait_ge(sem("f3_cnt"), at(it, "f3_cnt"))
            nc.vector.tensor_scalar(notsel[:], ps[4][:], KS - 0.5, None, ALU.is_ge).then_inc(sem("vector_step"), 1)
            dve.wait_ge(sem("vector_step"), step(it, "vector"))
            dve.wait_ge(sem("f3_qkvc"), at(it, "f3_qkvc"))
            qk = qkv4[R, 0:256].rearrange("p (u two f) -> p u two f", two=2, f=4)
            cos = cs[:, 0:4].rearrange("p (a b f) -> p a b f", a=1, b=1).broadcast_to([128, 32, 2, 4])
            sin = cs[:, 4:8].rearrange("p (a f) -> p a f", a=1).broadcast_to([128, 32, 4])
            ra = w[10][R, 0:256].rearrange("p (u two f) -> p u two f", two=2, f=4)
            rb = w[10][R, 256:512].rearrange("p (u two f) -> p u two f", two=2, f=4)
            ro = w[11][R, 0:256].rearrange("p (u two f) -> p u two f", two=2, f=4)
            nc.vector.tensor_tensor(ra, qk, cos, ALU.mult)
            nc.vector.tensor_tensor(rb[:, :, 0], qk[:, :, 1], sin, ALU.mult)
            nc.vector.tensor_tensor(rb[:, :, 1], qk[:, :, 0], sin, ALU.mult).then_inc(sem("vector_step"), 1)
            dve.wait_ge(sem("vector_step"), step(it, "vector"))
            nc.vector.tensor_tensor(ro[:, :, 0], ra[:, :, 0], rb[:, :, 0], ALU.subtract)
            nc.vector.tensor_tensor(ro[:, :, 1], ra[:, :, 1], rb[:, :, 1], ALU.add).then_inc(sem("f3_ro"), 1)
            dve.wait_ge(sem("f3_ro"), at(it, "f3_ro"))
            dve.wait_ge(sem("f3_msel"), at(it, "f3_msel"))
            nc.vector.tensor_copy(msel, ps[0][:, 0:64]).then_inc(sem("vector_step"), 1)
            dve.wait_ge(sem("vector_step"), step(it, "vector"))
            nc.vector.memset(msel[:, KS - 1:KS], NEG).then_inc(sem("vector_step"), 1)
            dve.wait_ge(sem("vector_step"), step(it, "vector"))
            dve.wait_ge(sem("f3_rot"), at(it, "f3_rot"))
            nc.vector.tensor_copy(narrow[:, 128:192], ps[4][:, 128:192]).then_inc(sem("vector_step"), 1)
            dve.wait_ge(sem("vector_step"), step(it, "vector"))
            for m in range(4):
                i = nc.vector.tensor_scalar(q4[:, 128 * m:128 * m + 128], ps[4][:, 0:128], k("head4")[:, m:m + 1], None, ALU.mult)
            i.then_inc(sem("f3_qk"), 1)
            s4v = s4.rearrange("p (u n) -> p u n", n=64)
            for g in range(4):
                u = slice(4 * g, 4 * g + 4)
                dve.wait_ge(sem("f3_s"), at(it, "f3_s", g + 1))
                nc.vector.scalar_tensor_tensor(out=s4v[:, u], in0=ps[(0, 1, 2, 5)[g]][R, 0:256].rearrange("p (u n) -> p u n", n=64), scalar=RS8,
                                               in1=msel.rearrange("p (o n) -> p o n", o=1).broadcast_to([128, 4, 64]), op0=ALU.mult, op1=ALU.add)\
                    .then_inc(sem("vector_step"), 1)
                dve.wait_ge(sem("vector_step"), step(it, "vector"))
                nc.vector.tensor_reduce(smx[:, u], s4v[:, u], AX.X, ALU.max).then_inc(sem("vector_step"), 1)
                dve.wait_ge(sem("vector_step"), step(it, "vector"))
                nc.vector.tensor_tensor(s4v[:, u], s4v[:, u], smx[:, u].rearrange("p (u o) -> p u o", o=1).broadcast_to([128, 4, 64]), ALU.subtract)\
                    .then_inc(sem("f3_smx"), 1)
            dve.wait_ge(sem("f3_smx"), at(it, "f3_smx"))
            dve.wait_ge(sem("f3_p"), at(it, "f3_p"))
            nc.vector.tensor_reduce(ssum, s4v, AX.X, ALU.add).then_inc(sem("vector_step"), 1)
            dve.wait_ge(sem("vector_step"), step(it, "vector"))
            nc.vector.reciprocal(srec, ssum).then_inc(sem("vector_step"), 1)
            dve.wait_ge(sem("vector_step"), step(it, "vector"))
            dve.wait_ge(sem("f3_o"), at(it, "f3_o"))
            for e in range(2):
                i = nc.vector.tensor_tensor(osel.rearrange("p (u e d) -> p e u d", e=2, d=HD4)[:, e], ps[3 + e][R, 0:64].rearrange("p (u d) -> p u d", d=HD4),
                                            srec.rearrange("p (u e o) -> p e u o", e=2, o=1)[:, e].broadcast_to([128, H4 // 2, HD4]), ALU.mult)
            i.then_inc(sem("f3_on"), 1)
            dve.wait_ge(sem("f3_on"), at(it, "f3_on"))
            dve.wait_ge(sem("f3_wo"), at(it, "f3_wo"))
            nc.vector.tensor_tensor(x1, xs, ps[5][R, 0:128], ALU.add).then_inc(sem("vector_step"), 1)
            dve.wait_ge(sem("vector_step"), step(it, "vector"))
            rms(x1, x2n, x2n, "f3_ms2", "f3_rt2", "f3_h2")
            dve.wait_ge(sem("f3_h2t"), at(it, "f3_h2t"))
            nc.vector.tensor_scalar(narrow[:, 0:128], ps[6][:, 0:128], vec("L3_ffn_ln2"), None, ALU.mult).then_inc(sem("f3_h2tc"), 1)
            dve.wait_ge(sem("f3_h2tc"), at(it, "f3_h2tc"))
            u, g, gg = w[10][:, 0:256], w[11][:, 0:256], w[11][:, 256:512]
            dve.wait_ge(sem("f3_u"), at(it, "f3_u"))
            nc.vector.tensor_copy(u, ps[7][:, 0:256]).then_inc(sem("vector_step"), 1)
            dve.wait_ge(sem("vector_step"), step(it, "vector"))
            nc.vector.tensor_tensor(gg, u, u, ALU.mult).then_inc(sem("vector_step"), 1)
            dve.wait_ge(sem("vector_step"), step(it, "vector"))
            nc.vector.tensor_scalar(gg, gg, 0.044715, 1.0, ALU.mult, ALU.add).then_inc(sem("vector_step"), 1)
            dve.wait_ge(sem("vector_step"), step(it, "vector"))
            nc.vector.tensor_tensor(g, gg, u, ALU.mult).then_inc(sem("f3_gu"), 1)
            dve.wait_ge(sem("f3_gu"), at(it, "f3_gu"))
            dve.wait_ge(sem("f3_th"), at(it, "f3_th"))
            nc.vector.tensor_scalar(g, g, 1.0, 0.5, ALU.add, ALU.mult).then_inc(sem("vector_step"), 1)
            dve.wait_ge(sem("vector_step"), step(it, "vector"))
            nc.vector.tensor_tensor(g, g, u, ALU.mult).then_inc(sem("f3_g"), 1)
            dve.wait_ge(sem("f3_g"), at(it, "f3_g"))
            dve.wait_ge(sem("f3_d"), at(it, "f3_d"))
            nc.vector.tensor_tensor(x2n[0:KS], x1[0:KS], ps[2][0:KS, 0:128], ALU.add).then_inc(sem("vector_step"), 1)
            dve.wait_ge(sem("vector_step"), step(it, "vector"))
            dve.wait_ge(sem("f3_hottc"), at(it, "f3_hottc"))
            nc.vector.tensor_scalar(proc[0:KS], x2n[0:KS], wsel[0:KS], None, ALU.mult).then_inc(sem("f3_proc"), 1)
            dve.wait_ge(sem("f3_proc"), at(it, "f3_proc"))
            nc.vector.tensor_tensor(notsel[:], notsel[:], h, ALU.mult).then_inc(sem("vector_step"), 1)
            dve.wait_ge(sem("vector_step"), step(it, "vector"))
            dve.wait_ge(sem("f3_back"), at(it, "f3_back"))
            nc.vector.tensor_tensor(notsel[:], notsel[:], ps[3][:], ALU.add).then_inc(sem("vector_step"), 1)
            dve.wait_ge(sem("vector_step"), step(it, "vector"))
            nc.vector.scalar_tensor_tensor(out=X[:], in0=notsel[:], scalar=mod(3, 5), in1=X[:], op0=ALU.mult, op1=ALU.add).then_inc(sem("x_done"), 1)
            dve.wait_ge(sem("x_done"), at(it, "x_done"))

        mabs = sb("mabs", [128, 4, 8])
        onesb = sb("onesb", [128, 128], BF16)
        to_gather = sb("to_gather", [128, NT, 137])
        rope_now = to_gather[:, :, 129:137]

        loads = [(const[:], d["const"])]
        loads += [(w[i][:], d["stack_const"][:, 512 * i:512 * i + 512]) for i in range(3)]
        loads += [(vec_rows[:], d["vectors"]), (bias_row[:], d["bias_row"]), (wq0[:], d["L0_attn_Wq"]), (wkv0[:], d["kv0"]),
                  (ctl[:], d["controller"]), (f1[:], d["L0_ffn_f1"].rearrange("d n s f -> d (n s) f")),
                  (bias0_rows[:], d["L0_ffn_bias"].rearrange("n (a e) f -> (n a) (e f)", e=2)),
                  (f2[:], d["f0_down"]), (w2s[:], d["f1_down"]), (wmod, d["wmod"]), (c_rows[:], d["c_rows"])]
        maw2 = d["L1_attn_time_maa_w2"]
        loads += [(w1mix[:], d["L1_attn_time_maa_w1"]), (w2mix[:], maw2[0:4].rearrange("s d c -> (s d) c")), (w2mix4[:], maw2[4]),
                  (dw1[:], d["L1_attn_time_decay_w1"]), (dw2[:], d["L1_attn_time_decay_w2"]), (w5[:], d["rkvgo"])]
        loads += [(gw1[:], d["L1_ffn_gate_w"]), (w1s[:], d["L1_ffn_w1"].rearrange("e d h -> d e h")),
                  (w3s[:], d["L1_ffn_w3"].rearrange("e d h -> d e h")),
                  (wqkv2[:], d["L2_attn_w_qkv"]), (wout2[:], d["L2_attn_w_out"]), (gate2_rows[:], d["L2_ffn_gate_w"]), (raw, d["f2_raw"])]
        loads += [(wqk3[:], d["qk3"]), (wv3_wide.rearrange("p a b -> p (a b)"), d["L3_attn_Wv"]), (router[:], d["L3_ffn_router_w"]),
                  (wqkv4[:], d["qkv4"]), (wo4[:], d["L3_ffn_wo"]), (w14[:], d["L3_ffn_w1"]),
                  (w24[:], d["L3_ffn_w2"].rearrange("(f p) d -> p f d", p=128))]

        block = ctx.enter_context(nc.Block())

        @block.sync
        def _(sync):
            for dst, src in loads:
                sync.dma_start(dst, src).then_inc(sem("loaded"), 16)
            sync.dma_start(pos_i[:], d["L3_ffn_position_ids"].rearrange("b (t p) -> (b t) p", p=128)).then_inc(sem("x_saved"), 16)

            def load_x(b):
                sync.dma_start(x_tok[:], d["L0_attn_x"][bass.ds(b, 1)].rearrange("o (t p) c -> p (o t) c", p=128)).then_inc(sem("x_in"), 16)

            def one(it, row, more=True):
                if more:
                    following = sync.snap(it + 1)
                    sync.wait_ge(sem("x_used"), at(it, "x_used"))
                    load_x(following)
                sync.wait_ge(sem("ln_x"), at(it, "ln_x", 6))
                sync.dma_start(msk[:], d["L3_ffn_attention_mask"][bass.ds(row, 1)].rearrange("o u (t p) c -> p (o u t) c", p=128))\
                    .then_inc(sem("mask_in"), 16)
                sync.wait_ge(sem("x_fin"), at(it, "x_fin"))
                sync.dma_start(out[bass.ds(it, 1)].rearrange("o (t p) c -> p (o t) c", p=128), x_fin[:]).then_inc(sem("x_saved"), 16)

            load_x(0)
            with sync.Fori(0, MB) as it:
                one(it, it)
            with sync.Fori(MB, B - 1) as it:
                one(it, MB - 1)
            one(B - 1, MB - 1, more=False)
            sync.wait_ge(sem("x_saved"), 16 * (B + 1))

        @block.tensor
        def _(pe):
            pe.wait_ge(sem("loaded"), 16 * len(loads))
            pe.wait_ge(sem("pos"), 1)
            nc.tensor.transpose(ps[0][:, 0:20], vec_rows[:], ident[0:20, 0:20])
            nc.tensor.transpose(ps[0][:, 32:64], bias0_rows[:], ident[0:32, 0:32])
            nc.tensor.transpose(ps[0][:, 64:96], c_rows[:], ident[0:32, 0:32])
            nc.tensor.transpose(ps[0][:, 96:104], gate2_rows[:], ident[0:8, 0:8])
            nc.tensor.transpose(ps[0][:, 112:128], pos_f[:], ident[0:16, 0:16])
            nc.tensor.matmul(ps[0][:, 130:131], ones[0:1, :], bias_row[0:1, 1408:1409], start=True, stop=True)
            for n in range(27):
                i = nc.tensor.transpose(ps[1 + n // 4][:, 128 * (n % 4):128 * (n % 4) + 128], raw[:, n, :], ident)
            i.then_inc(sem("weights_turned"), 1)
            pe.wait_ge(sem("silu_c"), 1)
            for n in range(24):
                i = nc.tensor.matmul(ps[0][:, 8 * n:8 * n + 8], wmod[:, n // 6, 128 * (n % 6):128 * (n % 6) + 128],
                                     silu_c[:, 8 * (n // 6):8 * (n // 6) + 8], start=True, stop=True)
            i.then_inc(sem("mod"), 1)
            pe.wait_ge(sem("prepared"), 1)
            with pe.Fori(0, B) as it:
                pe.wait_ge(sem("x_in"), at(it, "x_in"))
                for t in range(NT):
                    i = nc.tensor.transpose(ps[5][:, 128 * t:128 * t + 128], x_tok[:, t, :], ident)
                i.then_inc(sem("x_used"), 1)
                for n, stage in enumerate((a0_pe, f0_pe, a1_pe, f1_pe, a2_pe, f2_pe, None, a3_pe, f3_pe)):
                    ln_pe(pe, it, n + 1)
                    if stage:
                        stage(pe, it)

        @block.scalar
        def _(act):
            act.wait_ge(sem("c_turned"), 1)
            act.activation(silu_t[:], silu_c[:], ACT.Tanh, scale=0.5).then_inc(sem("c_tanh"), 1)
            act.wait_ge(sem("angles"), 1)
            act.activation(ang[:].rearrange("p a b -> p (a b)"), angt[:].rearrange("p a b -> p (a b)"), ACT.Sin).then_inc(sem("sines"), 1)
            with act.Fori(0, B) as it:
                enter("scalar")
                for n, stage in enumerate((a0_act, f0_act, a1_act, f1_act, a2_act, f2_act, None, a3_act, f3_act)):
                    ln_act(act, it, n + 1)
                    if stage:
                        stage(act, it)

        @block.vector
        def _(dve):
            it = None
            dve.wait_ge(sem("loaded"), 16 * len(loads))
            dve.wait_ge(sem("x_saved"), 16)
            nc.vector.tensor_copy(pos_f[:], pos_i[:]).then_inc(sem("pos"), 1)
            nc.vector.tensor_copy(identb[:], ident)
            nc.vector.tensor_copy(causalb[:], k("causal"))
            nc.vector.tensor_copy(onesb[:], ones)
            for i in range(2):
                nc.vector.tensor_copy(stack_rows[:].rearrange("p a b c e -> p (a b c e)")[:, 512 * i:512 * i + 512], w[i][:])
            nc.vector.tensor_copy(hot_max[:].rearrange("p a b -> p (a b)"), w[2][:])
            nc.vector.memset(max_part[:], 0.0)
            nc.vector.memset(max_rows[:], 0.0)
            nc.vector.memset(hp[:, 0:1], 0.0)
            nc.vector.memset(v1[:, :, 128:129], 1.0)
            nc.vector.memset(scoresT[:], 0.0)
            nc.vector.memset(shifted[:, :, 0:1], 0.0)
            nc.vector.tensor_reduce(wv3[:], wv3_wide.rearrange("p a (n r) -> p (a n) r", r=8), AX.X, ALU.add)
            nc.vector.tensor_reduce(bv3[:], bias_row[0:1, 384:1408].rearrange("p (n r) -> p n r", r=8), AX.X, ALU.add)
            nc.vector.tensor_copy(router_bc[:], router[:].broadcast_to([128, 128])).then_inc(sem("vector_step"), 1)
            dve.wait_ge(sem("vector_step"), step(it, "vector"))
            dve.wait_ge(sem("weights_turned"), 1)
            for n in range(7):
                m = 4 if n < 6 else 3
                nc.vector.tensor_copy(turned[:, 4 * n:4 * n + m, :].rearrange("p a b -> p (a b)"), ps[1 + n][:, 0:128 * m])
            nc.vector.tensor_copy(vecs[:], ps[0][:, 0:20])
            nc.vector.tensor_copy(bias0[:], ps[0][:, 32:64])
            nc.vector.tensor_copy(gate2[:], ps[0][:, 96:104])
            nc.vector.tensor_copy(pos_c[:], ps[0][:, 112:128])
            nc.vector.tensor_copy(router_b[:], ps[0][:, 130:131])
            nc.vector.tensor_copy(silu_c[:], ps[0][:, 64:96]).then_inc(sem("c_turned"), 1)
            dve.wait_ge(sem("c_tanh"), 1)
            nc.vector.scalar_tensor_tensor(out=silu_t[:], in0=silu_t[:], scalar=1.0, in1=silu_c[:], op0=ALU.add, op1=ALU.mult).then_inc(sem("vector_step"), 1)
            dve.wait_ge(sem("vector_step"), step(it, "vector"))
            nc.vector.tensor_scalar(silu_c[:], silu_t[:], 0.5, None, ALU.mult).then_inc(sem("silu_c"), 1)
            for half in range(2):
                nc.vector.tensor_tensor(ang[:, :, 4 * half:4 * half + 4], pos_c[:].rearrange("p (n o) -> p n o", o=1).broadcast_to([128, 16, 4]),
                                                k("freq").rearrange("p (o f) -> p o f", o=1).broadcast_to([128, 16, 4]), ALU.mult).then_inc(sem("vector_step"), 1)
                dve.wait_ge(sem("vector_step"), step(it, "vector"))
            a2 = ang[:].rearrange("p a b -> p (a b)")
            t2 = angt[:].rearrange("p a b -> p (a b)")
            q2 = small[:, 0:128]
            nc.vector.tensor_scalar(t2, a2, 1.0 / (2 * np.pi), None, ALU.mult).then_inc(sem("vector_step"), 1)
            dve.wait_ge(sem("vector_step"), step(it, "vector"))
            nc.vector.tensor_scalar(q2, t2, 12582912.0, None, ALU.add).then_inc(sem("vector_step"), 1)
            dve.wait_ge(sem("vector_step"), step(it, "vector"))
            nc.vector.tensor_scalar(q2, q2, -12582912.0, None, ALU.add).then_inc(sem("vector_step"), 1)
            dve.wait_ge(sem("vector_step"), step(it, "vector"))
            for part in (6.28125, 0.0019350051879882812, 3.019916050337359e-07):
                nc.vector.scalar_tensor_tensor(out=a2, in0=q2, scalar=-part, in1=a2, op0=ALU.mult, op1=ALU.add).then_inc(sem("vector_step"), 1)
                dve.wait_ge(sem("vector_step"), step(it, "vector"))
            nc.vector.tensor_scalar(ang[:, :, 0:4], ang[:, :, 0:4], np.pi / 2, None, ALU.add).then_inc(sem("vector_step"), 1)
            dve.wait_ge(sem("vector_step"), step(it, "vector"))
            nc.vector.tensor_scalar(t2, a2, np.pi, -2 * np.pi, ALU.is_gt, ALU.mult).then_inc(sem("vector_step"), 1)
            dve.wait_ge(sem("vector_step"), step(it, "vector"))
            nc.vector.tensor_tensor(t2, t2, a2, ALU.add).then_inc(sem("vector_step"), 1)
            dve.wait_ge(sem("vector_step"), step(it, "vector"))
            nc.vector.tensor_scalar(t2, t2, 3.1415925, -3.1415925, ALU.min, ALU.max).then_inc(sem("angles"), 1)
            dve.wait_ge(sem("mod"), 1)
            nc.vector.tensor_copy(mods[:].rearrange("p a b -> p (a b)"), ps[0][:, 0:192]).then_inc(sem("vector_step"), 1)
            dve.wait_ge(sem("vector_step"), step(it, "vector"))
            m4 = mods[:].rearrange("p (l j) b -> p l j b", l=4)
            for j in (1, 4):
                nc.vector.tensor_scalar(m4[:, :, j, :], m4[:, :, j, :], 1.0, None, ALU.add).then_inc(sem("vector_step"), 1)
                dve.wait_ge(sem("vector_step"), step(it, "vector"))
            for j in (2, 5):
                nc.vector.tensor_scalar(mtmp[:], m4[:, :, j, :], 0.0, 2.0, ALU.is_ge, ALU.mult).then_inc(sem("vector_step"), 1)
                dve.wait_ge(sem("vector_step"), step(it, "vector"))
                nc.vector.scalar_tensor_tensor(out=mabs[:], in0=m4[:, :, j, :], scalar=-1.0, in1=m4[:, :, j, :], op0=ALU.mult, op1=ALU.max).then_inc(sem("vector_step"), 1)
                dve.wait_ge(sem("vector_step"), step(it, "vector"))
                nc.vector.tensor_scalar(mabs[:], mabs[:], 0.25, None, ALU.max).then_inc(sem("vector_step"), 1)
                dve.wait_ge(sem("vector_step"), step(it, "vector"))
                nc.vector.scalar_tensor_tensor(out=m4[:, :, j, :], in0=mtmp[:], scalar=-1.0, in1=mabs[:], op0=ALU.add, op1=ALU.mult).then_inc(sem("vector_step"), 1)
                dve.wait_ge(sem("vector_step"), step(it, "vector"))
            dve.wait_ge(sem("sines"), 1)
            for b in range(B):
                i = nc.vector.tensor_copy(rope[:, b, :, :], ang[:, 4 * min(b, MB - 1):4 * min(b, MB - 1) + 4, :])
            i.then_inc(sem("vector_step"), 1)
            dve.wait_ge(sem("vector_step"), step(it, "vector"))
            nc.vector.memset(mtmp[:, 0, 0:1], 0.0).then_inc(sem("prepared"), 1)
            with dve.Fori(0, B) as it:
                enter("vector")
                nc.vector.tensor_copy(mod_now[:].rearrange("p (a o) -> p a o", o=1), mods[:, :, bass.ds(it, 1)]).then_inc(sem("vector_step"), 1)
                dve.wait_ge(sem("vector_step"), step(it, "vector"))
                dve.wait_ge(sem("x_used"), it + 1)
                nc.vector.tensor_copy(X[:], ps[5][:]).then_inc(sem("ln_x"), 1)
                dve.wait_ge(sem("ln_x"), at(it, "ln_x", 1))
                for n, stage in enumerate((a0_dve, f0_dve, a1_dve, f1_dve, a2_dve, f2_dve, None, a3_dve, f3_dve)):
                    l, j = (n // 2, n % 2) if n < 7 else ((3, 0) if n == 7 else (3, 1))
                    if n == 7:
                        ln_dve(dve, it, n + 1, h, vec("L3_attn_gamma"), vec("L3_attn_beta"))
                    else:
                        ln_dve(dve, it, n + 1, X[:], mod(l, 3 * j + 1), mod(l, 3 * j))
                    if stage is f3_dve:
                        f3_dve(dve, it)
                    elif stage:
                        stage(dve, it)
        assert {e: seen[e] for e in STEPS} == STEPS, seen


_INS = [
    'L0_attn_x', 'L0_attn_Wq', 'L0_attn_bq', 'L0_attn_Wk', 'L0_attn_bk', 'L0_attn_Wv', 'L0_attn_bv', 'L0_ffn_controller',
    'L0_ffn_f1', 'L0_ffn_f2', 'L0_ffn_bias', 'L0_c', 'L0_wmod', 'L1_attn_time_maa_x', 'L1_attn_time_maa_w',
    'L1_attn_time_maa_k', 'L1_attn_time_maa_v', 'L1_attn_time_maa_r', 'L1_attn_time_maa_g', 'L1_attn_time_maa_w1',
    'L1_attn_time_maa_w2', 'L1_attn_time_decay', 'L1_attn_time_decay_w1', 'L1_attn_time_decay_w2', 'L1_attn_time_faaaa',
    'L1_attn_Wr', 'L1_attn_Wk', 'L1_attn_Wv', 'L1_attn_Wg', 'L1_attn_Wo', 'L1_attn_ln_w', 'L1_attn_ln_b',
    'L1_ffn_gate_w', 'L1_ffn_w1', 'L1_ffn_w2', 'L1_ffn_w3', 'L1_c', 'L1_wmod', 'L2_attn_w_qkv', 'L2_attn_b_qkv',
    'L2_attn_w_out', 'L2_attn_b_out', 'L2_ffn_gate_w', 'L2_ffn_w_gate', 'L2_ffn_w_up', 'L2_ffn_w_down', 'L2_ffn_A1',
    'L2_ffn_B1', 'L2_ffn_A3', 'L2_ffn_B3', 'L2_ffn_A2', 'L2_ffn_B2', 'L2_c', 'L2_wmod', 'L3_attn_Wq', 'L3_attn_bq',
    'L3_attn_Wk', 'L3_attn_bk', 'L3_attn_Wv', 'L3_attn_bv', 'L3_attn_gamma', 'L3_attn_beta', 'L3_ffn_attention_mask',
    'L3_ffn_position_ids', 'L3_ffn_router_w', 'L3_ffn_router_b', 'L3_ffn_wq', 'L3_ffn_wk', 'L3_ffn_wv', 'L3_ffn_wo',
    'L3_ffn_w1', 'L3_ffn_w2', 'L3_ffn_ln1', 'L3_ffn_ln2', 'L3_c', 'L3_wmod']


PACKED_ONLY = {
    'L0_attn_bq', 'L0_attn_Wk', 'L0_attn_bk', 'L0_attn_Wv', 'L0_attn_bv', 'L0_ffn_controller', 'L0_ffn_f2', 'L0_c',
    'L0_wmod', 'L1_attn_time_maa_x', 'L1_attn_time_maa_w', 'L1_attn_time_maa_k', 'L1_attn_time_maa_v',
    'L1_attn_time_maa_r', 'L1_attn_time_maa_g', 'L1_attn_time_decay', 'L1_attn_time_faaaa', 'L1_attn_Wr',
    'L1_attn_Wk', 'L1_attn_Wv', 'L1_attn_Wg', 'L1_attn_Wo', 'L1_attn_ln_w', 'L1_attn_ln_b', 'L1_ffn_w2', 'L1_c',
    'L1_wmod', 'L2_attn_b_qkv', 'L2_attn_b_out', 'L2_ffn_w_gate', 'L2_ffn_w_up', 'L2_ffn_w_down', 'L2_ffn_A1',
    'L2_ffn_B1', 'L2_ffn_A3', 'L2_ffn_B3', 'L2_ffn_A2', 'L2_ffn_B2', 'L2_c', 'L2_wmod', 'L3_attn_Wq', 'L3_attn_bq',
    'L3_attn_Wk', 'L3_attn_bk', 'L3_attn_bv', 'L3_attn_gamma', 'L3_attn_beta', 'L3_ffn_router_b', 'L3_ffn_wq',
    'L3_ffn_wk', 'L3_ffn_wv', 'L3_ffn_ln1', 'L3_ffn_ln2', 'L3_c', 'L3_wmod',
}


def packed(a):
    rows = ["L0_attn_bq", "L1_attn_time_maa_x", "L1_attn_time_maa_w", "L1_attn_time_maa_k",
            "L1_attn_time_maa_v", "L1_attn_time_maa_r", "L1_attn_time_maa_g", "L1_attn_time_decay",
            "L1_attn_time_faaaa", "L1_attn_ln_w", "L1_attn_ln_b", "L2_attn_b_out", "L3_attn_bq",
            "L3_attn_bk", "L3_attn_gamma", "L3_attn_beta", "L3_ffn_ln1", "L3_ffn_ln2"]
    b2 = a["L2_attn_b_qkv"].reshape(-1)
    ctl = a["L0_ffn_controller"].reshape(C, NES)
    p = {
        "vectors": np.stack([a[n].reshape(-1) for n in rows] + [b2[0:128], b2[128:256]]),
        "bias_row": np.concatenate([a["L0_attn_bk"].reshape(-1), a["L0_attn_bv"].reshape(-1), b2[256:384],
                                    a["L3_attn_bv"].reshape(-1), a["L3_ffn_router_b"].reshape(-1)])[None],
        "kv0": np.concatenate([a["L0_attn_Wk"], a["L0_attn_Wv"]], axis=1),
        "controller": np.concatenate([ctl, ctl], axis=1),
        "f0_down": a["L0_ffn_f2"].reshape(NES // 2, 2 * EW, C).transpose(1, 0, 2),
        "f1_down": a["L1_ffn_w2"].reshape(E1 // 2, 2 * H1, C).transpose(1, 0, 2),
        "wmod": np.stack([a[f"L{l}_wmod"] for l in range(4)], axis=1),
        "c_rows": np.concatenate([a[f"L{l}_c"] for l in range(4)]),
        "rkvgo": np.stack([a["L1_attn_W" + n] for n in "rkvgo"], axis=1),
        "qk3": np.concatenate([a["L3_attn_Wq"], a["L3_attn_Wk"]], axis=1),
        "qkv4": np.concatenate([a["L3_ffn_w" + n] for n in "qkv"], axis=1),
    }
    er = E2 * R2
    blocks = [a["L2_ffn_w_gate"].reshape(4, 128, C), a["L2_ffn_w_up"].reshape(4, 128, C),
              a["L2_ffn_w_down"].reshape(C, 4, 128).transpose(1, 0, 2)]
    blocks += [a["L2_ffn_" + n].reshape(E2, 4, 128, R2).transpose(1, 2, 0, 3).reshape(4, 128, er) for n in ("B1", "B3")]
    blocks += [a["L2_ffn_A2"].reshape(er, 4, 128).transpose(1, 0, 2), a["L2_ffn_A1"].reshape(1, er, C),
               a["L2_ffn_A3"].reshape(1, er, C), a["L2_ffn_B2"].transpose(1, 0, 2).reshape(1, C, er)]
    p["f2_raw"] = np.concatenate(blocks).transpose(1, 0, 2)
    return p


def kernel(**inputs):
    import concourse.bacc as bacc
    from concourse.bass_utils import run_bass_kernel_spmd

    nc = bacc.Bacc("TRN2", target_bir_lowering=False, num_devices=1)
    arrays, aps = {}, {}
    data = {name: np.asarray(inputs[name]) for name in _INS}
    data.update(packed(data))
    data.update({"const": constant_table()[0], "stack_const": stack_table()})
    for name in sorted(set(data) - PACKED_ONLY):
        a = np.ascontiguousarray(data[name])
        arrays[f"in_{name}"] = a
        aps[name] = nc.dram_tensor(f"in_{name}", a.shape, mybir.dt.from_np(a.dtype), kind="ExternalInput").ap()
    out = nc.dram_tensor("out", (B, T, C), F32, kind="ExternalOutput").ap()
    build(nc, aps, out)
    r = run_bass_kernel_spmd(nc, [arrays], core_ids=[0])
    return r.results[0]["out"]
```
